# Optimizing a Trainium2 kernel written in Bass

```python
import numpy as np
import jax
import jax.numpy as jnp

def _softmax(x, axis=-1):
    return jax.nn.softmax(x, axis=axis)

def _gelu(x):
    return jax.nn.gelu(x, approximate=True)

def _silu(x):
    return jax.nn.silu(x)

def _sigmoid(x):
    return jax.nn.sigmoid(x)

def _layernorm(x, axis=-1, eps=1e-05):
    m = jnp.mean(x, axis=axis, keepdims=True)
    v = jnp.var(x, axis=axis, keepdims=True)
    return (x - m) / jnp.sqrt(v + eps)

def _scatter_add(tgt, idx, src, axis=0):
    return tgt.at[idx].add(src)

def _segment_sum(src, seg, n):
    return jax.ops.segment_sum(src, seg, n)
kernel_name = 'mk_lm_tower_d2_tok_ids512_r4_80dea3'

def setup_inputs(seed: int=0):
    np.random.seed(seed)
    _w = jnp.asarray

    def _rec_inputs():
        import jax
        import jax.numpy as jnp
        _rk = jax.random.key(seed)
        x = jax.random.randint(jax.random.fold_in(_rk, 1), (1, 2048), 0, 64, jnp.int32)
        return x
    x = _rec_inputs()

    def _L0_tok_setup():
        import jax, jax.numpy as jnp
        import numpy as np
        VOCAB = 64
        key = jax.random.key(seed)
        k1, k2 = jax.random.split(key)
        x = jax.random.randint(k1, (8, 2048), 0, VOCAB, dtype=jnp.int32)
        weights = jax.random.normal(k2, (VOCAB, 128), dtype=jnp.float32)
        return {'x': x, 'weights': weights}
    _L0_tok_all = _L0_tok_setup()
    _L0_tok_in = {k: v for k, v in _L0_tok_all.items() if k in ('weights',)}
    del _L0_tok_all

    def _L0_attn_setup():
        import jax, jax.numpy as jnp
        import numpy as np
        NUM_HEAD = 8
        DIM_MODEL = 128
        DIM_HEAD = DIM_MODEL // NUM_HEAD
        LN_EPS = 1e-05
        key = jax.random.key(seed)
        ks = jax.random.split(key, 12)
        B, L, D = (4, 512, DIM_MODEL)
        s = 0.02
        return {'x': jax.random.normal(ks[0], (B, L, D), dtype=jnp.float32), 'Wq': jax.random.normal(ks[1], (D, D), dtype=jnp.float32) * s, 'bq': jnp.zeros((D,), dtype=jnp.float32), 'Wk': jax.random.normal(ks[2], (D, D), dtype=jnp.float32) * s, 'bk': jnp.zeros((D,), dtype=jnp.float32), 'Wv': jax.random.normal(ks[3], (D, D), dtype=jnp.float32) * s, 'bv': jnp.zeros((D,), dtype=jnp.float32), 'Wo': jax.random.normal(ks[4], (D, D), dtype=jnp.float32) * s, 'bo': jnp.zeros((D,), dtype=jnp.float32), 'gamma': jnp.ones((D,), dtype=jnp.float32), 'beta': jnp.zeros((D,), dtype=jnp.float32)}
    _L0_attn_all = _L0_attn_setup()
    _L0_attn_in = {k: v for k, v in _L0_attn_all.items() if k in ('Wq', 'bq', 'Wk', 'bk', 'Wv', 'bv', 'Wo', 'bo', 'gamma', 'beta')}
    del _L0_attn_all

    def _L0_ffn_setup():
        import jax, jax.numpy as jnp
        import numpy as np
        DIM = 128
        INTER = 64
        SHARED_INTER = 256
        N_EXPERTS = 64
        TOP_K = 6
        key = jax.random.key(seed)
        ks = jax.random.split(key, 8)
        s = 0.05
        return {'x': jax.random.normal(ks[0], (2, 128, DIM), jnp.float32), 'w_gate': jax.random.normal(ks[1], (N_EXPERTS, DIM), jnp.float32) * s, 'w1': jax.random.normal(ks[2], (N_EXPERTS, INTER, DIM), jnp.float32) * s, 'w2': jax.random.normal(ks[3], (N_EXPERTS, INTER, DIM), jnp.float32) * s, 'w3': jax.random.normal(ks[4], (N_EXPERTS, INTER, DIM), jnp.float32) * s, 'w_sg': jax.random.normal(ks[5], (SHARED_INTER, DIM), jnp.float32) * s, 'w_su': jax.random.normal(ks[6], (SHARED_INTER, DIM), jnp.float32) * s, 'w_sd': jax.random.normal(ks[7], (DIM, SHARED_INTER), jnp.float32) * s}
    _L0_ffn_all = _L0_ffn_setup()
    _L0_ffn_in = {k: v for k, v in _L0_ffn_all.items() if k in ('w_gate', 'w1', 'w2', 'w3', 'w_sg', 'w_su', 'w_sd')}
    del _L0_ffn_all

    def _L1_attn_setup():
        import jax, jax.numpy as jnp
        import numpy as np
        import math
        B, L = (4, 512)
        D_MODEL = 128
        D_STATE = 8
        D_CONV = 3
        EXPAND = 6
        D_INNER = D_MODEL * EXPAND
        DT_RANK = -(-D_MODEL // 16)
        N_HEADS = 8
        HEAD_DIM = D_MODEL // N_HEADS
        MB = 8
        TTT_BASE_LR = 1.0
        WIN = 5

        def layer_norm(x, w, b, eps=1e-06):
            mu = x.mean(-1, keepdims=True)
            var = jnp.mean((x - mu) ** 2, -1, keepdims=True)
            return (x - mu) * jax.lax.rsqrt(var + eps) * w + b

        def ln_l2_bwd(x, target, g, b, eps=1e-06):
            mu = x.mean(-1, keepdims=True)
            var = jnp.mean((x - mu) ** 2, -1, keepdims=True)
            std = jnp.sqrt(var + eps)
            xhat = (x - mu) / std
            gxh = (g * xhat + b - target) * g
            return (gxh - gxh.mean(-1, keepdims=True) - xhat * (gxh * xhat).mean(-1, keepdims=True)) / std

        def rotary(x, pos):
            d = x.shape[-1]
            inv = 1.0 / 10000.0 ** (jnp.arange(0, d, 2, dtype=jnp.float32) / d)
            f = pos[:, None] * inv[None, :]
            emb = jnp.concatenate([f, f], -1)
            cos, sin = (jnp.cos(emb), jnp.sin(emb))
            x1, x2 = jnp.split(x, 2, -1)
            return x * cos + jnp.concatenate([-x2, x1], -1) * sin

        def longhorn_scan(xc, dtv, k, q, dt_b, Dp):

            def step(S, inp):
                x_t, dt_t, k_t, q_t = inp
                d = jax.nn.sigmoid(dt_t + dt_b)
                k2 = k_t * k_t
                d = d / (1.0 + d * jnp.sum(k2, -1, keepdims=True))
                S = S * (1.0 - d[:, :, None] * k2[:, None, :]) + (d * x_t)[:, :, None] * k_t[:, None, :]
                y_t = jnp.einsum('bdn,bn->bd', S, q_t) + Dp * x_t
                return (S, y_t)
            S0 = jnp.zeros((xc.shape[0], xc.shape[2], k.shape[2]), xc.dtype)
            xs = (xc.transpose(1, 0, 2), dtv.transpose(1, 0, 2), k.transpose(1, 0, 2), q.transpose(1, 0, 2))
            _, ys = jax.lax.scan(step, S0, xs)
            return ys.transpose(1, 0, 2)

        def ttt_linear(xn, wq, wk, wv, W1, b1, nw, nb, lr_w, lr_b, tid, pn_w, pn_b):
            Bb, Ll, C = xn.shape
            nmb = Ll // MB
            pos = jnp.arange(Ll, dtype=jnp.float32)
            proj = lambda w: (xn @ w.T).reshape(Bb, Ll, N_HEADS, HEAD_DIM).transpose(0, 2, 1, 3)
            XQ, XK, XV = (proj(wq), proj(wk), proj(wv))
            XQ, XK = (rotary(XQ, pos), rotary(XK, pos))
            mb = lambda t: t.reshape(Bb, N_HEADS, nmb, MB, HEAD_DIM).transpose(2, 0, 1, 3, 4)
            Xc = xn.reshape(Bb, nmb, MB, C)
            lr = jax.nn.sigmoid(jnp.einsum('bnkc,hdc->bhnkd', Xc, lr_w) + lr_b[None, :, None, None, None])
            lr = lr.transpose(0, 1, 2, 4, 3)
            token_idx = jnp.clip(1.0 / jnp.arange(1, MB + 1, dtype=jnp.float32) + tid, 0.0, None)
            eta = token_idx[None, None, None, :, None] * (TTT_BASE_LR * lr / HEAD_DIM)
            gamma = nw[None, :, None, :]
            beta = nb[None, :, None, :]
            W1_0 = jnp.broadcast_to(W1[None], (Bb, N_HEADS, HEAD_DIM, HEAD_DIM))
            b1_0 = jnp.broadcast_to(b1[None], (Bb, N_HEADS, 1, HEAD_DIM))

            def step(carry, inp):
                W1c, b1c = carry
                xq, xk, xv, et = inp
                Z1 = xk @ W1c + b1c
                grad = ln_l2_bwd(Z1, xv - xk, gamma, beta)
                attn = jnp.tril(xq @ xk.transpose(0, 1, 3, 2))
                b1_bar = b1c - jnp.tril(et) @ grad
                Z1_bar = xq @ W1c - et * attn @ grad + b1_bar
                last_eta = et[:, :, -1, :, None]
                W1n = W1c - jnp.einsum('bhmd,bhme->bhde', last_eta * xk, grad)
                b1n = b1c - jnp.sum(last_eta * grad, -2, keepdims=True)
                out = xq + layer_norm(Z1_bar, gamma, beta)
                return ((W1n, b1n), out)
            _, outs = jax.lax.scan(step, (W1_0, b1_0), (mb(XQ), mb(XK), mb(XV), eta.transpose(2, 0, 1, 3, 4)))
            y = outs.transpose(1, 2, 0, 3, 4).reshape(Bb, N_HEADS, Ll, HEAD_DIM)
            y = y.transpose(0, 2, 1, 3).reshape(Bb, Ll, C)
            return layer_norm(y, pn_w, pn_b)

        def _forward(x, ln_w, ln_b, in_proj_w, conv_w, conv_b, x_proj_w, dt_head_w, dt_head_b, D_param, reduce_w, wq, wk, wv, W1, b1, ttt_norm_w, ttt_norm_b, lr_w, lr_b, token_idx_delta, post_norm_w, post_norm_b, qnet_w, gain_q_w, gain_k_w):
            residual = x
            xn = layer_norm(x, ln_w, ln_b)
            xz = xn @ in_proj_w.T
            xl, z = jnp.split(xz, 2, -1)
            Lx = xl.shape[1]
            xp = jnp.pad(xl, ((0, 0), (D_CONV - 1, 0), (0, 0)))
            xc = conv_b
            for w in range(D_CONV):
                xc = xc + xp[:, w:w + Lx, :] * conv_w[:, w]
            xc = jax.nn.silu(xc)
            xdbl = xc @ x_proj_w.T
            dt_in, k, q = jnp.split(xdbl, [DT_RANK, DT_RANK + D_STATE], -1)
            dtv = dt_in @ dt_head_w.T
            y = longhorn_scan(xc, dtv, k, q, dt_head_b, D_param)
            y = y * jax.nn.silu(z)
            h_red = y @ reduce_w.T
            c_hidden = ttt_linear(xn, wq, wk, wv, W1, b1, ttt_norm_w, ttt_norm_b, lr_w, lr_b, token_idx_delta, post_norm_w, post_norm_b)
            z_long = h_red @ qnet_w.T
            z_ttt = c_hidden @ qnet_w.T
            qg = xn @ gain_q_w.T
            kg = xn @ gain_k_w.T
            Ll = xn.shape[1]
            idx = jnp.clip(jnp.arange(Ll)[:, None] + jnp.arange(-WIN, WIN + 1)[None, :], 0, Ll - 1)
            kw = kg[:, idx, :]
            scores = jnp.einsum('blc,blwc->blw', qg, kw) / math.sqrt(D_MODEL)
            attn = jax.nn.softmax(scores, -1)
            gain = jax.nn.sigmoid(attn.max(-1) * 4.0 - 2.0)[..., None]
            out = z_long + gain * (z_ttt - z_long)
            return (out, residual, gain)

        def _reference_tuple_inner(x, ln_w, ln_b, in_proj_w, conv_w, conv_b, x_proj_w, dt_head_w, dt_head_b, D_param, reduce_w, wq, wk, wv, W1, b1, ttt_norm_w, ttt_norm_b, lr_w, lr_b, token_idx_delta, post_norm_w, post_norm_b, qnet_w, gain_q_w, gain_k_w):
            return _forward(x, ln_w, ln_b, in_proj_w, conv_w, conv_b, x_proj_w, dt_head_w, dt_head_b, D_param, reduce_w, wq, wk, wv, W1, b1, ttt_norm_w, ttt_norm_b, lr_w, lr_b, token_idx_delta, post_norm_w, post_norm_b, qnet_w, gain_q_w, gain_k_w)
        key = jax.random.key(seed)
        ks = jax.random.split(key, 16)
        g = lambda k, shape, s: jax.random.normal(k, shape, jnp.float32) * s
        return {'x': g(ks[0], (B, L, D_MODEL), 1.0), 'ln_w': jnp.ones((D_MODEL,), jnp.float32), 'ln_b': jnp.zeros((D_MODEL,), jnp.float32), 'in_proj_w': g(ks[1], (2 * D_INNER, D_MODEL), D_MODEL ** (-0.5)), 'conv_w': g(ks[2], (D_INNER, D_CONV), D_CONV ** (-0.5)), 'conv_b': jnp.zeros((D_INNER,), jnp.float32), 'x_proj_w': g(ks[3], (DT_RANK + 2 * D_STATE, D_INNER), D_INNER ** (-0.5)), 'dt_head_w': g(ks[4], (D_INNER, DT_RANK), DT_RANK ** (-0.5)), 'dt_head_b': g(ks[5], (D_INNER,), 0.1), 'D_param': jnp.ones((D_INNER,), jnp.float32), 'reduce_w': g(ks[6], (D_MODEL, D_INNER), D_INNER ** (-0.5)), 'wq': g(ks[7], (D_MODEL, D_MODEL), D_MODEL ** (-0.5)), 'wk': g(ks[8], (D_MODEL, D_MODEL), D_MODEL ** (-0.5)), 'wv': g(ks[9], (D_MODEL, D_MODEL), D_MODEL ** (-0.5)), 'W1': g(ks[10], (N_HEADS, HEAD_DIM, HEAD_DIM), HEAD_DIM ** (-0.5)), 'b1': jnp.zeros((N_HEADS, 1, HEAD_DIM), jnp.float32), 'ttt_norm_w': jnp.ones((N_HEADS, HEAD_DIM), jnp.float32), 'ttt_norm_b': jnp.zeros((N_HEADS, HEAD_DIM), jnp.float32), 'lr_w': g(ks[11], (N_HEADS, 1, D_MODEL), D_MODEL ** (-0.5)), 'lr_b': jnp.zeros((N_HEADS,), jnp.float32), 'token_idx_delta': jnp.zeros((MB,), jnp.float32), 'post_norm_w': jnp.ones((D_MODEL,), jnp.float32), 'post_norm_b': jnp.zeros((D_MODEL,), jnp.float32), 'qnet_w': g(ks[12], (D_MODEL, D_MODEL), D_MODEL ** (-0.5)), 'gain_q_w': g(ks[13], (D_MODEL, D_MODEL), D_MODEL ** (-0.5)), 'gain_k_w': g(ks[14], (D_MODEL, D_MODEL), D_MODEL ** (-0.5))}
    _L1_attn_all = _L1_attn_setup()
    _L1_attn_in = {k: v for k, v in _L1_attn_all.items() if k in ('ln_w', 'ln_b', 'in_proj_w', 'conv_w', 'conv_b', 'x_proj_w', 'dt_head_w', 'dt_head_b', 'D_param', 'reduce_w', 'wq', 'wk', 'wv', 'W1', 'b1', 'ttt_norm_w', 'ttt_norm_b', 'lr_w', 'lr_b', 'token_idx_delta', 'post_norm_w', 'post_norm_b', 'qnet_w', 'gain_q_w', 'gain_k_w')}
    del _L1_attn_all

    def _L1_ffn_setup():
        import jax, jax.numpy as jnp
        import numpy as np
        N_DIM = 128
        HEADS = 8
        NUM_EXPERTS = 16384
        NUM_KEYS = 64
        DIM_KEY = 64
        TOPK = 16
        SCALE = 0.02
        key = jax.random.key(seed)
        k0, k1, k2, k3, k4 = jax.random.split(key, 5)
        x = jax.random.normal(k0, (1, 512, N_DIM), dtype=jnp.float32)
        W_q = jax.random.normal(k1, (N_DIM, 2 * HEADS * DIM_KEY), dtype=jnp.float32) * SCALE
        keys = jax.random.normal(k2, (HEADS, NUM_KEYS, 2, DIM_KEY), dtype=jnp.float32) * SCALE
        down_embed = jax.random.normal(k3, (NUM_EXPERTS, N_DIM), dtype=jnp.float32) * SCALE
        up_embed = jax.random.normal(k4, (NUM_EXPERTS, N_DIM), dtype=jnp.float32) * SCALE
        return {'x': x, 'W_q': W_q, 'keys': keys, 'down_embed': down_embed, 'up_embed': up_embed}
    _L1_ffn_all = _L1_ffn_setup()
    _L1_ffn_in = {k: v for k, v in _L1_ffn_all.items() if k in ('W_q', 'keys', 'down_embed', 'up_embed')}
    del _L1_ffn_all
    return {'x': x, 'L0_tok_weights': _L0_tok_in['weights'], 'L0_attn_Wq': _L0_attn_in['Wq'], 'L0_attn_bq': _L0_attn_in['bq'], 'L0_attn_Wk': _L0_attn_in['Wk'], 'L0_attn_bk': _L0_attn_in['bk'], 'L0_attn_Wv': _L0_attn_in['Wv'], 'L0_attn_bv': _L0_attn_in['bv'], 'L0_attn_Wo': _L0_attn_in['Wo'], 'L0_attn_bo': _L0_attn_in['bo'], 'L0_attn_gamma': _L0_attn_in['gamma'], 'L0_attn_beta': _L0_attn_in['beta'], 'L0_ffn_w_gate': _L0_ffn_in['w_gate'], 'L0_ffn_w1': _L0_ffn_in['w1'], 'L0_ffn_w2': _L0_ffn_in['w2'], 'L0_ffn_w3': _L0_ffn_in['w3'], 'L0_ffn_w_sg': _L0_ffn_in['w_sg'], 'L0_ffn_w_su': _L0_ffn_in['w_su'], 'L0_ffn_w_sd': _L0_ffn_in['w_sd'], 'L1_attn_ln_w': _L1_attn_in['ln_w'], 'L1_attn_ln_b': _L1_attn_in['ln_b'], 'L1_attn_in_proj_w': _L1_attn_in['in_proj_w'], 'L1_attn_conv_w': _L1_attn_in['conv_w'], 'L1_attn_conv_b': _L1_attn_in['conv_b'], 'L1_attn_x_proj_w': _L1_attn_in['x_proj_w'], 'L1_attn_dt_head_w': _L1_attn_in['dt_head_w'], 'L1_attn_dt_head_b': _L1_attn_in['dt_head_b'], 'L1_attn_D_param': _L1_attn_in['D_param'], 'L1_attn_reduce_w': _L1_attn_in['reduce_w'], 'L1_attn_wq': _L1_attn_in['wq'], 'L1_attn_wk': _L1_attn_in['wk'], 'L1_attn_wv': _L1_attn_in['wv'], 'L1_attn_W1': _L1_attn_in['W1'], 'L1_attn_b1': _L1_attn_in['b1'], 'L1_attn_ttt_norm_w': _L1_attn_in['ttt_norm_w'], 'L1_attn_ttt_norm_b': _L1_attn_in['ttt_norm_b'], 'L1_attn_lr_w': _L1_attn_in['lr_w'], 'L1_attn_lr_b': _L1_attn_in['lr_b'], 'L1_attn_token_idx_delta': _L1_attn_in['token_idx_delta'], 'L1_attn_post_norm_w': _L1_attn_in['post_norm_w'], 'L1_attn_post_norm_b': _L1_attn_in['post_norm_b'], 'L1_attn_qnet_w': _L1_attn_in['qnet_w'], 'L1_attn_gain_q_w': _L1_attn_in['gain_q_w'], 'L1_attn_gain_k_w': _L1_attn_in['gain_k_w'], 'L1_ffn_W_q': _L1_ffn_in['W_q'], 'L1_ffn_keys': _L1_ffn_in['keys'], 'L1_ffn_down_embed': _L1_ffn_in['down_embed'], 'L1_ffn_up_embed': _L1_ffn_in['up_embed']}

def reference(x, L0_tok_weights, L0_attn_Wq, L0_attn_bq, L0_attn_Wk, L0_attn_bk, L0_attn_Wv, L0_attn_bv, L0_attn_Wo, L0_attn_bo, L0_attn_gamma, L0_attn_beta, L0_ffn_w_gate, L0_ffn_w1, L0_ffn_w2, L0_ffn_w3, L0_ffn_w_sg, L0_ffn_w_su, L0_ffn_w_sd, L1_attn_ln_w, L1_attn_ln_b, L1_attn_in_proj_w, L1_attn_conv_w, L1_attn_conv_b, L1_attn_x_proj_w, L1_attn_dt_head_w, L1_attn_dt_head_b, L1_attn_D_param, L1_attn_reduce_w, L1_attn_wq, L1_attn_wk, L1_attn_wv, L1_attn_W1, L1_attn_b1, L1_attn_ttt_norm_w, L1_attn_ttt_norm_b, L1_attn_lr_w, L1_attn_lr_b, L1_attn_token_idx_delta, L1_attn_post_norm_w, L1_attn_post_norm_b, L1_attn_qnet_w, L1_attn_gain_q_w, L1_attn_gain_k_w, L1_ffn_W_q, L1_ffn_keys, L1_ffn_down_embed, L1_ffn_up_embed):
    import jax
    import jax.numpy as jnp

    def _L0_tok_ref(x, weights):
        import jax, jax.numpy as jnp
        import numpy as np
        VOCAB = 64
        oh = jax.nn.one_hot(x, VOCAB, dtype=weights.dtype)
        return jnp.einsum('bsv,vd->bsd', oh, weights)

    def _L0_attn_ref(x, Wq, bq, Wk, bk, Wv, bv, Wo, bo, gamma, beta):
        import jax, jax.numpy as jnp
        import numpy as np
        NUM_HEAD = 8
        DIM_MODEL = 128
        DIM_HEAD = DIM_MODEL // NUM_HEAD
        LN_EPS = 1e-05
        B, L, D = x.shape
        H, dh = (NUM_HEAD, D // NUM_HEAD)
        Q = x @ Wq.T + bq
        K = x @ Wk.T + bk
        V = x @ Wv.T + bv
        Q = Q.reshape(B * H, L, dh)
        K = K.reshape(B * H, L, dh)
        V = V.reshape(B * H, L, dh)
        scale = dh ** (-0.5)
        attn = jax.nn.softmax(jnp.einsum('bqd,bkd->bqk', Q, K) * scale, axis=-1)
        context = jnp.einsum('bqk,bkd->bqd', attn, V)
        context = context.reshape(B, L, D)
        out = context @ Wo.T + bo
        out = out + x
        mu = jnp.mean(out, axis=-1, keepdims=True)
        var = jnp.mean(jnp.square(out - mu), axis=-1, keepdims=True)
        out = (out - mu) / jnp.sqrt(var + LN_EPS) * gamma + beta
        return out

    def _L0_ffn_ref(x, w_gate, w1, w2, w3, w_sg, w_su, w_sd):
        import jax, jax.numpy as jnp
        import numpy as np
        DIM = 128
        INTER = 64
        SHARED_INTER = 256
        N_EXPERTS = 64
        TOP_K = 6
        orig_shape = x.shape
        xf = x.reshape(-1, x.shape[-1])
        T = xf.shape[0]
        scores = xf @ w_gate.T
        top_vals, top_idx = jax.lax.top_k(scores, TOP_K)
        expert_weights = jax.nn.softmax(top_vals, axis=-1)
        comb = jnp.zeros(scores.shape, xf.dtype).at[jnp.arange(T)[:, None], top_idx].set(expert_weights)
        x1 = jax.nn.silu(jnp.einsum('td,eid->tei', xf, w1))
        x3 = jnp.einsum('td,eid->tei', xf, w3)
        y = jnp.einsum('tei,eid->ted', x1 * x3, w2)
        routed = jnp.einsum('ted,te->td', y, comb)
        shared = jax.nn.silu(xf @ w_sg.T) * (xf @ w_su.T) @ w_sd.T
        return (routed + shared).reshape(orig_shape)

    def _L1_attn_ref(x, ln_w, ln_b, in_proj_w, conv_w, conv_b, x_proj_w, dt_head_w, dt_head_b, D_param, reduce_w, wq, wk, wv, W1, b1, ttt_norm_w, ttt_norm_b, lr_w, lr_b, token_idx_delta, post_norm_w, post_norm_b, qnet_w, gain_q_w, gain_k_w):
        import jax, jax.numpy as jnp
        import numpy as np
        import math
        B, L = (4, 512)
        D_MODEL = 128
        D_STATE = 8
        D_CONV = 3
        EXPAND = 6
        D_INNER = D_MODEL * EXPAND
        DT_RANK = -(-D_MODEL // 16)
        N_HEADS = 8
        HEAD_DIM = D_MODEL // N_HEADS
        MB = 8
        TTT_BASE_LR = 1.0
        WIN = 5

        def layer_norm(x, w, b, eps=1e-06):
            mu = x.mean(-1, keepdims=True)
            var = jnp.mean((x - mu) ** 2, -1, keepdims=True)
            return (x - mu) * jax.lax.rsqrt(var + eps) * w + b

        def ln_l2_bwd(x, target, g, b, eps=1e-06):
            mu = x.mean(-1, keepdims=True)
            var = jnp.mean((x - mu) ** 2, -1, keepdims=True)
            std = jnp.sqrt(var + eps)
            xhat = (x - mu) / std
            gxh = (g * xhat + b - target) * g
            return (gxh - gxh.mean(-1, keepdims=True) - xhat * (gxh * xhat).mean(-1, keepdims=True)) / std

        def rotary(x, pos):
            d = x.shape[-1]
            inv = 1.0 / 10000.0 ** (jnp.arange(0, d, 2, dtype=jnp.float32) / d)
            f = pos[:, None] * inv[None, :]
            emb = jnp.concatenate([f, f], -1)
            cos, sin = (jnp.cos(emb), jnp.sin(emb))
            x1, x2 = jnp.split(x, 2, -1)
            return x * cos + jnp.concatenate([-x2, x1], -1) * sin

        def longhorn_scan(xc, dtv, k, q, dt_b, Dp):

            def step(S, inp):
                x_t, dt_t, k_t, q_t = inp
                d = jax.nn.sigmoid(dt_t + dt_b)
                k2 = k_t * k_t
                d = d / (1.0 + d * jnp.sum(k2, -1, keepdims=True))
                S = S * (1.0 - d[:, :, None] * k2[:, None, :]) + (d * x_t)[:, :, None] * k_t[:, None, :]
                y_t = jnp.einsum('bdn,bn->bd', S, q_t) + Dp * x_t
                return (S, y_t)
            S0 = jnp.zeros((xc.shape[0], xc.shape[2], k.shape[2]), xc.dtype)
            xs = (xc.transpose(1, 0, 2), dtv.transpose(1, 0, 2), k.transpose(1, 0, 2), q.transpose(1, 0, 2))
            _, ys = jax.lax.scan(step, S0, xs)
            return ys.transpose(1, 0, 2)

        def ttt_linear(xn, wq, wk, wv, W1, b1, nw, nb, lr_w, lr_b, tid, pn_w, pn_b):
            Bb, Ll, C = xn.shape
            nmb = Ll // MB
            pos = jnp.arange(Ll, dtype=jnp.float32)
            proj = lambda w: (xn @ w.T).reshape(Bb, Ll, N_HEADS, HEAD_DIM).transpose(0, 2, 1, 3)
            XQ, XK, XV = (proj(wq), proj(wk), proj(wv))
            XQ, XK = (rotary(XQ, pos), rotary(XK, pos))
            mb = lambda t: t.reshape(Bb, N_HEADS, nmb, MB, HEAD_DIM).transpose(2, 0, 1, 3, 4)
            Xc = xn.reshape(Bb, nmb, MB, C)
            lr = jax.nn.sigmoid(jnp.einsum('bnkc,hdc->bhnkd', Xc, lr_w) + lr_b[None, :, None, None, None])
            lr = lr.transpose(0, 1, 2, 4, 3)
            token_idx = jnp.clip(1.0 / jnp.arange(1, MB + 1, dtype=jnp.float32) + tid, 0.0, None)
            eta = token_idx[None, None, None, :, None] * (TTT_BASE_LR * lr / HEAD_DIM)
            gamma = nw[None, :, None, :]
            beta = nb[None, :, None, :]
            W1_0 = jnp.broadcast_to(W1[None], (Bb, N_HEADS, HEAD_DIM, HEAD_DIM))
            b1_0 = jnp.broadcast_to(b1[None], (Bb, N_HEADS, 1, HEAD_DIM))

            def step(carry, inp):
                W1c, b1c = carry
                xq, xk, xv, et = inp
                Z1 = xk @ W1c + b1c
                grad = ln_l2_bwd(Z1, xv - xk, gamma, beta)
                attn = jnp.tril(xq @ xk.transpose(0, 1, 3, 2))
                b1_bar = b1c - jnp.tril(et) @ grad
                Z1_bar = xq @ W1c - et * attn @ grad + b1_bar
                last_eta = et[:, :, -1, :, None]
                W1n = W1c - jnp.einsum('bhmd,bhme->bhde', last_eta * xk, grad)
                b1n = b1c - jnp.sum(last_eta * grad, -2, keepdims=True)
                out = xq + layer_norm(Z1_bar, gamma, beta)
                return ((W1n, b1n), out)
            _, outs = jax.lax.scan(step, (W1_0, b1_0), (mb(XQ), mb(XK), mb(XV), eta.transpose(2, 0, 1, 3, 4)))
            y = outs.transpose(1, 2, 0, 3, 4).reshape(Bb, N_HEADS, Ll, HEAD_DIM)
            y = y.transpose(0, 2, 1, 3).reshape(Bb, Ll, C)
            return layer_norm(y, pn_w, pn_b)

        def _forward(x, ln_w, ln_b, in_proj_w, conv_w, conv_b, x_proj_w, dt_head_w, dt_head_b, D_param, reduce_w, wq, wk, wv, W1, b1, ttt_norm_w, ttt_norm_b, lr_w, lr_b, token_idx_delta, post_norm_w, post_norm_b, qnet_w, gain_q_w, gain_k_w):
            residual = x
            xn = layer_norm(x, ln_w, ln_b)
            xz = xn @ in_proj_w.T
            xl, z = jnp.split(xz, 2, -1)
            Lx = xl.shape[1]
            xp = jnp.pad(xl, ((0, 0), (D_CONV - 1, 0), (0, 0)))
            xc = conv_b
            for w in range(D_CONV):
                xc = xc + xp[:, w:w + Lx, :] * conv_w[:, w]
            xc = jax.nn.silu(xc)
            xdbl = xc @ x_proj_w.T
            dt_in, k, q = jnp.split(xdbl, [DT_RANK, DT_RANK + D_STATE], -1)
            dtv = dt_in @ dt_head_w.T
            y = longhorn_scan(xc, dtv, k, q, dt_head_b, D_param)
            y = y * jax.nn.silu(z)
            h_red = y @ reduce_w.T
            c_hidden = ttt_linear(xn, wq, wk, wv, W1, b1, ttt_norm_w, ttt_norm_b, lr_w, lr_b, token_idx_delta, post_norm_w, post_norm_b)
            z_long = h_red @ qnet_w.T
            z_ttt = c_hidden @ qnet_w.T
            qg = xn @ gain_q_w.T
            kg = xn @ gain_k_w.T
            Ll = xn.shape[1]
            idx = jnp.clip(jnp.arange(Ll)[:, None] + jnp.arange(-WIN, WIN + 1)[None, :], 0, Ll - 1)
            kw = kg[:, idx, :]
            scores = jnp.einsum('blc,blwc->blw', qg, kw) / math.sqrt(D_MODEL)
            attn = jax.nn.softmax(scores, -1)
            gain = jax.nn.sigmoid(attn.max(-1) * 4.0 - 2.0)[..., None]
            out = z_long + gain * (z_ttt - z_long)
            return (out, residual, gain)

        def _reference_tuple_inner(x, ln_w, ln_b, in_proj_w, conv_w, conv_b, x_proj_w, dt_head_w, dt_head_b, D_param, reduce_w, wq, wk, wv, W1, b1, ttt_norm_w, ttt_norm_b, lr_w, lr_b, token_idx_delta, post_norm_w, post_norm_b, qnet_w, gain_q_w, gain_k_w):
            return _forward(x, ln_w, ln_b, in_proj_w, conv_w, conv_b, x_proj_w, dt_head_w, dt_head_b, D_param, reduce_w, wq, wk, wv, W1, b1, ttt_norm_w, ttt_norm_b, lr_w, lr_b, token_idx_delta, post_norm_w, post_norm_b, qnet_w, gain_q_w, gain_k_w)
        return _reference_tuple_inner(x, ln_w, ln_b, in_proj_w, conv_w, conv_b, x_proj_w, dt_head_w, dt_head_b, D_param, reduce_w, wq, wk, wv, W1, b1, ttt_norm_w, ttt_norm_b, lr_w, lr_b, token_idx_delta, post_norm_w, post_norm_b, qnet_w, gain_q_w, gain_k_w)[0]

    def _L1_ffn_ref(x, W_q, keys, down_embed, up_embed):
        import jax, jax.numpy as jnp
        import numpy as np
        N_DIM = 128
        HEADS = 8
        NUM_EXPERTS = 16384
        NUM_KEYS = 64
        DIM_KEY = 64
        TOPK = 16
        SCALE = 0.02
        b, n, d = x.shape
        q = (x @ W_q).reshape(b, n, 2, HEADS, DIM_KEY).transpose(2, 0, 1, 3, 4)
        sim = jnp.einsum('pbnhd,hkpd->pbnhk', q, keys)
        sx, ix = jax.lax.top_k(sim[0], TOPK)
        sy, iy = jax.lax.top_k(sim[1], TOPK)
        all_scores = (sx[..., :, None] + sy[..., None, :]).reshape(b, n, HEADS, TOPK * TOPK)
        scores, pk_idx = jax.lax.top_k(all_scores, TOPK)
        w_down = down_embed[pk_idx]
        w_up = up_embed[pk_idx]
        h = jnp.einsum('bnd,bnhkd->bnhk', x, w_down)
        h = jax.nn.gelu(h, approximate=False)
        h = jax.nn.softmax(scores, axis=-1) * h
        return jnp.einsum('bnhk,bnhkd->bnd', h, w_up)
    h = _L0_tok_ref(x, L0_tok_weights)
    h = h + _L0_attn_ref(_layernorm(h, axis=-1), L0_attn_Wq, L0_attn_bq, L0_attn_Wk, L0_attn_bk, L0_attn_Wv, L0_attn_bv, L0_attn_Wo, L0_attn_bo, L0_attn_gamma, L0_attn_beta)
    h = h + _L0_ffn_ref(_layernorm(h, axis=-1), L0_ffn_w_gate, L0_ffn_w1, L0_ffn_w2, L0_ffn_w3, L0_ffn_w_sg, L0_ffn_w_su, L0_ffn_w_sd)
    h = h + _L1_attn_ref(_layernorm(h, axis=-1), L1_attn_ln_w, L1_attn_ln_b, L1_attn_in_proj_w, L1_attn_conv_w, L1_attn_conv_b, L1_attn_x_proj_w, L1_attn_dt_head_w, L1_attn_dt_head_b, L1_attn_D_param, L1_attn_reduce_w, L1_attn_wq, L1_attn_wk, L1_attn_wv, L1_attn_W1, L1_attn_b1, L1_attn_ttt_norm_w, L1_attn_ttt_norm_b, L1_attn_lr_w, L1_attn_lr_b, L1_attn_token_idx_delta, L1_attn_post_norm_w, L1_attn_post_norm_b, L1_attn_qnet_w, L1_attn_gain_q_w, L1_attn_gain_k_w)
    h = h + _L1_ffn_ref(_layernorm(h, axis=-1), L1_ffn_W_q, L1_ffn_keys, L1_ffn_down_embed, L1_ffn_up_embed)
    return h

_drawn_inputs = setup_inputs


def setup_inputs(seed=0):
    import zlib

    import numpy as np

    out = dict(_drawn_inputs(seed))
    spreads = {'L0_attn_bq': (0.0, 0.8),
     'L0_attn_bk': (0.0, 0.8),
     'L0_attn_bv': (0.0, 0.8),
     'L0_attn_bo': (0.0, 0.1),
     'L0_attn_gamma': (1.0, 0.2),
     'L0_attn_beta': (0.0, 0.1),
     'L1_attn_ln_w': (1.0, 0.2),
     'L1_attn_ln_b': (0.0, 0.1),
     'L1_attn_conv_b': (0.0, 0.306),
     'L1_attn_D_param': (1.0, 0.574),
     'L1_attn_b1': (0.0, 0.639),
     'L1_attn_ttt_norm_w': (1.0, 0.6),
     'L1_attn_ttt_norm_b': (0.0, 0.746),
     'L1_attn_lr_b': (0.0, 2.0),
     'L1_attn_token_idx_delta': (0.0, 0.1),
     'L1_attn_post_norm_w': (1.0, 0.2),
     'L1_attn_post_norm_b': (0.0, 0.562)}
    factors = {'L0_attn_Wq': 8.0,
     'L0_attn_Wk': 8.0,
     'L0_attn_Wv': 8.0,
     'L0_attn_Wo': 8.0,
     'L1_attn_dt_head_w': 4.841,
     'L1_attn_dt_head_b': 32.275,
     'L1_attn_wk': 2.859,
     'L1_attn_wv': 4.302,
     'L1_attn_lr_w': 8.0,
     'L1_ffn_W_q': 8.0,
     'L1_ffn_keys': 8.0,
     'L1_ffn_down_embed': 8.0,
     'L1_ffn_up_embed': 8.0}
    for name, (base, spread) in spreads.items():
        noise = np.random.default_rng([zlib.crc32(name.encode()), seed]).standard_normal(out[name].shape)
        drawn = base * np.exp(spread * noise) if base else spread * noise
        out[name] = jnp.asarray(drawn.astype(out[name].dtype))
    for name, factor in factors.items():
        out[name] = (out[name] * factor).astype(out[name].dtype)
    return out
```

```python
from contextlib import ExitStack
import numpy as np
import concourse.bass as bass
from concourse import mybir

F32 = mybir.dt.float32
BF16 = mybir.dt.bfloat16
I32 = mybir.dt.int32
ACT = mybir.ActivationFunctionType
ALU = mybir.AluOpType
AX_X = mybir.AxisListType.X

T = 2048
D = 128
VOCAB = 64
CH = 512
NCH = T // CH


class Scope:

    def __init__(self, nc, tag):
        self.nc, self.tag, self.stack, self.sems = nc, tag, ExitStack(), []

    def __enter__(self):
        self.stack.__enter__()
        return self

    def __exit__(self, *a):
        if self.sems:
            with self.nc.Block() as block:
                @block.gpsimd
                def _(pool):
                    for sem in self.sems:
                        pool.sem_clear(sem)
        return self.stack.__exit__(*a)

    def sb(self, name, shape, dt=F32):
        return self.stack.enter_context(self.nc.sbuf_tensor(f"{self.tag}_{name}", shape, dt))

    def ps(self, name, shape, dt=F32):
        return self.stack.enter_context(self.nc.psum_tensor(f"{self.tag}_{name}_ps", shape, dt))

    def sem(self, name):
        self.sems.append(self.stack.enter_context(self.nc.semaphore(f"{self.tag}_{name}")))
        return self.sems[-1]


def layer_norm(nc, tag, src, dst, ones_over_d, eps, gamma=None, beta=None, add_to=None):
    with Scope(nc, tag) as s:
        centred = s.sb("centred", [D, NCH, CH])
        squared = s.sb("squared", [D, NCH, CH])
        std = s.sb("std", [D, NCH, CH])
        eps_col = s.sb("eps", [D, 1])
        mean_ps = s.ps("mean", [D, NCH, CH])
        var_ps = s.ps("var", [D, NCH, CH])
        eps_set, mean_ready, centred_ready, squared_ready, var_ready, std_ready, rstd_ready, scaled_ready, done = (
            s.sem(n) for n in ("eps_set", "mean_ready", "centred_ready", "squared_ready", "var_ready",
                               "std_ready", "rstd_ready", "scaled_ready", "done"))
        cols = lambda c: slice(c * CH, (c + 1) * CH)
        with nc.Block() as block:
            @block.gpsimd
            def _(pool):
                pool.memset(eps_col[:], eps).then_inc(eps_set, 1)

            @block.tensor
            def _(pe):
                for c in range(NCH):
                    nc.tensor.matmul(mean_ps[:, c, :], ones_over_d[:], src[:, cols(c)],
                                     start=True, stop=True).then_inc(mean_ready, 1)
                for c in range(NCH):
                    pe.wait_ge(squared_ready, c + 1)
                    nc.tensor.matmul(var_ps[:, c, :], ones_over_d[:], squared[:, c, :],
                                     start=True, stop=True).then_inc(var_ready, 1)

            @block.scalar
            def _(act):
                act.wait_ge(eps_set, 1)
                for c in range(NCH):
                    act.wait_ge(centred_ready, c + 1)
                    nc.scalar.activation(squared[:, c, :], centred[:, c, :], ACT.Square).then_inc(squared_ready, 1)
                for c in range(NCH):
                    act.wait_ge(var_ready, c + 1)
                    nc.scalar.activation(std[:, c, :], var_ps[:, c, :], ACT.Sqrt,
                                         bias=eps_col[:]).then_inc(std_ready, 1)

            @block.vector
            def _(dve):
                for c in range(NCH):
                    dve.wait_ge(mean_ready, c + 1)
                    nc.vector.tensor_tensor(centred[:, c, :], src[:, cols(c)], mean_ps[:, c, :],
                                            ALU.subtract).then_inc(centred_ready, 1)
                for c in range(NCH):
                    dve.wait_ge(std_ready, c + 1)
                    nc.vector.reciprocal(std[:, c, :], std[:, c, :]).then_inc(rstd_ready, 1)
                    dve.wait_ge(rstd_ready, c + 1)
                    if gamma is None:
                        nc.vector.tensor_tensor(dst[:, cols(c)], centred[:, c, :], std[:, c, :],
                                                ALU.mult).then_inc(done, 1)
                        continue
                    nc.vector.scalar_tensor_tensor(out=squared[:, c, :], in0=centred[:, c, :], scalar=gamma,
                                                   in1=std[:, c, :], op0=ALU.mult,
                                                   op1=ALU.mult).then_inc(scaled_ready, 1)
                    dve.wait_ge(scaled_ready, c + 1)
                    if add_to is None:
                        nc.vector.tensor_scalar(dst[:, cols(c)], squared[:, c, :], beta, None,
                                                ALU.add).then_inc(done, 1)
                    else:
                        nc.vector.scalar_tensor_tensor(out=dst[:, cols(c)], in0=squared[:, c, :], scalar=beta,
                                                       in1=add_to[:, cols(c)], op0=ALU.add,
                                                       op1=ALU.add).then_inc(done, 1)


def embed(nc, ids, table, h):
    with Scope(nc, "emb") as s:
        ids_i = s.sb("ids_i", [VOCAB, T], I32)
        ids_f = s.sb("ids_f", [VOCAB, T])
        vocab_i = s.sb("vocab_i", [VOCAB, 1], I32)
        vocab_f = s.sb("vocab_f", [VOCAB, 1])
        onehot = s.sb("onehot", [VOCAB, T])
        table_sb = s.sb("table", [VOCAB, D])
        h_ps = s.ps("h", [D, NCH, CH])
        loaded, vocab_set, cast, onehot_ready, h_ready, done = (
            s.sem(n) for n in ("loaded", "vocab_set", "cast", "onehot_ready", "h_ready", "done"))
        with nc.Block() as block:
            @block.sync
            def _(sp):
                sp.dma_start(ids_i[:], ids.partition_broadcast(VOCAB)).then_inc(loaded, 16)
                sp.dma_start(table_sb[:], table).then_inc(loaded, 16)

            @block.gpsimd
            def _(pool):
                pool.iota(vocab_i[:], pattern=[[0, 1]], base=0, channel_multiplier=1).then_inc(vocab_set, 1)

            @block.vector
            def _(dve):
                dve.wait_ge(vocab_set, 1)
                nc.vector.tensor_copy(vocab_f[:], vocab_i[:]).then_inc(cast, 1)
                dve.wait_ge(loaded, 32)
                nc.vector.tensor_copy(ids_f[:], ids_i[:]).then_inc(cast, 1)
                dve.wait_ge(cast, 2)
                nc.vector.tensor_scalar(onehot[:], ids_f[:], vocab_f[:, 0:1], None,
                                        ALU.is_equal).then_inc(onehot_ready, 1)
                for c in range(NCH):
                    dve.wait_ge(h_ready, c + 1)
                    nc.vector.tensor_copy(h[:, c * CH:(c + 1) * CH], h_ps[:, c, :]).then_inc(done, 1)

            @block.tensor
            def _(pe):
                pe.wait_ge(onehot_ready, 1)
                for c in range(NCH):
                    nc.tensor.matmul(h_ps[:, c, :], table_sb[:], onehot[:, c * CH:(c + 1) * CH],
                                     start=True, stop=True).then_inc(h_ready, 1)


HEADS = 8
DH = D // HEADS
HT = T // HEADS
QCH = T // CH
KB = T // D
SPLIT = 6 * DH
MROWS = SPLIT + 2
SLOTS = HEADS + 2


def attention0(nc, dram, xn, ao):
    with Scope(nc, "att") as s:
        wq, wk = s.sb("wq", [D, HEADS * D]), s.sb("wk", [D, HEADS * D])
        bq, bk = s.sb("bq", [D, HEADS]), s.sb("bk", [D, HEADS])
        wv, bv = s.sb("wv", [D, D]), s.sb("bv", [D, D])
        wo, bo = s.sb("wo", [DH, HEADS * D]), s.sb("bo", [D, 1])
        masks = s.sb("masks", [D, 4])
        fold = s.sb("fold", [D, 48])
        ident = s.sb("ident", [D, D], BF16)
        ident_f = s.sb("ident_f", [D, D])
        q_all = s.sb("q_all", [D, SLOTS * T], BF16)
        k_all = s.sb("k_all", [D, SLOTS * T], BF16)
        v_all = s.sb("v_all", [D, T // D, HEADS, 2 * DH])
        v_head = s.sb("v_head", [D, 2, HEADS, 2 * DH])
        t0, t1 = s.sb("t0", [D, 2, CH]), s.sb("t1", [D, 2, CH])
        part1, part2 = s.sb("part1", [D, 2, CH], BF16), s.sb("part2", [D, 2, CH], BF16)
        half_max = s.sb("half_max", [D, KB, 2])
        neg_max = s.sb("neg_max", [D, KB])
        neg_parts = s.sb("neg_parts", [D, KB, 2], BF16)
        probs = s.sb("probs", [D, 2, CH])
        acc_sb = s.sb("acc_sb", [D, CH])
        rsum = s.sb("rsum", [DH, CH])
        ctx = s.sb("ctx", [DH, T])
        st_ps = s.ps("st", [D, 2, CH])
        s1_ps = s.ps("s1", [D, 2, 2 * CH])
        acc_ps = s.ps("acc", [D, CH])
        misc_ps = s.ps("misc", [D, CH])
        names = ("loaded v_ready v_stored consts_set proj_ready t0_ready part1_ready t1_ready part2_ready "
                 "stacked s1_ready half_done neg_ready lo_ready parts_ready mt_ready mrows_ready st_ready "
                 "exp_done pv_done acc_stored fold_ready rsum_ready ctx_ready out_ready out_stored "
                 "misc_free v_head_ready pool_passed").split()
        S = {n: s.sem(n) for n in names}
        groups = [(w, b, a, g) for w, b, a in ((wq, bq, q_all), (wk, bk, k_all)) for g in range(4)]
        NG = len(groups)

        with nc.Block() as block:
            @block.sync
            def _(sp):
                for dst, src in ((wq, "att_wq"), (wk, "att_wk"), (bq, "att_bq"), (bk, "att_bk"), (wv, "att_wv"),
                                 (wo, "att_wo"), (masks, "att_masks"), (fold, "att_fold"), (ident_f, "ident")):
                    sp.dma_start(dst[:], dram[src]).then_inc(S["loaded"], 16)
                sp.dma_start(bv[:], dram["att_bv"].partition_broadcast(D)).then_inc(S["loaded"], 16)
                sp.dma_start(bo[:], dram["att_bo"]).then_inc(S["loaded"], 16)
            LOADED = 11 * 16

            @block.gpsimd
            def _(pool):
                nc.gpsimd.memset(xn[:, T:], 0.0).then_inc(S["consts_set"], 1)
                nc.gpsimd.memset(v_all[:, :, :, DH:], 1.0).then_inc(S["consts_set"], 1)
                pool.wait_ge(S["consts_set"], 2)
                nc.gpsimd.memset(k_all[SPLIT:MROWS, :], 1.0).then_inc(S["consts_set"], 1)
                pool.wait_ge(S["consts_set"], 3)
                pool.wait_ge(S["loaded"], LOADED)
                nc.gpsimd.tensor_copy(ident[:], ident_f[:]).then_inc(S["consts_set"], 1)
                CONSTS = 4

                def split(H, g, n):
                    b = g % 2
                    pool.wait_ge(S["t0_ready"], n + 1)
                    pool.wait_ge(S["t1_ready"], n + 1)
                    pool.sem_inc(S["pool_passed"], 1)
                    nc.gpsimd.tensor_copy(part1[:, b, :], t0[:, b, :]).then_inc(S["part1_ready"], 1)

                def split2(H, g, n):
                    b = g % 2
                    pool.wait_ge(S["t1_ready"], n + 3)
                    pool.wait_ge(S["stacked"], n + 1)
                    pool.sem_inc(S["pool_passed"], 1)
                    nc.gpsimd.tensor_copy(part2[:, b, :], t1[:, b, :]).then_inc(S["part2_ready"], 1)

                def project(n0):
                    for g in range(NG):
                        split(None, g, n0 + g)
                        split2(None, g, n0 + g)

                project(0)
                project(NG)
                with pool.Fori(0, HEADS) as h:
                    pool.wait_ge(S["v_stored"], T // D)
                    pool.wait_ge(S["pv_done"], h * (QCH * KB) + 2)
                    pool.sem_inc(S["pool_passed"], 1)
                    nc.gpsimd.tensor_copy(v_head[:].rearrange("p a b c -> p (a b c)"),
                                          v_all[:, bass.ds(h * 2, 2), :, :].rearrange("p a b c -> p (a b c)")
                                          ).then_inc(S["v_head_ready"], 1)
                    project(h * NG + 2 * NG)

            def slots(run, H):
                for u in range(QCH * KB + 8):
                    run(u, H)

            PRE = 2
            UNITS = QCH * KB
            proj_slot = {2 + 6 * g: g for g in range(NG)}
            fold_slot = {16 * q + 18: q for q in range(QCH)}
            OUT_SLOT = UNITS + 5
            MT_SLOT = UNITS + 6

            @block.tensor
            def _(pe):
                pe.sem_inc(S["pv_done"], 2)
                pe.sem_inc(S["fold_ready"], 1)
                pe.sem_inc(S["out_ready"], 1)
                pe.wait_ge(S["loaded"], LOADED)
                pe.wait_ge(S["consts_set"], 4)
                for t in range(T // D):
                    if t >= 2:
                        pe.wait_ge(S["v_stored"], t - 1)
                    nc.tensor.matmul(st_ps[:, t % 2, 0:D], xn[:, t * D:(t + 1) * D], wv[:],
                                     start=True, stop=True).then_inc(S["v_ready"], 1)

                def project(H, g, misc):
                    w, b, a, c2 = groups[g]
                    pe.wait_ge(S["misc_free"], misc)
                    for c in (2 * c2, 2 * c2 + 1):
                        mm = nc.tensor.matmul(misc_ps[:, (c % 2) * HT:(c % 2 + 1) * HT], w[:, c * D:(c + 1) * D],
                                              xn[:, bass.ds(H * HT, HT)], start=(c % 2 == 0), stop=(c % 2 == 1),
                                              skip_group_check=True)
                    mm.then_inc(S["proj_ready"], 1)

                def first_pass(H, hh):
                    qt, half = hh // 2, hh % 2
                    pe.wait_ge(S["half_done"], H * 32 + hh + 1)
                    if hh == 0:
                        pe.wait_ge(S["stacked"], H * NG + NG + 2)
                    for j in range(2):
                        mm = nc.tensor.matmul(s1_ps[:, hh % 2, j * CH:(j + 1) * CH],
                                              q_all[0:SPLIT, bass.ds(H * T + qt * D, D)],
                                              k_all[0:SPLIT, bass.ds(H * T + (2 * half + j) * CH, CH)],
                                              start=True, stop=True)
                    mm.then_inc(S["s1_ready"], 1)

                def max_rows(H, misc):
                    pe.wait_ge(S["parts_ready"], H + 1)
                    mt = misc_ps[:].bitcast(BF16)
                    for r in range(2):
                        pe.wait_ge(S["misc_free"], misc + r)
                        for q in range(8):
                            mm = nc.tensor.transpose(mt[0:2, q * D:(q + 1) * D], neg_parts[:, 8 * r + q, :], ident[:])
                        mm.then_inc(S["mt_ready"], 1)

                pe.wait_ge(S["v_stored"], T // D)
                for g in range(2 * NG):
                    project(g // NG, g % NG, g + 1)
                misc = 2 * NG
                for hh in range(32):
                    first_pass(0, hh)
                max_rows(0, misc + 1)
                misc += 2
                MISC0 = misc
                PER = NG + QCH + 1 + 2

                def pv(H, u):
                    q, kb = u // KB, u % KB
                    g = kb % 4
                    pe.wait_ge(S["exp_done"], H * UNITS + u + 3)
                    if u == 0:
                        pe.wait_ge(S["v_head_ready"], H + 1)
                    if kb == 0:
                        pe.wait_ge(S["acc_stored"], H * QCH + q + 1)
                    nc.tensor.matmul(acc_ps[32 * g:32 * g + 32, :], v_head[:, kb % 2, kb // 2, :],
                                     probs[:, u % 2, :], start=(kb < 4), stop=(kb >= KB - 4),
                                     skip_group_check=True).then_inc(S["pv_done"], 1)

                with pe.Fori(0, HEADS) as h:
                    m = [0]

                    def next_misc():
                        m[0] += 1
                        return h * PER + (MISC0 + m[0])
                    for u in range(UNITS + 8):
                        if u < UNITS:
                            q, kb = u // KB, u % KB
                            pe.wait_ge(S["exp_done"], h * UNITS + u + 1)
                            if u == 0:
                                pe.wait_ge(S["mrows_ready"], 2 * h + 2)
                            nc.tensor.matmul(st_ps[:, u % 2, :], k_all[0:MROWS, bass.ds(h * T + kb * D, D)],
                                             q_all[0:MROWS, bass.ds(h * T + q * CH, CH)],
                                             start=True, stop=True).then_inc(S["st_ready"], 1)
                        if 1 <= u <= UNITS:
                            pv(h, u - 1)
                        if u % 2 == 1 and u // 2 < 32:
                            first_pass(h + 1, u // 2)
                        if u in proj_slot:
                            project(h + PRE, proj_slot[u], next_misc())
                        if u in fold_slot:
                            q = fold_slot[u]
                            pe.wait_ge(S["misc_free"], next_misc())
                            pe.wait_ge(S["acc_stored"], h * QCH + q + 2)
                            nc.tensor.matmul(misc_ps[0:48, :], fold[:], acc_sb[:], start=True,
                                             stop=True).then_inc(S["fold_ready"], 1)
                        if u == OUT_SLOT:
                            pe.wait_ge(S["misc_free"], next_misc())
                            pe.wait_ge(S["ctx_ready"], h * QCH + QCH)
                            for c in range(HEADS):
                                mm = nc.tensor.matmul(misc_ps[:, 0:HT], wo[:, c * D:(c + 1) * D],
                                                      ctx[:, c * HT:(c + 1) * HT], start=(c == 0),
                                                      stop=(c == HEADS - 1))
                            mm.then_inc(S["out_ready"], 1)
                        if u == MT_SLOT:
                            max_rows(h + 1, next_misc())
                            next_misc()

            @block.scalar
            def _(act):
                act.sem_inc(S["exp_done"], 2)
                act.sem_inc(S["misc_free"], 1)
                act.wait_ge(S["loaded"], LOADED)

                def store_projection(n, g):
                    w, b, a, c2 = groups[g]
                    act.wait_ge(S["proj_ready"], n + 1)
                    act.wait_ge(S["t1_ready"], n + 1)
                    for c in (2 * c2, 2 * c2 + 1):
                        half = slice((c % 2) * HT, (c % 2 + 1) * HT)
                        a_ = nc.scalar.activation(t0[:, g % 2, half], misc_ps[:, half], ACT.Identity,
                                                  bias=b[:, c:c + 1])
                    a_.then_inc(S["t0_ready"], 1)
                    act.wait_ge(S["t0_ready"], n + 1)
                    act.sem_inc(S["misc_free"], 1)

                def store_rows(H, n):
                    for r in range(2):
                        act.wait_ge(S["mt_ready"], n + r + 1)
                        nc.scalar.activation(q_all[SPLIT:MROWS, bass.ds(H * T + r * 1024, 1024)],
                                             misc_ps[:].bitcast(BF16)[0:2, :], ACT.Copy).then_inc(S["mrows_ready"], 1)
                        act.wait_ge(S["mrows_ready"], n + r + 1)
                        act.sem_inc(S["misc_free"], 1)

                for n in range(2 * NG):
                    store_projection(n, n % NG)
                store_rows(0, 0)
                with act.Fori(0, HEADS) as h:
                    for u in range(UNITS + 8):
                        if u < UNITS:
                            act.wait_ge(S["st_ready"], h * UNITS + u + 1)
                            act.wait_ge(S["pv_done"], h * UNITS + u + 1)
                            nc.scalar.activation(probs[:, u % 2, :], st_ps[:, u % 2, :], ACT.Exp,
                                                 scale=float(DH) ** -0.5).then_inc(S["exp_done"], 1)
                        if u in proj_slot:
                            store_projection(h * NG + (2 * NG + proj_slot[u]), proj_slot[u])
                        if u == MT_SLOT:
                            store_rows(h + 1, h * 2 + 2)

            @block.vector
            def _(dve):
                dve.sem_inc(S["t1_ready"], 2)
                dve.sem_inc(S["stacked"], 2)
                dve.sem_inc(S["half_done"], 2)
                dve.sem_inc(S["acc_stored"], 1)
                dve.wait_ge(S["loaded"], LOADED)
                dve.wait_ge(S["consts_set"], 4)
                for t in range(T // D):
                    dve.wait_ge(S["v_ready"], t + 1)
                    nc.vector.tensor_tensor(v_all[:, t, :, 0:DH], st_ps[:, t % 2, 0:D].rearrange("p (c d) -> p c d", d=DH),
                                            bv[:].rearrange("p (c d) -> p c d", d=DH), ALU.add).then_inc(S["v_stored"], 1)

                def remainder(n, g):
                    b = g % 2
                    dve.wait_ge(S["part1_ready"], n + 1)
                    dve.wait_ge(S["t0_ready"], n + 1)
                    nc.vector.scalar_tensor_tensor(out=t1[:, b, :], in0=part1[:, b, :], scalar=masks[:, 0 + 2 * (g // 4):1 + 2 * (g // 4)],
                                                   in1=t0[:, b, :], op0=ALU.mult, op1=ALU.add).then_inc(S["t1_ready"], 1)

                def stack(H, n, g):
                    w, bb, a, c2 = groups[g]
                    b = g % 2
                    dve.wait_ge(S["part2_ready"], n + 1)
                    dve.wait_ge(S["t1_ready"], n + 3)
                    nc.vector.scalar_tensor_tensor(out=a[0:SPLIT, bass.ds(H * T + c2 * CH, CH)], in0=part2[0:SPLIT, b, :],
                                                   scalar=masks[0:SPLIT, 1 + 2 * (g // 4):2 + 2 * (g // 4)],
                                                   in1=t1[0:SPLIT, b, :], op0=ALU.mult, op1=ALU.add).then_inc(S["stacked"], 1)

                def half_max_of(H, hh):
                    dve.wait_ge(S["s1_ready"], H * 32 + hh + 1)
                    nc.vector.reduce_max(half_max[:, hh // 2, hh % 2:hh % 2 + 1], s1_ps[:, hh % 2, :],
                                         AX_X).then_inc(S["half_done"], 1)

                def negative_maxima(H):
                    dve.wait_ge(S["half_done"], H * 32 + 34)
                    if not isinstance(H, int):
                        dve.wait_ge(S["mt_ready"], 2 * H)
                    nc.vector.tensor_reduce(neg_max[:], half_max[:], AX_X, ALU.max, negate=True).then_inc(S["neg_ready"], 1)
                    dve.wait_ge(S["neg_ready"], 3 * H + 1)
                    nc.vector.tensor_copy(neg_parts[:, :, 0], neg_max[:]).then_inc(S["neg_ready"], 1)
                    dve.wait_ge(S["neg_ready"], 3 * H + 2)
                    nc.vector.tensor_tensor(neg_parts[:, :, 1], neg_max[:], neg_parts[:, :, 0],
                                            ALU.subtract).then_inc(S["neg_ready"], 1)
                    dve.wait_ge(S["neg_ready"], 3 * H + 3)
                    dve.sem_inc(S["parts_ready"], 1)

                for n in range(2 * NG):
                    remainder(n, n % NG)
                    stack(n // NG, n, n % NG)
                for hh in range(32):
                    half_max_of(0, hh)
                negative_maxima(0)
                with dve.Fori(0, HEADS) as h:
                    for u in range(UNITS + 8):
                        if u + 1 in fold_slot:
                            q = fold_slot[u + 1]
                            dve.wait_ge(S["pv_done"], h * UNITS + (q + 1) * KB + 2)
                            dve.wait_ge(S["fold_ready"], h * QCH + q + 1)
                            nc.vector.tensor_copy(acc_sb[:], acc_ps[:]).then_inc(S["acc_stored"], 1)
                        if u % 2 == 1 and u // 2 < 32:
                            half_max_of(h + 1, u // 2)
                        if u - 2 in proj_slot:
                            remainder(h * NG + (2 * NG + proj_slot[u - 2]), proj_slot[u - 2])
                        if u - 4 in proj_slot:
                            stack(h + PRE, h * NG + (2 * NG + proj_slot[u - 4]), proj_slot[u - 4])
                        if u in fold_slot:
                            q = fold_slot[u]
                            dve.wait_ge(S["fold_ready"], h * QCH + q + 2)
                            nc.vector.reciprocal(rsum[:], misc_ps[32:48, :]).then_inc(S["rsum_ready"], 1)
                            dve.wait_ge(S["rsum_ready"], h * QCH + q + 1)
                            if q == 0:
                                dve.wait_ge(S["out_ready"], h + 1)
                            nc.vector.tensor_tensor(ctx[:, q * CH:(q + 1) * CH], misc_ps[0:DH, :], rsum[:],
                                                    ALU.mult).then_inc(S["ctx_ready"], 1)
                            dve.wait_ge(S["ctx_ready"], h * QCH + q + 1)
                            dve.sem_inc(S["misc_free"], 1)
                        if u == OUT_SLOT:
                            dve.wait_ge(S["out_ready"], h + 2)
                            nc.vector.scalar_tensor_tensor(out=ao[:, bass.ds(h * HT, HT)], in0=misc_ps[:, 0:HT],
                                                           scalar=bo[:], in1=xn[:, bass.ds(h * HT, HT)], op0=ALU.add,
                                                           op1=ALU.add).then_inc(S["out_stored"], 1)
                            dve.wait_ge(S["out_stored"], h + 1)
                            dve.sem_inc(S["misc_free"], 1)
                        if u == MT_SLOT:
                            negative_maxima(h + 1)


def lay_out_attention(inp):
    a = {k: np.asarray(v) for k, v in inp.items()}
    rep = lambda w: np.ascontiguousarray(
        np.broadcast_to(w.T.reshape(D, HEADS, 1, DH), (D, HEADS, 8, DH)).reshape(D, HEADS * D))
    repb = lambda b: np.ascontiguousarray(
        np.broadcast_to(b.reshape(HEADS, 1, DH), (HEADS, 8, DH)).reshape(HEADS, D).T)
    masks = np.zeros((D, 4), np.float32)
    for col, parts in ((0, (1, 1, 2, 2, 1, 3)), (2, (1, 2, 1, 2, 3, 1))):
        for g, p in enumerate(parts):
            masks[16 * g:16 * g + 16, col] = -1.0 if p >= 2 else 0.0
            masks[16 * g:16 * g + 16, col + 1] = -1.0 if p == 3 else 0.0
    fold = np.zeros((D, 48), np.float32)
    for g in range(4):
        for r in range(16):
            fold[32 * g + r, r] = 1.0
            fold[32 * g + 16 + r, 32 + r] = 1.0
    return {
        "ids": a["x"].astype(np.int32).reshape(T),
        "table": a["L0_tok_weights"],
        "att_wq": rep(a["L0_attn_Wq"]), "att_wk": rep(a["L0_attn_Wk"]),
        "att_bq": repb(a["L0_attn_bq"]), "att_bk": repb(a["L0_attn_bk"]),
        "att_wv": np.ascontiguousarray(a["L0_attn_Wv"].T), "att_bv": a["L0_attn_bv"],
        "att_wo": np.ascontiguousarray(a["L0_attn_Wo"].T.reshape(HEADS, DH, D).transpose(1, 0, 2).reshape(DH, HEADS * D)),
        "att_bo": a["L0_attn_bo"].reshape(D, 1),
        "att_gamma": a["L0_attn_gamma"].reshape(D, 1), "att_beta": a["L0_attn_beta"].reshape(D, 1),
        "att_masks": masks, "att_fold": fold, "ident": np.eye(D, dtype=np.float32),
        "ones_over_d": np.full((D, D), 1.0 / D, np.float32),
    }


EXPERTS = 64
INTER = 64
PAIRS = EXPERTS // 2
TOP_K = 6
BIG = 3.0e38
TT = T // D


def router(nc, dram, xn, comb_a, comb_b):
    with Scope(nc, "rt") as s:
        w_gate = s.sb("w_gate", [D, EXPERTS])
        ident = s.sb("ident", [D, D])
        row_masks = s.sb("row_masks", [D, 2])
        score = s.sb("score", [D, TT, EXPERTS])
        left = s.sb("left", [D, TT, EXPERTS])
        chosen = s.sb("chosen", [D, TT, EXPERTS])
        weight = s.sb("weight", [D, TT, EXPERTS])
        twice = s.sb("twice", [D, TT, 2, EXPERTS])
        top = s.sb("top", [D, TT, 8])
        best = s.sb("best", [D, TT, 1])
        total = s.sb("total", [D, TT])
        rest = s.sb("rest", [D, T])
        rest2 = s.sb("rest2", [D, T])
        part = s.sb("part", [D, T], BF16)
        score_ps = s.ps("score", [D, TT, EXPERTS])
        comb_ps = s.ps("comb", [D, NCH, CH])
        S = {n: s.sem(n) for n in ("loaded scores_ready stored top_ready cut left_ready shifted exp_ready "
                                   "chosen_ready masked total_ready inverse_ready weight_ready turned part_ready "
                                   "rest_ready a_ready part2_ready rest2_ready b_ready").split()}
        wide = lambda ap: ap.broadcast_to([D, TT, EXPERTS])
        with nc.Block() as block:
            @block.sync
            def _(sp):
                for dst, src in ((w_gate, "rt_gate"), (ident, "ident"), (row_masks, "rt_masks")):
                    sp.dma_start(dst[:], dram[src]).then_inc(S["loaded"], 16)

            @block.tensor
            def _(pe):
                pe.wait_ge(S["loaded"], 48)
                for t in range(TT):
                    mm = nc.tensor.matmul(score_ps[:, t, :], xn[:, t * D:(t + 1) * D], w_gate[:],
                                          start=(t % 8 == 0), stop=(t % 8 == 7), skip_group_check=True)
                mm.then_inc(S["scores_ready"], 1)
                pe.wait_ge(S["weight_ready"], 2)
                for t in range(TT):
                    nc.tensor.transpose(comb_ps[:, t // 4, (t % 4) * D:(t % 4 + 1) * D],
                                        twice[:, t, :, :].rearrange("p a e -> p (a e)"),
                                        ident[:]).then_inc(S["turned"], 1)

            @block.scalar
            def _(act):
                act.wait_ge(S["shifted"], 1)
                nc.scalar.activation(weight[:], weight[:], ACT.Exp).then_inc(S["exp_ready"], 1)
                for c in range(NCH):
                    act.wait_ge(S["turned"], 4 * c + 4)
                    cols = slice(c * CH, (c + 1) * CH)
                    nc.scalar.activation(part[:, cols], comb_ps[:, c, :], ACT.Copy).then_inc(S["part_ready"], 1)
                for c in range(NCH):
                    cols = slice(c * CH, (c + 1) * CH)
                    act.wait_ge(S["rest_ready"], c + 1)
                    nc.scalar.activation(comb_a[:, cols], rest[:, cols], ACT.Copy).then_inc(S["a_ready"], 1)

            @block.vector
            def _(dve):
                dve.wait_ge(S["scores_ready"], 1)
                nc.vector.tensor_copy(score[:], score_ps[:]).then_inc(S["stored"], 1)
                dve.wait_ge(S["stored"], 1)
                for t in range(TT):
                    mx = nc.vector.max(top[:, t, :], score[:, t, :])
                mx.then_inc(S["top_ready"], 1)
                dve.wait_ge(S["top_ready"], 1)
                nc.vector.tensor_copy(best[:], top[:, :, 0:1]).then_inc(S["cut"], 1)
                nc.vector.memset(top[:, :, TOP_K:8], BIG).then_inc(S["cut"], 1)
                dve.wait_ge(S["cut"], 2)
                nc.vector.tensor_tensor(weight[:], score[:], wide(best[:]), ALU.subtract).then_inc(S["shifted"], 1)
                for t in range(TT):
                    mr = nc.vector.match_replace(left[:, t, :], top[:, t, :], score[:, t, :], -BIG)
                mr.then_inc(S["left_ready"], 1)
                dve.wait_ge(S["left_ready"], 1)
                nc.vector.tensor_tensor(chosen[:], left[:], score[:], ALU.not_equal).then_inc(S["chosen_ready"], 1)
                dve.wait_ge(S["chosen_ready"], 1)
                dve.wait_ge(S["exp_ready"], 1)
                nc.vector.tensor_tensor(left[:], weight[:], chosen[:], ALU.mult).then_inc(S["masked"], 1)
                dve.wait_ge(S["masked"], 1)
                nc.vector.reduce_sum(total[:], left[:], AX_X).then_inc(S["total_ready"], 1)
                dve.wait_ge(S["total_ready"], 1)
                nc.vector.reciprocal(total[:], total[:]).then_inc(S["inverse_ready"], 1)
                dve.wait_ge(S["inverse_ready"], 1)
                for a in range(2):
                    nc.vector.tensor_tensor(twice[:, :, a, :], left[:], wide(total[:].unsqueeze(2)),
                                            ALU.mult).then_inc(S["weight_ready"], 1)
                for c in range(NCH):
                    cols = slice(c * CH, (c + 1) * CH)
                    dve.wait_ge(S["part_ready"], c + 1)
                    nc.vector.scalar_tensor_tensor(out=rest[:, cols], in0=part[:, cols], scalar=row_masks[:, 0:1],
                                                   in1=comb_ps[:, c, :], op0=ALU.mult,
                                                   op1=ALU.add).then_inc(S["rest_ready"], 1)
                for c in range(NCH):
                    cols = slice(c * CH, (c + 1) * CH)
                    dve.wait_ge(S["a_ready"], c + 1)
                    nc.vector.tensor_tensor(rest2[:, cols], rest[:, cols], comb_a[:, cols],
                                            ALU.subtract).then_inc(S["rest2_ready"], 1)
                    dve.wait_ge(S["rest2_ready"], c + 1)
                    nc.vector.tensor_scalar(comb_b[:, cols], rest2[:, cols], row_masks[:, 1:2], None,
                                            ALU.mult).then_inc(S["b_ready"], 1)


def experts(nc, dram, xn, h, comb_a, comb_b):
    with Scope(nc, "moe") as s:
        shared = s.sb("shared", [D, 2, 3, D])
        w = [s.sb(f"w{b}", [D, 3, D]) for b in range(2)]
        ident = s.sb("ident", [D, EXPERTS])
        pick = s.sb("pick", [D, EXPERTS * INTER], BF16)
        gate = s.sb("gate", [D, 2, CH])
        gated = s.sb("gated", [D, 2, CH])
        hidden = s.sb("hidden", [D, 2, CH])
        x1_ps, x3_ps, cb_ps = s.ps("x1", [D, CH]), s.ps("x3", [D, CH]), s.ps("cb", [D, CH])
        out_ps = s.ps("out", [D, NCH, CH])
        S = {n: s.sem(n) for n in ("loaded pick_ready w_a w_b w_used x1_ready x3_ready cb_ready gate_ready "
                                   "gated_ready hidden_ready out_done stored").split()}
        w_loaded = (S["w_a"], S["w_b"])
        packed = dram["moe_w"]
        with nc.Block() as block:
            @block.sync
            def _(sp):
                sp.dma_start(shared[:].rearrange("p a b d -> p (a b d)"), dram["moe_shared"]).then_inc(S["loaded"], 16)
                sp.dma_start(ident[:], dram["moe_ident"]).then_inc(S["loaded"], 16)
                sp.sem_inc(S["w_used"], 2)
                with sp.Fori(0, PAIRS // 2) as i:
                    for b in range(2):
                        sp.wait_ge(S["w_used"], 2 * i + (b + 1))
                        sp.dma_start(w[b][:].rearrange("p b d -> p (b d)"),
                                     packed[bass.ds((i * 2 + b) * D, D), :]).then_inc(w_loaded[b], 16)

            @block.gpsimd
            def _(pool):
                pool.wait_ge(S["loaded"], 32)
                nc.gpsimd.tensor_copy(pick[:].rearrange("p (e i) -> p e i", i=INTER),
                                      ident[:].unsqueeze(2).broadcast_to([D, EXPERTS, INTER])).then_inc(S["pick_ready"], 1)

            @block.tensor
            def _(pe):
                pe.sem_inc(S["out_done"], 2)
                pe.wait_ge(S["loaded"], 32)

                def item(n, c, wt, pair):
                    cols = slice(c * CH, (c + 1) * CH)
                    pe.wait_ge(S["gate_ready"], n + 1)
                    nc.tensor.matmul(x1_ps[:], wt[:, 0, :], xn[:, cols], start=True, stop=True).then_inc(S["x1_ready"], 1)
                    pe.wait_ge(S["gated_ready"], n + 1)
                    nc.tensor.matmul(x3_ps[:], wt[:, 1, :], xn[:, cols], start=True, stop=True).then_inc(S["x3_ready"], 1)
                    if pair is not None:
                        pe.wait_ge(S["hidden_ready"], n + 1)
                        sel = pick[:, bass.ds(pair * D, D)]
                        nc.tensor.matmul(cb_ps[:], sel, comb_a[:, cols], start=True, stop=False)
                        nc.tensor.matmul(cb_ps[:], sel, comb_b[:, cols], start=False, stop=True).then_inc(S["cb_ready"], 1)

                def down(n, c, b, wt, first):
                    pe.wait_ge(S["hidden_ready"], n + 2)
                    return nc.tensor.matmul(out_ps[:, c, :], wt[:, 2, :], hidden[:, b, :], start=first, stop=True,
                                            skip_group_check=True).then_inc(S["out_done"], 1)

                for st in range(2):
                    for c in range(NCH):
                        item(st * NCH + c, c, shared[:, st], None)
                        down(st * NCH + c, c, c % 2, shared[:, st], st == 0)
                pe.wait_ge(S["pick_ready"], 1)
                with pe.Fori(0, PAIRS // 2) as i:
                    for b in range(2):
                        pe.wait_ge(w_loaded[b], 16 * i + 16)
                        base = i * (2 * NCH) + (2 + b) * NCH
                        for c in range(NCH):
                            item(base + c, c, w[b], i * 2 + b)
                            if c:
                                down(base + c - 1, c - 1, (c - 1) % 2, w[b], False)
                        down(base + NCH - 1, NCH - 1, (NCH - 1) % 2, w[b], False)
                        pe.wait_ge(S["out_done"], base + NCH + 2)
                        pe.sem_inc(S["w_used"], 1)

            @block.scalar
            def _(act):
                act.sem_inc(S["gate_ready"], 1)

                def gate_of(n, b):
                    act.wait_ge(S["x1_ready"], n + 1)
                    act.wait_ge(S["gated_ready"], n + 1)
                    nc.scalar.activation(gate[:, b, :], x1_ps[:], ACT.Silu).then_inc(S["gate_ready"], 1)
                for n in range(2 * NCH):
                    gate_of(n, n % 2)
                with act.Fori(0, PAIRS) as e:
                    for c in range(NCH):
                        gate_of(e * NCH + (2 * NCH + c), c % 2)

            @block.vector
            def _(dve):
                dve.sem_inc(S["gated_ready"], 1)
                dve.sem_inc(S["hidden_ready"], 1)

                def hide(n, b, cb):
                    dve.wait_ge(S["gate_ready"], n + 2)
                    dve.wait_ge(S["x3_ready"], n + 1)
                    dve.wait_ge(S["out_done"], n + 1)
                    if cb is None:
                        nc.vector.tensor_tensor(hidden[:, b, :], gate[:, b, :], x3_ps[:], ALU.mult).then_inc(S["gated_ready"], 1)
                        dve.wait_ge(S["gated_ready"], n + 2)
                        dve.sem_inc(S["hidden_ready"], 1)
                        return
                    nc.vector.tensor_tensor(gated[:, b, :], gate[:, b, :], x3_ps[:], ALU.mult).then_inc(S["gated_ready"], 1)
                    dve.wait_ge(S["gated_ready"], n + 2)
                    dve.wait_ge(S["cb_ready"], cb)
                    nc.vector.tensor_tensor(hidden[:, b, :], gated[:, b, :], cb_ps[:], ALU.mult).then_inc(S["hidden_ready"], 1)
                for n in range(2 * NCH):
                    hide(n, n % 2, None)
                with dve.Fori(0, PAIRS) as e:
                    for c in range(NCH):
                        hide(e * NCH + (2 * NCH + c), c % 2, e * NCH + (c + 1))
                for c in range(NCH):
                    dve.wait_ge(S["out_done"], (PAIRS + 2) * NCH + 2)
                    cols = slice(c * CH, (c + 1) * CH)
                    nc.vector.tensor_tensor(h[:, cols], h[:, cols], out_ps[:, c, :], ALU.add).then_inc(S["stored"], 1)


def lay_out_moe(inp):
    a = {k: np.asarray(v) for k, v in inp.items()}
    w1, w3, w2 = (a[f"L0_ffn_{n}"].reshape(PAIRS, D, D) for n in ("w1", "w3", "w2"))
    packed = np.stack([w1.transpose(0, 2, 1), w3.transpose(0, 2, 1), w2], axis=2).reshape(PAIRS * D, 3 * D)
    sg, su, sd = a["L0_ffn_w_sg"], a["L0_ffn_w_su"], a["L0_ffn_w_sd"]
    shared = np.stack([np.stack([sg[i * D:(i + 1) * D].T, su[i * D:(i + 1) * D].T, sd[:, i * D:(i + 1) * D].T], 1)
                       for i in range(2)], 1).reshape(D, 6 * D)
    masks = np.zeros((D, 2), np.float32)
    masks[64:, 0] = -1.0
    masks[64:, 1] = 1.0
    eye = np.eye(EXPERTS, dtype=np.float32)
    return {"rt_gate": np.ascontiguousarray(a["L0_ffn_w_gate"].T), "rt_masks": masks,
            "moe_w": np.ascontiguousarray(packed), "moe_shared": np.ascontiguousarray(shared),
            "moe_ident": np.concatenate([eye, eye])}


PK_HEADS = 8
N_KEYS = 64
TOPK = 16
GROUPS = 2 * PK_HEADS
ROWS = [TOPK // (i + 1) for i in range(TOPK)]
SINGLE = ROWS.index(1)
STARTS = [sum(ROWS[:i]) for i in range(TOPK)]
CAND = sum(ROWS)
NSIM = GROUPS * N_KEYS


def product_keys(nc, dram, xn, h):
    with Scope(nc, "pk") as s:
        wq = s.sb("wq", [N_KEYS, GROUPS, D])
        keys = s.sb("keys", [N_KEYS, GROUPS, N_KEYS])
        up = s.sb("up", [CAND, D])
        ident = s.sb("ident", [D, D])
        w = s.sb("w", [D, NSIM + CAND])
        delta = s.sb("delta", [D, TT + 1, D])
        buf = []
        for b in range(2):
            buf.append({n: s.sb(f"{n}{b}", shape) for n, shape in dict(
                xt=[D, D], left=[D, GROUPS, N_KEYS], top=[D, GROUPS, TOPK], cand=[D, PK_HEADS, CAND],
                left2=[D, PK_HEADS, CAND], left3=[D, PK_HEADS, CAND], top2=[D, PK_HEADS, TOPK],
                shifted=[D, PK_HEADS, CAND], chosen=[D, PK_HEADS, CAND], masked=[D, PK_HEADS, CAND],
                total=[D, PK_HEADS], inverse=[D, PK_HEADS], act=[D, CAND], weight=[D, CAND], gw=[D, CAND],
                gwt=[CAND, D]).items()})
            buf[b]["sim"] = s.ps(f"sim{b}", [D, GROUPS, N_KEYS])
        xd_ps = s.ps("xd", [D, 2, CH])
        turn_ps = s.ps("turn", [D, D])
        out_ps = s.ps("out", [D, D])
        S = {n: s.sem(n) for n in ("loaded w_ps_ready w_stored xt_ready sims_ready xd_ready top_a cut_a top1_done "
                                   "cand_ready gelu_ready top_b cut_b top_c cut_c shifted exp_ready chosen masked "
                                   "total inverse scaled weight gw_ready turned gwt_ready out_ready delta_stored "
                                   "zeroed added dve_passed pe_passed").split()}
        flat = lambda ap: ap.rearrange("p a b -> p (a b)")
        with nc.Block() as block:
            @block.sync
            def _(sp):
                for dst, src in ((flat(wq[:]), "pk_wq"), (flat(keys[:]), "pk_keys"), (up[:], "pk_up"),
                                 (ident[:], "ident"), (w[:, NSIM:], "pk_down")):
                    sp.dma_start(dst, dram[src]).then_inc(S["loaded"], 16)

            @block.gpsimd
            def _(pool):
                pool.sem_inc(S["cand_ready"], 2)
                nc.gpsimd.memset(xn[:, T:], 0.0).then_inc(S["zeroed"], 1)
                nc.gpsimd.memset(buf[1]["gwt"][:], 0.0).then_inc(S["zeroed"], 1)

                def candidates(n, b):
                    pool.wait_ge(S["top1_done"], n + 3)
                    pool.wait_ge(S["shifted"], n + 1)
                    pool.wait_ge(S["chosen"], n + 1)
                    top, cand = buf[b]["top"], buf[b]["cand"]
                    for i in range(SINGLE):
                        nc.gpsimd.tensor_tensor(
                            cand[:, :, STARTS[i]:STARTS[i] + ROWS[i]],
                            top[:, 0:PK_HEADS, i:i + 1].broadcast_to([D, PK_HEADS, ROWS[i]]),
                            top[:, PK_HEADS:, 0:ROWS[i]], ALU.add)
                    n1 = TOPK - SINGLE
                    nc.gpsimd.tensor_tensor(cand[:, :, STARTS[SINGLE]:], top[:, 0:PK_HEADS, SINGLE:],
                                            top[:, PK_HEADS:, 0:1].broadcast_to([D, PK_HEADS, n1]),
                                            ALU.add).then_inc(S["cand_ready"], 1)
                candidates(0, 0)
                with pool.Fori(0, TT // 2) as i:
                    for b in range(2):
                        candidates(i * 2 + (b + 1), 1 - b)

            @block.tensor
            def _(pe):
                pe.sem_inc(S["xd_ready"], 2)
                pe.wait_ge(S["loaded"], 80)
                for g in range(GROUPS):
                    mm = nc.tensor.matmul(buf[0]["sim"][:, g, :], wq[:, g, :], keys[:, g, :], start=(g % 8 == 0),
                                          stop=(g % 8 == 7), skip_group_check=True)
                mm.then_inc(S["w_ps_ready"], 1)
                pe.wait_ge(S["w_stored"], 1)
                pe.wait_ge(S["zeroed"], 2)
                nc.tensor.matmul(out_ps[:], up[:], buf[1]["gwt"][:], start=True, stop=True).then_inc(S["out_ready"], 1)

                def sims(n, b):
                    pe.wait_ge(S["xt_ready"], n + 1)
                    pe.wait_ge(S["top1_done"], n + 1)
                    sim = flat(buf[b]["sim"][:])
                    for j in range(2):
                        mm = nc.tensor.matmul(sim[:, j * CH:(j + 1) * CH], buf[b]["xt"][:],
                                              w[:, j * CH:(j + 1) * CH], start=True, stop=True)
                    mm.then_inc(S["sims_ready"], 1)
                    pe.wait_ge(S["gelu_ready"], n + 1)
                    nc.tensor.matmul(xd_ps[:, b, 0:CAND], buf[b]["xt"][:], w[:, NSIM:], start=True, stop=True,
                                     skip_group_check=True).then_inc(S["xd_ready"], 1)
                sims(0, 0)
                with pe.Fori(0, TT // 2) as i:
                    for b in range(2):
                        n = i * 2 + b
                        sims(n + 1, 1 - b)
                        pe.wait_ge(S["gw_ready"], n + 1)
                        pe.sem_inc(S["pe_passed"], 1)
                        nc.tensor.transpose(turn_ps[0:CAND, :], buf[b]["gw"][:], ident[:]).then_inc(S["turned"], 1)
                        pe.wait_ge(S["gwt_ready"], n + 1)
                        pe.wait_ge(S["delta_stored"], n + 1)
                        nc.tensor.matmul(out_ps[:], up[:], buf[b]["gwt"][:], start=True,
                                         stop=True).then_inc(S["out_ready"], 1)

            @block.scalar
            def _(act):
                act.sem_inc(S["gelu_ready"], 2)
                act.wait_ge(S["zeroed"], 2)

                def stage_tile(n, b):
                    act.wait_ge(S["xd_ready"], n + 1)
                    nc.scalar.activation(buf[b]["xt"][:], xn[:, bass.ds(n * D, D)], ACT.Copy).then_inc(S["xt_ready"], 1)
                stage_tile(0, 0)
                with act.Fori(0, TT // 2) as i:
                    for b in range(2):
                        n = i * 2 + b
                        stage_tile(n + 1, 1 - b)
                        act.wait_ge(S["xd_ready"], n + 3)
                        nc.scalar.activation(buf[b]["act"][:], xd_ps[:, b, 0:CAND], ACT.Gelu).then_inc(S["gelu_ready"], 1)
                        act.wait_ge(S["shifted"], n + 3)
                        nc.scalar.activation(buf[b]["shifted"][:], buf[b]["shifted"][:], ACT.Exp).then_inc(S["exp_ready"], 1)
                        act.wait_ge(S["turned"], n + 1)
                        nc.scalar.activation(buf[b]["gwt"][:], turn_ps[0:CAND, :], ACT.Copy).then_inc(S["gwt_ready"], 1)
                act.wait_ge(S["xd_ready"], TT + 3)

            @block.vector
            def _(dve):
                dve.sem_inc(S["top1_done"], 2)
                dve.sem_inc(S["shifted"], 2)
                dve.sem_inc(S["chosen"], 2)
                dve.wait_ge(S["w_ps_ready"], 1)
                nc.vector.tensor_copy(w[:, 0:NSIM], flat(buf[0]["sim"][:])).then_inc(S["w_stored"], 1)

                def rank_keys(n, b):
                    sim, left, top = buf[b]["sim"], buf[b]["left"], buf[b]["top"]
                    dve.wait_ge(S["sims_ready"], n + 1)
                    dve.wait_ge(S["cand_ready"], n + 1)
                    dve.sem_inc(S["dve_passed"], 1)
                    for g in range(GROUPS):
                        x = nc.vector.max(top[:, g, 0:8], sim[:, g, :])
                    x.then_inc(S["top_a"], 1)
                    dve.wait_ge(S["top_a"], n + 1)
                    dve.sem_inc(S["dve_passed"], 1)
                    for g in range(GROUPS):
                        x = nc.vector.match_replace(left[:, g, :], top[:, g, 0:8], sim[:, g, :], -BIG)
                    x.then_inc(S["cut_a"], 1)
                    dve.wait_ge(S["cut_a"], n + 1)
                    dve.sem_inc(S["dve_passed"], 1)
                    for g in range(GROUPS):
                        x = nc.vector.max(top[:, g, 8:16], left[:, g, :])
                    x.then_inc(S["top1_done"], 1)

                def rank_sums(n, b):
                    B = buf[b]
                    dve.wait_ge(S["cand_ready"], n + 3)
                    dve.sem_inc(S["dve_passed"], 1)
                    for g in range(PK_HEADS):
                        x = nc.vector.max(B["top2"][:, g, 0:8], B["cand"][:, g, :])
                    x.then_inc(S["top_b"], 1)
                    dve.wait_ge(S["top_b"], n + 1)
                    nc.vector.tensor_tensor(B["shifted"][:], B["cand"][:],
                                            B["top2"][:, :, 0:1].broadcast_to([D, PK_HEADS, CAND]),
                                            ALU.subtract).then_inc(S["shifted"], 1)
                    dve.sem_inc(S["dve_passed"], 1)
                    for g in range(PK_HEADS):
                        x = nc.vector.match_replace(B["left2"][:, g, :], B["top2"][:, g, 0:8], B["cand"][:, g, :], -BIG)
                    x.then_inc(S["cut_b"], 1)
                    dve.wait_ge(S["cut_b"], n + 1)
                    dve.sem_inc(S["dve_passed"], 1)
                    for g in range(PK_HEADS):
                        x = nc.vector.max(B["top2"][:, g, 8:16], B["left2"][:, g, :])
                    x.then_inc(S["top_c"], 1)
                    dve.wait_ge(S["top_c"], n + 1)
                    dve.sem_inc(S["dve_passed"], 1)
                    for g in range(PK_HEADS):
                        x = nc.vector.match_replace(B["left3"][:, g, :], B["top2"][:, g, 8:16], B["left2"][:, g, :], -BIG)
                    x.then_inc(S["cut_c"], 1)
                    dve.wait_ge(S["cut_c"], n + 1)
                    nc.vector.tensor_tensor(B["chosen"][:], B["left3"][:], B["cand"][:],
                                            ALU.not_equal).then_inc(S["chosen"], 1)

                def store_delta(n):
                    dve.wait_ge(S["out_ready"], n + 1)
                    nc.vector.tensor_copy(delta[:, bass.ds(n, 1), :].rearrange("p a b -> p (a b)"), out_ps[:]).then_inc(S["delta_stored"], 1)

                def weigh(n, b):
                    B = buf[b]
                    dve.wait_ge(S["chosen"], n + 3)
                    dve.wait_ge(S["exp_ready"], n + 1)
                    nc.vector.tensor_tensor(B["masked"][:], B["shifted"][:], B["chosen"][:], ALU.mult).then_inc(S["masked"], 1)
                    dve.wait_ge(S["masked"], n + 1)
                    nc.vector.reduce_sum(B["total"][:], B["masked"][:], AX_X).then_inc(S["total"], 1)
                    dve.wait_ge(S["total"], n + 1)
                    nc.vector.reciprocal(B["inverse"][:], B["total"][:]).then_inc(S["inverse"], 1)
                    dve.wait_ge(S["inverse"], n + 1)
                    nc.vector.tensor_tensor(B["chosen"][:], B["masked"][:],
                                            B["inverse"][:].unsqueeze(2).broadcast_to([D, PK_HEADS, CAND]),
                                            ALU.mult).then_inc(S["scaled"], 1)
                    dve.wait_ge(S["scaled"], n + 1)
                    nc.vector.reduce_sum(B["weight"][:], B["chosen"][:].rearrange("p h c -> p c h"), AX_X).then_inc(S["weight"], 1)
                    dve.wait_ge(S["weight"], n + 1)
                    dve.wait_ge(S["gelu_ready"], n + 3)
                    nc.vector.tensor_tensor(B["gw"][:], B["weight"][:], B["act"][:], ALU.mult).then_inc(S["gw_ready"], 1)

                rank_keys(0, 0)
                with dve.Fori(0, TT // 2) as i:
                    for b in range(2):
                        n = i * 2 + b
                        rank_sums(n, b)
                        store_delta(n)
                        rank_keys(n + 1, 1 - b)
                        weigh(n, b)
                store_delta(TT)
                dve.wait_ge(S["delta_stored"], TT + 1)
                nc.vector.tensor_tensor(h[:], h[:], flat(delta[:, 1:, :]), ALU.add).then_inc(S["added"], 1)


def lay_out_pk(inp):
    a = {k: np.asarray(v) for k, v in inp.items()}
    places = [i * TOPK + j for i in range(TOPK) for j in range(ROWS[i])]
    wq = a["L1_ffn_W_q"].T.reshape(GROUPS, N_KEYS, D).transpose(1, 0, 2).reshape(N_KEYS, GROUPS * D)
    keys = a["L1_ffn_keys"].transpose(3, 2, 0, 1).reshape(N_KEYS, GROUPS * N_KEYS)
    return {"pk_wq": np.ascontiguousarray(wq), "pk_keys": np.ascontiguousarray(keys),
            "pk_down": np.ascontiguousarray(a["L1_ffn_down_embed"][places].T),
            "pk_up": np.ascontiguousarray(a["L1_ffn_up_embed"][places])}


MB = 8
NMB = T // MB
RW = MB * HEADS
QUAD = 4
EXT = DH + 1
TTT_EPS = 1e-6


def ttt_project(nc, dram, xn, kT, qT, rows, eta):
    turned = nc.dram_tensor("turned_scratch", [3, T, D], F32, kind="Internal").ap()
    with Scope(nc, "tp") as s:
        wk, wkp, wq, wqp, wv = (s.sb(n, [D, D]) for n in ("wk", "wkp", "wq", "wqp", "wv"))
        cos, sin = s.sb("cos", [D, T]), s.sb("sin", [D, T])
        lr_w, lr_b = s.sb("lr_w", [D, MB, RW]), s.sb("lr_b", [RW, 1])
        ident = s.sb("ident", [D, D])
        kv = s.sb("kv", [D, T])
        ca, sa = s.sb("ca", [D, 2, CH]), s.sb("sa", [D, 2, CH])
        token = s.sb("token", [D, 2, CH])
        pr = [s.ps(f"pr{j}", [D, CH]) for j in range(5)]
        lr_ps = s.ps("lr", [RW, NMB])
        turn_ps = s.ps("turn", [D, 2, CH])
        S = {n: s.sem(n) for n in ("loaded projected cos_done sin_done rotated kv_done lr_ready lr_stored "
                                   "turned token_ready even_written odd_written rows_read halved").split()}
        written = (S["even_written"], S["odd_written"])
        cols = lambda c: slice(c * CH, (c + 1) * CH)
        weights = (wk, wkp, wq, wqp, wv)
        with nc.Block() as block:
            @block.sync
            def _(sp):
                for dst, src in zip(weights, ("ttt_wk", "ttt_wkp", "ttt_wq", "ttt_wqp", "ttt_wv")):
                    sp.dma_start(dst[:], dram[src]).then_inc(S["loaded"], 16)
                for dst, src in ((cos, "cos"), (sin, "sin"), (lr_b, "ttt_lrb"), (ident, "ident")):
                    sp.dma_start(dst[:], dram[src]).then_inc(S["loaded"], 16)
                sp.dma_start(lr_w[:].rearrange("p a b -> p (a b)"), dram["ttt_lrw"]).then_inc(S["loaded"], 16)
                for n in range(3 * NCH):
                    a, c = n // NCH, n % NCH
                    sp.wait_ge(S["token_ready"], n + 1)
                    sp.dma_start(turned[a, cols(c), :].rearrange("(q p) d -> p q d", p=D),
                                 token[:, n % 2, :].rearrange("p (q d) -> p q d", d=D)).then_inc(written[n % 2], 16)
                for x in written:
                    sp.wait_ge(x, 16 * 3 * NCH // 2)
                by_row = lambda a: turned[a].rearrange("(n m) (h e) -> (m h) n e", m=MB, e=DH)
                sp.dma_start(rows[0:RW, 0, 0:NMB], by_row(0)).then_inc(S["rows_read"], 16)
                sp.dma_start(rows[0:RW, 1, 0:NMB], by_row(1)).then_inc(S["rows_read"], 16)
                sp.dma_start(rows[RW:D, 0, 0:NMB], by_row(2)).then_inc(S["rows_read"], 16)
                sp.wait_ge(S["rows_read"], 48)

            @block.tensor
            def _(pe):
                pe.wait_ge(S["loaded"], 160)
                for c in range(NCH):
                    for j in range(5):
                        if c:
                            pe.wait_ge(S["sin_done"], 2 * c)
                            pe.wait_ge(S["kv_done"], c)
                        nc.tensor.matmul(pr[j][:], weights[j][:], xn[:, cols(c)], start=True,
                                         stop=True).then_inc(S["projected"], 1)
                by_token = xn[:, 0:T].rearrange("p (n m) -> p m n", m=MB)
                for m in range(MB):
                    mm = nc.tensor.matmul(lr_ps[:], lr_w[:, m, :], by_token[:, m, :], start=(m == 0), stop=(m == MB - 1))
                mm.then_inc(S["lr_ready"], 1)
                pe.wait_ge(S["rotated"], 2 * NCH)
                pe.wait_ge(S["kv_done"], NCH)
                for n in range(3 * NCH):
                    a, c = n // NCH, n % NCH
                    src = (kv, kT, qT)[a]
                    if n >= 2:
                        pe.wait_ge(S["token_ready"], n - 1)
                    for q in range(4):
                        mm = nc.tensor.transpose(turn_ps[:, n % 2, q * D:(q + 1) * D],
                                                 src[:, c * CH + q * D:c * CH + (q + 1) * D], ident[:])
                    mm.then_inc(S["turned"], 1)

            @block.scalar
            def _(act):
                act.wait_ge(S["lr_ready"], 1)
                nc.scalar.activation(eta[:, 0:NMB], lr_ps[:], ACT.Sigmoid, bias=lr_b[:]).then_inc(S["lr_stored"], 1)
                for n in range(3 * NCH):
                    act.wait_ge(S["turned"], n + 1)
                    if n >= 2:
                        act.wait_ge(written[n % 2], 16 * (n // 2))
                    nc.scalar.activation(token[:, n % 2, :], turn_ps[:, n % 2, :], ACT.Copy).then_inc(S["token_ready"], 1)

            @block.vector
            def _(dve):
                dve.wait_ge(S["loaded"], 160)
                for c in range(NCH):
                    dve.wait_ge(S["projected"], 5 * c + 5)
                    for j, dst in enumerate((kT, qT)):
                        n = 2 * c + j
                        nc.vector.tensor_tensor(ca[:, j, :], pr[2 * j][:], cos[:, cols(c)], ALU.mult).then_inc(S["cos_done"], 1)
                        nc.vector.tensor_tensor(sa[:, j, :], pr[2 * j + 1][:], sin[:, cols(c)], ALU.mult).then_inc(S["sin_done"], 1)
                        dve.wait_ge(S["sin_done"], n + 1)
                        dve.wait_ge(S["cos_done"], n + 1)
                        nc.vector.tensor_tensor(dst[:, cols(c)], ca[:, j, :], sa[:, j, :], ALU.add).then_inc(S["rotated"], 1)
                    dve.wait_ge(S["rotated"], 2 * c + 2)
                    nc.vector.tensor_tensor(kv[:, cols(c)], kT[:, cols(c)], pr[4][:], ALU.subtract).then_inc(S["kv_done"], 1)
                dve.wait_ge(S["lr_stored"], 1)
                nc.vector.tensor_scalar(eta[:, 0:NMB], eta[:, 0:NMB], 1.0 / DH, None, ALU.mult).then_inc(S["halved"], 1)


def ttt_chain(nc, dram, kT, qT, rows, eta, zbar):
    with Scope(nc, "tc") as s:
        cc = rows[0:RW, 0, 0:NMB]
        krow, krow_pad = rows[0:RW, 1, 0:NMB], rows[0:RW, 1]
        first = s.sb("first", [D, D])
        kq = [s.sb(f"kq{b}", [D, QUAD, 2, RW]) for b in range(2)]
        ab = [s.sb(f"ab{b}", [D, QUAD, D]) for b in range(2)]
        up = [s.sb(f"up{b}", [RW, QUAD, HEADS, DH]) for b in range(2)]
        bup = [s.sb(f"bup{b}", [RW, QUAD, D]) for b in range(2)]
        em = [s.sb(f"em{b}", [RW, QUAD, D]) for b in range(2)]
        head_cols = s.sb("head_cols", [D, HEADS])
        head_rows = s.sb("head_rows", [RW, HEADS])
        mask_ab, mask_b = s.sb("mask_ab", [RW, 2, MB, HEADS]), s.sb("mask_b", [RW, D])
        tok = s.sb("tok", [RW, 2 * MB])
        tok_delta = s.sb("tok_delta", [RW, MB])
        g, bn = s.sb("g", [RW, DH]), s.sb("bn", [RW, DH])
        g16 = s.sb("g16", [RW, DH])
        ident = s.sb("ident", [D, D])
        w0, b0 = s.sb("w0", [D, EXT]), s.sb("b0", [D, EXT])
        wb_mean = s.sb("wb_mean", [D, 2])
        cmean = s.sb("cmean", [RW, NMB])
        w_sb = [s.sb(f"w_sb{b}", [D, EXT]) for b in range(2)]
        gb = [s.sb(f"gb{b}", [D, EXT]) for b in range(2)]
        zs = [s.sb(f"zs{b}", [D, EXT]) for b in range(2)]
        gz, prod, sq, v2, u = (s.sb(n, [RW, EXT]) for n in ("gz", "prod", "sq", "v2", "u"))
        prod2 = s.sb("prod2", [RW, EXT])
        sums = s.sb("sums", [RW, 4])
        tiny = s.sb("tiny", [RW, 8])
        p_ps = [s.ps(f"p{b}", [D, CH]) for b in range(2)]
        state_ps = s.ps("state", [D, CH])
        gram_ps = [s.ps(f"gram{b}", [RW, QUAD, D]) for b in range(2)]
        S = {n: s.sem(n) for n in (
            "loaded consts kq_ready em_ready up_ready bup_ready gram_ready ab_ready z_ready z_stored sq_done "
            "gz_done sc_done s2_done r_inv_done root_done scaled alpha_done mean_done v2_done k_done u_done "
            "grad_done state_ready w_stored b_stored zbar_stored prep chain_init ones_set").split()}

        CONSTS = 3 + 4 * QUAD + 4
        with nc.Block() as block:
            @block.sync
            def _(sp):
                for dst, src in ((head_cols[:], "ttt_head_cols"), (head_rows[:], "ttt_head_rows"),
                                 (mask_ab[:].rearrange("p a b c -> p (a b c)"), "ttt_mask_ab"), (mask_b[:], "ttt_mask_b"),
                                 (tok[:, 0:MB], "ttt_inv"), (g[:], "ttt_g"), (bn[:], "ttt_b"), (ident[:], "ident"),
                                 (w0[:, 0:DH], "ttt_w0"), (b0[RW:D, 0:DH], "ttt_b0")):
                    sp.dma_start(dst, dram[src]).then_inc(S["loaded"], 16)
                sp.dma_start(tok_delta[:], dram["ttt_tid"].partition_broadcast(RW)).then_inc(S["loaded"], 16)
            LOADED = 16 * 11

            @block.gpsimd
            def _(pool):
                for x in (first, gb[0], gb[1]):
                    nc.gpsimd.memset(x[:], 0.0).then_inc(S["consts"], 1)
                pool.wait_ge(S["loaded"], LOADED)
                pool.wait_ge(S["consts"], 3)
                for x in range(2):
                    for j in range(QUAD):
                        for half in range(2):
                            nc.gpsimd.tensor_copy(ab[x][RW:D, j, half * RW:(half + 1) * RW],
                                                  ident[RW:D, RW:D]).then_inc(S["consts"], 1)
                pool.wait_ge(S["consts"], 3 + 4 * QUAD)
                for x in (kT[:, T:], qT[:, T:], eta[:, NMB:], rows[0:RW, 1, NMB:]):
                    nc.gpsimd.memset(x, 0.0).then_inc(S["consts"], 1)
                pool.wait_ge(S["consts"], CONSTS)
                pool.wait_ge(S["prep"], 1)
                nc.gpsimd.tensor_tensor(first[:, 0:RW].rearrange("p (m h) -> p m h", h=HEADS),
                                        kT[:, 0:MB].unsqueeze(2).broadcast_to([D, MB, HEADS]),
                                        head_cols[:].unsqueeze(1).broadcast_to([D, MB, HEADS]),
                                        ALU.mult).then_inc(S["ones_set"], 1)

                def prepare(q, b):
                    shape = [D, QUAD, MB, HEADS]
                    if not isinstance(q, int):
                        pool.wait_ge(S["state_ready"], q * QUAD - (QUAD - 1))
                    for half, (src, off) in enumerate(((kT, MB), (qT, 0))):
                        x = src[:, bass.ds(q * (QUAD * MB) + off, QUAD * MB)] if half == 0 else \
                            src[:, bass.ds(q * (QUAD * MB), QUAD * MB)]
                        x = x.rearrange("p (j m) -> p j m", m=MB)
                        for j in range(QUAD):
                            i_ = nc.gpsimd.tensor_tensor(
                                kq[b][:, j, half, :].rearrange("p (m h) -> p m h", h=HEADS),
                                x[:, j, :].unsqueeze(2).broadcast_to([D, MB, HEADS]),
                                head_cols[:].unsqueeze(1).broadcast_to([D, MB, HEADS]), ALU.mult)
                    i_.then_inc(S["kq_ready"], 1)
                    eq = eta[:, bass.ds(q * QUAD, QUAD)].unsqueeze(2).broadcast_to([RW, QUAD, D])
                    if not isinstance(q, int):
                        pool.wait_ge(S["ab_ready"], q * QUAD - QUAD)
                    nc.gpsimd.tensor_tensor(em[b][:], eq,
                                            mask_ab[:].rearrange("p a b c -> p (a b c)").unsqueeze(1).broadcast_to([RW, QUAD, D]),
                                            ALU.mult).then_inc(S["em_ready"], 1)
                    kr = krow_pad[:, bass.ds(q * QUAD, QUAD), :]
                    for j in range(QUAD):
                        i_ = nc.gpsimd.tensor_tensor(up[b][:, j], kr[:, j, :].unsqueeze(1).broadcast_to([RW, HEADS, DH]),
                                                     head_rows[:].unsqueeze(2).broadcast_to([RW, HEADS, DH]), ALU.mult)
                    i_.then_inc(S["up_ready"], 1)
                    nc.gpsimd.tensor_tensor(bup[b][:], eq, mask_b[:].unsqueeze(1).broadcast_to([RW, QUAD, D]),
                                            ALU.mult).then_inc(S["bup_ready"], 1)

                prepare(0, 0)
                prepare(1, 1)
                with pool.Fori(0, NMB // (2 * QUAD)) as i:
                    for b in range(2):
                        prepare(i * 2 + (b + 2), b)

            @block.tensor
            def _(pe):
                pe.wait_ge(S["loaded"], LOADED)
                pe.wait_ge(S["chain_init"], 1)
                pe.wait_ge(S["consts"], CONSTS)
                pe.wait_ge(S["ones_set"], 1)
                nc.tensor.matmul(state_ps[:, 0:EXT], ident[:], w0[:], start=True, stop=True, skip_group_check=True)
                nc.tensor.matmul(state_ps[:, 32:32 + EXT], ident[:], b0[:], start=False, stop=True,
                                 skip_group_check=True).then_inc(S["state_ready"], 1)
                nc.tensor.matmul(p_ps[0][:, 0:EXT], first[:], w0[:], start=True, stop=False, skip_group_check=True)
                pe.wait_ge(S["b_stored"], 1)
                pe.wait_ge(S["em_ready"], 1)
                nc.tensor.matmul(p_ps[0][:, 0:EXT], ab[0][RW:D, 0, :], gb[0][RW:D, :], start=False, stop=True,
                                 skip_group_check=True).then_inc(S["z_ready"], 1)

                def gram(q, b):
                    start = isinstance(q, int)
                    pe.wait_ge(S["kq_ready"], q + 1)
                    if not start:
                        pe.wait_ge(S["ab_ready"], q * QUAD - QUAD)
                    for j in range(QUAD):
                        lhs = kq[b][:, j - 1, 0, :] if j else first[:, 0:RW] if start else kq[1 - b][:, QUAD - 1, 0, :]
                        mm = nc.tensor.matmul(gram_ps[b][:, j, :], lhs, kq[b][:, j].rearrange("p a b -> p (a b)"),
                                              start=(j == 0), stop=(j == QUAD - 1), skip_group_check=True)
                    mm.then_inc(S["gram_ready"], 1)
                gram(0, 0)
                with pe.Fori(0, NMB // (2 * QUAD)) as i:
                    for b in range(2):
                        for j in range(QUAD):
                            n = i * (2 * QUAD) + (b * QUAD + j)
                            pb = (j + 1) % 2
                            pe.wait_ge(S["z_stored"], n + 1)
                            pe.wait_ge(S["w_stored"], n + 1)
                            nc.tensor.matmul(p_ps[pb][:, 0:EXT], kq[b][:, j].rearrange("p a b -> p (a b)"), w_sb[j % 2][:],
                                             start=True, stop=False, skip_group_check=True)
                            if j == 0:
                                pe.wait_ge(S["up_ready"], 2 * i + (b + 1))
                                pe.wait_ge(S["bup_ready"], 2 * i + (b + 1))
                            pe.wait_ge(S["ab_ready"], n + 1)
                            pe.wait_ge(S["b_stored"], n + 1)
                            pe.wait_ge(S["grad_done"], n + 1)
                            nc.tensor.matmul(p_ps[pb][:, 0:EXT], ab[b][:, j, :], gb[j % 2][:],
                                             start=False, stop=True, skip_group_check=True).then_inc(S["z_ready"], 1)
                            nc.tensor.matmul(state_ps[:, 0:EXT], up[b][:, j].rearrange("p a b -> p (a b)"), gb[j % 2][0:RW, :],
                                             start=False, stop=True, skip_group_check=True)
                            nc.tensor.matmul(state_ps[:, 32:32 + EXT], bup[b][:, j, :], gb[j % 2][0:RW, :],
                                             start=False, stop=True, skip_group_check=True).then_inc(S["state_ready"], 1)
                            if j == 0:
                                gram(i * 2 + (b + 1), 1 - b)

            @block.scalar
            def _(act):
                def store_state(n, j):
                    act.wait_ge(S["state_ready"], n + 1)
                    nc.scalar.activation(w_sb[j % 2][:], state_ps[:, 0:EXT], ACT.Copy).then_inc(S["w_stored"], 1)
                    nc.scalar.activation(gb[j % 2][RW:D, :], state_ps[RW:D, 32:32 + EXT], ACT.Copy).then_inc(S["b_stored"], 1)

                def keep_zbar(n, jj):
                    nc.scalar.activation(zbar[RW:D, bass.ds(n, 1), :].rearrange("p a e -> p (a e)"),
                                         zs[jj % 2][RW:D, 0:DH], ACT.Copy).then_inc(S["zbar_stored"], 1)
                act.wait_ge(S["consts"], 3)
                store_state(0, 0)
                with act.Fori(0, NMB // (2 * QUAD)) as i:
                    for jj in range(2 * QUAD):
                        n = i * (2 * QUAD) + jj
                        act.wait_ge(S["z_stored"], n + 2)
                        nc.scalar.activation(sq[:], zs[jj % 2][0:RW, :], ACT.Square, accum_out=tiny[:, 6:7]).then_inc(S["sq_done"], 1)
                        act.wait_ge(S["r_inv_done"], n + 1)
                        nc.scalar.activation(tiny[:, 1:2], tiny[:, 0:1], ACT.Sqrt, scale=float(DH)).then_inc(S["root_done"], 1)
                        store_state(n + 1, jj + 1)
                        keep_zbar(n, jj)
                act.wait_ge(S["z_stored"], NMB + 2)
                keep_zbar(NMB, 0)

            @block.vector
            def _(dve):
                dve.wait_ge(S["loaded"], LOADED)
                count = [0]

                def then(x):
                    count[0] += 1
                    x.then_inc(S["mean_done"], 1)
                    dve.wait_ge(S["mean_done"], count[0])
                V = nc.vector
                then(V.tensor_tensor(tok[:, MB:], tok[:, 0:MB], tok_delta[:], ALU.add))
                then(V.tensor_scalar(tok[:, 0:MB], tok[:, MB:], 0.0, None, ALU.max))
                then(V.tensor_tensor(mask_ab[:, 1], mask_ab[:, 1], tok[:, 0:MB].unsqueeze(2).broadcast_to([RW, MB, HEADS]), ALU.mult))
                then(V.tensor_scalar(mask_ab[:, 0], mask_ab[:, 0], tok[:, MB - 1:MB], None, ALU.mult))
                then(V.tensor_scalar(mask_b[:], mask_b[:], tok[:, MB - 1:MB], None, ALU.mult))
                then(V.tensor_tensor(krow, krow, eta[:, 0:NMB].unsqueeze(2).broadcast_to([RW, NMB, DH]), ALU.mult))
                then(V.tensor_scalar(krow, krow, tok[:, MB - 1:MB], -1.0, ALU.mult, ALU.mult))
                wide = lambda a: a[:].unsqueeze(1).broadcast_to([RW, NMB, DH])
                then(V.tensor_tensor(cc, cc, wide(bn), ALU.add))
                then(V.tensor_tensor(cc, cc, wide(g), ALU.mult))
                then(V.reduce_sum(cmean[:], cc, AX_X))
                then(V.tensor_scalar(cmean[:], cmean[:], 1.0 / DH, None, ALU.mult))
                then(V.tensor_tensor(cc, cc, cmean[:].unsqueeze(2).broadcast_to([RW, NMB, DH]), ALU.subtract))
                then(V.scalar_tensor_tensor(out=g16[:], in0=g[:], scalar=float(DH), in1=g[:], op0=ALU.mult, op1=ALU.mult))
                then(V.memset(b0[0:RW, :], 0.0))
                for x, p in ((w0, slice(0, D)), (b0, slice(RW, D))):
                    then(V.reduce_sum(wb_mean[p, 0:1], x[p, 0:DH], AX_X))
                    then(V.tensor_scalar(wb_mean[p, 1:2], wb_mean[p, 0:1], 1.0 / DH, None, ALU.mult))
                    then(V.tensor_scalar(x[p, 0:DH], x[p, 0:DH], wb_mean[p, 1:2], None, ALU.subtract))
                then(V.memset(w0[:, DH:], 0.0))
                then(V.memset(b0[RW:D, DH:], (DH * TTT_EPS) ** 0.5))
                dve.sem_inc(S["prep"], 1)
                dve.sem_inc(S["chain_init"], 1)
                dve.sem_inc(S["z_stored"], 1)
                dve.wait_ge(S["consts"], CONSTS)

                def make_ab(q, b, j):
                    if j == 0:
                        dve.wait_ge(S["em_ready"], q + 1)
                        dve.wait_ge(S["gram_ready"], q + 1)
                        if not isinstance(q, int):
                            dve.wait_ge(S["state_ready"], q * QUAD - (QUAD - 1))
                    V.scalar_tensor_tensor(out=ab[b][0:RW, j, :], in0=gram_ps[b][:, j, :], scalar=1.0, in1=em[b][:, j, :],
                                           op0=ALU.add, op1=ALU.mult).then_inc(S["ab_ready"], 1)
                for j in range(QUAD):
                    make_ab(0, 0, j)

                def store_z(n, jj):
                    dve.wait_ge(S["z_ready"], n + 1)
                    dve.wait_ge(S["zbar_stored"], n + 1)
                    V.tensor_copy(zs[jj % 2][:], p_ps[jj % 2][:, 0:EXT]).then_inc(S["z_stored"], 1)
                dve.sem_inc(S["zbar_stored"], 2)
                with dve.Fori(0, NMB // (2 * QUAD)) as i:
                    for jj in range(2 * QUAD):
                        b, j = jj // QUAD, jj % QUAD
                        n = i * (2 * QUAD) + jj
                        z = zs[jj % 2][0:RW, 0:DH]
                        c = cc[:, bass.ds(n, 1), :].rearrange("p a e -> p (a e)")
                        store_z(n, jj)
                        dve.wait_ge(S["z_stored"], n + 2)
                        V.scalar_tensor_tensor(out=gz[:, 0:DH], in0=z, scalar=1.0, in1=g16[:], op0=ALU.mult, op1=ALU.mult,
                                               accum_out=sums[:, 2:3]).then_inc(S["gz_done"], 1)
                        V.scalar_tensor_tensor(out=prod[:, 0:DH], in0=z, scalar=1.0, in1=c, op0=ALU.mult, op1=ALU.mult,
                                               accum_out=sums[:, 1:2]).then_inc(S["sc_done"], 1)
                        dve.wait_ge(S["gz_done"], n + 1)
                        V.scalar_tensor_tensor(out=prod2[:, 0:DH], in0=z, scalar=1.0, in1=gz[:, 0:DH], op0=ALU.mult, op1=ALU.mult,
                                               accum_out=sums[:, 0:1]).then_inc(S["s2_done"], 1)
                        dve.wait_ge(S["sq_done"], n + 1)
                        V.reciprocal(tiny[:, 0:1], tiny[:, 6:7]).then_inc(S["r_inv_done"], 1)
                        V.tensor_scalar(sums[:, 3:4], sums[:, 2:3], 1.0 / DH, None, ALU.mult).then_inc(S["k_done"], 1)
                        dve.wait_ge(S["s2_done"], n + 1)
                        dve.wait_ge(S["sc_done"], n + 1)
                        dve.wait_ge(S["r_inv_done"], n + 1)
                        V.tensor_scalar(tiny[:, 2:4], sums[:, 0:2], tiny[:, 0:1], -1.0, ALU.mult, ALU.mult).then_inc(S["scaled"], 1)
                        dve.wait_ge(S["k_done"], 2 * n + 1)
                        V.tensor_scalar(v2[:, 0:DH], gz[:, 0:DH], sums[:, 3:4], tiny[:, 0:1], ALU.subtract, ALU.mult).then_inc(S["v2_done"], 1)
                        dve.wait_ge(S["scaled"], n + 1)
                        V.tensor_scalar(tiny[:, 4:5], tiny[:, 2:3], tiny[:, 0:1], None, ALU.mult).then_inc(S["alpha_done"], 1)
                        dve.wait_ge(S["root_done"], n + 1)
                        dve.wait_ge(S["v2_done"], n + 1)
                        V.scalar_tensor_tensor(out=u[:, 0:DH], in0=c, scalar=tiny[:, 1:2], in1=v2[:, 0:DH], op0=ALU.mult,
                                               op1=ALU.add).then_inc(S["u_done"], 1)
                        dve.wait_ge(S["alpha_done"], n + 1)
                        V.tensor_scalar(tiny[:, 5:6], tiny[:, 3:4], tiny[:, 1:2], tiny[:, 4:5], ALU.mult,
                                        ALU.add).then_inc(S["k_done"], 1)
                        dve.wait_ge(S["k_done"], 2 * n + 2)
                        dve.wait_ge(S["u_done"], n + 1)
                        V.scalar_tensor_tensor(out=gb[jj % 2][0:RW, 0:DH], in0=z, scalar=tiny[:, 5:6], in1=u[:, 0:DH],
                                               op0=ALU.mult, op1=ALU.add).then_inc(S["grad_done"], 1)
                        for jn in {0: (), 1: (0,), 2: (1,), 3: (2, 3)}[j]:
                            make_ab(i * 2 + (b + 1), 1 - b, jn)
                store_z(NMB, 0)


def ttt_finish(nc, dram, rows, zbar, hidden):
    scratch = nc.dram_tensor("hidden_scratch", [T, D], F32, kind="Internal").ap()
    with Scope(nc, "tf") as s:
        H = slice(RW, D)
        g, bn = s.sb("g", [D, DH]), s.sb("bn", [D, DH])
        sq = s.sb("sq", [D, NMB, DH])
        y = s.sb("y", [D, NMB, DH])
        var = s.sb("var", [D, NMB])
        eps = s.sb("eps", [D, 1])
        tokens = s.sb("tokens", [D, TT, D])
        ident = s.sb("ident", [D, D])
        turn_ps = s.ps("turn", [D, NCH, CH])
        S = {n: s.sem(n) for n in "loaded sq_done var_done root_done step y_done written read turned stored eps_set".split()}
        zb = zbar[H, 1:NMB + 1, :]
        wide = lambda a: a[H].unsqueeze(1).broadcast_to([RW, NMB, DH])
        with nc.Block() as block:
            @block.sync
            def _(sp):
                sp.dma_start(g[H], dram["ttt_g"]).then_inc(S["loaded"], 16)
                sp.dma_start(bn[H], dram["ttt_b"]).then_inc(S["loaded"], 16)
                sp.dma_start(ident[:], dram["ident"]).then_inc(S["loaded"], 16)
                sp.wait_ge(S["y_done"], 1)
                sp.dma_start(scratch.rearrange("(n m) (h e) -> (m h) n e", m=MB, e=DH), y[H]).then_inc(S["written"], 16)
                sp.wait_ge(S["written"], 16)
                sp.dma_start(tokens[:], scratch.rearrange("(t p) d -> p t d", p=D)).then_inc(S["read"], 16)

            @block.gpsimd
            def _(pool):
                pool.memset(eps[:], TTT_EPS).then_inc(S["eps_set"], 1)

            @block.scalar
            def _(act):
                act.wait_ge(S["eps_set"], 1)
                nc.scalar.activation(sq[H], zb, ACT.Square).then_inc(S["sq_done"], 1)
                act.wait_ge(S["var_done"], 1)
                nc.scalar.activation(var[H], var[H], ACT.Sqrt, scale=1.0 / DH, bias=eps[H]).then_inc(S["root_done"], 1)

            @block.vector
            def _(dve):
                V = nc.vector
                dve.wait_ge(S["sq_done"], 1)
                V.reduce_sum(var[H], sq[H], AX_X).then_inc(S["var_done"], 1)
                dve.wait_ge(S["root_done"], 1)
                dve.wait_ge(S["loaded"], 48)
                V.reciprocal(var[H], var[H]).then_inc(S["step"], 1)
                dve.wait_ge(S["step"], 1)
                V.tensor_tensor(y[H], zb, var[H].unsqueeze(2).broadcast_to([RW, NMB, DH]), ALU.mult).then_inc(S["step"], 1)
                dve.wait_ge(S["step"], 2)
                V.tensor_tensor(y[H], y[H], wide(g), ALU.mult).then_inc(S["step"], 1)
                dve.wait_ge(S["step"], 3)
                V.tensor_tensor(y[H], y[H], wide(bn), ALU.add).then_inc(S["step"], 1)
                dve.wait_ge(S["step"], 4)
                V.tensor_tensor(y[H], y[H], rows[H, 0, 0:NMB], ALU.add).then_inc(S["y_done"], 1)
                for c in range(NCH):
                    dve.wait_ge(S["turned"], c + 1)
                    V.tensor_copy(hidden[:, c * CH:(c + 1) * CH], turn_ps[:, c, :]).then_inc(S["stored"], 1)

            @block.tensor
            def _(pe):
                pe.wait_ge(S["loaded"], 48)
                pe.wait_ge(S["read"], 16)
                for c in range(NCH):
                    for q in range(4):
                        mm = nc.tensor.transpose(turn_ps[:, c, q * D:(q + 1) * D], tokens[:, 4 * c + q, :], ident[:])
                    mm.then_inc(S["turned"], 1)


def lay_out_ttt(inp):
    a = {k: np.asarray(v) for k, v in inp.items()}
    wk, wq, wv = (a[f"L1_attn_{n}"] for n in ("wk", "wq", "wv"))
    feat = np.arange(D)
    d = feat % DH
    perm = np.where(d < DH // 2, feat + DH // 2, feat - DH // 2)
    inv = (1.0 / np.float32(10000.0) ** (np.arange(0, DH, 2, dtype=np.float32) / np.float32(DH))).astype(np.float32)
    f = np.arange(T, dtype=np.float32)[None, :] * inv[d % (DH // 2)][:, None]
    sign = np.where(d < DH // 2, -1.0, 1.0).astype(np.float32)[:, None]
    lrw = a["L1_attn_lr_w"][:, 0, :]
    lr = np.zeros((D, MB, MB, HEADS), np.float32)
    for m in range(MB):
        lr[:, m, m, :] = lrw.T
    row_head = np.arange(RW) % HEADS
    row_tok = np.arange(RW) // HEADS
    same = row_head[:, None, None] == np.arange(HEADS)[None, None, :]
    mask = np.zeros((RW, 2, MB, HEADS), np.float32)
    mask[:, 0] = np.where(same, -1.0, 0.0)
    mask[:, 1] = np.where(same & (row_tok[:, None, None] <= np.arange(MB)[None, :, None]), -1.0, 0.0)
    mask_b = np.zeros((RW, D), np.float32)
    mask_b[:, RW:] = np.where(row_head[:, None] == row_head[None, :], -1.0, 0.0)
    tile_rows = lambda x: np.ascontiguousarray(np.tile(x, (MB, 1)))
    return {
        "ttt_wk": np.ascontiguousarray(wk.T), "ttt_wkp": np.ascontiguousarray(wk[perm].T),
        "ttt_wq": np.ascontiguousarray(wq.T), "ttt_wqp": np.ascontiguousarray(wq[perm].T),
        "ttt_wv": np.ascontiguousarray(wv.T),
        "cos": np.cos(f).astype(np.float32), "sin": (np.sin(f) * sign).astype(np.float32),
        "ttt_lrw": lr.reshape(D, MB * RW), "ttt_lrb": tile_rows(a["L1_attn_lr_b"].reshape(HEADS, 1)),
        "ttt_head_cols": (np.arange(D)[:, None] // DH == np.arange(HEADS)[None, :]).astype(np.float32),
        "ttt_head_rows": (row_head[:, None] == np.arange(HEADS)[None, :]).astype(np.float32),
        "ttt_mask_ab": mask.reshape(RW, D), "ttt_mask_b": mask_b,
        "ttt_inv": np.tile((np.float32(1) / np.arange(1, MB + 1, dtype=np.float32))[None], (RW, 1)),
        "ttt_tid": a["L1_attn_token_idx_delta"],
        "ttt_g": tile_rows(a["L1_attn_ttt_norm_w"]), "ttt_b": tile_rows(a["L1_attn_ttt_norm_b"]),
        "ttt_w0": a["L1_attn_W1"].reshape(D, DH), "ttt_b0": tile_rows(a["L1_attn_b1"][:, 0, :]),
        "ln1_w": a["L1_attn_ln_w"].reshape(D, 1), "ln1_b": a["L1_attn_ln_b"].reshape(D, 1),
        "post_w": a["L1_attn_post_norm_w"].reshape(D, 1), "post_b": a["L1_attn_post_norm_b"].reshape(D, 1),
    }


NT = 6
NS = 8
XD = 72
WIN = 5


def longhorn_inputs(nc, dram, xn, xc, xd):
    with Scope(nc, "li") as s:
        w_in = [s.sb(f"w_in{b}", [D, D]) for b in range(2)]
        w_x = s.sb("w_x", [D, NT, XD])
        conv_w, conv_b = s.sb("conv_w", [D, NT, 3]), s.sb("conv_b", [D, NT])
        xl = [s.sb(f"xl{b}", [D, 2 + T]) for b in range(2)]
        acc = [s.sb(f"acc{b}", [D, T]) for b in range(2)]
        acc2 = [s.sb(f"acc2{b}", [D, T]) for b in range(2)]
        xl_ps = s.ps("xl", [D, NCH, CH])
        xd_ps = s.ps("xd", [XD, NCH, CH])
        S = {n: s.sem(n) for n in ("loaded w_a w_b padded xl_ready xl_stored first_tap second_tap third_tap "
                                   "xc_ready w_used xd_ready xd_stored").split()}
        w_loaded = (S["w_a"], S["w_b"])
        flat = lambda ap: ap.rearrange("p a b -> p (a b)")
        with nc.Block() as block:
            @block.sync
            def _(sp):
                for i in range(NT):
                    if i >= 2:
                        sp.wait_ge(S["w_used"], i - 1)
                    sp.dma_start(w_in[i % 2][:], dram["lh_in"][i * D:(i + 1) * D, :]).then_inc(w_loaded[i % 2], 16)
                    if i == 0:
                        sp.dma_start(flat(w_x[:]), dram["lh_x"]).then_inc(S["loaded"], 16)
                        sp.dma_start(flat(conv_w[:]), dram["lh_conv_w"]).then_inc(S["loaded"], 16)
                        sp.dma_start(conv_b[:], dram["lh_conv_b"]).then_inc(S["loaded"], 16)

            @block.gpsimd
            def _(pool):
                for b in range(2):
                    pool.memset(xl[b][:, 0:2], 0.0).then_inc(S["padded"], 1)

            @block.tensor
            def _(pe):
                pe.wait_ge(S["loaded"], 48)
                for i in range(NT):
                    pe.wait_ge(w_loaded[i % 2], 16 * (i // 2 + 1))
                    for c in range(NCH):
                        if i:
                            pe.wait_ge(S["xl_stored"], (i - 1) * NCH + c + 1)
                        mm = nc.tensor.matmul(xl_ps[:, c, :], w_in[i % 2][:], xn[:, c * CH:(c + 1) * CH], start=True,
                                              stop=True)
                        mm.then_inc(S["xl_ready"], 1)
                        if c == NCH - 1:
                            pe.wait_ge(S["xl_ready"], (i + 1) * NCH)
                            pe.sem_inc(S["w_used"], 1)
                for i in range(NT):
                    pe.wait_ge(S["xc_ready"], i + 1)
                    for c in range(NCH):
                        mm = nc.tensor.matmul(xd_ps[:, c, :], w_x[:, i, :], xc[:, i, c * CH:(c + 1) * CH],
                                              start=(i == 0), stop=(i == NT - 1))
                mm.then_inc(S["xd_ready"], 1)

            @block.scalar
            def _(act):
                act.wait_ge(S["loaded"], 48)
                act.wait_ge(S["padded"], 2)
                for i in range(NT):
                    b = i % 2
                    for c in range(NCH):
                        act.wait_ge(S["xl_ready"], i * NCH + c + 1)
                        if i >= 2 and c == 0:
                            act.wait_ge(S["third_tap"], i - 1)
                        nc.scalar.activation(xl[b][:, 2 + c * CH:2 + (c + 1) * CH], xl_ps[:, c, :],
                                             ACT.Copy).then_inc(S["xl_stored"], 1)
                    act.wait_ge(S["xl_stored"], (i + 1) * NCH)
                    nc.scalar.activation(acc[b][:], xl[b][:, 0:T], ACT.Identity, scale=conv_w[:, i, 0:1],
                                         bias=conv_b[:, i:i + 1]).then_inc(S["first_tap"], 1)
                    act.wait_ge(S["third_tap"], i + 1)
                    nc.scalar.activation(xc[:, i, :], acc[b][:], ACT.Silu).then_inc(S["xc_ready"], 1)
                act.wait_ge(S["xd_ready"], 1)
                nc.scalar.activation(xd[:], flat(xd_ps[:]), ACT.Copy).then_inc(S["xd_stored"], 1)

            @block.vector
            def _(dve):
                for i in range(NT):
                    b = i % 2
                    dve.wait_ge(S["first_tap"], i + 1)
                    nc.vector.scalar_tensor_tensor(out=acc2[b][:], in0=xl[b][:, 1:1 + T], scalar=conv_w[:, i, 1:2],
                                                   in1=acc[b][:], op0=ALU.mult, op1=ALU.add).then_inc(S["second_tap"], 1)
                    dve.wait_ge(S["second_tap"], i + 1)
                    nc.vector.scalar_tensor_tensor(out=acc[b][:], in0=xl[b][:, 2:2 + T], scalar=conv_w[:, i, 2:3],
                                                   in1=acc2[b][:], op0=ALU.mult, op1=ALU.add).then_inc(S["third_tap"], 1)


def longhorn_scan(nc, dram, xn, xc, xd, h_red):
    PAIRS_N = NS // 2
    with Scope(nc, "ls") as s:
        w_z = s.sb("w_z", [D, NT, D])
        w_dt = s.sb("w_dt", [XD, NT, D])
        w_red = s.sb("w_red", [D, NT, D])
        dt_b, neg_b, d_par = s.sb("dt_b", [D, NT]), s.sb("neg_b", [D, NT]), s.sb("d_par", [D, NT])
        pick_k, pick_q = s.sb("pick_k", [XD, NS, D]), s.sb("pick_q", [XD, NS, D])
        sum_k = s.sb("sum_k", [XD, D])
        ident = s.sb("ident", [D, D])
        d_diag = s.sb("d_diag", [D, NT, D])
        kk, qq, nk2 = (s.sb(n, [D, NS, CH]) for n in ("kk", "qq", "nk2"))
        zg = s.sb("zg", [D, NT, CH])
        xd_sq = s.sb("xd_sq", [XD, CH])
        ks = s.sb("ks", [D, CH])
        ex = [s.sb(f"ex{b}", [D, CH]) for b in range(2)]
        dd = s.sb("dd", [D, CH])
        dx = s.sb("dx", [D, CH])
        a_ = [s.sb(f"a{b}", [D, 2, CH]) for b in range(2)]
        b_ = [s.sb(f"b{b}", [D, 2, CH]) for b in range(2)]
        st = [s.sb(f"st{b}", [D, 2, CH]) for b in range(2)]
        qs = [s.sb(f"qs{b}", [D, 2, CH]) for b in range(2)]
        carry = s.sb("carry", [D, NT, NS])
        yg = s.sb("yg", [D, CH])
        bc_ps = s.ps("bc", [D, 2, CH])
        dt_ps = s.ps("dt", [D, CH])
        y_ps = s.ps("y", [D, 2, CH])
        red_ps = s.ps("red", [D, CH])
        S = {n: s.sem(n) for n in (
            "loaded negated diag zero_carry bc_ready bc_stored z_done sq_done ks_ready ks_stored nk2_done dt_ready ex_ready "
            "den_ready dd_ready dx_ready a_ready a1_ready b_ready st_ready carry_ready qs_ready y_ready yg_ready red_ready "
            "red_stored").split()}
        flat = lambda ap: ap.rearrange("p a b -> p (a b)")
        LOADED = 16 * 9
        NB = 2 * NS + 1 + NT
        with nc.Block() as block:
            @block.sync
            def _(sp):
                for dst, src in ((flat(w_z[:]), "lh_z"), (flat(w_dt[:]), "lh_dt"), (flat(w_red[:]), "lh_red"),
                                 (dt_b[:], "lh_dt_b"), (d_par[:], "lh_d"), (flat(pick_k[:]), "lh_pick_k"),
                                 (flat(pick_q[:]), "lh_pick_q"), (sum_k[:], "lh_sum_k"), (ident[:], "ident")):
                    sp.dma_start(dst, dram[src]).then_inc(S["loaded"], 16)

            @block.gpsimd
            def _(pool):
                nc.gpsimd.memset(carry[:], 0.0).then_inc(S["zero_carry"], 1)
                with pool.Fori(0, NCH) as c:
                    for i in range(NT):
                        for p in range(PAIRS_N):
                            n = c * (NT * PAIRS_N) + (i * PAIRS_N + p)
                            pool.wait_ge(S["dx_ready"], c * NT + (i + 1))
                            if i == 0 and p == 0:
                                pool.wait_ge(S["bc_stored"], c * NB + (2 * NS + 2))
                            pool.wait_ge(S["st_ready"], n + 1)
                            nc.gpsimd.tensor_tensor(b_[p % 2][:], dx[:].unsqueeze(1).broadcast_to([D, 2, CH]),
                                                    kk[:, 2 * p:2 * p + 2, :], ALU.mult).then_inc(S["b_ready"], 1)

            @block.tensor
            def _(pe):
                pe.sem_inc(S["y_ready"], 2)
                pe.sem_inc(S["red_ready"], 1)
                pe.wait_ge(S["loaded"], LOADED)
                pe.wait_ge(S["diag"], NT)
                with pe.Fori(0, NCH) as c:
                    cols = bass.ds(c * CH, CH)
                    m = 0

                    def through(lhs, rhs):
                        nonlocal m
                        pe.wait_ge(S["bc_stored"], c * NB + (m + 1))
                        nc.tensor.matmul(bc_ps[:, m % 2, :], lhs, rhs, start=True, stop=True).then_inc(S["bc_ready"], 1)
                        m += 1
                    for n in range(NS):
                        through(pick_k[:, n, :], xd[:, cols])
                    for n in range(NS):
                        through(pick_q[:, n, :], xd[:, cols])
                    pe.wait_ge(S["sq_done"], c + 1)
                    through(sum_k[:], xd_sq[:])
                    for i in range(NT):
                        through(w_z[:, i, :], xn[:, cols])
                    for i in range(NT):
                        k = c * NT + i
                        pe.wait_ge(S["ex_ready"], k + 1)
                        nc.tensor.matmul(dt_ps[:], w_dt[:, i, :], xd[:, cols], start=True, stop=True).then_inc(S["dt_ready"], 1)
                        pe.wait_ge(S["yg_ready"], k + 1)
                        nc.tensor.matmul(y_ps[:, i % 2, :], d_diag[:, i, :], xc[:, i, cols], start=True, stop=False)
                        for p in range(PAIRS_N):
                            pe.wait_ge(S["qs_ready"], c * (NT * PAIRS_N) + (i * PAIRS_N + p + 3))
                            for j in range(2):
                                mm = nc.tensor.matmul(y_ps[:, i % 2, :], ident[:], qs[p % 2][:, j, :], start=False,
                                                      stop=(p == PAIRS_N - 1 and j == 1))
                            mm.then_inc(S["y_ready"], 1)
                        pe.wait_ge(S["yg_ready"], k + 3)
                        if i == 0:
                            pe.wait_ge(S["red_stored"], c + 1)
                        nc.tensor.matmul(red_ps[:], w_red[:, i, :], yg[:], start=(i == 0),
                                         stop=(i == NT - 1)).then_inc(S["red_ready"], 1)

            @block.scalar
            def _(act):
                act.sem_inc(S["bc_stored"], 2)
                act.sem_inc(S["ex_ready"], 1)
                act.sem_inc(S["red_stored"], 1)
                act.wait_ge(S["loaded"], LOADED)
                nc.scalar.activation(neg_b[:], dt_b[:], ACT.Copy, scale=-1.0).then_inc(S["negated"], 1)
                act.wait_ge(S["negated"], 1)
                with act.Fori(0, NCH) as c:
                    cols = bass.ds(c * CH, CH)
                    act.wait_ge(S["qs_ready"], c * (NT * PAIRS_N) + 2)
                    act.wait_ge(S["yg_ready"], c * NT + 2)
                    nc.scalar.activation(xd_sq[:], xd[:, cols], ACT.Square).then_inc(S["sq_done"], 1)
                    for n in range(NS):
                        act.wait_ge(S["bc_ready"], c * NB + (n + 1))
                        nc.scalar.activation(kk[:, n, :], bc_ps[:, n % 2, :], ACT.Copy).then_inc(S["bc_stored"], 1)
                    for n in range(NS):
                        act.wait_ge(S["bc_ready"], c * NB + (NS + n + 1))
                        nc.scalar.activation(qq[:, n, :], bc_ps[:, n % 2, :], ACT.Copy).then_inc(S["bc_stored"], 1)
                    act.wait_ge(S["bc_ready"], c * NB + (2 * NS + 1))
                    nc.scalar.activation(ks[:], bc_ps[:, 0, :], ACT.Copy).then_inc(S["bc_stored"], 1)
                    for i in range(NT):
                        act.wait_ge(S["bc_ready"], c * NB + (2 * NS + 2 + i))
                        nc.scalar.activation(zg[:, i, :], bc_ps[:, (i + 1) % 2, :], ACT.Silu).then_inc(S["bc_stored"], 1)
                    for i in range(NT):
                        k = c * NT + i
                        act.wait_ge(S["dt_ready"], k + 1)
                        act.wait_ge(S["den_ready"], k + 1)
                        nc.scalar.activation(ex[i % 2][:], dt_ps[:], ACT.Exp, scale=-1.0,
                                             bias=neg_b[:, i:i + 1]).then_inc(S["ex_ready"], 1)
                        for p in range(PAIRS_N):
                            n = c * (NT * PAIRS_N) + (i * PAIRS_N + p)
                            act.wait_ge(S["a_ready"], n + 1)
                            nc.scalar.activation(a_[p % 2][:], a_[p % 2][:], ACT.Copy, bias=1.0).then_inc(S["a1_ready"], 1)
                    act.wait_ge(S["red_ready"], c * NT + (NT + 1))
                    nc.scalar.activation(h_red[:, cols], red_ps[:], ACT.Copy).then_inc(S["red_stored"], 1)

            @block.vector
            def _(dve):
                V = nc.vector
                dve.sem_inc(S["den_ready"], 2)
                dve.sem_inc(S["st_ready"], 2)
                dve.sem_inc(S["qs_ready"], 2)
                dve.sem_inc(S["yg_ready"], 2)
                dve.wait_ge(S["loaded"], LOADED)
                for i in range(NT):
                    V.tensor_scalar(d_diag[:, i, :], ident[:], d_par[:, i:i + 1], None, ALU.mult).then_inc(S["diag"], 1)
                dve.wait_ge(S["zero_carry"], 1)
                with dve.Fori(0, NCH) as c:
                    cols = bass.ds(c * CH, CH)
                    dve.wait_ge(S["bc_stored"], c * NB + (2 * NS + 3))
                    V.scalar_tensor_tensor(out=flat(nk2[:]), in0=flat(kk[:]), scalar=-1.0, in1=flat(kk[:]), op0=ALU.mult,
                                           op1=ALU.mult).then_inc(S["nk2_done"], 1)
                    dve.wait_ge(S["nk2_done"], c + 1)
                    for i in range(NT):
                        k = c * NT + i
                        dve.wait_ge(S["ex_ready"], k + 2)
                        V.scalar_tensor_tensor(out=dd[:], in0=ex[i % 2][:], scalar=1.0, in1=ks[:], op0=ALU.add,
                                               op1=ALU.add).then_inc(S["den_ready"], 1)
                        dve.wait_ge(S["den_ready"], k + 3)
                        V.reciprocal(dd[:], dd[:]).then_inc(S["dd_ready"], 1)
                        dve.wait_ge(S["dd_ready"], k + 1)
                        if i:
                            dve.wait_ge(S["b_ready"], c * (NT * PAIRS_N) + i * PAIRS_N)
                        V.tensor_tensor(dx[:], dd[:], xc[:, i, cols], ALU.mult).then_inc(S["dx_ready"], 1)

                        def make_a(p):
                            V.tensor_tensor(a_[p % 2][:], dd[:].unsqueeze(1).broadcast_to([D, 2, CH]),
                                            nk2[:, 2 * p:2 * p + 2, :], ALU.mult).then_inc(S["a_ready"], 1)
                        make_a(0)
                        for p in range(PAIRS_N):
                            n = c * (NT * PAIRS_N) + (i * PAIRS_N + p)
                            if p + 1 < PAIRS_N:
                                make_a(p + 1)
                            dve.wait_ge(S["a1_ready"], n + 1)
                            dve.wait_ge(S["b_ready"], n + 1)
                            for j in range(2):
                                x = V.tensor_tensor_scan(st[p % 2][:, j, :], a_[p % 2][:, j, :], b_[p % 2][:, j, :],
                                                         carry[:, i, 2 * p + j:2 * p + j + 1], ALU.mult, ALU.add)
                            x.then_inc(S["st_ready"], 1)
                            dve.wait_ge(S["st_ready"], n + 3)
                            V.tensor_copy(carry[:, i, 2 * p:2 * p + 2], st[p % 2][:, :, CH - 1]).then_inc(S["carry_ready"], 1)
                            dve.wait_ge(S["y_ready"], n + 1)
                            V.tensor_tensor(qs[p % 2][:], st[p % 2][:], qq[:, 2 * p:2 * p + 2, :],
                                            ALU.mult).then_inc(S["qs_ready"], 1)
                        dve.wait_ge(S["y_ready"], k * PAIRS_N + (PAIRS_N + 2))
                        dve.wait_ge(S["bc_stored"], c * NB + (2 * NS + 4 + i))
                        dve.wait_ge(S["red_ready"], k + 1)
                        V.tensor_tensor(yg[:], y_ps[:, i % 2, :], zg[:, i, :], ALU.mult).then_inc(S["yg_ready"], 1)


def gains(nc, dram, xn, gain):
    W = D + 2 * WIN
    with Scope(nc, "gn") as s:
        w_q, w_k = s.sb("w_q", [D, D]), s.sb("w_k", [D, D])
        ident = s.sb("ident", [D, D])
        ones = s.sb("ones", [D, D])
        band = s.sb("band", [D, W])
        qg, kg = s.sb("qg", [D, T]), s.sb("kg", [D, T + 2 * WIN])
        sc = s.sb("sc", [D, TT, W])
        mx, nmx, tot, inv, gcol = (s.sb(n, [D, TT]) for n in ("mx", "nmx", "tot", "inv", "gcol"))
        junk = s.sb("junk", [D, TT, W])
        diag = [s.sb(f"diag{b}", [D, D]) for b in range(2)]
        two = s.sb("two", [D, 1])
        pr_ps = s.ps("pr", [D, 2, CH])
        sc_ps = s.ps("sc", [D, 2, CH])
        g_ps = s.ps("g", [D, NCH, CH])
        S = {n: s.sem(n) for n in ("loaded set pr_ready pr_stored edges sc_ready sc_masked mx_ready nmx_ready ex_ready "
                                   "inv_ready g_ready diag_ready out_ready stored").split()}
        with nc.Block() as block:
            @block.sync
            def _(sp):
                for dst, src in ((w_q, "gn_q"), (w_k, "gn_k"), (ident, "ident"), (band, "gn_band")):
                    sp.dma_start(dst[:], dram[src]).then_inc(S["loaded"], 16)

            @block.gpsimd
            def _(pool):
                pool.memset(ones[:], 1.0).then_inc(S["set"], 1)
                pool.memset(two[:], -2.0).then_inc(S["set"], 1)

            @block.tensor
            def _(pe):
                pe.wait_ge(S["loaded"], 64)
                for n in range(2 * NCH):
                    c = n // 2
                    if n >= 2:
                        pe.wait_ge(S["pr_stored"], n - 1)
                    nc.tensor.matmul(pr_ps[:, n % 2, :], (w_q, w_k)[n % 2][:], xn[:, c * CH:(c + 1) * CH], start=True,
                                     stop=True).then_inc(S["pr_ready"], 1)
                pe.wait_ge(S["pr_stored"], 2 * NCH)
                pe.wait_ge(S["edges"], 1)
                for t in range(TT):
                    if t >= 2:
                        pe.wait_ge(S["sc_masked"], t - 1)
                    nc.tensor.matmul(sc_ps[:, t % 2, 0:W], qg[:, t * D:(t + 1) * D], kg[:, t * D:t * D + W], start=True,
                                     stop=True).then_inc(S["sc_ready"], 1)
                pe.wait_ge(S["set"], 2)
                for t in range(TT):
                    pe.wait_ge(S["diag_ready"], t + 1)
                    nc.tensor.matmul(g_ps[:, t // 4, (t % 4) * D:(t % 4 + 1) * D], ones[:], diag[t % 2][:],
                                     start=(t % 4 == 0), stop=(t % 4 == 3), skip_group_check=True).then_inc(S["out_ready"], 1)

            @block.scalar
            def _(act):
                for n in range(2 * NCH):
                    c = n // 2
                    act.wait_ge(S["pr_ready"], n + 1)
                    dst = kg[:, WIN + c * CH:WIN + (c + 1) * CH] if n % 2 else qg[:, c * CH:(c + 1) * CH]
                    nc.scalar.activation(dst, pr_ps[:, n % 2, :], ACT.Copy).then_inc(S["pr_stored"], 1)
                for t in range(TT):
                    act.wait_ge(S["nmx_ready"], 1)
                    x = nc.scalar.activation(junk[:, t, :], sc[:, t, :], ACT.Exp, scale=float(D) ** -0.5,
                                             bias=nmx[:, t:t + 1], accum_out=tot[:, t:t + 1])
                x.then_inc(S["ex_ready"], 1)
                act.wait_ge(S["inv_ready"], 1)
                act.wait_ge(S["set"], 2)
                nc.scalar.activation(gcol[:], inv[:], ACT.Sigmoid, scale=4.0, bias=two[:]).then_inc(S["g_ready"], 1)

            @block.vector
            def _(dve):
                V = nc.vector
                dve.wait_ge(S["pr_stored"], 2 * NCH)
                V.tensor_copy(kg[:, 0:WIN], kg[:, WIN:WIN + 1].broadcast_to([D, WIN]))
                V.tensor_copy(kg[:, WIN + T:], kg[:, WIN + T - 1:WIN + T].broadcast_to([D, WIN])).then_inc(S["edges"], 1)
                dve.wait_ge(S["loaded"], 64)
                for t in range(TT):
                    dve.wait_ge(S["sc_ready"], t + 1)
                    V.tensor_tensor(sc[:, t, :], sc_ps[:, t % 2, 0:W], band[:], ALU.add).then_inc(S["sc_masked"], 1)
                dve.wait_ge(S["sc_masked"], TT)
                V.reduce_max(mx[:], sc[:], AX_X).then_inc(S["mx_ready"], 1)
                dve.wait_ge(S["mx_ready"], 1)
                V.tensor_scalar(nmx[:], mx[:], -float(D) ** -0.5, None, ALU.mult).then_inc(S["nmx_ready"], 1)
                dve.wait_ge(S["ex_ready"], 1)
                V.reciprocal(inv[:], tot[:]).then_inc(S["inv_ready"], 1)
                dve.wait_ge(S["g_ready"], 1)
                for t in range(TT):
                    if t >= 2:
                        dve.wait_ge(S["out_ready"], t - 1)
                    V.tensor_scalar(diag[t % 2][:], ident[:], gcol[:, t:t + 1], None, ALU.mult).then_inc(S["diag_ready"], 1)
                for c in range(NCH):
                    dve.wait_ge(S["out_ready"], TT)
                    V.tensor_copy(gain[:, c * CH:(c + 1) * CH], g_ps[:, c, :]).then_inc(S["stored"], 1)


def mix(nc, dram, h_red, hidden, gain, h):
    with Scope(nc, "mx") as s:
        w = s.sb("w", [D, D])
        m = s.sb("m", [D, T])
        ps = s.ps("out", [D, NCH, CH])
        S = {n: s.sem(n) for n in "loaded diff scaled mixed out_ready added".split()}
        with nc.Block() as block:
            @block.sync
            def _(sp):
                sp.dma_start(w[:], dram["qnet"]).then_inc(S["loaded"], 16)

            @block.tensor
            def _(pe):
                pe.wait_ge(S["loaded"], 16)
                for c in range(NCH):
                    pe.wait_ge(S["mixed"], c + 1)
                    nc.tensor.matmul(ps[:, c, :], w[:], m[:, c * CH:(c + 1) * CH], start=True, stop=True).then_inc(S["out_ready"], 1)

            @block.vector
            def _(dve):
                V = nc.vector
                for c in range(NCH):
                    cols = slice(c * CH, (c + 1) * CH)
                    V.tensor_tensor(m[:, cols], hidden[:, cols], h_red[:, cols], ALU.subtract).then_inc(S["diff"], 1)
                    dve.wait_ge(S["diff"], c + 1)
                    V.tensor_tensor(m[:, cols], m[:, cols], gain[:, cols], ALU.mult).then_inc(S["scaled"], 1)
                    dve.wait_ge(S["scaled"], c + 1)
                    V.tensor_tensor(m[:, cols], m[:, cols], h_red[:, cols], ALU.add).then_inc(S["mixed"], 1)
                for c in range(NCH):
                    cols = slice(c * CH, (c + 1) * CH)
                    dve.wait_ge(S["out_ready"], c + 1)
                    V.tensor_tensor(h[:, cols], h[:, cols], ps[:, c, :], ALU.add).then_inc(S["added"], 1)


def lay_out_lh(inp):
    a = {k: np.asarray(v) for k, v in inp.items()}
    w_in = a["L1_attn_in_proj_w"]
    DI = NT * D
    by_tile = lambda w: np.ascontiguousarray(w.reshape(NT, D, -1).transpose(2, 0, 1).reshape(w.shape[1], NT * D))
    col = lambda v: np.ascontiguousarray(v.reshape(NT, D).T)
    xp = a["L1_attn_x_proj_w"]
    w_x = np.zeros((D, NT, XD), np.float32)
    for j in range(3):
        w_x[:, :, 32 * j:32 * j + NS] = xp[NS * j:NS * (j + 1)].reshape(NS, NT, D).transpose(2, 1, 0)
    w_dt = np.zeros((XD, NT * D), np.float32)
    w_dt[:NS] = by_tile(a["L1_attn_dt_head_w"])
    pick = np.zeros((2, XD, NS, D), np.float32)
    for n in range(NS):
        pick[0, 32 + n, n] = 1.0
        pick[1, 64 + n, n] = 1.0
    sum_k = np.zeros((XD, D), np.float32)
    sum_k[32:32 + NS] = 1.0
    W = D + 2 * WIN
    off = np.arange(W)[None, :] - np.arange(D)[:, None]
    band = np.where((off >= 0) & (off <= 2 * WIN), 0.0, -1e30).astype(np.float32)
    return {
        "lh_in": np.ascontiguousarray(w_in[:DI].reshape(NT, D, D).transpose(0, 2, 1).reshape(NT * D, D)),
        "lh_z": by_tile(w_in[DI:]), "lh_x": w_x.reshape(D, NT * XD),
        "lh_conv_w": np.ascontiguousarray(a["L1_attn_conv_w"].reshape(NT, D, 3).transpose(1, 0, 2).reshape(D, NT * 3)),
        "lh_conv_b": col(a["L1_attn_conv_b"]), "lh_dt": w_dt,
        "lh_dt_b": col(a["L1_attn_dt_head_b"]), "lh_d": col(a["L1_attn_D_param"]),
        "lh_red": np.ascontiguousarray(a["L1_attn_reduce_w"].reshape(D, NT, D).transpose(2, 1, 0).reshape(D, NT * D)),
        "lh_pick_k": pick[0].reshape(XD, NS * D), "lh_pick_q": pick[1].reshape(XD, NS * D), "lh_sum_k": sum_k,
        "gn_q": np.ascontiguousarray(a["L1_attn_gain_q_w"].T), "gn_k": np.ascontiguousarray(a["L1_attn_gain_k_w"].T),
        "gn_band": band, "qnet": np.ascontiguousarray(a["L1_attn_qnet_w"].T),
    }


def tower(nc, dram, out):
    with Scope(nc, "top") as s:
        h = s.sb("h", [D, T])
        ones_over_d = s.sb("ones_over_d", [D, D])
        norms = s.sb("norms", [D, 6])
        loaded, stored = s.sem("loaded"), s.sem("stored")
        with nc.Block() as block:
            @block.sync
            def _(sp):
                sp.dma_start(ones_over_d[:], dram["ones_over_d"]).then_inc(loaded, 16)
                for n, name in enumerate(("att_gamma", "att_beta", "ln1_w", "ln1_b", "post_w", "post_b")):
                    sp.dma_start(norms[:, n:n + 1], dram[name]).then_inc(loaded, 16)
                sp.wait_ge(loaded, 16 * 7)
        embed(nc, dram["ids"], dram["table"], h)

        with Scope(nc, "l0a") as a:
            xn = a.sb("xn", [D, SLOTS * HT])
            ao = a.sb("ao", [D, T])
            layer_norm(nc, "ln_a", h, xn, ones_over_d, 1e-5)
            attention0(nc, dram, xn, ao)
            layer_norm(nc, "ln_b", ao, h, ones_over_d, 1e-5, gamma=norms[:, 0:1], beta=norms[:, 1:2], add_to=h)

        with Scope(nc, "l0f") as a:
            xn = a.sb("xn", [D, T])
            comb_a, comb_b = a.sb("comb_a", [D, T], BF16), a.sb("comb_b", [D, T], BF16)
            layer_norm(nc, "ln_c", h, xn, ones_over_d, 1e-5)
            router(nc, dram, xn, comb_a, comb_b)
            experts(nc, dram, xn, h, comb_a, comb_b)

        with Scope(nc, "l1a") as a:
            xn = a.sb("xn", [D, T])
            h_red = a.sb("h_red", [D, T])
            layer_norm(nc, "ln_d", h, h_red, ones_over_d, 1e-5)
            layer_norm(nc, "ln_e", h_red, xn, ones_over_d, 1e-6, gamma=norms[:, 2:3], beta=norms[:, 3:4])
            with Scope(nc, "l1s") as b:
                xc = b.sb("xc", [D, NT, T])
                xd = b.sb("xd", [XD, T])
                longhorn_inputs(nc, dram, xn, xc, xd)
                longhorn_scan(nc, dram, xn, xc, xd, h_red)
            gain = a.sb("gain", [D, T])
            hidden = a.sb("hidden", [D, T])
            gains(nc, dram, xn, gain)
            with Scope(nc, "l1t") as b:
                kT, qT = b.sb("kT", [D, T + 9 * MB]), b.sb("qT", [D, T + 8 * MB])
                rows = b.sb("rows", [D, 2, NMB + 2 * QUAD, DH])
                eta = b.sb("eta", [RW, NMB + 2 * QUAD])
                zbar = b.sb("zbar", [D, NMB + 1, DH])
                raw = b.sb("raw", [D, T])
                ttt_project(nc, dram, xn, kT, qT, rows, eta)
                ttt_chain(nc, dram, kT, qT, rows, eta, zbar)
                ttt_finish(nc, dram, rows, zbar, raw)
                layer_norm(nc, "ln_f", raw, hidden, ones_over_d, TTT_EPS, gamma=norms[:, 4:5], beta=norms[:, 5:6])
            mix(nc, dram, h_red, hidden, gain, h)

        with Scope(nc, "l1f") as a:
            xn = a.sb("xn", [D, T + D])
            layer_norm(nc, "ln_g", h, xn, ones_over_d, 1e-5)
            product_keys(nc, dram, xn, h)

        turn_out(nc, dram["ident"], h, out)


def turn_out(nc, ident_dram, h, out):
    with Scope(nc, "out") as s:
        ident = s.sb("ident", [D, D])
        tokens = s.sb("tokens", [D, TT, D])
        ps = s.ps("turn", [D, NCH, CH])
        loaded, turned, copied, stored = (s.sem(n) for n in ("loaded", "turned", "copied", "stored"))
        with nc.Block() as block:
            @block.sync
            def _(sp):
                sp.dma_start(ident[:], ident_dram).then_inc(loaded, 16)
                for c in range(NCH):
                    sp.wait_ge(copied, c + 1)
                    sp.dma_start(out[c * CH:(c + 1) * CH, :].rearrange("(q p) d -> p q d", p=D),
                                 tokens[:, 4 * c:4 * c + 4, :]).then_inc(stored, 16)
                sp.wait_ge(stored, 16 * NCH)

            @block.tensor
            def _(pe):
                pe.wait_ge(loaded, 16)
                for c in range(NCH):
                    for q in range(4):
                        t = 4 * c + q
                        mm = nc.tensor.transpose(ps[:, c, q * D:(q + 1) * D], h[:, t * D:(t + 1) * D], ident[:])
                    mm.then_inc(turned, 1)

            @block.vector
            def _(dve):
                for c in range(NCH):
                    dve.wait_ge(turned, c + 1)
                    nc.vector.tensor_copy(tokens[:, 4 * c:4 * c + 4, :].rearrange("p a b -> p (a b)"),
                                          ps[:, c, :]).then_inc(copied, 1)


def kernel(**inputs):
    import concourse.bacc as _bacc
    from concourse.bass_utils import run_bass_kernel_spmd as _run

    laid_out = {}
    for lay_out in (lay_out_attention, lay_out_moe, lay_out_lh, lay_out_ttt, lay_out_pk):
        laid_out.update(lay_out(inputs))
    nc = _bacc.Bacc("TRN2", target_bir_lowering=False, num_devices=1)
    arrays, dram = {}, {}
    for name, a in laid_out.items():
        arrays[f"in_{name}"] = np.ascontiguousarray(a)
        dram[name] = nc.dram_tensor(f"in_{name}", a.shape, mybir.dt.from_np(a.dtype), kind="ExternalInput").ap()
    out = nc.dram_tensor("out_0", (T, D), F32, kind="ExternalOutput").ap()
    tower(nc, dram, out)
    r = _run(nc, [arrays], core_ids=[0])
    return r.results[0]["out_0"].reshape(1, T, D)
```

```python
from contextlib import ExitStack
import numpy as np
import concourse.bass as bass
from concourse import mybir

F32 = mybir.dt.float32
BF16 = mybir.dt.bfloat16
I32 = mybir.dt.int32
ACT = mybir.ActivationFunctionType
ALU = mybir.AluOpType
AX_X = mybir.AxisListType.X

T = 2048
D = 128
VOCAB = 64
CH = 512
NCH = T // CH


class Scope:

    def __init__(self, nc, tag):
        self.nc, self.tag, self.stack, self.sems = nc, tag, ExitStack(), []

    def __enter__(self):
        self.stack.__enter__()
        return self

    def __exit__(self, *a):
        if self.sems:
            with self.nc.Block() as block:
                @block.gpsimd
                def _(pool):
                    for sem in self.sems:
                        pool.sem_clear(sem)
        return self.stack.__exit__(*a)

    def sb(self, name, shape, dt=F32):
        return self.stack.enter_context(self.nc.sbuf_tensor(f"{self.tag}_{name}", shape, dt))

    def ps(self, name, shape, dt=F32):
        return self.stack.enter_context(self.nc.psum_tensor(f"{self.tag}_{name}_ps", shape, dt))

    def sem(self, name):
        self.sems.append(self.stack.enter_context(self.nc.semaphore(f"{self.tag}_{name}")))
        return self.sems[-1]


def layer_norm(nc, tag, src, dst, ones_over_d, eps, gamma=None, beta=None, add_to=None):
    HALF = CH // 2
    with Scope(nc, tag) as s:
        centred = s.sb("centred", [D, NCH, CH])
        squared = s.sb("squared", [D, NCH, CH])
        std, rstd = s.sb("std", [D, CH]), s.sb("rstd", [D, CH])
        eps_col = s.sb("eps", [D, 1])
        spread = s.sb("spread", [D, NCH, D])
        mean_ps = s.ps("mean", [D, NCH, CH])
        var_ps = s.ps("var", [D, CH])
        (const_set, mean_ready, centred_ready, squared_ready, var_ready, std_ready, rstd_ready, spread_ready,
         scaled_ready, done) = (
            s.sem(n) for n in ("const_set", "mean_ready", "centred_ready", "squared_ready", "var_ready",
                               "std_ready", "rstd_ready", "spread_ready", "scaled_ready", "done"))
        cols = lambda c: slice(c * CH, (c + 1) * CH)
        half = lambda k: slice(k * HALF, (k + 1) * HALF)
        pair = lambda k: slice(2 * k, 2 * k + 2)
        by_chunk = lambda x: x[:, 0:T].rearrange("p (c t) -> p c t", t=CH)
        with nc.Block() as block:
            @block.gpsimd
            def _(pool):
                pool.memset(eps_col[:], eps).then_inc(const_set, 1)
                pool.memset(spread[:], 0.0).then_inc(const_set, 1)
                pool.wait_ge(const_set, 2)
                for c in range(NCH):
                    pool.memset(spread[32 * c:32 * c + 32, c, :], 1.0 / 32).then_inc(const_set, 1)

            @block.tensor
            def _(pe):
                for c in range(NCH):
                    nc.tensor.matmul(mean_ps[:, c, :], ones_over_d[:], src[:, cols(c)],
                                     start=True, stop=True).then_inc(mean_ready, 1)
                for c in range(NCH):
                    pe.wait_ge(squared_ready, c + 1)
                    nc.tensor.matmul(var_ps[32 * c:32 * c + 32, :], ones_over_d[:, 0:32], squared[:, c, :],
                                     start=True, stop=True, skip_group_check=True).then_inc(var_ready, 1)
                pe.wait_ge(const_set, 2 + NCH)
                pe.wait_ge(centred_ready, NCH)
                for k in range(2):
                    pe.wait_ge(rstd_ready, k + 1)
                    for c in range(NCH):
                        mm = nc.tensor.matmul(mean_ps[:, c, half(k)], spread[:, c, :], rstd[:, half(k)],
                                              start=True, stop=True, skip_group_check=True)
                    mm.then_inc(spread_ready, 1)

            @block.scalar
            def _(act):
                act.wait_ge(const_set, 1)
                for c in range(NCH):
                    act.wait_ge(centred_ready, c + 1)
                    nc.scalar.activation(squared[:, c, :], centred[:, c, :], ACT.Square).then_inc(squared_ready, 1)
                act.wait_ge(var_ready, NCH)
                for k in range(2):
                    nc.scalar.activation(std[:, half(k)], var_ps[:, half(k)], ACT.Sqrt,
                                         bias=eps_col[:]).then_inc(std_ready, 1)
                if gamma is not None and add_to is None:
                    for k in range(2):
                        act.wait_ge(scaled_ready, k + 1)
                        nc.scalar.activation(by_chunk(dst)[:, pair(k), :], squared[:, pair(k), :], ACT.Identity,
                                             bias=beta).then_inc(done, 1)

            @block.vector
            def _(dve):
                for c in range(NCH):
                    dve.wait_ge(mean_ready, c + 1)
                    nc.vector.tensor_tensor(centred[:, c, :], src[:, cols(c)], mean_ps[:, c, :],
                                            ALU.subtract).then_inc(centred_ready, 1)
                for k in range(2):
                    dve.wait_ge(std_ready, k + 1)
                    nc.vector.reciprocal(rstd[:, half(k)], std[:, half(k)]).then_inc(rstd_ready, 1)
                dve.wait_ge(spread_ready, 2)
                for k in range(2):
                    if gamma is None:
                        nc.vector.tensor_tensor(by_chunk(dst)[:, pair(k), :], centred[:, pair(k), :],
                                                mean_ps[:, pair(k), :], ALU.mult).then_inc(done, 1)
                    else:
                        nc.vector.scalar_tensor_tensor(out=squared[:, pair(k), :], in0=centred[:, pair(k), :],
                                                       scalar=gamma, in1=mean_ps[:, pair(k), :], op0=ALU.mult,
                                                       op1=ALU.mult).then_inc(scaled_ready, 1)
                if add_to is not None:
                    for k in range(2):
                        dve.wait_ge(scaled_ready, k + 1)
                        nc.vector.scalar_tensor_tensor(out=by_chunk(dst)[:, pair(k), :], in0=squared[:, pair(k), :],
                                                       scalar=beta, in1=by_chunk(add_to)[:, pair(k), :],
                                                       op0=ALU.add, op1=ALU.add).then_inc(done, 1)


def embed(nc, ids, table, h):
    with Scope(nc, "emb") as s:
        ids_i = s.sb("ids_i", [VOCAB, T], I32)
        ids_f = s.sb("ids_f", [VOCAB, T])
        vocab_i = s.sb("vocab_i", [VOCAB, 1], I32)
        vocab_f = s.sb("vocab_f", [VOCAB, 1])
        onehot = s.sb("onehot", [VOCAB, T])
        table_sb = s.sb("table", [VOCAB, D])
        h_ps = s.ps("h", [D, NCH, CH])
        loaded, vocab_set, cast, onehot_ready, h_ready, done = (
            s.sem(n) for n in ("loaded", "vocab_set", "cast", "onehot_ready", "h_ready", "done"))
        with nc.Block() as block:
            @block.sync
            def _(sp):
                sp.dma_start(ids_i[:], ids.partition_broadcast(VOCAB)).then_inc(loaded, 16)
                sp.dma_start(table_sb[:], table).then_inc(loaded, 16)

            @block.gpsimd
            def _(pool):
                pool.iota(vocab_i[:], pattern=[[0, 1]], base=0, channel_multiplier=1).then_inc(vocab_set, 1)

            @block.vector
            def _(dve):
                dve.wait_ge(vocab_set, 1)
                nc.vector.tensor_copy(vocab_f[:], vocab_i[:]).then_inc(cast, 1)
                dve.wait_ge(loaded, 32)
                nc.vector.tensor_copy(ids_f[:], ids_i[:]).then_inc(cast, 1)
                dve.wait_ge(cast, 2)
                nc.vector.tensor_scalar(onehot[:], ids_f[:], vocab_f[:, 0:1], None,
                                        ALU.is_equal).then_inc(onehot_ready, 1)
                for c in range(NCH):
                    dve.wait_ge(h_ready, c + 1)
                    nc.vector.tensor_copy(h[:, c * CH:(c + 1) * CH], h_ps[:, c, :]).then_inc(done, 1)

            @block.tensor
            def _(pe):
                pe.wait_ge(onehot_ready, 1)
                for c in range(NCH):
                    nc.tensor.matmul(h_ps[:, c, :], table_sb[:], onehot[:, c * CH:(c + 1) * CH],
                                     start=True, stop=True).then_inc(h_ready, 1)


HEADS = 8
DH = D // HEADS
HT = T // HEADS
QCH = T // CH
KB = T // D
SPLIT = 6 * DH
MROWS = SPLIT + 2
SLOTS = HEADS + 2
FOLD = 96


def attention0(nc, dram, xn, ao):
    x = xn[:, HT:]
    with Scope(nc, "att") as s:
        wq, wk = s.sb("wq", [D, HEADS * D]), s.sb("wk", [D, HEADS * D])
        bq, bk = s.sb("bq", [D, HEADS]), s.sb("bk", [D, HEADS])
        wv, bv = s.sb("wv", [D, D]), s.sb("bv", [D, D])
        wo, bo = s.sb("wo", [D, D]), s.sb("bo", [D, 1])
        masks = s.sb("masks", [D, 4])
        fold = s.sb("fold", [D, FOLD])
        ident = s.sb("ident", [D, D], BF16)
        ident_f = s.sb("ident_f", [D, D])
        q_all = s.sb("q_all", [D, SLOTS * T], BF16)
        k_all = s.sb("k_all", [D, SLOTS * T], BF16)
        v_all = s.sb("v_all", [D, T // D, HEADS, 2 * DH])
        v_head = s.sb("v_head", [D, 2, HEADS, 2 * DH])
        t0, t1 = s.sb("t0", [D, 2, CH]), s.sb("t1", [D, 2, CH])
        part1, part2 = s.sb("part1", [D, 2, CH], BF16), s.sb("part2", [D, 2, CH], BF16)
        half_max = s.sb("half_max", [D, KB, 2])
        neg_max = s.sb("neg_max", [D, KB])
        neg_parts = s.sb("neg_parts", [D, KB, 2], BF16)
        probs = s.sb("probs", [D, 8, CH])
        acc_sb = s.sb("acc_sb", [D, CH])
        rsum = s.sb("rsum", [D, 4])
        ctx_q = s.sb("ctx_q", [D, 2, HEADS, DH])
        ctx = s.sb("ctx", [D, HT])
        st_ps = s.ps("st", [D, 2, CH])
        s1_ps = s.ps("s1", [D, 2, 2 * CH])
        acc_ps = s.ps("acc", [D, CH])
        misc_ps = s.ps("misc", [D, CH])
        fold_ps = misc_ps[:, 0:4 * FOLD].rearrange("p (b f) -> p b f", f=FOLD)
        names = ("loaded ones_set v_ready v_stored consts_set proj_ready part1_ready t1_ready part2_ready "
                 "stacked s1_ready half_done neg_ready parts_ready mt_ready mrows_ready st_ready "
                 "exp_done pv_done acc_stored fold_ready rsum_ready ctx_q_ready turned ctx_ready out_ready "
                 "out_stored v_head_ready pool_passed").split()
        S = {n: s.sem(n) for n in names}
        groups = [(w, b, a, g) for w, b, a in ((wq, bq, q_all), (wk, bk, k_all)) for g in range(4)]
        NG = len(groups)
        UNITS = QCH * KB
        HALVES = 2 * KB
        LOADED = 11 * 16

        ROUND = UNITS + 2
        pv_step = {4 * j + 5: j for j in range(UNITS // 4)}
        MAX1_STEP, LAST_FOLD_STEP, TURN_STEP, OUT_STEP, MAX0_STEP = 2, 4, 7, 10, 49
        fold_step = {KB * q + 20: q for q in range(QCH - 1)}
        proj_step = {13: 0, 16: 1, 23: 2, 26: 3, 29: 4, 32: 5, 40: 6, 43: 7}

        with nc.Block() as block:
            @block.sync
            def _(sp):
                for dst, src in ((wq, "att_wq"), (wk, "att_wk"), (bq, "att_bq"), (bk, "att_bk"), (wv, "att_wv"),
                                 (wo, "att_wo"), (masks, "att_masks"), (fold, "att_fold"), (ident_f, "ident")):
                    sp.dma_start(dst[:], dram[src]).then_inc(S["loaded"], 16)
                sp.dma_start(bv[:], dram["att_bv"].partition_broadcast(D)).then_inc(S["loaded"], 16)
                sp.dma_start(bo[:], dram["att_bo"]).then_inc(S["loaded"], 16)

            @block.gpsimd
            def _(pool):
                nc.gpsimd.memset(xn[:, 0:HT], 0.0).then_inc(S["consts_set"], 1)
                nc.gpsimd.memset(x[:, T:], 0.0).then_inc(S["consts_set"], 1)
                nc.gpsimd.memset(v_all[:, :, :, DH:], 1.0).then_inc(S["consts_set"], 1)
                nc.gpsimd.memset(acc_sb[:], 1.0).then_inc(S["consts_set"], 1)
                nc.gpsimd.memset(ctx_q[:].rearrange("p a b c -> p (a b c)"), 1.0).then_inc(S["consts_set"], 1)
                pool.wait_ge(S["consts_set"], 5)
                nc.gpsimd.memset(k_all[SPLIT:MROWS, 0:T], 1.0).then_inc(S["ones_set"], 1)
                pool.wait_ge(S["ones_set"], 1)
                pool.wait_ge(S["loaded"], LOADED)
                nc.gpsimd.tensor_copy(ident[:], ident_f[:]).then_inc(S["consts_set"], 1)

                def second_part(n, g):
                    pool.wait_ge(S["t1_ready"], n + 3)
                    pool.wait_ge(S["stacked"], n + 1)
                    pool.sem_inc(S["pool_passed"], 1)
                    nc.gpsimd.tensor_copy(part2[:, g % 2, :], t1[:, g % 2, :]).then_inc(S["part2_ready"], 1)

                for n in range(2 * NG):
                    second_part(n, n % NG)
                pool.wait_ge(S["part2_ready"], 2 * NG)
                nc.gpsimd.memset(k_all[SPLIT:MROWS, T:], 1.0).then_inc(S["ones_set"], 1)
                pool.wait_ge(S["ones_set"], 2)
                pool.wait_ge(S["v_stored"], T // D)
                with pool.Fori(0, HEADS) as h:
                    pool.wait_ge(S["pv_done"], h * (UNITS // 4) + 1)
                    pool.sem_inc(S["pool_passed"], 1)
                    nc.gpsimd.tensor_copy(v_head[:].rearrange("p a b c -> p (a b c)"),
                                          v_all[:, bass.ds(h * 2, 2), :, :].rearrange("p a b c -> p (a b c)")
                                          ).then_inc(S["v_head_ready"], 1)
                    for g in range(NG):
                        second_part(h * NG + (2 * NG + g), g)

            @block.tensor
            def _(pe):
                pe.sem_inc(S["pv_done"], 1)
                pe.sem_inc(S["fold_ready"], 1)
                pe.sem_inc(S["turned"], 1)
                pe.sem_inc(S["out_ready"], 1)
                pe.sem_inc(S["mt_ready"], 1)
                pe.wait_ge(S["loaded"], LOADED)
                for t in range(T // D):
                    if t >= 2:
                        pe.wait_ge(S["v_stored"], t - 1)
                    nc.tensor.matmul(st_ps[:, t % 2, 0:D], x[:, t * D:(t + 1) * D], wv[:],
                                     start=True, stop=True).then_inc(S["v_ready"], 1)

                def project(H, g):
                    w, b, a, c2 = groups[g]
                    for c in (2 * c2, 2 * c2 + 1):
                        mm = nc.tensor.matmul(misc_ps[:, (c % 2) * HT:(c % 2 + 1) * HT], w[:, c * D:(c + 1) * D],
                                              x[:, bass.ds(H * HT, HT)], start=(c % 2 == 0), stop=(c % 2 == 1),
                                              skip_group_check=True)
                    mm.then_inc(S["proj_ready"], 1)

                def first_pass(H, hh):
                    qt, half = hh // 2, hh % 2
                    pe.wait_ge(S["half_done"], H * HALVES + hh + 1)
                    if hh == 0:
                        pe.wait_ge(S["stacked"], H * NG + NG + 2)
                    for j in range(2):
                        mm = nc.tensor.matmul(s1_ps[:, hh % 2, j * CH:(j + 1) * CH],
                                              q_all[0:SPLIT, bass.ds(H * T + qt * D, D)],
                                              k_all[0:SPLIT, bass.ds(H * T + (2 * half + j) * CH, CH)],
                                              start=True, stop=True)
                    mm.then_inc(S["s1_ready"], 1)

                def max_rows(r, n):
                    pe.wait_ge(S["parts_ready"], n + 1)
                    for q in range(8):
                        mm = nc.tensor.transpose(misc_ps[:].bitcast(BF16)[0:2, q * D:(q + 1) * D],
                                                 neg_parts[:, 8 * r + q, :], ident[:])
                    mm.then_inc(S["mt_ready"], 1)

                def fold_groups():
                    for b in range(4):
                        mm = nc.tensor.matmul(fold_ps[:, b, :], acc_sb[:, b * D:(b + 1) * D], fold[:],
                                              start=(b == 0), stop=(b == 3), skip_group_check=True)
                    mm.then_inc(S["fold_ready"], 1)

                def turn_context(H1):
                    pe.wait_ge(S["ctx_q_ready"], H1 * QCH + 2)
                    for half in range(2):
                        mm = nc.tensor.transpose(misc_ps[:, half * D:(half + 1) * D],
                                                 ctx_q[:, half].rearrange("p c e -> p (c e)"), ident_f[:])
                    mm.then_inc(S["turned"], 1)

                def project_out(H1):
                    pe.wait_ge(S["ctx_ready"], H1 + 1)
                    nc.tensor.matmul(misc_ps[:, 0:HT], wo[:], ctx[:], start=True,
                                     stop=True).then_inc(S["out_ready"], 1)

                pe.wait_ge(S["v_stored"], T // D)
                for n in range(2 * NG):
                    if n:
                        pe.wait_ge(S["part1_ready"], n)
                    project(n // NG, n % NG)
                for hh in range(HALVES):
                    first_pass(0, hh)
                pe.wait_ge(S["part1_ready"], 2 * NG)
                max_rows(0, 0)
                pe.wait_ge(S["ones_set"], 2)

                with pe.Fori(0, HEADS) as h:
                    for u in range(ROUND):
                        if u < UNITS:
                            q, kb = u // KB, u % KB
                            pe.wait_ge(S["exp_done"], h * UNITS + u + 1)
                            if u % (UNITS // 2) == 0:
                                pe.wait_ge(S["mrows_ready"], 2 * h + (1 + u // (UNITS // 2)))
                            nc.tensor.matmul(st_ps[:, u % 2, :], k_all[0:MROWS, bass.ds(h * T + kb * D, D)],
                                             q_all[0:MROWS, bass.ds(h * T + q * CH, CH)],
                                             start=True, stop=True).then_inc(S["st_ready"], 1)
                        if u in pv_step:
                            j = pv_step[u]
                            q = j // 4
                            if j == 0:
                                pe.wait_ge(S["v_head_ready"], h + 1)
                            if j % 4 == 0:
                                pe.wait_ge(S["acc_stored"], h * QCH + (q + 1))
                            pe.wait_ge(S["exp_done"], h * UNITS + (4 * j + 6))
                            for g in range(4):
                                kb = 4 * (j % 4) + g
                                mm = nc.tensor.matmul(acc_ps[32 * g:32 * g + 32, :], v_head[:, kb % 2, kb // 2, :],
                                                      probs[:, (4 * j + g) % 8, :], start=(kb < 4),
                                                      stop=(kb >= KB - 4), skip_group_check=True)
                            mm.then_inc(S["pv_done"], 1)
                        if u % 2 == 1 and u // 2 < HALVES:
                            first_pass(h + 1, u // 2)
                        if u == MAX1_STEP:
                            pe.wait_ge(S["mrows_ready"], 2 * h + 1)
                            pe.wait_ge(S["ctx_q_ready"], h * QCH + 1)
                            max_rows(1, 2 * h + 1)
                        if u == LAST_FOLD_STEP:
                            pe.wait_ge(S["mrows_ready"], 2 * h + 2)
                            pe.wait_ge(S["acc_stored"], h * QCH + 1)
                            fold_groups()
                        if u == TURN_STEP:
                            turn_context(h)
                        if u == OUT_STEP:
                            project_out(h)
                        if u in proj_step:
                            g = proj_step[u]
                            if g == 0:
                                pe.wait_ge(S["out_stored"], h + 1)
                            elif u in (23, 40):
                                pe.wait_ge(S["ctx_q_ready"], h * QCH + (3 if u == 23 else 4))
                            else:
                                pe.wait_ge(S["part1_ready"], h * NG + (2 * NG + g))
                            project(h + 2, g)
                        if u in fold_step:
                            q = fold_step[u]
                            pe.wait_ge(S["acc_stored"], h * QCH + (q + 2))
                            pe.wait_ge(S["part1_ready"], h * NG + (2 * NG + {0: 2, 1: 6, 2: 8}[q]))
                            if q == 2:
                                pe.wait_ge(S["mrows_ready"], 2 * h + 3)
                            fold_groups()
                        if u == MAX0_STEP:
                            pe.wait_ge(S["part1_ready"], h * NG + 3 * NG)
                            max_rows(0, 2 * h + 2)
                pe.wait_ge(S["mrows_ready"], 2 * HEADS + 1)
                pe.wait_ge(S["ctx_q_ready"], HEADS * QCH + 1)
                pe.wait_ge(S["acc_stored"], HEADS * QCH + 1)
                fold_groups()
                turn_context(HEADS)
                project_out(HEADS)

            @block.scalar
            def _(act):
                act.sem_inc(S["exp_done"], 2)
                act.sem_inc(S["acc_stored"], 1)
                act.wait_ge(S["loaded"], LOADED)

                def store_projection(n, g):
                    w, b, a, c2 = groups[g]
                    act.wait_ge(S["proj_ready"], n + 1)
                    act.wait_ge(S["t1_ready"], n + 1)
                    for dst in (t0, part1):
                        for c in (2 * c2, 2 * c2 + 1):
                            half = slice((c % 2) * HT, (c % 2 + 1) * HT)
                            a_ = nc.scalar.activation(dst[:, g % 2, half], misc_ps[:, half], ACT.Identity,
                                                      bias=b[:, c:c + 1])
                    a_.then_inc(S["part1_ready"], 1)

                def store_rows(H, r, n):
                    act.wait_ge(S["mt_ready"], n + 2)
                    nc.scalar.activation(q_all[SPLIT:MROWS, bass.ds(H * T + r * 1024, 1024)],
                                         misc_ps[:].bitcast(BF16)[0:2, :], ACT.Copy).then_inc(S["mrows_ready"], 1)

                def store_context(H1):
                    act.wait_ge(S["turned"], H1 + 2)
                    act.wait_ge(S["out_ready"], H1 + 1)
                    nc.scalar.activation(ctx[:], misc_ps[:, 0:HT], ACT.Copy).then_inc(S["ctx_ready"], 1)

                for n in range(2 * NG):
                    store_projection(n, n % NG)
                store_rows(0, 0, 0)
                with act.Fori(0, HEADS) as h:
                    for u in range(ROUND):
                        if u < UNITS:
                            act.wait_ge(S["st_ready"], h * UNITS + (u + 1))
                            if u % 4 == 0:
                                act.wait_ge(S["pv_done"], h * (UNITS // 4) + (u // 4) if u >= 4 else h * (UNITS // 4) + 1)
                            nc.scalar.activation(probs[:, u % 8, :], st_ps[:, u % 2, :], ACT.Exp,
                                                 scale=float(DH) ** -0.5).then_inc(S["exp_done"], 1)
                        if u >= KB and u % KB == 1:
                            q = u // KB - 1
                            act.wait_ge(S["pv_done"], h * (UNITS // 4) + (4 * q + 5))
                            act.wait_ge(S["fold_ready"], h * QCH + (q + 2))
                            nc.scalar.activation(acc_sb[:], acc_ps[:], ACT.Copy).then_inc(S["acc_stored"], 1)
                        if u - 1 in proj_step:
                            store_projection(h * NG + (2 * NG + proj_step[u - 1]), proj_step[u - 1])
                        if u - 1 == MAX1_STEP:
                            store_rows(h, 1, 2 * h + 1)
                        if u - 1 == MAX0_STEP:
                            store_rows(h + 1, 0, 2 * h + 2)
                        if u - 1 == TURN_STEP:
                            store_context(h)
                store_context(HEADS)

            @block.vector
            def _(dve):
                dve.sem_inc(S["t1_ready"], 2)
                dve.sem_inc(S["stacked"], 2)
                dve.sem_inc(S["half_done"], 2)
                dve.sem_inc(S["ctx_q_ready"], 1)
                dve.wait_ge(S["loaded"], LOADED)
                dve.wait_ge(S["consts_set"], 6)
                for t in range(T // D):
                    dve.wait_ge(S["v_ready"], t + 1)
                    nc.vector.tensor_tensor(v_all[:, t, :, 0:DH], st_ps[:, t % 2, 0:D].rearrange("p (c d) -> p c d", d=DH),
                                            bv[:].rearrange("p (c d) -> p c d", d=DH), ALU.add).then_inc(S["v_stored"], 1)

                def remainder(n, g):
                    b, col = g % 2, 2 * (g // 4)
                    dve.wait_ge(S["part1_ready"], n + 1)
                    dve.wait_ge(S["stacked"], n + 1)
                    nc.vector.scalar_tensor_tensor(out=t1[:, b, :], in0=part1[:, b, :], scalar=masks[:, col:col + 1],
                                                   in1=t0[:, b, :], op0=ALU.mult, op1=ALU.add).then_inc(S["t1_ready"], 1)

                def stack(H, n, g):
                    w, bb, a, c2 = groups[g]
                    b, col = g % 2, 2 * (g // 4) + 1
                    dve.wait_ge(S["part2_ready"], n + 1)
                    dve.wait_ge(S["t1_ready"], n + 3)
                    nc.vector.scalar_tensor_tensor(out=a[0:SPLIT, bass.ds(H * T + c2 * CH, CH)], in0=part2[0:SPLIT, b, :],
                                                   scalar=masks[0:SPLIT, col:col + 1],
                                                   in1=t1[0:SPLIT, b, :], op0=ALU.mult, op1=ALU.add).then_inc(S["stacked"], 1)

                def half_max_of(H, hh):
                    dve.wait_ge(S["s1_ready"], H * HALVES + hh + 1)
                    nc.vector.reduce_max(half_max[:, hh // 2, hh % 2:hh % 2 + 1], s1_ps[:, hh % 2, :],
                                         AX_X).then_inc(S["half_done"], 1)

                def negative_maxima(H, r, n):
                    tiles = slice(8 * r, 8 * r + 8)
                    dve.wait_ge(S["half_done"], H * HALVES + (16 * r + 18))
                    nc.vector.tensor_reduce(neg_max[:, tiles], half_max[:, tiles, :], AX_X, ALU.max,
                                            negate=True).then_inc(S["neg_ready"], 1)
                    dve.wait_ge(S["neg_ready"], 2 * n + 1)
                    nc.vector.tensor_copy(neg_parts[:, tiles, 0], neg_max[:, tiles]).then_inc(S["neg_ready"], 1)
                    dve.wait_ge(S["neg_ready"], 2 * n + 2)
                    nc.vector.tensor_tensor(neg_parts[:, tiles, 1], neg_max[:, tiles], neg_parts[:, tiles, 0],
                                            ALU.subtract).then_inc(S["parts_ready"], 1)

                def divide(n, q):
                    dve.wait_ge(S["fold_ready"], n + 2)
                    nc.vector.reciprocal(rsum[:], fold_ps[:, :, DH]).then_inc(S["rsum_ready"], 1)
                    dve.wait_ge(S["rsum_ready"], n + 1)
                    nc.vector.tensor_tensor(ctx_q[:].rearrange("p half c e -> p c half e")[:, 2 * q:2 * q + 2],
                                            fold_ps.rearrange("p (c half) f -> p c half f", half=2)[:, :, :, 0:DH],
                                            rsum[:].rearrange("p (c half) -> p c half", half=2)
                                            .unsqueeze(3).broadcast_to([D, 2, 2, DH]), ALU.mult).then_inc(S["ctx_q_ready"], 1)

                def add_residual(H1):
                    dve.wait_ge(S["out_ready"], H1 + 2)
                    nc.vector.scalar_tensor_tensor(out=ao[:, bass.ds(H1 * HT, HT)], in0=misc_ps[:, 0:HT],
                                                   scalar=bo[:], in1=xn[:, bass.ds(H1 * HT, HT)], op0=ALU.add,
                                                   op1=ALU.add).then_inc(S["out_stored"], 1)

                for n in range(2 * NG):
                    remainder(n, n % NG)
                    stack(n // NG, n, n % NG)
                for hh in range(HALVES):
                    half_max_of(0, hh)
                negative_maxima(0, 0, 0)
                with dve.Fori(0, HEADS) as h:
                    for u in range(ROUND):
                        if u == 0:
                            dve.wait_ge(S["mt_ready"], 2 * h + 1)
                            negative_maxima(h, 1, 2 * h + 1)
                        if u == LAST_FOLD_STEP + 1:
                            divide(h * QCH, QCH - 1)
                        if u - 1 in fold_step:
                            q = fold_step[u - 1]
                            if q == 0:
                                dve.wait_ge(S["turned"], h + 2)
                            divide(h * QCH + (q + 1), q)
                        if u == OUT_STEP + 1:
                            add_residual(h)
                        if u % 2 == 1 and u // 2 < HALVES:
                            half_max_of(h + 1, u // 2)
                        if u - 3 in proj_step:
                            g = proj_step[u - 3]
                            remainder(h * NG + (2 * NG + g), g)
                        if u - 6 in proj_step:
                            g = proj_step[u - 6]
                            stack(h + 2, h * NG + (2 * NG + g), g)
                        if u == HALVES + 4:
                            dve.wait_ge(S["mt_ready"], 2 * h + 2)
                            negative_maxima(h + 1, 0, 2 * h + 2)
                divide(HEADS * QCH, QCH - 1)
                add_residual(HEADS)


def lay_out_attention(inp):
    a = {k: np.asarray(v) for k, v in inp.items()}
    rep = lambda w: np.ascontiguousarray(
        np.broadcast_to(w.T.reshape(D, HEADS, 1, DH), (D, HEADS, 8, DH)).reshape(D, HEADS * D))
    repb = lambda b: np.ascontiguousarray(
        np.broadcast_to(b.reshape(HEADS, 1, DH), (HEADS, 8, DH)).reshape(HEADS, D).T)
    masks = np.zeros((D, 4), np.float32)
    for col, parts in ((0, (1, 1, 2, 2, 1, 3)), (2, (1, 2, 1, 2, 3, 1))):
        for g, p in enumerate(parts):
            masks[16 * g:16 * g + 16, col] = -1.0 if p >= 2 else 0.0
            masks[16 * g:16 * g + 16, col + 1] = -1.0 if p == 3 else 0.0
    fold = np.tile(np.eye(2 * DH, dtype=np.float32), (D // (2 * DH), FOLD // (2 * DH)))
    return {
        "ids": a["x"].astype(np.int32).reshape(T),
        "table": a["L0_tok_weights"],
        "att_wq": rep(a["L0_attn_Wq"]), "att_wk": rep(a["L0_attn_Wk"]),
        "att_bq": repb(a["L0_attn_bq"]), "att_bk": repb(a["L0_attn_bk"]),
        "att_wv": np.ascontiguousarray(a["L0_attn_Wv"].T), "att_bv": a["L0_attn_bv"],
        "att_wo": np.ascontiguousarray(a["L0_attn_Wo"].T),
        "att_bo": a["L0_attn_bo"].reshape(D, 1),
        "att_gamma": a["L0_attn_gamma"].reshape(D, 1), "att_beta": a["L0_attn_beta"].reshape(D, 1),
        "att_masks": masks, "att_fold": fold, "ident": np.eye(D, dtype=np.float32),
        "ones_over_d": np.full((D, D), 1.0 / D, np.float32),
    }


EXPERTS = 64
INTER = 64
PAIRS = EXPERTS // 2
TOP_K = 6
BIG = 3.0e38
TT = T // D


def router(nc, dram, xn, comb_a, comb_b):
    with Scope(nc, "rt") as s:
        w_gate = s.sb("w_gate", [D, EXPERTS])
        ident = s.sb("ident", [D, D])
        row_masks = s.sb("row_masks", [D, 2])
        score = s.sb("score", [D, TT, EXPERTS])
        left = s.sb("left", [D, TT, EXPERTS])
        chosen = s.sb("chosen", [D, TT, EXPERTS])
        weight = s.sb("weight", [D, TT, EXPERTS])
        twice = s.sb("twice", [D, TT, 2, EXPERTS])
        top = s.sb("top", [D, TT, 8])
        best = s.sb("best", [D, TT, 1])
        total = s.sb("total", [D, TT])
        rest = s.sb("rest", [D, T])
        rest2 = s.sb("rest2", [D, T])
        part = s.sb("part", [D, T], BF16)
        score_ps = s.ps("score", [D, TT, EXPERTS])
        comb_ps = s.ps("comb", [D, NCH, CH])
        S = {n: s.sem(n) for n in ("loaded scores_ready stored top_ready cut left_ready shifted exp_ready "
                                   "chosen_ready masked total_ready inverse_ready weight_ready turned part_ready "
                                   "rest_ready a_ready part2_ready rest2_ready b_ready").split()}
        wide = lambda ap: ap.broadcast_to([D, TT, EXPERTS])
        with nc.Block() as block:
            @block.sync
            def _(sp):
                for dst, src in ((w_gate, "rt_gate"), (ident, "ident"), (row_masks, "rt_masks")):
                    sp.dma_start(dst[:], dram[src]).then_inc(S["loaded"], 16)

            @block.tensor
            def _(pe):
                pe.wait_ge(S["loaded"], 48)
                for t in range(TT):
                    mm = nc.tensor.matmul(score_ps[:, t, :], xn[:, t * D:(t + 1) * D], w_gate[:],
                                          start=(t % 8 == 0), stop=(t % 8 == 7), skip_group_check=True)
                mm.then_inc(S["scores_ready"], 1)
                pe.wait_ge(S["weight_ready"], 2)
                for t in range(TT):
                    nc.tensor.transpose(comb_ps[:, t // 4, (t % 4) * D:(t % 4 + 1) * D],
                                        twice[:, t, :, :].rearrange("p a e -> p (a e)"),
                                        ident[:]).then_inc(S["turned"], 1)

            @block.scalar
            def _(act):
                act.wait_ge(S["shifted"], 1)
                nc.scalar.activation(weight[:], weight[:], ACT.Exp).then_inc(S["exp_ready"], 1)
                for c in range(NCH):
                    act.wait_ge(S["turned"], 4 * c + 4)
                    cols = slice(c * CH, (c + 1) * CH)
                    nc.scalar.activation(part[:, cols], comb_ps[:, c, :], ACT.Copy).then_inc(S["part_ready"], 1)
                for c in range(NCH):
                    cols = slice(c * CH, (c + 1) * CH)
                    act.wait_ge(S["rest_ready"], c + 1)
                    nc.scalar.activation(comb_a[:, cols], rest[:, cols], ACT.Copy).then_inc(S["a_ready"], 1)

            @block.vector
            def _(dve):
                dve.wait_ge(S["scores_ready"], 1)
                nc.vector.tensor_copy(score[:], score_ps[:]).then_inc(S["stored"], 1)
                dve.wait_ge(S["stored"], 1)
                for t in range(TT):
                    mx = nc.vector.max(top[:, t, :], score[:, t, :])
                mx.then_inc(S["top_ready"], 1)
                dve.wait_ge(S["top_ready"], 1)
                nc.vector.tensor_copy(best[:], top[:, :, 0:1]).then_inc(S["cut"], 1)
                nc.vector.memset(top[:, :, TOP_K:8], BIG).then_inc(S["cut"], 1)
                dve.wait_ge(S["cut"], 2)
                nc.vector.tensor_tensor(weight[:], score[:], wide(best[:]), ALU.subtract).then_inc(S["shifted"], 1)
                for t in range(TT):
                    mr = nc.vector.match_replace(left[:, t, :], top[:, t, :], score[:, t, :], -BIG)
                mr.then_inc(S["left_ready"], 1)
                dve.wait_ge(S["left_ready"], 1)
                nc.vector.tensor_tensor(chosen[:], left[:], score[:], ALU.not_equal).then_inc(S["chosen_ready"], 1)
                dve.wait_ge(S["chosen_ready"], 1)
                dve.wait_ge(S["exp_ready"], 1)
                nc.vector.tensor_tensor(left[:], weight[:], chosen[:], ALU.mult).then_inc(S["masked"], 1)
                dve.wait_ge(S["masked"], 1)
                nc.vector.reduce_sum(total[:], left[:], AX_X).then_inc(S["total_ready"], 1)
                dve.wait_ge(S["total_ready"], 1)
                nc.vector.reciprocal(total[:], total[:]).then_inc(S["inverse_ready"], 1)
                dve.wait_ge(S["inverse_ready"], 1)
                for a in range(2):
                    nc.vector.tensor_tensor(twice[:, :, a, :], left[:], wide(total[:].unsqueeze(2)),
                                            ALU.mult).then_inc(S["weight_ready"], 1)
                for c in range(NCH):
                    cols = slice(c * CH, (c + 1) * CH)
                    dve.wait_ge(S["part_ready"], c + 1)
                    nc.vector.scalar_tensor_tensor(out=rest[:, cols], in0=part[:, cols], scalar=row_masks[:, 0:1],
                                                   in1=comb_ps[:, c, :], op0=ALU.mult,
                                                   op1=ALU.add).then_inc(S["rest_ready"], 1)
                for c in range(NCH):
                    cols = slice(c * CH, (c + 1) * CH)
                    dve.wait_ge(S["a_ready"], c + 1)
                    nc.vector.tensor_tensor(rest2[:, cols], rest[:, cols], comb_a[:, cols],
                                            ALU.subtract).then_inc(S["rest2_ready"], 1)
                    dve.wait_ge(S["rest2_ready"], c + 1)
                    nc.vector.tensor_scalar(comb_b[:, cols], rest2[:, cols], row_masks[:, 1:2], None,
                                            ALU.mult).then_inc(S["b_ready"], 1)


def experts(nc, dram, xn, h, comb_a, comb_b):
    with Scope(nc, "moe") as s:
        shared = s.sb("shared", [D, 2, 3, D])
        w = [s.sb(f"w{b}", [D, 3, D]) for b in range(2)]
        ident = s.sb("ident", [D, EXPERTS])
        pick = s.sb("pick", [D, EXPERTS * INTER], BF16)
        gate = s.sb("gate", [D, 2, CH])
        gated = s.sb("gated", [D, 2, CH])
        hidden = s.sb("hidden", [D, 2, CH])
        x1_ps, x3_ps, cb_ps = s.ps("x1", [D, CH]), s.ps("x3", [D, CH]), s.ps("cb", [D, CH])
        out_ps = s.ps("out", [D, NCH, CH])
        S = {n: s.sem(n) for n in ("loaded pick_ready w_a w_b w_used x1_ready x3_ready cb_ready gate_ready "
                                   "gated_ready hidden_ready out_done stored").split()}
        w_loaded = (S["w_a"], S["w_b"])
        packed = dram["moe_w"]
        with nc.Block() as block:
            @block.sync
            def _(sp):
                sp.dma_start(shared[:].rearrange("p a b d -> p (a b d)"), dram["moe_shared"]).then_inc(S["loaded"], 16)
                sp.dma_start(ident[:], dram["moe_ident"]).then_inc(S["loaded"], 16)
                sp.sem_inc(S["w_used"], 2)
                with sp.Fori(0, PAIRS // 2) as i:
                    for b in range(2):
                        sp.wait_ge(S["w_used"], 2 * i + (b + 1))
                        sp.dma_start(w[b][:].rearrange("p b d -> p (b d)"),
                                     packed[bass.ds((i * 2 + b) * D, D), :]).then_inc(w_loaded[b], 16)

            @block.gpsimd
            def _(pool):
                pool.wait_ge(S["loaded"], 32)
                nc.gpsimd.tensor_copy(pick[:].rearrange("p (e i) -> p e i", i=INTER),
                                      ident[:].unsqueeze(2).broadcast_to([D, EXPERTS, INTER])).then_inc(S["pick_ready"], 1)

            @block.tensor
            def _(pe):
                pe.sem_inc(S["out_done"], 2)
                pe.wait_ge(S["loaded"], 32)

                def item(n, c, wt, pair):
                    cols = slice(c * CH, (c + 1) * CH)
                    pe.wait_ge(S["gate_ready"], n + 1)
                    nc.tensor.matmul(x1_ps[:], wt[:, 0, :], xn[:, cols], start=True, stop=True).then_inc(S["x1_ready"], 1)
                    pe.wait_ge(S["gated_ready"], n + 1)
                    nc.tensor.matmul(x3_ps[:], wt[:, 1, :], xn[:, cols], start=True, stop=True).then_inc(S["x3_ready"], 1)
                    if pair is not None:
                        pe.wait_ge(S["hidden_ready"], n + 1)
                        sel = pick[:, bass.ds(pair * D, D)]
                        nc.tensor.matmul(cb_ps[:], sel, comb_a[:, cols], start=True, stop=False)
                        nc.tensor.matmul(cb_ps[:], sel, comb_b[:, cols], start=False, stop=True).then_inc(S["cb_ready"], 1)

                def down(n, c, b, wt, first):
                    pe.wait_ge(S["hidden_ready"], n + 2)
                    return nc.tensor.matmul(out_ps[:, c, :], wt[:, 2, :], hidden[:, b, :], start=first, stop=True,
                                            skip_group_check=True).then_inc(S["out_done"], 1)

                for st in range(2):
                    for c in range(NCH):
                        item(st * NCH + c, c, shared[:, st], None)
                        down(st * NCH + c, c, c % 2, shared[:, st], st == 0)
                pe.wait_ge(S["pick_ready"], 1)
                with pe.Fori(0, PAIRS // 2) as i:
                    for b in range(2):
                        pe.wait_ge(w_loaded[b], 16 * i + 16)
                        base = i * (2 * NCH) + (2 + b) * NCH
                        for c in range(NCH):
                            item(base + c, c, w[b], i * 2 + b)
                            if c:
                                down(base + c - 1, c - 1, (c - 1) % 2, w[b], False)
                        down(base + NCH - 1, NCH - 1, (NCH - 1) % 2, w[b], False)
                        pe.wait_ge(S["out_done"], base + NCH + 2)
                        pe.sem_inc(S["w_used"], 1)

            @block.scalar
            def _(act):
                act.sem_inc(S["gate_ready"], 1)

                def gate_of(n, b):
                    act.wait_ge(S["x1_ready"], n + 1)
                    act.wait_ge(S["gated_ready"], n + 1)
                    nc.scalar.activation(gate[:, b, :], x1_ps[:], ACT.Silu).then_inc(S["gate_ready"], 1)
                for n in range(2 * NCH):
                    gate_of(n, n % 2)
                with act.Fori(0, PAIRS) as e:
                    for c in range(NCH):
                        gate_of(e * NCH + (2 * NCH + c), c % 2)

            @block.vector
            def _(dve):
                dve.sem_inc(S["gated_ready"], 1)
                dve.sem_inc(S["hidden_ready"], 1)

                def hide(n, b, cb):
                    dve.wait_ge(S["gate_ready"], n + 2)
                    dve.wait_ge(S["x3_ready"], n + 1)
                    dve.wait_ge(S["out_done"], n + 1)
                    if cb is None:
                        nc.vector.tensor_tensor(hidden[:, b, :], gate[:, b, :], x3_ps[:], ALU.mult).then_inc(S["gated_ready"], 1)
                        dve.wait_ge(S["gated_ready"], n + 2)
                        dve.sem_inc(S["hidden_ready"], 1)
                        return
                    nc.vector.tensor_tensor(gated[:, b, :], gate[:, b, :], x3_ps[:], ALU.mult).then_inc(S["gated_ready"], 1)
                    dve.wait_ge(S["gated_ready"], n + 2)
                    dve.wait_ge(S["cb_ready"], cb)
                    nc.vector.tensor_tensor(hidden[:, b, :], gated[:, b, :], cb_ps[:], ALU.mult).then_inc(S["hidden_ready"], 1)
                for n in range(2 * NCH):
                    hide(n, n % 2, None)
                with dve.Fori(0, PAIRS) as e:
                    for c in range(NCH):
                        hide(e * NCH + (2 * NCH + c), c % 2, e * NCH + (c + 1))
                for c in range(NCH):
                    dve.wait_ge(S["out_done"], (PAIRS + 2) * NCH + 2)
                    cols = slice(c * CH, (c + 1) * CH)
                    nc.vector.tensor_tensor(h[:, cols], h[:, cols], out_ps[:, c, :], ALU.add).then_inc(S["stored"], 1)


def lay_out_moe(inp):
    a = {k: np.asarray(v) for k, v in inp.items()}
    w1, w3, w2 = (a[f"L0_ffn_{n}"].reshape(PAIRS, D, D) for n in ("w1", "w3", "w2"))
    packed = np.stack([w1.transpose(0, 2, 1), w3.transpose(0, 2, 1), w2], axis=2).reshape(PAIRS * D, 3 * D)
    sg, su, sd = a["L0_ffn_w_sg"], a["L0_ffn_w_su"], a["L0_ffn_w_sd"]
    shared = np.stack([np.stack([sg[i * D:(i + 1) * D].T, su[i * D:(i + 1) * D].T, sd[:, i * D:(i + 1) * D].T], 1)
                       for i in range(2)], 1).reshape(D, 6 * D)
    masks = np.zeros((D, 2), np.float32)
    masks[64:, 0] = -1.0
    masks[64:, 1] = 1.0
    eye = np.eye(EXPERTS, dtype=np.float32)
    return {"rt_gate": np.ascontiguousarray(a["L0_ffn_w_gate"].T), "rt_masks": masks,
            "moe_w": np.ascontiguousarray(packed), "moe_shared": np.ascontiguousarray(shared),
            "moe_ident": np.concatenate([eye, eye])}


PK_HEADS = 8
N_KEYS = 64
TOPK = 16
GROUPS = 2 * PK_HEADS
ROWS = [TOPK // (i + 1) for i in range(TOPK)]
SINGLE = ROWS.index(1)
STARTS = [sum(ROWS[:i]) for i in range(TOPK)]
CAND = sum(ROWS)
NSIM = GROUPS * N_KEYS


def product_keys(nc, dram, xn, h):
    with Scope(nc, "pk") as s:
        wq = s.sb("wq", [N_KEYS, GROUPS, D])
        keys = s.sb("keys", [N_KEYS, GROUPS, N_KEYS])
        up = s.sb("up", [CAND, D])
        ident = s.sb("ident", [D, D])
        w = s.sb("w", [D, NSIM + CAND])
        delta = s.sb("delta", [D, TT + 1, D])
        buf = []
        for b in range(2):
            buf.append({n: s.sb(f"{n}{b}", shape) for n, shape in dict(
                xt=[D, D], left=[D, GROUPS, N_KEYS], top=[D, GROUPS, TOPK], cand=[D, PK_HEADS, CAND],
                left2=[D, PK_HEADS, CAND], left3=[D, PK_HEADS, CAND], top2=[D, PK_HEADS, TOPK],
                shifted=[D, PK_HEADS, CAND], chosen=[D, PK_HEADS, CAND], masked=[D, PK_HEADS, CAND],
                total=[D, PK_HEADS], inverse=[D, PK_HEADS], act=[D, CAND], weight=[D, CAND], gw=[D, CAND],
                gwt=[CAND, D]).items()})
            buf[b]["sim"] = s.ps(f"sim{b}", [D, GROUPS, N_KEYS])
        xd_ps = s.ps("xd", [D, 2, CH])
        turn_ps = s.ps("turn", [D, D])
        out_ps = s.ps("out", [D, D])
        S = {n: s.sem(n) for n in ("loaded w_ps_ready w_stored xt_ready sims_ready xd_ready top_a cut_a top1_done "
                                   "cand_ready gelu_ready top_b cut_b top_c cut_c shifted exp_ready chosen masked "
                                   "total inverse scaled weight gw_ready turned gwt_ready out_ready delta_stored "
                                   "zeroed added dve_passed pe_passed").split()}
        flat = lambda ap: ap.rearrange("p a b -> p (a b)")
        with nc.Block() as block:
            @block.sync
            def _(sp):
                for dst, src in ((flat(wq[:]), "pk_wq"), (flat(keys[:]), "pk_keys"), (up[:], "pk_up"),
                                 (ident[:], "ident"), (w[:, NSIM:], "pk_down")):
                    sp.dma_start(dst, dram[src]).then_inc(S["loaded"], 16)

            @block.gpsimd
            def _(pool):
                pool.sem_inc(S["cand_ready"], 2)
                nc.gpsimd.memset(xn[:, T:], 0.0).then_inc(S["zeroed"], 1)
                nc.gpsimd.memset(buf[1]["gwt"][:], 0.0).then_inc(S["zeroed"], 1)

                def candidates(n, b):
                    pool.wait_ge(S["top1_done"], n + 3)
                    pool.wait_ge(S["shifted"], n + 1)
                    pool.wait_ge(S["chosen"], n + 1)
                    top, cand = buf[b]["top"], buf[b]["cand"]
                    for i in range(SINGLE):
                        nc.gpsimd.tensor_tensor(
                            cand[:, :, STARTS[i]:STARTS[i] + ROWS[i]],
                            top[:, 0:PK_HEADS, i:i + 1].broadcast_to([D, PK_HEADS, ROWS[i]]),
                            top[:, PK_HEADS:, 0:ROWS[i]], ALU.add)
                    n1 = TOPK - SINGLE
                    nc.gpsimd.tensor_tensor(cand[:, :, STARTS[SINGLE]:], top[:, 0:PK_HEADS, SINGLE:],
                                            top[:, PK_HEADS:, 0:1].broadcast_to([D, PK_HEADS, n1]),
                                            ALU.add).then_inc(S["cand_ready"], 1)
                candidates(0, 0)
                with pool.Fori(0, TT // 2) as i:
                    for b in range(2):
                        candidates(i * 2 + (b + 1), 1 - b)

            @block.tensor
            def _(pe):
                pe.sem_inc(S["xd_ready"], 2)
                pe.wait_ge(S["loaded"], 80)
                for g in range(GROUPS):
                    mm = nc.tensor.matmul(buf[0]["sim"][:, g, :], wq[:, g, :], keys[:, g, :], start=(g % 8 == 0),
                                          stop=(g % 8 == 7), skip_group_check=True)
                mm.then_inc(S["w_ps_ready"], 1)
                pe.wait_ge(S["w_stored"], 1)
                pe.wait_ge(S["zeroed"], 2)
                nc.tensor.matmul(out_ps[:], up[:], buf[1]["gwt"][:], start=True, stop=True).then_inc(S["out_ready"], 1)

                def sims(n, b):
                    pe.wait_ge(S["xt_ready"], n + 1)
                    pe.wait_ge(S["top1_done"], n + 1)
                    sim = flat(buf[b]["sim"][:])
                    for j in range(2):
                        mm = nc.tensor.matmul(sim[:, j * CH:(j + 1) * CH], buf[b]["xt"][:],
                                              w[:, j * CH:(j + 1) * CH], start=True, stop=True)
                    mm.then_inc(S["sims_ready"], 1)
                    pe.wait_ge(S["gelu_ready"], n + 1)
                    nc.tensor.matmul(xd_ps[:, b, 0:CAND], buf[b]["xt"][:], w[:, NSIM:], start=True, stop=True,
                                     skip_group_check=True).then_inc(S["xd_ready"], 1)
                sims(0, 0)
                with pe.Fori(0, TT // 2) as i:
                    for b in range(2):
                        n = i * 2 + b
                        sims(n + 1, 1 - b)
                        pe.wait_ge(S["gw_ready"], n + 1)
                        pe.sem_inc(S["pe_passed"], 1)
                        nc.tensor.transpose(turn_ps[0:CAND, :], buf[b]["gw"][:], ident[:]).then_inc(S["turned"], 1)
                        pe.wait_ge(S["gwt_ready"], n + 1)
                        pe.wait_ge(S["delta_stored"], n + 1)
                        nc.tensor.matmul(out_ps[:], up[:], buf[b]["gwt"][:], start=True,
                                         stop=True).then_inc(S["out_ready"], 1)

            @block.scalar
            def _(act):
                act.sem_inc(S["gelu_ready"], 2)
                act.wait_ge(S["zeroed"], 2)

                def stage_tile(n, b):
                    act.wait_ge(S["xd_ready"], n + 1)
                    nc.scalar.activation(buf[b]["xt"][:], xn[:, bass.ds(n * D, D)], ACT.Copy).then_inc(S["xt_ready"], 1)
                stage_tile(0, 0)
                with act.Fori(0, TT // 2) as i:
                    for b in range(2):
                        n = i * 2 + b
                        stage_tile(n + 1, 1 - b)
                        act.wait_ge(S["xd_ready"], n + 3)
                        nc.scalar.activation(buf[b]["act"][:], xd_ps[:, b, 0:CAND], ACT.Gelu).then_inc(S["gelu_ready"], 1)
                        act.wait_ge(S["shifted"], n + 3)
                        nc.scalar.activation(buf[b]["shifted"][:], buf[b]["shifted"][:], ACT.Exp).then_inc(S["exp_ready"], 1)
                        act.wait_ge(S["turned"], n + 1)
                        nc.scalar.activation(buf[b]["gwt"][:], turn_ps[0:CAND, :], ACT.Copy).then_inc(S["gwt_ready"], 1)
                act.wait_ge(S["xd_ready"], TT + 3)

            @block.vector
            def _(dve):
                dve.sem_inc(S["top1_done"], 2)
                dve.sem_inc(S["shifted"], 2)
                dve.sem_inc(S["chosen"], 2)
                dve.wait_ge(S["w_ps_ready"], 1)
                nc.vector.tensor_copy(w[:, 0:NSIM], flat(buf[0]["sim"][:])).then_inc(S["w_stored"], 1)

                def rank_keys(n, b):
                    sim, left, top = buf[b]["sim"], buf[b]["left"], buf[b]["top"]
                    dve.wait_ge(S["sims_ready"], n + 1)
                    dve.wait_ge(S["cand_ready"], n + 1)
                    dve.sem_inc(S["dve_passed"], 1)
                    for g in range(GROUPS):
                        x = nc.vector.max(top[:, g, 0:8], sim[:, g, :])
                    x.then_inc(S["top_a"], 1)
                    dve.wait_ge(S["top_a"], n + 1)
                    dve.sem_inc(S["dve_passed"], 1)
                    for g in range(GROUPS):
                        x = nc.vector.match_replace(left[:, g, :], top[:, g, 0:8], sim[:, g, :], -BIG)
                    x.then_inc(S["cut_a"], 1)
                    dve.wait_ge(S["cut_a"], n + 1)
                    dve.sem_inc(S["dve_passed"], 1)
                    for g in range(GROUPS):
                        x = nc.vector.max(top[:, g, 8:16], left[:, g, :])
                    x.then_inc(S["top1_done"], 1)

                def rank_sums(n, b):
                    B = buf[b]
                    dve.wait_ge(S["cand_ready"], n + 3)
                    dve.sem_inc(S["dve_passed"], 1)
                    for g in range(PK_HEADS):
                        x = nc.vector.max(B["top2"][:, g, 0:8], B["cand"][:, g, :])
                    x.then_inc(S["top_b"], 1)
                    dve.wait_ge(S["top_b"], n + 1)
                    nc.vector.tensor_tensor(B["shifted"][:], B["cand"][:],
                                            B["top2"][:, :, 0:1].broadcast_to([D, PK_HEADS, CAND]),
                                            ALU.subtract).then_inc(S["shifted"], 1)
                    dve.sem_inc(S["dve_passed"], 1)
                    for g in range(PK_HEADS):
                        x = nc.vector.match_replace(B["left2"][:, g, :], B["top2"][:, g, 0:8], B["cand"][:, g, :], -BIG)
                    x.then_inc(S["cut_b"], 1)
                    dve.wait_ge(S["cut_b"], n + 1)
                    dve.sem_inc(S["dve_passed"], 1)
                    for g in range(PK_HEADS):
                        x = nc.vector.max(B["top2"][:, g, 8:16], B["left2"][:, g, :])
                    x.then_inc(S["top_c"], 1)
                    dve.wait_ge(S["top_c"], n + 1)
                    dve.sem_inc(S["dve_passed"], 1)
                    for g in range(PK_HEADS):
                        x = nc.vector.match_replace(B["left3"][:, g, :], B["top2"][:, g, 8:16], B["left2"][:, g, :], -BIG)
                    x.then_inc(S["cut_c"], 1)
                    dve.wait_ge(S["cut_c"], n + 1)
                    nc.vector.tensor_tensor(B["chosen"][:], B["left3"][:], B["cand"][:],
                                            ALU.not_equal).then_inc(S["chosen"], 1)

                def store_delta(n):
                    dve.wait_ge(S["out_ready"], n + 1)
                    nc.vector.tensor_copy(delta[:, bass.ds(n, 1), :].rearrange("p a b -> p (a b)"), out_ps[:]).then_inc(S["delta_stored"], 1)

                def weigh(n, b):
                    B = buf[b]
                    dve.wait_ge(S["chosen"], n + 3)
                    dve.wait_ge(S["exp_ready"], n + 1)
                    nc.vector.tensor_tensor(B["masked"][:], B["shifted"][:], B["chosen"][:], ALU.mult).then_inc(S["masked"], 1)
                    dve.wait_ge(S["masked"], n + 1)
                    nc.vector.reduce_sum(B["total"][:], B["masked"][:], AX_X).then_inc(S["total"], 1)
                    dve.wait_ge(S["total"], n + 1)
                    nc.vector.reciprocal(B["inverse"][:], B["total"][:]).then_inc(S["inverse"], 1)
                    dve.wait_ge(S["inverse"], n + 1)
                    nc.vector.tensor_tensor(B["chosen"][:], B["masked"][:],
                                            B["inverse"][:].unsqueeze(2).broadcast_to([D, PK_HEADS, CAND]),
                                            ALU.mult).then_inc(S["scaled"], 1)
                    dve.wait_ge(S["scaled"], n + 1)
                    nc.vector.reduce_sum(B["weight"][:], B["chosen"][:].rearrange("p h c -> p c h"), AX_X).then_inc(S["weight"], 1)
                    dve.wait_ge(S["weight"], n + 1)
                    dve.wait_ge(S["gelu_ready"], n + 3)
                    nc.vector.tensor_tensor(B["gw"][:], B["weight"][:], B["act"][:], ALU.mult).then_inc(S["gw_ready"], 1)

                rank_keys(0, 0)
                with dve.Fori(0, TT // 2) as i:
                    for b in range(2):
                        n = i * 2 + b
                        rank_sums(n, b)
                        store_delta(n)
                        rank_keys(n + 1, 1 - b)
                        weigh(n, b)
                store_delta(TT)
                dve.wait_ge(S["delta_stored"], TT + 1)
                nc.vector.tensor_tensor(h[:], h[:], flat(delta[:, 1:, :]), ALU.add).then_inc(S["added"], 1)


def lay_out_pk(inp):
    a = {k: np.asarray(v) for k, v in inp.items()}
    places = [i * TOPK + j for i in range(TOPK) for j in range(ROWS[i])]
    wq = a["L1_ffn_W_q"].T.reshape(GROUPS, N_KEYS, D).transpose(1, 0, 2).reshape(N_KEYS, GROUPS * D)
    keys = a["L1_ffn_keys"].transpose(3, 2, 0, 1).reshape(N_KEYS, GROUPS * N_KEYS)
    return {"pk_wq": np.ascontiguousarray(wq), "pk_keys": np.ascontiguousarray(keys),
            "pk_down": np.ascontiguousarray(a["L1_ffn_down_embed"][places].T),
            "pk_up": np.ascontiguousarray(a["L1_ffn_up_embed"][places])}


MB = 8
NMB = T // MB
RW = MB * HEADS
QUAD = 4
EXT = DH + 1
TTT_EPS = 1e-6


def ttt_project(nc, dram, xn, kT, qT, rows, eta):
    turned = nc.dram_tensor("turned_scratch", [3, T, D], F32, kind="Internal").ap()
    with Scope(nc, "tp") as s:
        wk, wkp, wq, wqp, wv = (s.sb(n, [D, D]) for n in ("wk", "wkp", "wq", "wqp", "wv"))
        cos, sin = s.sb("cos", [D, T]), s.sb("sin", [D, T])
        lr_w, lr_b = s.sb("lr_w", [D, MB, RW]), s.sb("lr_b", [RW, 1])
        ident = s.sb("ident", [D, D])
        kv = s.sb("kv", [D, T])
        ca, sa = s.sb("ca", [D, 2, CH]), s.sb("sa", [D, 2, CH])
        token = s.sb("token", [D, 2, CH])
        pr = [s.ps(f"pr{j}", [D, CH]) for j in range(5)]
        lr_ps = s.ps("lr", [RW, NMB])
        turn_ps = s.ps("turn", [D, 2, CH])
        S = {n: s.sem(n) for n in ("loaded projected cos_done sin_done rotated kv_done lr_ready lr_stored "
                                   "turned token_ready even_written odd_written rows_read halved").split()}
        written = (S["even_written"], S["odd_written"])
        cols = lambda c: slice(c * CH, (c + 1) * CH)
        weights = (wk, wkp, wq, wqp, wv)
        with nc.Block() as block:
            @block.sync
            def _(sp):
                for dst, src in zip(weights, ("ttt_wk", "ttt_wkp", "ttt_wq", "ttt_wqp", "ttt_wv")):
                    sp.dma_start(dst[:], dram[src]).then_inc(S["loaded"], 16)
                for dst, src in ((cos, "cos"), (sin, "sin"), (lr_b, "ttt_lrb"), (ident, "ident")):
                    sp.dma_start(dst[:], dram[src]).then_inc(S["loaded"], 16)
                sp.dma_start(lr_w[:].rearrange("p a b -> p (a b)"), dram["ttt_lrw"]).then_inc(S["loaded"], 16)
                for n in range(3 * NCH):
                    a, c = n // NCH, n % NCH
                    sp.wait_ge(S["token_ready"], n + 1)
                    sp.dma_start(turned[a, cols(c), :].rearrange("(q p) d -> p q d", p=D),
                                 token[:, n % 2, :].rearrange("p (q d) -> p q d", d=D)).then_inc(written[n % 2], 16)
                for x in written:
                    sp.wait_ge(x, 16 * 3 * NCH // 2)
                by_row = lambda a: turned[a].rearrange("(n m) (h e) -> (m h) n e", m=MB, e=DH)
                sp.dma_start(rows[0:RW, 0, 0:NMB], by_row(0)).then_inc(S["rows_read"], 16)
                sp.dma_start(rows[0:RW, 1, 0:NMB], by_row(1)).then_inc(S["rows_read"], 16)
                sp.dma_start(rows[RW:D, 0, 0:NMB], by_row(2)).then_inc(S["rows_read"], 16)
                sp.wait_ge(S["rows_read"], 48)

            @block.tensor
            def _(pe):
                pe.wait_ge(S["loaded"], 160)
                for c in range(NCH):
                    for j in range(5):
                        if c:
                            pe.wait_ge(S["sin_done"], 2 * c)
                            pe.wait_ge(S["kv_done"], c)
                        nc.tensor.matmul(pr[j][:], weights[j][:], xn[:, cols(c)], start=True,
                                         stop=True).then_inc(S["projected"], 1)
                by_token = xn[:, 0:T].rearrange("p (n m) -> p m n", m=MB)
                for m in range(MB):
                    mm = nc.tensor.matmul(lr_ps[:], lr_w[:, m, :], by_token[:, m, :], start=(m == 0), stop=(m == MB - 1))
                mm.then_inc(S["lr_ready"], 1)
                pe.wait_ge(S["rotated"], 2 * NCH)
                pe.wait_ge(S["kv_done"], NCH)
                for n in range(3 * NCH):
                    a, c = n // NCH, n % NCH
                    src = (kv, kT, qT)[a]
                    if n >= 2:
                        pe.wait_ge(S["token_ready"], n - 1)
                    for q in range(4):
                        mm = nc.tensor.transpose(turn_ps[:, n % 2, q * D:(q + 1) * D],
                                                 src[:, c * CH + q * D:c * CH + (q + 1) * D], ident[:])
                    mm.then_inc(S["turned"], 1)

            @block.scalar
            def _(act):
                act.wait_ge(S["lr_ready"], 1)
                nc.scalar.activation(eta[:, 0:NMB], lr_ps[:], ACT.Sigmoid, bias=lr_b[:]).then_inc(S["lr_stored"], 1)
                for n in range(3 * NCH):
                    act.wait_ge(S["turned"], n + 1)
                    if n >= 2:
                        act.wait_ge(written[n % 2], 16 * (n // 2))
                    nc.scalar.activation(token[:, n % 2, :], turn_ps[:, n % 2, :], ACT.Copy).then_inc(S["token_ready"], 1)

            @block.vector
            def _(dve):
                dve.wait_ge(S["loaded"], 160)
                for c in range(NCH):
                    dve.wait_ge(S["projected"], 5 * c + 5)
                    for j, dst in enumerate((kT, qT)):
                        n = 2 * c + j
                        nc.vector.tensor_tensor(ca[:, j, :], pr[2 * j][:], cos[:, cols(c)], ALU.mult).then_inc(S["cos_done"], 1)
                        nc.vector.tensor_tensor(sa[:, j, :], pr[2 * j + 1][:], sin[:, cols(c)], ALU.mult).then_inc(S["sin_done"], 1)
                        dve.wait_ge(S["sin_done"], n + 1)
                        dve.wait_ge(S["cos_done"], n + 1)
                        nc.vector.tensor_tensor(dst[:, cols(c)], ca[:, j, :], sa[:, j, :], ALU.add).then_inc(S["rotated"], 1)
                    dve.wait_ge(S["rotated"], 2 * c + 2)
                    nc.vector.tensor_tensor(kv[:, cols(c)], kT[:, cols(c)], pr[4][:], ALU.subtract).then_inc(S["kv_done"], 1)
                dve.wait_ge(S["lr_stored"], 1)
                nc.vector.tensor_scalar(eta[:, 0:NMB], eta[:, 0:NMB], 1.0 / DH, None, ALU.mult).then_inc(S["halved"], 1)


def ttt_chain(nc, dram, kT, qT, rows, eta, zbar):
    with Scope(nc, "tc") as s:
        cc = rows[0:RW, 0, 0:NMB]
        krow, krow_pad = rows[0:RW, 1, 0:NMB], rows[0:RW, 1]
        first = s.sb("first", [D, D])
        kq = [s.sb(f"kq{b}", [D, QUAD, 2, RW]) for b in range(2)]
        ab = [s.sb(f"ab{b}", [D, QUAD, D]) for b in range(2)]
        up = [s.sb(f"up{b}", [RW, QUAD, HEADS, DH]) for b in range(2)]
        bup = [s.sb(f"bup{b}", [RW, QUAD, RW]) for b in range(2)]
        em = [s.sb(f"em{b}", [RW, QUAD, D]) for b in range(2)]
        head_cols = s.sb("head_cols", [D, HEADS])
        head_rows = s.sb("head_rows", [RW, HEADS])
        mask_ab, mask_b = s.sb("mask_ab", [RW, 2, MB, HEADS]), s.sb("mask_b", [RW, RW])
        tok = s.sb("tok", [RW, 2 * MB])
        tok_delta = s.sb("tok_delta", [RW, MB])
        g, bn = s.sb("g", [RW, DH]), s.sb("bn", [RW, DH])
        g2 = s.sb("g2", [RW, DH])
        ident = s.sb("ident", [D, D])
        w0, b0 = s.sb("w0", [D, EXT]), s.sb("b0", [D, EXT])
        wb_mean = s.sb("wb_mean", [D, 2])
        cmean = s.sb("cmean", [RW, NMB])
        w_sb = [s.sb(f"w_sb{b}", [D, EXT]) for b in range(2)]
        gb = [s.sb(f"gb{b}", [D, EXT]) for b in range(2)]
        zs = [s.sb(f"zs{b}", [RW, EXT]) for b in range(2)]
        gz, prod, square, prod2, w, cr = (s.sb(n, [RW, EXT]) for n in ("gz", "prod", "square", "prod2", "w", "cr"))
        sums = s.sb("sums", [RW, 4])
        tiny = s.sb("tiny", [RW, 5])
        p_ps = [s.ps(f"p{b}", [D, CH]) for b in range(2)]
        state_ps = s.ps("state", [D, CH])
        gram_ps = [s.ps(f"gram{x}", [RW, 2, D]) for x in range(2)]
        S = {n: s.sem(n) for n in (
            "loaded consts kq_ready em_ready up_ready bup_ready gram_ready ab_ready z_ready z_stored var_done "
            "gz_done prod_done prod2_done r2_done root_done scaled mean_done factor_done cr_done w_done "
            "grad_done state_ready zbar_ready w_stored b_stored zbar_stored prep chain_init ones_set").split()}

        CONSTS = 3 + 4 * QUAD + 4
        with nc.Block() as block:
            @block.sync
            def _(sp):
                for dst, src in ((head_cols[:], "ttt_head_cols"), (head_rows[:], "ttt_head_rows"),
                                 (mask_ab[:].rearrange("p a b c -> p (a b c)"), "ttt_mask_ab"), (mask_b[:], "ttt_mask_b"),
                                 (tok[:, 0:MB], "ttt_inv"), (g[:], "ttt_g"), (bn[:], "ttt_b"), (ident[:], "ident"),
                                 (w0[:, 0:DH], "ttt_w0"), (b0[RW:D, 0:DH], "ttt_b0")):
                    sp.dma_start(dst, dram[src]).then_inc(S["loaded"], 16)
                sp.dma_start(tok_delta[:], dram["ttt_tid"].partition_broadcast(RW)).then_inc(S["loaded"], 16)
            LOADED = 16 * 11

            @block.gpsimd
            def _(pool):
                for x in (first, gb[0], gb[1]):
                    nc.gpsimd.memset(x[:], 0.0).then_inc(S["consts"], 1)
                pool.wait_ge(S["loaded"], LOADED)
                pool.wait_ge(S["consts"], 3)
                for x in range(2):
                    for j in range(QUAD):
                        for half in range(2):
                            nc.gpsimd.tensor_copy(ab[x][RW:D, j, half * RW:(half + 1) * RW],
                                                  ident[RW:D, RW:D]).then_inc(S["consts"], 1)
                pool.wait_ge(S["consts"], 3 + 4 * QUAD)
                for x in (kT[:, T:], qT[:, T:], eta[:, NMB:], rows[0:RW, 1, NMB:]):
                    nc.gpsimd.memset(x, 0.0).then_inc(S["consts"], 1)
                pool.wait_ge(S["consts"], CONSTS)
                pool.wait_ge(S["prep"], 1)
                nc.gpsimd.tensor_tensor(first[:, 0:RW].rearrange("p (m h) -> p m h", h=HEADS),
                                        kT[:, 0:MB].unsqueeze(2).broadcast_to([D, MB, HEADS]),
                                        head_cols[:].unsqueeze(1).broadcast_to([D, MB, HEADS]),
                                        ALU.mult).then_inc(S["ones_set"], 1)

                def prepare(q, b):
                    shape = [D, QUAD, MB, HEADS]
                    if not isinstance(q, int):
                        pool.wait_ge(S["state_ready"], q * QUAD - (QUAD - 1))
                    for half, (src, off) in enumerate(((kT, MB), (qT, 0))):
                        x = src[:, bass.ds(q * (QUAD * MB) + off, QUAD * MB)] if half == 0 else \
                            src[:, bass.ds(q * (QUAD * MB), QUAD * MB)]
                        x = x.rearrange("p (j m) -> p j m", m=MB)
                        for j in range(QUAD):
                            i_ = nc.gpsimd.tensor_tensor(
                                kq[b][:, j, half, :].rearrange("p (m h) -> p m h", h=HEADS),
                                x[:, j, :].unsqueeze(2).broadcast_to([D, MB, HEADS]),
                                head_cols[:].unsqueeze(1).broadcast_to([D, MB, HEADS]), ALU.mult)
                    i_.then_inc(S["kq_ready"], 1)
                    eq = eta[:, bass.ds(q * QUAD, QUAD)].unsqueeze(2).broadcast_to([RW, QUAD, D])
                    if not isinstance(q, int):
                        pool.wait_ge(S["ab_ready"], q * QUAD - (QUAD - 1))
                    nc.gpsimd.tensor_tensor(em[b][:], eq,
                                            mask_ab[:].rearrange("p a b c -> p (a b c)").unsqueeze(1).broadcast_to([RW, QUAD, D]),
                                            ALU.mult).then_inc(S["em_ready"], 1)
                    kr = krow_pad[:, bass.ds(q * QUAD, QUAD), :]
                    for j in range(QUAD):
                        i_ = nc.gpsimd.tensor_tensor(up[b][:, j], kr[:, j, :].unsqueeze(1).broadcast_to([RW, HEADS, DH]),
                                                     head_rows[:].unsqueeze(2).broadcast_to([RW, HEADS, DH]), ALU.mult)
                    i_.then_inc(S["up_ready"], 1)
                    nc.gpsimd.tensor_tensor(bup[b][:], eq[:, :, 0:RW], mask_b[:].unsqueeze(1).broadcast_to([RW, QUAD, RW]),
                                            ALU.mult).then_inc(S["bup_ready"], 1)

                prepare(0, 0)
                prepare(1, 1)
                with pool.Fori(0, NMB // (2 * QUAD)) as i:
                    for b in range(2):
                        prepare(i * 2 + (b + 2), b)

            @block.tensor
            def _(pe):
                pe.wait_ge(S["loaded"], LOADED)
                pe.wait_ge(S["chain_init"], 1)
                pe.sem_inc(S["zbar_ready"], 1)
                pe.wait_ge(S["consts"], CONSTS)
                pe.wait_ge(S["ones_set"], 1)
                nc.tensor.matmul(state_ps[:, 0:EXT], ident[:], w0[:], start=True, stop=True, skip_group_check=True)
                nc.tensor.matmul(state_ps[:, 32:32 + EXT], ident[:], b0[:], start=False, stop=True,
                                 skip_group_check=True).then_inc(S["state_ready"], 1)
                nc.tensor.matmul(p_ps[0][:, 0:EXT], first[:], w0[:], start=True, stop=False, skip_group_check=True)
                pe.wait_ge(S["b_stored"], 1)
                pe.wait_ge(S["em_ready"], 1)
                nc.tensor.matmul(p_ps[0][:, 0:EXT], ab[0][RW:D, 0, :], gb[0][RW:D, :], start=False, stop=True,
                                 skip_group_check=True).then_inc(S["z_ready"], 1)

                def gram(q, b, j):
                    start = isinstance(q, int)
                    if j == 0:
                        pe.wait_ge(S["kq_ready"], q + 1)
                    if j % 2 == 0 and not start:
                        pe.wait_ge(S["ab_ready"], q * QUAD - (1 - j))
                    lhs = kq[b][:, j - 1, 0, :] if j else first[:, 0:RW] if start else kq[1 - b][:, QUAD - 1, 0, :]
                    nc.tensor.matmul(gram_ps[j // 2][:, j % 2, :], lhs, kq[b][:, j].rearrange("p a b -> p (a b)"),
                                     start=(j % 2 == 0), stop=(j % 2 == 1),
                                     skip_group_check=True).then_inc(S["gram_ready"], 1)
                for j in range(QUAD):
                    gram(0, 0, j)
                with pe.Fori(0, NMB // (2 * QUAD)) as i:
                    for b in range(2):
                        for j in range(QUAD):
                            n = i * (2 * QUAD) + (b * QUAD + j)
                            pb = (j + 1) % 2
                            pe.wait_ge(S["z_stored"], n + 1)
                            pe.wait_ge(S["zbar_stored"], n + 1)
                            pe.wait_ge(S["w_stored"], n + 2)
                            nc.tensor.matmul(p_ps[pb][:, 0:EXT], kq[b][:, j].rearrange("p a b -> p (a b)"), w_sb[j % 2][:],
                                             start=True, stop=False, skip_group_check=True)
                            if j == 0:
                                pe.wait_ge(S["up_ready"], 2 * i + (b + 1))
                                pe.wait_ge(S["bup_ready"], 2 * i + (b + 1))
                            pe.wait_ge(S["ab_ready"], n + 2)
                            pe.wait_ge(S["b_stored"], n + 2)
                            pe.wait_ge(S["grad_done"], n + 1)
                            nc.tensor.matmul(p_ps[pb][0:RW, 0:EXT], ab[b][:, j, 0:RW], gb[j % 2][:],
                                             start=False, stop=True, skip_group_check=True).then_inc(S["z_ready"], 1)
                            nc.tensor.matmul(state_ps[:, 0:EXT], up[b][:, j].rearrange("p a b -> p (a b)"), gb[j % 2][0:RW, :],
                                             start=False, stop=True, skip_group_check=True)
                            nc.tensor.matmul(state_ps[RW:D, 32:32 + EXT], bup[b][:, j, :], gb[j % 2][0:RW, :],
                                             start=False, stop=True, skip_group_check=True).then_inc(S["state_ready"], 1)
                            nc.tensor.matmul(p_ps[pb][RW:D, 0:EXT], ab[b][:, j, RW:D], gb[j % 2][:], start=False,
                                             stop=True, skip_group_check=True).then_inc(S["zbar_ready"], 1)
                            gram(i * 2 + (b + 1), 1 - b, j)

            @block.scalar
            def _(act):
                def store_state(n, j):
                    act.wait_ge(S["state_ready"], n + 1)
                    nc.scalar.activation(w_sb[j % 2][:], state_ps[:, 0:EXT], ACT.Copy).then_inc(S["w_stored"], 1)
                    nc.scalar.activation(gb[j % 2][RW:D, :], state_ps[RW:D, 32:32 + EXT], ACT.Copy).then_inc(S["b_stored"], 1)

                def keep_zbar(n, jj):
                    act.wait_ge(S["zbar_ready"], n + 1)
                    nc.scalar.activation(zbar[RW:D, bass.ds(n, 1), :].rearrange("p a e -> p (a e)"),
                                         p_ps[jj % 2][RW:D, 0:DH], ACT.Copy).then_inc(S["zbar_stored"], 1)
                act.sem_inc(S["zbar_stored"], 1)
                act.wait_ge(S["consts"], 3)
                store_state(0, 0)
                with act.Fori(0, NMB // (2 * QUAD)) as i:
                    for jj in range(2 * QUAD):
                        n = i * (2 * QUAD) + jj
                        act.wait_ge(S["r2_done"], n + 1)
                        nc.scalar.activation(tiny[:, 1:2], tiny[:, 0:1], ACT.Sqrt).then_inc(S["root_done"], 1)
                        store_state(n, jj)
                        keep_zbar(n, jj)
                keep_zbar(NMB, 0)

            @block.vector
            def _(dve):
                dve.wait_ge(S["loaded"], LOADED)
                count = [0]

                def then(x):
                    count[0] += 1
                    x.then_inc(S["mean_done"], 1)
                    dve.wait_ge(S["mean_done"], count[0])
                V = nc.vector
                then(V.tensor_tensor(tok[:, MB:], tok[:, 0:MB], tok_delta[:], ALU.add))
                then(V.tensor_scalar(tok[:, 0:MB], tok[:, MB:], 0.0, None, ALU.max))
                then(V.tensor_tensor(mask_ab[:, 1], mask_ab[:, 1], tok[:, 0:MB].unsqueeze(2).broadcast_to([RW, MB, HEADS]), ALU.mult))
                then(V.tensor_scalar(mask_ab[:, 0], mask_ab[:, 0], tok[:, MB - 1:MB], None, ALU.mult))
                then(V.tensor_scalar(mask_b[:], mask_b[:], tok[:, MB - 1:MB], None, ALU.mult))
                then(V.tensor_tensor(krow, krow, eta[:, 0:NMB].unsqueeze(2).broadcast_to([RW, NMB, DH]), ALU.mult))
                then(V.tensor_scalar(krow, krow, tok[:, MB - 1:MB], -1.0, ALU.mult, ALU.mult))
                wide = lambda a: a[:].unsqueeze(1).broadcast_to([RW, NMB, DH])
                then(V.tensor_tensor(cc, cc, wide(bn), ALU.add))
                then(V.tensor_tensor(cc, cc, wide(g), ALU.mult))
                then(V.reduce_sum(cmean[:], cc, AX_X))
                then(V.tensor_scalar(cmean[:], cmean[:], 1.0 / DH, None, ALU.mult))
                then(V.tensor_tensor(cc, cc, cmean[:].unsqueeze(2).broadcast_to([RW, NMB, DH]), ALU.subtract))
                then(V.scalar_tensor_tensor(out=g2[:], in0=g[:], scalar=1.0, in1=g[:], op0=ALU.mult, op1=ALU.mult))
                then(V.memset(b0[0:RW, :], 0.0))
                for x, p in ((w0, slice(0, D)), (b0, slice(RW, D))):
                    then(V.reduce_sum(wb_mean[p, 0:1], x[p, 0:DH], AX_X))
                    then(V.tensor_scalar(wb_mean[p, 1:2], wb_mean[p, 0:1], 1.0 / DH, None, ALU.mult))
                    then(V.tensor_scalar(x[p, 0:DH], x[p, 0:DH], wb_mean[p, 1:2], None, ALU.subtract))
                then(V.memset(w0[:, DH:], 0.0))
                then(V.memset(b0[RW:D, DH:], (DH * TTT_EPS) ** 0.5))
                dve.sem_inc(S["prep"], 1)
                dve.sem_inc(S["chain_init"], 1)
                dve.sem_inc(S["z_stored"], 1)
                dve.sem_inc(S["ab_ready"], 1)
                dve.wait_ge(S["consts"], CONSTS)

                def make_ab(q, b, j):
                    if j == 0:
                        dve.wait_ge(S["em_ready"], q + 1)
                        if not isinstance(q, int):
                            dve.wait_ge(S["state_ready"], q * QUAD - (QUAD - 1))
                    dve.wait_ge(S["gram_ready"], q * QUAD + (2 + j // 2 * 2))
                    V.scalar_tensor_tensor(out=ab[b][0:RW, j, :], in0=gram_ps[j // 2][:, j % 2, :], scalar=1.0,
                                           in1=em[b][:, j, :], op0=ALU.add, op1=ALU.mult).then_inc(S["ab_ready"], 1)
                for j in range(2):
                    make_ab(0, 0, j)

                def store_z(n, jj):
                    dve.wait_ge(S["z_ready"], n + 1)
                    V.tensor_copy(zs[jj % 2][:], p_ps[jj % 2][0:RW, 0:EXT]).then_inc(S["z_stored"], 1)
                with dve.Fori(0, NMB // (2 * QUAD)) as i:
                    for jj in range(2 * QUAD):
                        b, j = jj // QUAD, jj % QUAD
                        n = i * (2 * QUAD) + jj
                        z = zs[jj % 2][0:RW, 0:DH]
                        c = cc[:, bass.ds(n, 1), :].rearrange("p a e -> p (a e)")
                        store_z(n, jj)
                        dve.wait_ge(S["z_stored"], n + 2)
                        V.scalar_tensor_tensor(out=square[:], in0=zs[jj % 2][0:RW, :], scalar=1.0 / DH, in1=zs[jj % 2][0:RW, :],
                                               op0=ALU.mult, op1=ALU.mult, accum_out=sums[:, 3:4]).then_inc(S["var_done"], 1)
                        V.scalar_tensor_tensor(out=gz[:, 0:DH], in0=z, scalar=1.0, in1=g2[:], op0=ALU.mult, op1=ALU.mult,
                                               accum_out=sums[:, 1:2]).then_inc(S["gz_done"], 1)
                        dve.wait_ge(S["var_done"], n + 1)
                        V.reciprocal(tiny[:, 0:1], sums[:, 3:4]).then_inc(S["r2_done"], 1)
                        dve.wait_ge(S["gz_done"], n + 1)
                        V.scalar_tensor_tensor(out=prod2[:, 0:DH], in0=z, scalar=1.0, in1=gz[:, 0:DH], op0=ALU.mult, op1=ALU.mult,
                                               accum_out=sums[:, 0:1]).then_inc(S["prod2_done"], 1)
                        V.scalar_tensor_tensor(out=prod[:, 0:DH], in0=z, scalar=-1.0 / DH, in1=c, op0=ALU.mult, op1=ALU.mult,
                                               accum_out=sums[:, 2:3]).then_inc(S["prod_done"], 1)
                        dve.wait_ge(S["prod2_done"], n + 1)
                        V.tensor_scalar(tiny[:, 2:4], sums[:, 0:2], tiny[:, 0:1], -1.0 / DH, ALU.mult,
                                        ALU.mult).then_inc(S["scaled"], 1)
                        dve.wait_ge(S["scaled"], n + 1)
                        dve.wait_ge(S["root_done"], n + 1)
                        V.tensor_scalar(tiny[:, 4:5], sums[:, 2:3], tiny[:, 1:2], tiny[:, 2:3], ALU.mult,
                                        ALU.add).then_inc(S["factor_done"], 1)
                        V.tensor_scalar(cr[:, 0:DH], c, tiny[:, 1:2], tiny[:, 3:4], ALU.mult, ALU.add).then_inc(S["cr_done"], 1)
                        dve.wait_ge(S["factor_done"], n + 1)
                        V.scalar_tensor_tensor(out=w[:, 0:DH], in0=z, scalar=tiny[:, 4:5], in1=gz[:, 0:DH], op0=ALU.mult,
                                               op1=ALU.add).then_inc(S["w_done"], 1)
                        dve.wait_ge(S["w_done"], n + 1)
                        V.scalar_tensor_tensor(out=gb[jj % 2][0:RW, 0:DH], in0=w[:, 0:DH], scalar=tiny[:, 0:1], in1=cr[:, 0:DH],
                                               op0=ALU.mult, op1=ALU.add).then_inc(S["grad_done"], 1)
                        if j < 2:
                            make_ab(i * 2 + b, b, j + 2)
                        else:
                            make_ab(i * 2 + (b + 1), 1 - b, j - 2)


def ttt_finish(nc, dram, rows, zbar, hidden):
    scratch = nc.dram_tensor("hidden_scratch", [T, D], F32, kind="Internal").ap()
    with Scope(nc, "tf") as s:
        H = slice(RW, D)
        g, bn = s.sb("g", [D, DH]), s.sb("bn", [D, DH])
        sq = s.sb("sq", [D, NMB, DH])
        y = s.sb("y", [D, NMB, DH])
        var = s.sb("var", [D, NMB])
        eps = s.sb("eps", [D, 1])
        tokens = s.sb("tokens", [D, TT, D])
        ident = s.sb("ident", [D, D])
        turn_ps = s.ps("turn", [D, NCH, CH])
        S = {n: s.sem(n) for n in "loaded sq_done var_done root_done step y_done written read turned stored eps_set".split()}
        zb = zbar[H, 1:NMB + 1, :]
        wide = lambda a: a[H].unsqueeze(1).broadcast_to([RW, NMB, DH])
        with nc.Block() as block:
            @block.sync
            def _(sp):
                sp.dma_start(g[H], dram["ttt_g"]).then_inc(S["loaded"], 16)
                sp.dma_start(bn[H], dram["ttt_b"]).then_inc(S["loaded"], 16)
                sp.dma_start(ident[:], dram["ident"]).then_inc(S["loaded"], 16)
                sp.wait_ge(S["y_done"], 1)
                sp.dma_start(scratch.rearrange("(n m) (h e) -> (m h) n e", m=MB, e=DH), y[H]).then_inc(S["written"], 16)
                sp.wait_ge(S["written"], 16)
                sp.dma_start(tokens[:], scratch.rearrange("(t p) d -> p t d", p=D)).then_inc(S["read"], 16)

            @block.gpsimd
            def _(pool):
                pool.memset(eps[:], TTT_EPS).then_inc(S["eps_set"], 1)

            @block.scalar
            def _(act):
                act.wait_ge(S["eps_set"], 1)
                nc.scalar.activation(sq[H], zb, ACT.Square).then_inc(S["sq_done"], 1)
                act.wait_ge(S["var_done"], 1)
                nc.scalar.activation(var[H], var[H], ACT.Sqrt, scale=1.0 / DH, bias=eps[H]).then_inc(S["root_done"], 1)

            @block.vector
            def _(dve):
                V = nc.vector
                dve.wait_ge(S["sq_done"], 1)
                V.reduce_sum(var[H], sq[H], AX_X).then_inc(S["var_done"], 1)
                dve.wait_ge(S["root_done"], 1)
                dve.wait_ge(S["loaded"], 48)
                V.reciprocal(var[H], var[H]).then_inc(S["step"], 1)
                dve.wait_ge(S["step"], 1)
                V.tensor_tensor(y[H], zb, var[H].unsqueeze(2).broadcast_to([RW, NMB, DH]), ALU.mult).then_inc(S["step"], 1)
                dve.wait_ge(S["step"], 2)
                V.tensor_tensor(y[H], y[H], wide(g), ALU.mult).then_inc(S["step"], 1)
                dve.wait_ge(S["step"], 3)
                V.tensor_tensor(y[H], y[H], wide(bn), ALU.add).then_inc(S["step"], 1)
                dve.wait_ge(S["step"], 4)
                V.tensor_tensor(y[H], y[H], rows[H, 0, 0:NMB], ALU.add).then_inc(S["y_done"], 1)
                for c in range(NCH):
                    dve.wait_ge(S["turned"], c + 1)
                    V.tensor_copy(hidden[:, c * CH:(c + 1) * CH], turn_ps[:, c, :]).then_inc(S["stored"], 1)

            @block.tensor
            def _(pe):
                pe.wait_ge(S["loaded"], 48)
                pe.wait_ge(S["read"], 16)
                for c in range(NCH):
                    for q in range(4):
                        mm = nc.tensor.transpose(turn_ps[:, c, q * D:(q + 1) * D], tokens[:, 4 * c + q, :], ident[:])
                    mm.then_inc(S["turned"], 1)


def lay_out_ttt(inp):
    a = {k: np.asarray(v) for k, v in inp.items()}
    wk, wq, wv = (a[f"L1_attn_{n}"] for n in ("wk", "wq", "wv"))
    feat = np.arange(D)
    d = feat % DH
    perm = np.where(d < DH // 2, feat + DH // 2, feat - DH // 2)
    inv = (1.0 / np.float32(10000.0) ** (np.arange(0, DH, 2, dtype=np.float32) / np.float32(DH))).astype(np.float32)
    f = np.arange(T, dtype=np.float32)[None, :] * inv[d % (DH // 2)][:, None]
    sign = np.where(d < DH // 2, -1.0, 1.0).astype(np.float32)[:, None]
    lrw = a["L1_attn_lr_w"][:, 0, :]
    lr = np.zeros((D, MB, MB, HEADS), np.float32)
    for m in range(MB):
        lr[:, m, m, :] = lrw.T
    row_head = np.arange(RW) % HEADS
    row_tok = np.arange(RW) // HEADS
    same = row_head[:, None, None] == np.arange(HEADS)[None, None, :]
    mask = np.zeros((RW, 2, MB, HEADS), np.float32)
    mask[:, 0] = np.where(same, -1.0, 0.0)
    mask[:, 1] = np.where(same & (row_tok[:, None, None] <= np.arange(MB)[None, :, None]), -1.0, 0.0)
    mask_b = np.where(row_head[:, None] == row_head[None, :], -1.0, 0.0).astype(np.float32)
    tile_rows = lambda x: np.ascontiguousarray(np.tile(x, (MB, 1)))
    return {
        "ttt_wk": np.ascontiguousarray(wk.T), "ttt_wkp": np.ascontiguousarray(wk[perm].T),
        "ttt_wq": np.ascontiguousarray(wq.T), "ttt_wqp": np.ascontiguousarray(wq[perm].T),
        "ttt_wv": np.ascontiguousarray(wv.T),
        "cos": np.cos(f).astype(np.float32), "sin": (np.sin(f) * sign).astype(np.float32),
        "ttt_lrw": lr.reshape(D, MB * RW), "ttt_lrb": tile_rows(a["L1_attn_lr_b"].reshape(HEADS, 1)),
        "ttt_head_cols": (np.arange(D)[:, None] // DH == np.arange(HEADS)[None, :]).astype(np.float32),
        "ttt_head_rows": (row_head[:, None] == np.arange(HEADS)[None, :]).astype(np.float32),
        "ttt_mask_ab": mask.reshape(RW, D), "ttt_mask_b": mask_b,
        "ttt_inv": np.tile((np.float32(1) / np.arange(1, MB + 1, dtype=np.float32))[None], (RW, 1)),
        "ttt_tid": a["L1_attn_token_idx_delta"],
        "ttt_g": tile_rows(a["L1_attn_ttt_norm_w"]), "ttt_b": tile_rows(a["L1_attn_ttt_norm_b"]),
        "ttt_w0": a["L1_attn_W1"].reshape(D, DH), "ttt_b0": tile_rows(a["L1_attn_b1"][:, 0, :]),
        "ln1_w": a["L1_attn_ln_w"].reshape(D, 1), "ln1_b": a["L1_attn_ln_b"].reshape(D, 1),
        "post_w": a["L1_attn_post_norm_w"].reshape(D, 1), "post_b": a["L1_attn_post_norm_b"].reshape(D, 1),
    }


NT = 6
NS = 8
XD = 104
WIN = 5


def longhorn_inputs(nc, dram, xn, xc, xd):
    with Scope(nc, "li") as s:
        w_in = [s.sb(f"w_in{b}", [D, D]) for b in range(2)]
        w_x = s.sb("w_x", [D, NT, XD])
        conv_w, conv_b = s.sb("conv_w", [D, NT, 3]), s.sb("conv_b", [D, NT])
        xl = [s.sb(f"xl{b}", [D, 2 + T]) for b in range(2)]
        acc = [s.sb(f"acc{b}", [D, T]) for b in range(2)]
        acc2 = [s.sb(f"acc2{b}", [D, T]) for b in range(2)]
        sum_k = s.sb("sum_k", [XD, XD])
        sq = s.sb("sq", [XD, T])
        den, inv = s.sb("den", [NS, T]), s.sb("inv", [NS, T])
        xl_ps = s.ps("xl", [D, NCH, CH])
        xd_ps = s.ps("xd", [XD, NCH, CH])
        S = {n: s.sem(n) for n in ("loaded w_a w_b padded xl_ready xl_stored first_tap second_tap third_tap "
                                   "xc_ready w_used xd_ready xd_stored cleared sq_done ks_ready log_done den_ready "
                                   "inv_ready k_ready nk2_ready").split()}
        w_loaded = (S["w_a"], S["w_b"])
        flat = lambda ap: ap.rearrange("p a b -> p (a b)")
        with nc.Block() as block:
            @block.sync
            def _(sp):
                for i in range(NT):
                    if i >= 2:
                        sp.wait_ge(S["w_used"], i - 1)
                    sp.dma_start(w_in[i % 2][:], dram["lh_in"][i * D:(i + 1) * D, :]).then_inc(w_loaded[i % 2], 16)
                    if i == 0:
                        sp.dma_start(flat(w_x[:]), dram["lh_x"]).then_inc(S["loaded"], 16)
                        sp.dma_start(flat(conv_w[:]), dram["lh_conv_w"]).then_inc(S["loaded"], 16)
                        sp.dma_start(conv_b[:], dram["lh_conv_b"]).then_inc(S["loaded"], 16)
                        sp.dma_start(sum_k[:], dram["lh_sum_k"]).then_inc(S["loaded"], 16)

            @block.gpsimd
            def _(pool):
                for b in range(2):
                    pool.memset(xl[b][:, 0:2], 0.0).then_inc(S["padded"], 1)
                pool.memset(xd[:], 0.0).then_inc(S["cleared"], 1)

            @block.tensor
            def _(pe):
                pe.wait_ge(S["loaded"], 64)
                for i in range(NT):
                    pe.wait_ge(w_loaded[i % 2], 16 * (i // 2 + 1))
                    for c in range(NCH):
                        if i:
                            pe.wait_ge(S["xl_stored"], (i - 1) * NCH + c + 1)
                        mm = nc.tensor.matmul(xl_ps[:, c, :], w_in[i % 2][:], xn[:, c * CH:(c + 1) * CH], start=True,
                                              stop=True)
                        mm.then_inc(S["xl_ready"], 1)
                        if c == NCH - 1:
                            pe.wait_ge(S["xl_ready"], (i + 1) * NCH)
                            pe.sem_inc(S["w_used"], 1)
                for i in range(NT):
                    pe.wait_ge(S["xc_ready"], i + 1)
                    for c in range(NCH):
                        mm = nc.tensor.matmul(xd_ps[:, c, :], w_x[:, i, :], xc[:, i, c * CH:(c + 1) * CH],
                                              start=(i == 0), stop=(i == NT - 1))
                        if i == NT - 1:
                            mm.then_inc(S["xd_ready"], 1)
                for c in range(NCH):
                    pe.wait_ge(S["sq_done"], c + 1)
                    nc.tensor.matmul(xl_ps[0:XD, c, :], sum_k[:], sq[:, c * CH:(c + 1) * CH], start=True,
                                     stop=True).then_inc(S["ks_ready"], 1)

            @block.scalar
            def _(act):
                act.wait_ge(S["loaded"], 64)
                act.wait_ge(S["padded"], 2)
                for i in range(NT):
                    b = i % 2
                    for c in range(NCH):
                        act.wait_ge(S["xl_ready"], i * NCH + c + 1)
                        if i >= 2 and c == 0:
                            act.wait_ge(S["third_tap"], i - 1)
                        nc.scalar.activation(xl[b][:, 2 + c * CH:2 + (c + 1) * CH], xl_ps[:, c, :],
                                             ACT.Copy).then_inc(S["xl_stored"], 1)
                    act.wait_ge(S["xl_stored"], (i + 1) * NCH)
                    nc.scalar.activation(acc[b][:], xl[b][:, 0:T], ACT.Identity, scale=conv_w[:, i, 0:1],
                                         bias=conv_b[:, i:i + 1]).then_inc(S["first_tap"], 1)
                    act.wait_ge(S["third_tap"], i + 1)
                    nc.scalar.activation(xc[:, i, :], acc[b][:], ACT.Silu).then_inc(S["xc_ready"], 1)
                for c in range(NCH):
                    act.wait_ge(S["xd_ready"], c + 1)
                    nc.scalar.activation(sq[:, c * CH:(c + 1) * CH], xd_ps[:, c, :], ACT.Square).then_inc(S["sq_done"], 1)
                act.wait_ge(S["cleared"], 1)
                act.wait_ge(S["ks_ready"], NCH)
                nc.scalar.activation(xd[0:2 * NS, 0:T], flat(xl_ps[0:2 * NS]), ACT.Ln, bias=1.0).then_inc(S["log_done"], 1)
                nc.scalar.activation(xd[64:64 + NS, 0:T], flat(xd_ps[64:64 + NS]), ACT.Copy).then_inc(S["xd_stored"], 1)
                act.wait_ge(S["log_done"], 1)
                nc.scalar.activation(xd[0:NS, 0:T], flat(xd_ps[0:NS]), ACT.Copy).then_inc(S["xd_stored"], 1)

            @block.vector
            def _(dve):
                for i in range(NT):
                    b = i % 2
                    dve.wait_ge(S["first_tap"], i + 1)
                    nc.vector.scalar_tensor_tensor(out=acc2[b][:], in0=xl[b][:, 1:1 + T], scalar=conv_w[:, i, 1:2],
                                                   in1=acc[b][:], op0=ALU.mult, op1=ALU.add).then_inc(S["second_tap"], 1)
                    dve.wait_ge(S["second_tap"], i + 1)
                    nc.vector.scalar_tensor_tensor(out=acc[b][:], in0=xl[b][:, 2:2 + T], scalar=conv_w[:, i, 2:3],
                                                   in1=acc2[b][:], op0=ALU.mult, op1=ALU.add).then_inc(S["third_tap"], 1)
                dve.wait_ge(S["cleared"], 1)
                K = slice(32, 32 + NS)
                for c in range(NCH):
                    cols = slice(c * CH, (c + 1) * CH)
                    dve.wait_ge(S["ks_ready"], c + 1)
                    nc.vector.tensor_scalar(den[:, cols], xl_ps[K, c, :], 1.0, None, ALU.add).then_inc(S["den_ready"], 1)
                    dve.wait_ge(S["den_ready"], c + 1)
                    nc.vector.reciprocal(inv[:, cols], den[:, cols]).then_inc(S["inv_ready"], 1)
                    dve.wait_ge(S["inv_ready"], c + 1)
                    nc.vector.tensor_tensor(xd[K, cols], xd_ps[K, c, :], inv[:, cols], ALU.mult).then_inc(S["k_ready"], 1)
                    dve.wait_ge(S["k_ready"], c + 1)
                    nc.vector.scalar_tensor_tensor(out=xd[96:96 + NS, cols], in0=xd_ps[K, c, :], scalar=-1.0,
                                                   in1=xd[K, cols], op0=ALU.mult, op1=ALU.mult).then_inc(S["nk2_ready"], 1)


def longhorn_scan(nc, dram, xn, xc, xd, h_red):
    PAIRS_N = NS // 2
    PA = PAIRS_N - 1
    ITEMS = 6
    PER = NT * PAIRS_N
    ROWS = PAIRS_N * ITEMS
    with Scope(nc, "ls") as s:
        w_z = s.sb("w_z", [D, NT, D])
        w_dt = s.sb("w_dt", [XD, NT, D])
        w_red = s.sb("w_red", [D, NT, D])
        dt_b, d_par = s.sb("dt_b", [D, NT]), s.sb("d_par", [D, NT])
        picks = [s.sb(f"pick_{x}", [XD, NS, D]) for x in ("nk2", "k", "q")]
        ident = s.sb("ident", [D, D])
        d_diag = s.sb("d_diag", [D, NT, D])
        nk2, kk, qq = (s.sb(n, [D, NS, CH]) for n in ("nk2", "kk", "qq"))
        zg = [s.sb(f"zg{b}", [D, CH]) for b in range(2)]
        sig = [s.sb(f"sig{b}", [D, CH]) for b in range(2)]
        dx = [s.sb(f"dx{b}", [D, CH]) for b in range(2)]
        a_ = [s.sb(f"a{b}", [D, 2, CH]) for b in range(2)]
        b_ = [s.sb(f"b{b}", [D, 2, CH]) for b in range(2)]
        st = [s.sb(f"st{b}", [D, 2, CH]) for b in range(2)]
        qs = [s.sb(f"qs{b}", [D, 2, CH]) for b in range(2)]
        carry = s.sb("carry", [D, NT, NS])
        yg = s.sb("yg", [D, CH])
        bc_ps = s.ps("bc", [D, 2, CH])
        dt_ps, z_ps = s.ps("dt", [D, CH]), s.ps("z", [D, CH])
        y_ps = s.ps("y", [D, 2, CH])
        red_ps = s.ps("red", [D, CH])
        S = {n: s.sem(n) for n in (
            "loaded diag zero_carry bc_ready bc_stored z_ready zg_ready dt_ready sig_ready dx_ready a_ready "
            "last_a_ready a1_ready b_ready st_ready carry_ready qs_ready y_ready yg_ready red_ready red_stored").split()}
        flat = lambda ap: ap.rearrange("p a b -> p (a b)")
        LOADED = 16 * 9
        item = lambda m: ((nk2, kk, qq)[m // 2], picks[m // 2], m % 2)
        with nc.Block() as block:
            @block.sync
            def _(sp):
                for dst, src in ((flat(picks[0][:]), "lh_pick_nk2"), (flat(picks[1][:]), "lh_pick_k"),
                                 (flat(picks[2][:]), "lh_pick_q"), (flat(w_dt[:]), "lh_dt"), (dt_b[:], "lh_dt_b"),
                                 (flat(w_z[:]), "lh_z"), (ident[:], "ident"), (d_par[:], "lh_d"),
                                 (flat(w_red[:]), "lh_red")):
                    sp.dma_start(dst, dram[src]).then_inc(S["loaded"], 16)

            @block.gpsimd
            def _(pool):
                wide = lambda x: x[:].unsqueeze(1).broadcast_to([D, 2, CH])
                nc.gpsimd.memset(carry[:], 0.0).then_inc(S["zero_carry"], 1)
                with pool.Fori(0, NCH) as c:
                    for i in range(NT):
                        for p in range(PAIRS_N):
                            n = c * PER + (i * PAIRS_N + p)
                            pair = slice(2 * p, 2 * p + 2)
                            if p == 0:
                                pool.wait_ge(S["dx_ready"], c * NT + (i + 1))
                            if i == 0:
                                pool.wait_ge(S["bc_stored"], c * ROWS + (ITEMS * (p + 1) + 2))
                            pool.wait_ge(S["st_ready"], n + 1)
                            if p == PAIRS_N - 1:
                                nc.gpsimd.tensor_tensor(a_[p % 2][:], wide(sig[i % 2]), nk2[:, pair, :],
                                                        ALU.mult).then_inc(S["last_a_ready"], 1)
                            nc.gpsimd.tensor_tensor(b_[p % 2][:], wide(dx[i % 2]), kk[:, pair, :],
                                                    ALU.mult).then_inc(S["b_ready"], 1)

            @block.tensor
            def _(pe):
                pe.sem_inc(S["y_ready"], 2)
                pe.sem_inc(S["red_ready"], 1)
                pe.wait_ge(S["loaded"], LOADED)

                def refill(p, chunk, first):
                    for m in range(ITEMS):
                        array, pick, j = item(m)
                        pe.wait_ge(S["bc_stored"], first + (m + 1))
                        nc.tensor.matmul(bc_ps[:, m % 2, :], pick[:, 2 * p + j, :], xd[:, bass.ds(chunk * CH, CH)],
                                         start=True, stop=True).then_inc(S["bc_ready"], 1)

                def project_dt(k, i, chunk):
                    nc.tensor.matmul(dt_ps[:], w_dt[:, i, :], xd[:, bass.ds(chunk * CH, CH)], start=True,
                                     stop=True).then_inc(S["dt_ready"], 1)

                project_dt(0, 0, 0)
                for p in range(PAIRS_N - 1):
                    refill(p, 0, ITEMS * p)
                pe.wait_ge(S["diag"], NT)
                with pe.Fori(0, NCH) as c:
                    cols = bass.ds(c * CH, CH)

                    def reduce_tile(i):
                        k = c * NT + i
                        pe.wait_ge(S["yg_ready"], k + 3)
                        if i == 0:
                            pe.wait_ge(S["red_stored"], c + 1)
                        nc.tensor.matmul(red_ps[:], w_red[:, i, :], yg[:], start=(i == 0),
                                         stop=(i == NT - 1)).then_inc(S["red_ready"], 1)

                    for i in range(NT):
                        k = c * NT + i
                        pe.wait_ge(S["zg_ready"], k + 1)
                        nc.tensor.matmul(z_ps[:], w_z[:, i, :], xn[:, cols], start=True, stop=True).then_inc(S["z_ready"], 1)
                        pe.wait_ge(S["sig_ready"], k + 1)
                        project_dt(k + 1, (i + 1) % NT, c + (i + 1) // NT)
                        pe.wait_ge(S["yg_ready"], k + 1)
                        nc.tensor.matmul(y_ps[:, i % 2, :], d_diag[:, i, :], xc[:, i, cols], start=True, stop=False)
                        for p in range(PAIRS_N):
                            pe.wait_ge(S["qs_ready"], c * PER + (i * PAIRS_N + p + 3))
                            for j in range(2):
                                mm = nc.tensor.matmul(y_ps[:, i % 2, :], ident[:], qs[p % 2][:, j, :], start=False,
                                                      stop=(p == PAIRS_N - 1 and j == 1))
                            mm.then_inc(S["y_ready"], 1)
                            if i and p == 1:
                                reduce_tile(i - 1)
                            if i == 0 and p == 0:
                                refill(PAIRS_N - 1, c, c * ROWS + (PAIRS_N - 1) * ITEMS)
                            if i == NT - 1 and p < PAIRS_N - 1:
                                refill(p, c + 1, c * ROWS + (PAIRS_N + p) * ITEMS)
                    reduce_tile(NT - 1)

            @block.scalar
            def _(act):
                act.sem_inc(S["bc_stored"], 2)
                act.sem_inc(S["zg_ready"], 1)
                act.sem_inc(S["red_stored"], 1)
                act.wait_ge(S["loaded"], LOADED)

                def refill(p, first):
                    for m in range(ITEMS):
                        array, pick, j = item(m)
                        act.wait_ge(S["bc_ready"], first + (m + 1))
                        nc.scalar.activation(array[:, 2 * p + j, :], bc_ps[:, m % 2, :], ACT.Copy).then_inc(S["bc_stored"], 1)

                def gate(k, i):
                    act.wait_ge(S["dt_ready"], k + 1)
                    nc.scalar.activation(sig[i % 2][:], dt_ps[:], ACT.Sigmoid,
                                         bias=dt_b[:, i:i + 1]).then_inc(S["sig_ready"], 1)

                gate(0, 0)
                for p in range(PAIRS_N - 1):
                    refill(p, ITEMS * p)
                with act.Fori(0, NCH) as c:
                    cols = bass.ds(c * CH, CH)
                    for i in range(NT):
                        k = c * NT + i
                        for p in range(PAIRS_N):
                            n = c * PER + (i * PAIRS_N + p)
                            if p < PA:
                                act.wait_ge(S["a_ready"], k * PA + (p + 1))
                            else:
                                act.wait_ge(S["last_a_ready"], k + 1)
                            nc.scalar.activation(a_[p % 2][:], a_[p % 2][:], ACT.Copy, bias=1.0).then_inc(S["a1_ready"], 1)
                            if i == NT - 1 and p >= 1:
                                act.wait_ge(S["b_ready"], n)
                                act.wait_ge(S["qs_ready"], n + 2)
                                refill(p - 1, c * ROWS + (PAIRS_N + p - 1) * ITEMS)
                            if p == 1:
                                gate(k + 1, (i + 1) % NT)
                                act.wait_ge(S["z_ready"], k + 1)
                                act.wait_ge(S["yg_ready"], k + 1)
                                nc.scalar.activation(zg[i % 2][:], z_ps[:], ACT.Silu).then_inc(S["zg_ready"], 1)
                            if i == 0 and p == 1:
                                act.wait_ge(S["b_ready"], n)
                                act.wait_ge(S["qs_ready"], c * PER + 2)
                                refill(PAIRS_N - 1, c * ROWS + (PAIRS_N - 1) * ITEMS)
                    act.wait_ge(S["red_ready"], c * NT + (NT + 1))
                    nc.scalar.activation(h_red[:, cols], red_ps[:], ACT.Copy).then_inc(S["red_stored"], 1)

            @block.vector
            def _(dve):
                V = nc.vector
                dve.sem_inc(S["st_ready"], 2)
                dve.sem_inc(S["qs_ready"], 2)
                dve.sem_inc(S["yg_ready"], 2)
                dve.wait_ge(S["loaded"], LOADED)
                for i in range(NT):
                    V.tensor_scalar(d_diag[:, i, :], ident[:], d_par[:, i:i + 1], None, ALU.mult).then_inc(S["diag"], 1)
                dve.wait_ge(S["zero_carry"], 1)
                with dve.Fori(0, NCH) as c:
                    cols = bass.ds(c * CH, CH)

                    def make_a(i, p):
                        if i == 0:
                            dve.wait_ge(S["bc_stored"], c * ROWS + (ITEMS * (p + 1) + 2))
                        V.tensor_tensor(a_[p % 2][:], sig[i % 2][:].unsqueeze(1).broadcast_to([D, 2, CH]),
                                        nk2[:, 2 * p:2 * p + 2, :], ALU.mult).then_inc(S["a_ready"], 1)

                    def gate_tile(i):
                        k = c * NT + i
                        dve.wait_ge(S["y_ready"], k * PAIRS_N + (PAIRS_N + 2))
                        dve.wait_ge(S["zg_ready"], k + 2)
                        dve.wait_ge(S["red_ready"], k + 1)
                        V.tensor_tensor(yg[:], y_ps[:, i % 2, :], zg[i % 2][:], ALU.mult).then_inc(S["yg_ready"], 1)

                    for i in range(NT):
                        k = c * NT + i
                        dve.wait_ge(S["sig_ready"], k + 1)
                        V.tensor_tensor(dx[i % 2][:], sig[i % 2][:], xc[:, i, cols], ALU.mult).then_inc(S["dx_ready"], 1)
                        make_a(i, 0)
                        for p in range(PAIRS_N):
                            n = c * PER + (i * PAIRS_N + p)
                            if p + 1 < PA:
                                make_a(i, p + 1)
                            dve.wait_ge(S["a1_ready"], n + 1)
                            dve.wait_ge(S["b_ready"], n + 1)
                            for j in range(2):
                                x = V.tensor_tensor_scan(st[p % 2][:, j, :], a_[p % 2][:, j, :], b_[p % 2][:, j, :],
                                                         carry[:, i, 2 * p + j:2 * p + j + 1], ALU.mult, ALU.add)
                            x.then_inc(S["st_ready"], 1)
                            dve.wait_ge(S["st_ready"], n + 3)
                            V.tensor_copy(carry[:, i, 2 * p:2 * p + 2], st[p % 2][:, :, CH - 1]).then_inc(S["carry_ready"], 1)
                            dve.wait_ge(S["y_ready"], n + 1)
                            if i == 0 and p == PAIRS_N - 1:
                                dve.wait_ge(S["bc_stored"], c * ROWS + (ROWS + 2))
                            V.tensor_tensor(qs[p % 2][:], st[p % 2][:], qq[:, 2 * p:2 * p + 2, :],
                                            ALU.mult).then_inc(S["qs_ready"], 1)
                            if i and p == 0:
                                gate_tile(i - 1)
                    gate_tile(NT - 1)


def gains(nc, dram, xn, gain):
    W = D + 2 * WIN
    with Scope(nc, "gn") as s:
        w_q, w_k = s.sb("w_q", [D, D]), s.sb("w_k", [D, D])
        ident = s.sb("ident", [D, D])
        ones = s.sb("ones", [D, D])
        band = s.sb("band", [D, W])
        qg, kg = s.sb("qg", [D, T]), s.sb("kg", [D, T + 2 * WIN])
        sc = s.sb("sc", [D, TT, W])
        mx, nmx, tot, inv, gcol = (s.sb(n, [D, TT]) for n in ("mx", "nmx", "tot", "inv", "gcol"))
        junk = s.sb("junk", [D, TT, W])
        diag = [s.sb(f"diag{b}", [D, D]) for b in range(2)]
        two = s.sb("two", [D, 1])
        pr_ps = s.ps("pr", [D, 2, CH])
        sc_ps = s.ps("sc", [D, 2, CH])
        g_ps = s.ps("g", [D, NCH, CH])
        S = {n: s.sem(n) for n in ("loaded set pr_ready pr_stored edges sc_ready sc_masked mx_ready nmx_ready ex_ready "
                                   "inv_ready g_ready diag_ready out_ready stored").split()}
        with nc.Block() as block:
            @block.sync
            def _(sp):
                for dst, src in ((w_q, "gn_q"), (w_k, "gn_k"), (ident, "ident"), (band, "gn_band")):
                    sp.dma_start(dst[:], dram[src]).then_inc(S["loaded"], 16)

            @block.gpsimd
            def _(pool):
                pool.memset(ones[:], 1.0).then_inc(S["set"], 1)
                pool.memset(two[:], -2.0).then_inc(S["set"], 1)

            @block.tensor
            def _(pe):
                pe.wait_ge(S["loaded"], 64)
                for n in range(2 * NCH):
                    c = n // 2
                    if n >= 2:
                        pe.wait_ge(S["pr_stored"], n - 1)
                    nc.tensor.matmul(pr_ps[:, n % 2, :], (w_q, w_k)[n % 2][:], xn[:, c * CH:(c + 1) * CH], start=True,
                                     stop=True).then_inc(S["pr_ready"], 1)
                pe.wait_ge(S["pr_stored"], 2 * NCH)
                pe.wait_ge(S["edges"], 1)
                for t in range(TT):
                    if t >= 2:
                        pe.wait_ge(S["sc_masked"], t - 1)
                    nc.tensor.matmul(sc_ps[:, t % 2, 0:W], qg[:, t * D:(t + 1) * D], kg[:, t * D:t * D + W], start=True,
                                     stop=True).then_inc(S["sc_ready"], 1)
                pe.wait_ge(S["set"], 2)
                for t in range(TT):
                    pe.wait_ge(S["diag_ready"], t + 1)
                    nc.tensor.matmul(g_ps[:, t // 4, (t % 4) * D:(t % 4 + 1) * D], ones[:], diag[t % 2][:],
                                     start=(t % 4 == 0), stop=(t % 4 == 3), skip_group_check=True).then_inc(S["out_ready"], 1)

            @block.scalar
            def _(act):
                for n in range(2 * NCH):
                    c = n // 2
                    act.wait_ge(S["pr_ready"], n + 1)
                    dst = kg[:, WIN + c * CH:WIN + (c + 1) * CH] if n % 2 else qg[:, c * CH:(c + 1) * CH]
                    nc.scalar.activation(dst, pr_ps[:, n % 2, :], ACT.Copy).then_inc(S["pr_stored"], 1)
                for t in range(TT):
                    act.wait_ge(S["nmx_ready"], 1)
                    x = nc.scalar.activation(junk[:, t, :], sc[:, t, :], ACT.Exp, scale=float(D) ** -0.5,
                                             bias=nmx[:, t:t + 1], accum_out=tot[:, t:t + 1])
                x.then_inc(S["ex_ready"], 1)
                act.wait_ge(S["inv_ready"], 1)
                act.wait_ge(S["set"], 2)
                nc.scalar.activation(gcol[:], inv[:], ACT.Sigmoid, scale=4.0, bias=two[:]).then_inc(S["g_ready"], 1)

            @block.vector
            def _(dve):
                V = nc.vector
                dve.wait_ge(S["pr_stored"], 2 * NCH)
                V.tensor_copy(kg[:, 0:WIN], kg[:, WIN:WIN + 1].broadcast_to([D, WIN]))
                V.tensor_copy(kg[:, WIN + T:], kg[:, WIN + T - 1:WIN + T].broadcast_to([D, WIN])).then_inc(S["edges"], 1)
                dve.wait_ge(S["loaded"], 64)
                for t in range(TT):
                    dve.wait_ge(S["sc_ready"], t + 1)
                    V.tensor_tensor(sc[:, t, :], sc_ps[:, t % 2, 0:W], band[:], ALU.add).then_inc(S["sc_masked"], 1)
                dve.wait_ge(S["sc_masked"], TT)
                V.reduce_max(mx[:], sc[:], AX_X).then_inc(S["mx_ready"], 1)
                dve.wait_ge(S["mx_ready"], 1)
                V.tensor_scalar(nmx[:], mx[:], -float(D) ** -0.5, None, ALU.mult).then_inc(S["nmx_ready"], 1)
                dve.wait_ge(S["ex_ready"], 1)
                V.reciprocal(inv[:], tot[:]).then_inc(S["inv_ready"], 1)
                dve.wait_ge(S["g_ready"], 1)
                for t in range(TT):
                    if t >= 2:
                        dve.wait_ge(S["out_ready"], t - 1)
                    V.tensor_scalar(diag[t % 2][:], ident[:], gcol[:, t:t + 1], None, ALU.mult).then_inc(S["diag_ready"], 1)
                for c in range(NCH):
                    dve.wait_ge(S["out_ready"], TT)
                    V.tensor_copy(gain[:, c * CH:(c + 1) * CH], g_ps[:, c, :]).then_inc(S["stored"], 1)


def mix(nc, dram, h_red, hidden, gain, h):
    with Scope(nc, "mx") as s:
        w = s.sb("w", [D, D])
        m = s.sb("m", [D, T])
        ps = s.ps("out", [D, NCH, CH])
        S = {n: s.sem(n) for n in "loaded diff scaled mixed out_ready added".split()}
        with nc.Block() as block:
            @block.sync
            def _(sp):
                sp.dma_start(w[:], dram["qnet"]).then_inc(S["loaded"], 16)

            @block.tensor
            def _(pe):
                pe.wait_ge(S["loaded"], 16)
                for c in range(NCH):
                    pe.wait_ge(S["mixed"], c + 1)
                    nc.tensor.matmul(ps[:, c, :], w[:], m[:, c * CH:(c + 1) * CH], start=True, stop=True).then_inc(S["out_ready"], 1)

            @block.vector
            def _(dve):
                V = nc.vector
                for c in range(NCH):
                    cols = slice(c * CH, (c + 1) * CH)
                    V.tensor_tensor(m[:, cols], hidden[:, cols], h_red[:, cols], ALU.subtract).then_inc(S["diff"], 1)
                    dve.wait_ge(S["diff"], c + 1)
                    V.tensor_tensor(m[:, cols], m[:, cols], gain[:, cols], ALU.mult).then_inc(S["scaled"], 1)
                    dve.wait_ge(S["scaled"], c + 1)
                    V.tensor_tensor(m[:, cols], m[:, cols], h_red[:, cols], ALU.add).then_inc(S["mixed"], 1)
                for c in range(NCH):
                    cols = slice(c * CH, (c + 1) * CH)
                    dve.wait_ge(S["out_ready"], c + 1)
                    V.tensor_tensor(h[:, cols], h[:, cols], ps[:, c, :], ALU.add).then_inc(S["added"], 1)


def lay_out_lh(inp):
    a = {k: np.asarray(v) for k, v in inp.items()}
    w_in = a["L1_attn_in_proj_w"]
    DI = NT * D
    by_tile = lambda w: np.ascontiguousarray(w.reshape(NT, D, -1).transpose(2, 0, 1).reshape(w.shape[1], NT * D))
    col = lambda v: np.ascontiguousarray(v.reshape(NT, D).T)
    xp = a["L1_attn_x_proj_w"]
    w_x = np.zeros((D, NT, XD), np.float32)
    for j in range(3):
        w_x[:, :, 32 * j:32 * j + NS] = xp[NS * j:NS * (j + 1)].reshape(NS, NT, D).transpose(2, 1, 0)
    w_dt = np.zeros((XD, NT * D), np.float32)
    w_dt[:NS] = by_tile(a["L1_attn_dt_head_w"])
    w_dt[NS] = 1.0
    pick = np.zeros((3, XD, NS, D), np.float32)
    for n in range(NS):
        for x in range(3):
            pick[x, 32 * (x + 1) + n, n] = 1.0
    sum_k = np.zeros((XD, XD), np.float32)
    sum_k[32:32 + NS] = 1.0
    W = D + 2 * WIN
    off = np.arange(W)[None, :] - np.arange(D)[:, None]
    band = np.where((off >= 0) & (off <= 2 * WIN), 0.0, -1e30).astype(np.float32)
    return {
        "lh_in": np.ascontiguousarray(w_in[:DI].reshape(NT, D, D).transpose(0, 2, 1).reshape(NT * D, D)),
        "lh_z": by_tile(w_in[DI:]), "lh_x": w_x.reshape(D, NT * XD),
        "lh_conv_w": np.ascontiguousarray(a["L1_attn_conv_w"].reshape(NT, D, 3).transpose(1, 0, 2).reshape(D, NT * 3)),
        "lh_conv_b": col(a["L1_attn_conv_b"]), "lh_dt": w_dt,
        "lh_dt_b": col(a["L1_attn_dt_head_b"]), "lh_d": col(a["L1_attn_D_param"]),
        "lh_red": np.ascontiguousarray(a["L1_attn_reduce_w"].reshape(D, NT, D).transpose(2, 1, 0).reshape(D, NT * D)),
        "lh_pick_k": pick[0].reshape(XD, NS * D), "lh_pick_q": pick[1].reshape(XD, NS * D),
        "lh_pick_nk2": pick[2].reshape(XD, NS * D), "lh_sum_k": sum_k,
        "gn_q": np.ascontiguousarray(a["L1_attn_gain_q_w"].T), "gn_k": np.ascontiguousarray(a["L1_attn_gain_k_w"].T),
        "gn_band": band, "qnet": np.ascontiguousarray(a["L1_attn_qnet_w"].T),
    }


def tower(nc, dram, out):
    with Scope(nc, "top") as s:
        h = s.sb("h", [D, T])
        ones_over_d = s.sb("ones_over_d", [D, D])
        norms = s.sb("norms", [D, 6])
        loaded, stored = s.sem("loaded"), s.sem("stored")
        with nc.Block() as block:
            @block.sync
            def _(sp):
                sp.dma_start(ones_over_d[:], dram["ones_over_d"]).then_inc(loaded, 16)
                for n, name in enumerate(("att_gamma", "att_beta", "ln1_w", "ln1_b", "post_w", "post_b")):
                    sp.dma_start(norms[:, n:n + 1], dram[name]).then_inc(loaded, 16)
                sp.wait_ge(loaded, 16 * 7)
        embed(nc, dram["ids"], dram["table"], h)

        with Scope(nc, "l0a") as a:
            xn = a.sb("xn", [D, HT + SLOTS * HT])
            ao = a.sb("ao", [D, HT + T])
            layer_norm(nc, "ln_a", h, xn[:, HT:], ones_over_d, 1e-5)
            attention0(nc, dram, xn, ao)
            layer_norm(nc, "ln_b", ao[:, HT:], h, ones_over_d, 1e-5, gamma=norms[:, 0:1], beta=norms[:, 1:2], add_to=h)

        with Scope(nc, "l0f") as a:
            xn = a.sb("xn", [D, T])
            comb_a, comb_b = a.sb("comb_a", [D, T], BF16), a.sb("comb_b", [D, T], BF16)
            layer_norm(nc, "ln_c", h, xn, ones_over_d, 1e-5)
            router(nc, dram, xn, comb_a, comb_b)
            experts(nc, dram, xn, h, comb_a, comb_b)

        with Scope(nc, "l1a") as a:
            xn = a.sb("xn", [D, T])
            h_red = a.sb("h_red", [D, T])
            layer_norm(nc, "ln_d", h, h_red, ones_over_d, 1e-5)
            layer_norm(nc, "ln_e", h_red, xn, ones_over_d, 1e-6, gamma=norms[:, 2:3], beta=norms[:, 3:4])
            with Scope(nc, "l1s") as b:
                xc = b.sb("xc", [D, NT, T])
                xd = b.sb("xd", [XD, T + CH])
                longhorn_inputs(nc, dram, xn, xc, xd)
                longhorn_scan(nc, dram, xn, xc, xd, h_red)
            gain = a.sb("gain", [D, T])
            hidden = a.sb("hidden", [D, T])
            gains(nc, dram, xn, gain)
            with Scope(nc, "l1t") as b:
                kT, qT = b.sb("kT", [D, T + 9 * MB]), b.sb("qT", [D, T + 8 * MB])
                rows = b.sb("rows", [D, 2, NMB + 2 * QUAD, DH])
                eta = b.sb("eta", [RW, NMB + 2 * QUAD])
                zbar = b.sb("zbar", [D, NMB + 1, DH])
                raw = b.sb("raw", [D, T])
                ttt_project(nc, dram, xn, kT, qT, rows, eta)
                ttt_chain(nc, dram, kT, qT, rows, eta, zbar)
                ttt_finish(nc, dram, rows, zbar, raw)
                layer_norm(nc, "ln_f", raw, hidden, ones_over_d, TTT_EPS, gamma=norms[:, 4:5], beta=norms[:, 5:6])
            mix(nc, dram, h_red, hidden, gain, h)

        with Scope(nc, "l1f") as a:
            xn = a.sb("xn", [D, T + D])
            layer_norm(nc, "ln_g", h, xn, ones_over_d, 1e-5)
            product_keys(nc, dram, xn, h)

        turn_out(nc, dram["ident"], h, out)


def turn_out(nc, ident_dram, h, out):
    with Scope(nc, "out") as s:
        ident = s.sb("ident", [D, D])
        tokens = s.sb("tokens", [D, TT, D])
        ps = s.ps("turn", [D, NCH, CH])
        loaded, turned, copied, stored = (s.sem(n) for n in ("loaded", "turned", "copied", "stored"))
        with nc.Block() as block:
            @block.sync
            def _(sp):
                sp.dma_start(ident[:], ident_dram).then_inc(loaded, 16)
                for c in range(NCH):
                    sp.wait_ge(copied, c + 1)
                    sp.dma_start(out[c * CH:(c + 1) * CH, :].rearrange("(q p) d -> p q d", p=D),
                                 tokens[:, 4 * c:4 * c + 4, :]).then_inc(stored, 16)
                sp.wait_ge(stored, 16 * NCH)

            @block.tensor
            def _(pe):
                pe.wait_ge(loaded, 16)
                for c in range(NCH):
                    for q in range(4):
                        t = 4 * c + q
                        mm = nc.tensor.transpose(ps[:, c, q * D:(q + 1) * D], h[:, t * D:(t + 1) * D], ident[:])
                    mm.then_inc(turned, 1)

            @block.vector
            def _(dve):
                for c in range(NCH):
                    dve.wait_ge(turned, c + 1)
                    nc.vector.tensor_copy(tokens[:, 4 * c:4 * c + 4, :].rearrange("p a b -> p (a b)"),
                                          ps[:, c, :]).then_inc(copied, 1)


def kernel(**inputs):
    import concourse.bacc as _bacc
    from concourse.bass_utils import run_bass_kernel_spmd as _run

    laid_out = {}
    for lay_out in (lay_out_attention, lay_out_moe, lay_out_lh, lay_out_ttt, lay_out_pk):
        laid_out.update(lay_out(inputs))
    nc = _bacc.Bacc("TRN2", target_bir_lowering=False, num_devices=1)
    arrays, dram = {}, {}
    for name, a in laid_out.items():
        arrays[f"in_{name}"] = np.ascontiguousarray(a)
        dram[name] = nc.dram_tensor(f"in_{name}", a.shape, mybir.dt.from_np(a.dtype), kind="ExternalInput").ap()
    out = nc.dram_tensor("out_0", (T, D), F32, kind="ExternalOutput").ap()
    tower(nc, dram, out)
    r = _run(nc, [arrays], core_ids=[0])
    return r.results[0]["out_0"].reshape(1, T, D)
```

```python
from contextlib import ExitStack
import numpy as np
import concourse.bass as bass
from concourse import mybir

F32 = mybir.dt.float32
BF16 = mybir.dt.bfloat16
I32 = mybir.dt.int32
ACT = mybir.ActivationFunctionType
ALU = mybir.AluOpType
AX_X = mybir.AxisListType.X

T = 2048
D = 128
VOCAB = 64
CH = 512
NCH = T // CH


class Scope:

    def __init__(self, nc, tag):
        self.nc, self.tag, self.stack, self.sems = nc, tag, ExitStack(), []

    def __enter__(self):
        self.stack.__enter__()
        return self

    def __exit__(self, *a):
        if self.sems:
            with self.nc.Block() as block:
                @block.gpsimd
                def _(pool):
                    for sem in self.sems:
                        pool.sem_clear(sem)
        return self.stack.__exit__(*a)

    def sb(self, name, shape, dt=F32):
        return self.stack.enter_context(self.nc.sbuf_tensor(f"{self.tag}_{name}", shape, dt))

    def ps(self, name, shape, dt=F32):
        return self.stack.enter_context(self.nc.psum_tensor(f"{self.tag}_{name}_ps", shape, dt))

    def sem(self, name):
        self.sems.append(self.stack.enter_context(self.nc.semaphore(f"{self.tag}_{name}")))
        return self.sems[-1]


def layer_norm(nc, tag, src, dst, ones_over_d, eps, gamma=None, beta=None, add_to=None):
    HALF = CH // 2
    with Scope(nc, tag) as s:
        centred = s.sb("centred", [D, NCH, CH])
        squared = s.sb("squared", [D, NCH, CH])
        std, rstd = s.sb("std", [D, CH]), s.sb("rstd", [D, CH])
        eps_col = s.sb("eps", [D, 1])
        spread = s.sb("spread", [D, NCH, D])
        mean_ps = s.ps("mean", [D, NCH, CH])
        var_ps = s.ps("var", [D, CH])
        (const_set, mean_ready, centred_ready, squared_ready, var_ready, std_ready, rstd_ready, spread_ready,
         scaled_ready, done) = (
            s.sem(n) for n in ("const_set", "mean_ready", "centred_ready", "squared_ready", "var_ready",
                               "std_ready", "rstd_ready", "spread_ready", "scaled_ready", "done"))
        cols = lambda c: slice(c * CH, (c + 1) * CH)
        half = lambda k: slice(k * HALF, (k + 1) * HALF)
        pair = lambda k: slice(2 * k, 2 * k + 2)
        by_chunk = lambda x: x[:, 0:T].rearrange("p (c t) -> p c t", t=CH)
        with nc.Block() as block:
            @block.gpsimd
            def _(pool):
                pool.memset(eps_col[:], eps).then_inc(const_set, 1)
                pool.memset(spread[:], 0.0).then_inc(const_set, 1)
                pool.wait_ge(const_set, 2)
                for c in range(NCH):
                    pool.memset(spread[32 * c:32 * c + 32, c, :], 1.0 / 32).then_inc(const_set, 1)

            @block.tensor
            def _(pe):
                for c in range(NCH):
                    nc.tensor.matmul(mean_ps[:, c, :], ones_over_d[:], src[:, cols(c)],
                                     start=True, stop=True).then_inc(mean_ready, 1)
                for c in range(NCH):
                    pe.wait_ge(squared_ready, c + 1)
                    nc.tensor.matmul(var_ps[32 * c:32 * c + 32, :], ones_over_d[:, 0:32], squared[:, c, :],
                                     start=True, stop=True, skip_group_check=True).then_inc(var_ready, 1)
                pe.wait_ge(const_set, 2 + NCH)
                pe.wait_ge(centred_ready, NCH)
                for k in range(2):
                    pe.wait_ge(rstd_ready, k + 1)
                    for c in range(NCH):
                        mm = nc.tensor.matmul(mean_ps[:, c, half(k)], spread[:, c, :], rstd[:, half(k)],
                                              start=True, stop=True, skip_group_check=True)
                    mm.then_inc(spread_ready, 1)

            @block.scalar
            def _(act):
                act.wait_ge(const_set, 1)
                for c in range(NCH):
                    act.wait_ge(centred_ready, c + 1)
                    nc.scalar.activation(squared[:, c, :], centred[:, c, :], ACT.Square).then_inc(squared_ready, 1)
                act.wait_ge(var_ready, NCH)
                for k in range(2):
                    nc.scalar.activation(std[:, half(k)], var_ps[:, half(k)], ACT.Sqrt,
                                         bias=eps_col[:]).then_inc(std_ready, 1)
                if gamma is not None and add_to is None:
                    for k in range(2):
                        act.wait_ge(scaled_ready, k + 1)
                        nc.scalar.activation(by_chunk(dst)[:, pair(k), :], squared[:, pair(k), :], ACT.Identity,
                                             bias=beta).then_inc(done, 1)

            @block.vector
            def _(dve):
                for c in range(NCH):
                    dve.wait_ge(mean_ready, c + 1)
                    nc.vector.tensor_tensor(centred[:, c, :], src[:, cols(c)], mean_ps[:, c, :],
                                            ALU.subtract).then_inc(centred_ready, 1)
                for k in range(2):
                    dve.wait_ge(std_ready, k + 1)
                    nc.vector.reciprocal(rstd[:, half(k)], std[:, half(k)]).then_inc(rstd_ready, 1)
                dve.wait_ge(spread_ready, 2)
                for k in range(2):
                    if gamma is None:
                        nc.vector.tensor_tensor(by_chunk(dst)[:, pair(k), :], centred[:, pair(k), :],
                                                mean_ps[:, pair(k), :], ALU.mult).then_inc(done, 1)
                    else:
                        nc.vector.scalar_tensor_tensor(out=squared[:, pair(k), :], in0=centred[:, pair(k), :],
                                                       scalar=gamma, in1=mean_ps[:, pair(k), :], op0=ALU.mult,
                                                       op1=ALU.mult).then_inc(scaled_ready, 1)
                if add_to is not None:
                    for k in range(2):
                        dve.wait_ge(scaled_ready, k + 1)
                        nc.vector.scalar_tensor_tensor(out=by_chunk(dst)[:, pair(k), :], in0=squared[:, pair(k), :],
                                                       scalar=beta, in1=by_chunk(add_to)[:, pair(k), :],
                                                       op0=ALU.add, op1=ALU.add).then_inc(done, 1)


def embed(nc, ids, table, h):
    with Scope(nc, "emb") as s:
        ids_i = s.sb("ids_i", [VOCAB, T], I32)
        ids_f = s.sb("ids_f", [VOCAB, T])
        vocab_i = s.sb("vocab_i", [VOCAB, 1], I32)
        vocab_f = s.sb("vocab_f", [VOCAB, 1])
        onehot = s.sb("onehot", [VOCAB, T])
        table_sb = s.sb("table", [VOCAB, D])
        h_ps = s.ps("h", [D, NCH, CH])
        loaded, vocab_set, cast, onehot_ready, h_ready, done = (
            s.sem(n) for n in ("loaded", "vocab_set", "cast", "onehot_ready", "h_ready", "done"))
        with nc.Block() as block:
            @block.sync
            def _(sp):
                sp.dma_start(ids_i[:], ids.partition_broadcast(VOCAB)).then_inc(loaded, 16)
                sp.dma_start(table_sb[:], table).then_inc(loaded, 16)

            @block.gpsimd
            def _(pool):
                pool.iota(vocab_i[:], pattern=[[0, 1]], base=0, channel_multiplier=1).then_inc(vocab_set, 1)

            @block.vector
            def _(dve):
                dve.wait_ge(vocab_set, 1)
                nc.vector.tensor_copy(vocab_f[:], vocab_i[:]).then_inc(cast, 1)
                dve.wait_ge(loaded, 32)
                nc.vector.tensor_copy(ids_f[:], ids_i[:]).then_inc(cast, 1)
                dve.wait_ge(cast, 2)
                nc.vector.tensor_scalar(onehot[:], ids_f[:], vocab_f[:, 0:1], None,
                                        ALU.is_equal).then_inc(onehot_ready, 1)
                for c in range(NCH):
                    dve.wait_ge(h_ready, c + 1)
                    nc.vector.tensor_copy(h[:, c * CH:(c + 1) * CH], h_ps[:, c, :]).then_inc(done, 1)

            @block.tensor
            def _(pe):
                pe.wait_ge(onehot_ready, 1)
                for c in range(NCH):
                    nc.tensor.matmul(h_ps[:, c, :], table_sb[:], onehot[:, c * CH:(c + 1) * CH],
                                     start=True, stop=True).then_inc(h_ready, 1)


HEADS = 8
DH = D // HEADS
HT = T // HEADS
QCH = T // CH
KB = T // D
SPLIT = 6 * DH
MROWS = SPLIT + 2
SLOTS = HEADS + 2
FOLD = 96


def attention0(nc, dram, xn, ao):
    x = xn[:, HT:]
    with Scope(nc, "att") as s:
        wq, wk = s.sb("wq", [D, HEADS * D]), s.sb("wk", [D, HEADS * D])
        bq, bk = s.sb("bq", [D, HEADS]), s.sb("bk", [D, HEADS])
        wv, bv = s.sb("wv", [D, D]), s.sb("bv", [D, D])
        wo, bo = s.sb("wo", [D, D]), s.sb("bo", [D, 1])
        masks = s.sb("masks", [D, 4])
        fold = s.sb("fold", [D, FOLD])
        ident = s.sb("ident", [D, D], BF16)
        ident_f = s.sb("ident_f", [D, D])
        q_all = s.sb("q_all", [D, SLOTS * T], BF16)
        k_all = s.sb("k_all", [D, SLOTS * T], BF16)
        v_all = s.sb("v_all", [D, T // D, HEADS, 2 * DH])
        v_head = s.sb("v_head", [D, 2, HEADS, 2 * DH])
        t0, t1 = s.sb("t0", [D, 2, CH]), s.sb("t1", [D, 2, CH])
        part1, part2 = s.sb("part1", [D, 2, CH], BF16), s.sb("part2", [D, 2, CH], BF16)
        half_max = s.sb("half_max", [D, KB, 2])
        neg_max = s.sb("neg_max", [D, KB])
        neg_parts = s.sb("neg_parts", [D, KB, 2], BF16)
        probs = s.sb("probs", [D, 8, CH])
        acc_sb = s.sb("acc_sb", [D, CH])
        rsum = s.sb("rsum", [D, 4])
        ctx_q = s.sb("ctx_q", [D, 2, HEADS, DH])
        ctx = s.sb("ctx", [D, HT])
        st_ps = s.ps("st", [D, 2, CH])
        s1_ps = s.ps("s1", [D, 2, 2 * CH])
        acc_ps = s.ps("acc", [D, CH])
        misc_ps = s.ps("misc", [D, CH])
        fold_ps = misc_ps[:, 0:4 * FOLD].rearrange("p (b f) -> p b f", f=FOLD)
        names = ("loaded ones_set v_ready v_stored consts_set proj_ready part1_ready t1_ready part2_ready "
                 "stacked s1_ready half_done neg_ready parts_ready mt_ready mrows_ready st_ready "
                 "exp_done pv_done acc_stored fold_ready rsum_ready ctx_q_ready turned ctx_ready out_ready "
                 "out_stored v_head_ready pool_passed").split()
        S = {n: s.sem(n) for n in names}
        groups = [(w, b, a, g) for w, b, a in ((wq, bq, q_all), (wk, bk, k_all)) for g in range(4)]
        NG = len(groups)
        UNITS = QCH * KB
        HALVES = 2 * KB
        LOADED = 11 * 16

        ROUND = UNITS + 3
        pv_step = {2 * j + 4: j for j in range(UNITS // 2)}
        MAX1_STEP, LAST_FOLD_STEP, TURN_STEP, OUT_STEP, MAX0_STEP = 2, 4, 7, 10, 49
        fold_step = {KB * q + 21: q for q in range(QCH - 1)}
        proj_step = {13: 0, 17: 1, 24: 2, 28: 3, 32: 4, 41: 5, 45: 6, 57: 7}
        after_fold = {24: 0, 41: 1, 57: 2}

        with nc.Block() as block:
            @block.sync
            def _(sp):
                for dst, src in ((wq, "att_wq"), (wk, "att_wk"), (bq, "att_bq"), (bk, "att_bk"), (wv, "att_wv"),
                                 (wo, "att_wo"), (masks, "att_masks"), (fold, "att_fold"), (ident_f, "ident")):
                    sp.dma_start(dst[:], dram[src]).then_inc(S["loaded"], 16)
                sp.dma_start(bv[:], dram["att_bv"].partition_broadcast(D)).then_inc(S["loaded"], 16)
                sp.dma_start(bo[:], dram["att_bo"]).then_inc(S["loaded"], 16)

            @block.gpsimd
            def _(pool):
                nc.gpsimd.memset(xn[:, 0:HT], 0.0).then_inc(S["consts_set"], 1)
                nc.gpsimd.memset(x[:, T:], 0.0).then_inc(S["consts_set"], 1)
                nc.gpsimd.memset(v_all[:, :, :, DH:], 1.0).then_inc(S["consts_set"], 1)
                nc.gpsimd.memset(acc_sb[:], 1.0).then_inc(S["consts_set"], 1)
                nc.gpsimd.memset(ctx_q[:].rearrange("p a b c -> p (a b c)"), 1.0).then_inc(S["consts_set"], 1)
                pool.wait_ge(S["consts_set"], 5)
                nc.gpsimd.memset(k_all[SPLIT:MROWS, 0:T], 1.0).then_inc(S["ones_set"], 1)
                pool.wait_ge(S["ones_set"], 1)
                pool.wait_ge(S["loaded"], LOADED)
                nc.gpsimd.tensor_copy(ident[:], ident_f[:]).then_inc(S["consts_set"], 1)

                def second_part(n, g):
                    pool.wait_ge(S["t1_ready"], n + 3)
                    pool.wait_ge(S["stacked"], n + 1)
                    pool.sem_inc(S["pool_passed"], 1)
                    nc.gpsimd.tensor_copy(part2[:, g % 2, :], t1[:, g % 2, :]).then_inc(S["part2_ready"], 1)

                for n in range(2 * NG):
                    second_part(n, n % NG)
                pool.wait_ge(S["part2_ready"], 2 * NG)
                nc.gpsimd.memset(k_all[SPLIT:MROWS, T:], 1.0).then_inc(S["ones_set"], 1)
                pool.wait_ge(S["ones_set"], 2)
                pool.wait_ge(S["v_stored"], T // D)
                with pool.Fori(0, HEADS) as h:
                    pool.wait_ge(S["pv_done"], h * (UNITS // 2) + 1)
                    pool.sem_inc(S["pool_passed"], 1)
                    nc.gpsimd.tensor_copy(v_head[:].rearrange("p a b c -> p (a b c)"),
                                          v_all[:, bass.ds(h * 2, 2), :, :].rearrange("p a b c -> p (a b c)")
                                          ).then_inc(S["v_head_ready"], 1)
                    for g in range(NG):
                        second_part(h * NG + (2 * NG + g), g)

            @block.tensor
            def _(pe):
                pe.sem_inc(S["pv_done"], 1)
                pe.sem_inc(S["fold_ready"], 1)
                pe.sem_inc(S["turned"], 1)
                pe.sem_inc(S["out_ready"], 1)
                pe.sem_inc(S["mt_ready"], 1)
                pe.wait_ge(S["loaded"], LOADED)
                for t in range(T // D):
                    if t >= 2:
                        pe.wait_ge(S["v_stored"], t - 1)
                    nc.tensor.matmul(st_ps[:, t % 2, 0:D], x[:, t * D:(t + 1) * D], wv[:],
                                     start=True, stop=True).then_inc(S["v_ready"], 1)

                def project(H, g):
                    w, b, a, c2 = groups[g]
                    for c in (2 * c2, 2 * c2 + 1):
                        mm = nc.tensor.matmul(misc_ps[:, (c % 2) * HT:(c % 2 + 1) * HT], w[:, c * D:(c + 1) * D],
                                              x[:, bass.ds(H * HT, HT)], start=(c % 2 == 0), stop=(c % 2 == 1),
                                              skip_group_check=True)
                    mm.then_inc(S["proj_ready"], 1)

                def first_pass(H, hh):
                    qt, half = hh // 2, hh % 2
                    pe.wait_ge(S["half_done"], H * HALVES + hh + 1)
                    if hh == 0:
                        pe.wait_ge(S["stacked"], H * NG + NG + 2)
                    for j in range(2):
                        mm = nc.tensor.matmul(s1_ps[:, hh % 2, j * CH:(j + 1) * CH],
                                              q_all[0:SPLIT, bass.ds(H * T + qt * D, D)],
                                              k_all[0:SPLIT, bass.ds(H * T + (2 * half + j) * CH, CH)],
                                              start=True, stop=True)
                    mm.then_inc(S["s1_ready"], 1)

                def max_rows(r, n):
                    pe.wait_ge(S["parts_ready"], n + 1)
                    for q in range(8):
                        mm = nc.tensor.transpose(misc_ps[:].bitcast(BF16)[0:2, q * D:(q + 1) * D],
                                                 neg_parts[:, 8 * r + q, :], ident[:])
                    mm.then_inc(S["mt_ready"], 1)

                def fold_groups():
                    for b in range(4):
                        mm = nc.tensor.matmul(fold_ps[:, b, :], acc_sb[:, b * D:(b + 1) * D], fold[:],
                                              start=(b == 0), stop=(b == 3), skip_group_check=True)
                    mm.then_inc(S["fold_ready"], 1)

                def turn_context(H1):
                    pe.wait_ge(S["ctx_q_ready"], H1 * QCH + 2)
                    for half in range(2):
                        mm = nc.tensor.transpose(misc_ps[:, half * D:(half + 1) * D],
                                                 ctx_q[:, half].rearrange("p c e -> p (c e)"), ident_f[:])
                    mm.then_inc(S["turned"], 1)

                def project_out(H1):
                    pe.wait_ge(S["ctx_ready"], H1 + 1)
                    nc.tensor.matmul(misc_ps[:, 0:HT], wo[:], ctx[:], start=True,
                                     stop=True).then_inc(S["out_ready"], 1)

                pe.wait_ge(S["v_stored"], T // D)
                for n in range(2 * NG):
                    if n:
                        pe.wait_ge(S["part1_ready"], n)
                    project(n // NG, n % NG)
                for hh in range(HALVES):
                    first_pass(0, hh)
                pe.wait_ge(S["part1_ready"], 2 * NG)
                max_rows(0, 0)
                pe.wait_ge(S["ones_set"], 2)

                with pe.Fori(0, HEADS) as h:
                    for u in range(ROUND):
                        if u < UNITS:
                            q, kb = u // KB, u % KB
                            pe.wait_ge(S["exp_done"], h * UNITS + u + 1)
                            if u % (UNITS // 2) == 0:
                                pe.wait_ge(S["mrows_ready"], 2 * h + (1 + u // (UNITS // 2)))
                            nc.tensor.matmul(st_ps[:, u % 2, :], k_all[0:MROWS, bass.ds(h * T + kb * D, D)],
                                             q_all[0:MROWS, bass.ds(h * T + q * CH, CH)],
                                             start=True, stop=True).then_inc(S["st_ready"], 1)
                        if u in pv_step:
                            j = pv_step[u]
                            q = j // (KB // 2)
                            if j == 0:
                                pe.wait_ge(S["v_head_ready"], h + 1)
                            if j % (KB // 2) == 0:
                                pe.wait_ge(S["acc_stored"], h * QCH + (q + 1))
                            pe.wait_ge(S["exp_done"], h * UNITS + (2 * j + 4))
                            for y in range(2):
                                kb = 2 * (j % (KB // 2)) + y
                                g = kb % 4
                                mm = nc.tensor.matmul(acc_ps[32 * g:32 * g + 32, :], v_head[:, kb % 2, kb // 2, :],
                                                      probs[:, (2 * j + y) % 8, :], start=(kb < 4),
                                                      stop=(kb >= KB - 4), skip_group_check=True)
                            mm.then_inc(S["pv_done"], 1)
                        if u % 2 == 1 and u // 2 < HALVES:
                            first_pass(h + 1, u // 2)
                        if u == MAX1_STEP:
                            pe.wait_ge(S["mrows_ready"], 2 * h + 1)
                            pe.wait_ge(S["part1_ready"], h * NG + 2 * NG)
                            max_rows(1, 2 * h + 1)
                        if u == LAST_FOLD_STEP:
                            pe.wait_ge(S["mrows_ready"], 2 * h + 2)
                            pe.wait_ge(S["acc_stored"], h * QCH + 1)
                            fold_groups()
                        if u == TURN_STEP:
                            turn_context(h)
                        if u == OUT_STEP:
                            project_out(h)
                        if u in proj_step:
                            g = proj_step[u]
                            if g == 0:
                                pe.wait_ge(S["out_stored"], h + 1)
                            elif u in after_fold:
                                pe.wait_ge(S["ctx_q_ready"], h * QCH + (after_fold[u] + 3))
                            else:
                                pe.wait_ge(S["part1_ready"], h * NG + (2 * NG + g))
                            project(h + 2, g)
                        if u in fold_step:
                            q = fold_step[u]
                            pe.wait_ge(S["acc_stored"], h * QCH + (q + 2))
                            pe.wait_ge(S["part1_ready"], h * NG + (2 * NG + {0: 2, 1: 5, 2: 7}[q]))
                            if q == 2:
                                pe.wait_ge(S["mrows_ready"], 2 * h + 3)
                            fold_groups()
                        if u == MAX0_STEP:
                            pe.wait_ge(S["part1_ready"], h * NG + (3 * NG - 1))
                            max_rows(0, 2 * h + 2)
                pe.wait_ge(S["part1_ready"], (HEADS + 2) * NG)
                pe.wait_ge(S["acc_stored"], HEADS * QCH + 1)
                fold_groups()
                turn_context(HEADS)
                project_out(HEADS)

            @block.scalar
            def _(act):
                act.sem_inc(S["exp_done"], 2)
                act.sem_inc(S["acc_stored"], 1)
                act.wait_ge(S["loaded"], LOADED)

                def store_projection(n, g, dst):
                    w, b, a, c2 = groups[g]
                    if dst is t0:
                        act.wait_ge(S["proj_ready"], n + 1)
                        act.wait_ge(S["t1_ready"], n + 1)
                    for c in (2 * c2, 2 * c2 + 1):
                        half = slice((c % 2) * HT, (c % 2 + 1) * HT)
                        a_ = nc.scalar.activation(dst[:, g % 2, half], misc_ps[:, half], ACT.Identity,
                                                  bias=b[:, c:c + 1])
                    if dst is part1:
                        a_.then_inc(S["part1_ready"], 1)

                def store_rows(H, r, n):
                    act.wait_ge(S["mt_ready"], n + 2)
                    nc.scalar.activation(q_all[SPLIT:MROWS, bass.ds(H * T + r * 1024, 1024)],
                                         misc_ps[:].bitcast(BF16)[0:2, :], ACT.Copy).then_inc(S["mrows_ready"], 1)

                def store_context(H1):
                    act.wait_ge(S["turned"], H1 + 2)
                    act.wait_ge(S["out_ready"], H1 + 1)
                    nc.scalar.activation(ctx[:], misc_ps[:, 0:HT], ACT.Copy).then_inc(S["ctx_ready"], 1)

                for n in range(2 * NG):
                    for dst in (t0, part1):
                        store_projection(n, n % NG, dst)
                store_rows(0, 0, 0)
                with act.Fori(0, HEADS) as h:
                    for u in range(ROUND):
                        if u < UNITS:
                            act.wait_ge(S["st_ready"], h * UNITS + (u + 1))
                            if u % 2 == 0:
                                act.wait_ge(S["pv_done"], h * (UNITS // 2) + max(u // 2 - 2, 1))
                            nc.scalar.activation(probs[:, u % 8, :], st_ps[:, u % 2, :], ACT.Exp,
                                                 scale=float(DH) ** -0.5).then_inc(S["exp_done"], 1)
                        if u >= KB and u % KB == 2:
                            q = u // KB - 1
                            act.wait_ge(S["pv_done"], h * (UNITS // 2) + (KB // 2 * (q + 1) + 1))
                            act.wait_ge(S["fold_ready"], h * QCH + (q + 2))
                            nc.scalar.activation(acc_sb[:], acc_ps[:], ACT.Copy).then_inc(S["acc_stored"], 1)
                        for late, dst in ((1, t0), (2, part1)):
                            if u - late in proj_step:
                                g = proj_step[u - late]
                                store_projection(h * NG + (2 * NG + g), g, dst)
                        if u - 1 == MAX1_STEP:
                            store_rows(h, 1, 2 * h + 1)
                        if u - 1 == MAX0_STEP:
                            store_rows(h + 1, 0, 2 * h + 2)
                        if u - 1 == TURN_STEP:
                            store_context(h)
                store_context(HEADS)

            @block.vector
            def _(dve):
                dve.sem_inc(S["t1_ready"], 2)
                dve.sem_inc(S["stacked"], 2)
                dve.sem_inc(S["half_done"], 2)
                dve.sem_inc(S["ctx_q_ready"], 1)
                dve.wait_ge(S["loaded"], LOADED)
                dve.wait_ge(S["consts_set"], 6)
                for t in range(T // D):
                    dve.wait_ge(S["v_ready"], t + 1)
                    nc.vector.tensor_tensor(v_all[:, t, :, 0:DH], st_ps[:, t % 2, 0:D].rearrange("p (c d) -> p c d", d=DH),
                                            bv[:].rearrange("p (c d) -> p c d", d=DH), ALU.add).then_inc(S["v_stored"], 1)

                def remainder(n, g):
                    b, col = g % 2, 2 * (g // 4)
                    dve.wait_ge(S["part1_ready"], n + 1)
                    dve.wait_ge(S["stacked"], n + 1)
                    nc.vector.scalar_tensor_tensor(out=t1[:, b, :], in0=part1[:, b, :], scalar=masks[:, col:col + 1],
                                                   in1=t0[:, b, :], op0=ALU.mult, op1=ALU.add).then_inc(S["t1_ready"], 1)

                def stack(H, n, g):
                    w, bb, a, c2 = groups[g]
                    b, col = g % 2, 2 * (g // 4) + 1
                    dve.wait_ge(S["part2_ready"], n + 1)
                    dve.wait_ge(S["t1_ready"], n + 3)
                    nc.vector.scalar_tensor_tensor(out=a[0:SPLIT, bass.ds(H * T + c2 * CH, CH)], in0=part2[0:SPLIT, b, :],
                                                   scalar=masks[0:SPLIT, col:col + 1],
                                                   in1=t1[0:SPLIT, b, :], op0=ALU.mult, op1=ALU.add).then_inc(S["stacked"], 1)

                def half_max_of(H, hh):
                    dve.wait_ge(S["s1_ready"], H * HALVES + hh + 1)
                    nc.vector.reduce_max(half_max[:, hh // 2, hh % 2:hh % 2 + 1], s1_ps[:, hh % 2, :],
                                         AX_X).then_inc(S["half_done"], 1)

                def negative_maxima(H, r, n):
                    tiles = slice(8 * r, 8 * r + 8)
                    dve.wait_ge(S["half_done"], H * HALVES + (16 * r + 18))
                    nc.vector.tensor_reduce(neg_max[:, tiles], half_max[:, tiles, :], AX_X, ALU.max,
                                            negate=True).then_inc(S["neg_ready"], 1)
                    dve.wait_ge(S["neg_ready"], 2 * n + 1)
                    nc.vector.tensor_copy(neg_parts[:, tiles, 0], neg_max[:, tiles]).then_inc(S["neg_ready"], 1)
                    dve.wait_ge(S["neg_ready"], 2 * n + 2)
                    nc.vector.tensor_tensor(neg_parts[:, tiles, 1], neg_max[:, tiles], neg_parts[:, tiles, 0],
                                            ALU.subtract).then_inc(S["parts_ready"], 1)

                def divide(n, q):
                    dve.wait_ge(S["fold_ready"], n + 2)
                    nc.vector.reciprocal(rsum[:], fold_ps[:, :, DH]).then_inc(S["rsum_ready"], 1)
                    dve.wait_ge(S["rsum_ready"], n + 1)
                    nc.vector.tensor_tensor(ctx_q[:].rearrange("p half c e -> p c half e")[:, 2 * q:2 * q + 2],
                                            fold_ps.rearrange("p (c half) f -> p c half f", half=2)[:, :, :, 0:DH],
                                            rsum[:].rearrange("p (c half) -> p c half", half=2)
                                            .unsqueeze(3).broadcast_to([D, 2, 2, DH]), ALU.mult).then_inc(S["ctx_q_ready"], 1)

                def add_residual(H1):
                    dve.wait_ge(S["out_ready"], H1 + 2)
                    nc.vector.scalar_tensor_tensor(out=ao[:, bass.ds(H1 * HT, HT)], in0=misc_ps[:, 0:HT],
                                                   scalar=bo[:], in1=xn[:, bass.ds(H1 * HT, HT)], op0=ALU.add,
                                                   op1=ALU.add).then_inc(S["out_stored"], 1)

                for n in range(2 * NG):
                    remainder(n, n % NG)
                    stack(n // NG, n, n % NG)
                for hh in range(HALVES):
                    half_max_of(0, hh)
                negative_maxima(0, 0, 0)
                with dve.Fori(0, HEADS) as h:
                    for u in range(ROUND):
                        if u == 0:
                            dve.wait_ge(S["mt_ready"], 2 * h + 1)
                            negative_maxima(h, 1, 2 * h + 1)
                        if u == LAST_FOLD_STEP + 1:
                            divide(h * QCH, QCH - 1)
                        if u - 1 in fold_step:
                            q = fold_step[u - 1]
                            if q == 0:
                                dve.wait_ge(S["turned"], h + 2)
                            divide(h * QCH + (q + 1), q)
                        if u == OUT_STEP + 1:
                            add_residual(h)
                        if u % 2 == 1 and u // 2 < HALVES:
                            half_max_of(h + 1, u // 2)
                        if u - 4 in proj_step:
                            g = proj_step[u - 4]
                            remainder(h * NG + (2 * NG + g), g)
                        if u - 7 in proj_step:
                            g = proj_step[u - 7]
                            stack(h + 2, h * NG + (2 * NG + g), g)
                        if u == HALVES + 4:
                            dve.wait_ge(S["mt_ready"], 2 * h + 2)
                            negative_maxima(h + 1, 0, 2 * h + 2)
                divide(HEADS * QCH, QCH - 1)
                add_residual(HEADS)


def lay_out_attention(inp):
    a = {k: np.asarray(v) for k, v in inp.items()}
    rep = lambda w: np.ascontiguousarray(
        np.broadcast_to(w.T.reshape(D, HEADS, 1, DH), (D, HEADS, 8, DH)).reshape(D, HEADS * D))
    repb = lambda b: np.ascontiguousarray(
        np.broadcast_to(b.reshape(HEADS, 1, DH), (HEADS, 8, DH)).reshape(HEADS, D).T)
    masks = np.zeros((D, 4), np.float32)
    for col, parts in ((0, (1, 1, 2, 2, 1, 3)), (2, (1, 2, 1, 2, 3, 1))):
        for g, p in enumerate(parts):
            masks[16 * g:16 * g + 16, col] = -1.0 if p >= 2 else 0.0
            masks[16 * g:16 * g + 16, col + 1] = -1.0 if p == 3 else 0.0
    fold = np.tile(np.eye(2 * DH, dtype=np.float32), (D // (2 * DH), FOLD // (2 * DH)))
    return {
        "ids": a["x"].astype(np.int32).reshape(T),
        "table": a["L0_tok_weights"],
        "att_wq": rep(a["L0_attn_Wq"]), "att_wk": rep(a["L0_attn_Wk"]),
        "att_bq": repb(a["L0_attn_bq"]), "att_bk": repb(a["L0_attn_bk"]),
        "att_wv": np.ascontiguousarray(a["L0_attn_Wv"].T), "att_bv": a["L0_attn_bv"],
        "att_wo": np.ascontiguousarray(a["L0_attn_Wo"].T),
        "att_bo": a["L0_attn_bo"].reshape(D, 1),
        "att_gamma": a["L0_attn_gamma"].reshape(D, 1), "att_beta": a["L0_attn_beta"].reshape(D, 1),
        "att_masks": masks, "att_fold": fold, "ident": np.eye(D, dtype=np.float32),
        "ones_over_d": np.full((D, D), 1.0 / D, np.float32),
    }


EXPERTS = 64
INTER = 64
PAIRS = EXPERTS // 2
TOP_K = 6
BIG = 3.0e38
TT = T // D


def router(nc, dram, xn, comb_a, comb_b):
    with Scope(nc, "rt") as s:
        w_gate = s.sb("w_gate", [D, EXPERTS])
        ident = s.sb("ident", [D, D])
        row_masks = s.sb("row_masks", [D, 2])
        score = s.sb("score", [D, TT, EXPERTS])
        left = s.sb("left", [D, TT, EXPERTS])
        chosen = s.sb("chosen", [D, TT, EXPERTS])
        weight = s.sb("weight", [D, TT, EXPERTS])
        twice = s.sb("twice", [D, TT, 2, EXPERTS])
        top = s.sb("top", [D, TT, 8])
        best = s.sb("best", [D, TT, 1])
        total = s.sb("total", [D, TT])
        rest = s.sb("rest", [D, T])
        rest2 = s.sb("rest2", [D, T])
        part = s.sb("part", [D, T], BF16)
        score_ps = s.ps("score", [D, TT, EXPERTS])
        comb_ps = s.ps("comb", [D, NCH, CH])
        S = {n: s.sem(n) for n in ("loaded scores_ready stored top_ready cut left_ready shifted exp_ready "
                                   "chosen_ready masked total_ready inverse_ready weight_ready turned part_ready "
                                   "rest_ready a_ready rest2_ready b_ready").split()}
        wide = lambda ap: ap.broadcast_to([D, TT, EXPERTS])
        with nc.Block() as block:
            @block.sync
            def _(sp):
                for dst, src in ((w_gate, "rt_gate"), (ident, "ident"), (row_masks, "rt_masks")):
                    sp.dma_start(dst[:], dram[src]).then_inc(S["loaded"], 16)

            @block.tensor
            def _(pe):
                pe.wait_ge(S["loaded"], 48)
                for t in range(TT):
                    mm = nc.tensor.matmul(score_ps[:, t, :], xn[:, t * D:(t + 1) * D], w_gate[:],
                                          start=(t % 8 == 0), stop=(t % 8 == 7), skip_group_check=True)
                mm.then_inc(S["scores_ready"], 1)
                pe.wait_ge(S["weight_ready"], 2)
                for t in range(TT):
                    nc.tensor.transpose(comb_ps[:, t // 4, (t % 4) * D:(t % 4 + 1) * D],
                                        twice[:, t, :, :].rearrange("p a e -> p (a e)"),
                                        ident[:]).then_inc(S["turned"], 1)

            @block.scalar
            def _(act):
                act.wait_ge(S["shifted"], 1)
                nc.scalar.activation(weight[:], weight[:], ACT.Exp).then_inc(S["exp_ready"], 1)
                for c in range(NCH):
                    act.wait_ge(S["turned"], 4 * c + 4)
                    cols = slice(c * CH, (c + 1) * CH)
                    nc.scalar.activation(part[:, cols], comb_ps[:, c, :], ACT.Copy).then_inc(S["part_ready"], 1)
                for c in range(NCH):
                    cols = slice(c * CH, (c + 1) * CH)
                    act.wait_ge(S["rest_ready"], c + 1)
                    nc.scalar.activation(comb_a[:, cols], rest[:, cols], ACT.Copy).then_inc(S["a_ready"], 1)

            @block.vector
            def _(dve):
                dve.wait_ge(S["scores_ready"], 1)
                nc.vector.tensor_copy(score[:], score_ps[:]).then_inc(S["stored"], 1)
                dve.wait_ge(S["stored"], 1)
                for t in range(TT):
                    mx = nc.vector.max(top[:, t, :], score[:, t, :])
                mx.then_inc(S["top_ready"], 1)
                dve.wait_ge(S["top_ready"], 1)
                nc.vector.tensor_copy(best[:], top[:, :, 0:1]).then_inc(S["cut"], 1)
                nc.vector.memset(top[:, :, TOP_K:8], BIG).then_inc(S["cut"], 1)
                dve.wait_ge(S["cut"], 2)
                nc.vector.tensor_tensor(weight[:], score[:], wide(best[:]), ALU.subtract).then_inc(S["shifted"], 1)
                for t in range(TT):
                    mr = nc.vector.match_replace(left[:, t, :], top[:, t, :], score[:, t, :], -BIG)
                mr.then_inc(S["left_ready"], 1)
                dve.wait_ge(S["left_ready"], 1)
                nc.vector.tensor_tensor(chosen[:], left[:], score[:], ALU.not_equal).then_inc(S["chosen_ready"], 1)
                dve.wait_ge(S["chosen_ready"], 1)
                dve.wait_ge(S["exp_ready"], 1)
                nc.vector.tensor_tensor(left[:], weight[:], chosen[:], ALU.mult).then_inc(S["masked"], 1)
                dve.wait_ge(S["masked"], 1)
                nc.vector.reduce_sum(total[:], left[:], AX_X).then_inc(S["total_ready"], 1)
                dve.wait_ge(S["total_ready"], 1)
                nc.vector.reciprocal(total[:], total[:]).then_inc(S["inverse_ready"], 1)
                dve.wait_ge(S["inverse_ready"], 1)
                for a in range(2):
                    nc.vector.tensor_tensor(twice[:, :, a, :], left[:], wide(total[:].unsqueeze(2)),
                                            ALU.mult).then_inc(S["weight_ready"], 1)
                for c in range(NCH):
                    cols = slice(c * CH, (c + 1) * CH)
                    dve.wait_ge(S["part_ready"], c + 1)
                    nc.vector.scalar_tensor_tensor(out=rest[:, cols], in0=part[:, cols], scalar=row_masks[:, 0:1],
                                                   in1=comb_ps[:, c, :], op0=ALU.mult,
                                                   op1=ALU.add).then_inc(S["rest_ready"], 1)
                for c in range(NCH):
                    cols = slice(c * CH, (c + 1) * CH)
                    dve.wait_ge(S["a_ready"], c + 1)
                    nc.vector.tensor_tensor(rest2[:, cols], rest[:, cols], comb_a[:, cols],
                                            ALU.subtract).then_inc(S["rest2_ready"], 1)
                    dve.wait_ge(S["rest2_ready"], c + 1)
                    nc.vector.tensor_scalar(comb_b[:, cols], rest2[:, cols], row_masks[:, 1:2], None,
                                            ALU.mult).then_inc(S["b_ready"], 1)


def experts(nc, dram, xn, h, comb_a, comb_b):
    with Scope(nc, "moe") as s:
        shared = s.sb("shared", [D, 2, 3, D])
        w = [s.sb(f"w{b}", [D, 3, D]) for b in range(2)]
        ident = s.sb("ident", [D, EXPERTS])
        pick = s.sb("pick", [D, EXPERTS * INTER], BF16)
        gate = s.sb("gate", [D, 2, CH])
        gated = s.sb("gated", [D, 2, CH])
        hidden = s.sb("hidden", [D, 2, CH])
        x1_ps, x3_ps, cb_ps = s.ps("x1", [D, CH]), s.ps("x3", [D, CH]), s.ps("cb", [D, CH])
        out_ps = s.ps("out", [D, NCH, CH])
        S = {n: s.sem(n) for n in ("loaded pick_ready w_a w_b w_used x1_ready x3_ready cb_ready gate_ready "
                                   "gated_ready hidden_ready out_done stored").split()}
        w_loaded = (S["w_a"], S["w_b"])
        packed = dram["moe_w"]
        with nc.Block() as block:
            @block.sync
            def _(sp):
                sp.dma_start(shared[:].rearrange("p a b d -> p (a b d)"), dram["moe_shared"]).then_inc(S["loaded"], 16)
                sp.dma_start(ident[:], dram["moe_ident"]).then_inc(S["loaded"], 16)
                sp.sem_inc(S["w_used"], 2)
                with sp.Fori(0, PAIRS // 2) as i:
                    for b in range(2):
                        sp.wait_ge(S["w_used"], 2 * i + (b + 1))
                        sp.dma_start(w[b][:].rearrange("p b d -> p (b d)"),
                                     packed[bass.ds((i * 2 + b) * D, D), :]).then_inc(w_loaded[b], 16)

            @block.gpsimd
            def _(pool):
                pool.wait_ge(S["loaded"], 32)
                nc.gpsimd.tensor_copy(pick[:].rearrange("p (e i) -> p e i", i=INTER),
                                      ident[:].unsqueeze(2).broadcast_to([D, EXPERTS, INTER])).then_inc(S["pick_ready"], 1)

            @block.tensor
            def _(pe):
                pe.sem_inc(S["out_done"], 2)
                pe.wait_ge(S["loaded"], 32)

                def item(n, c, wt, pair):
                    cols = slice(c * CH, (c + 1) * CH)
                    pe.wait_ge(S["gate_ready"], n + 1)
                    nc.tensor.matmul(x1_ps[:], wt[:, 0, :], xn[:, cols], start=True, stop=True).then_inc(S["x1_ready"], 1)
                    pe.wait_ge(S["gated_ready"], n + 1)
                    nc.tensor.matmul(x3_ps[:], wt[:, 1, :], xn[:, cols], start=True, stop=True).then_inc(S["x3_ready"], 1)
                    if pair is not None:
                        pe.wait_ge(S["hidden_ready"], n + 1)
                        sel = pick[:, bass.ds(pair * D, D)]
                        nc.tensor.matmul(cb_ps[:], sel, comb_a[:, cols], start=True, stop=False)
                        nc.tensor.matmul(cb_ps[:], sel, comb_b[:, cols], start=False, stop=True).then_inc(S["cb_ready"], 1)

                def down(n, c, b, wt, first):
                    pe.wait_ge(S["hidden_ready"], n + 2)
                    return nc.tensor.matmul(out_ps[:, c, :], wt[:, 2, :], hidden[:, b, :], start=first, stop=True,
                                            skip_group_check=True).then_inc(S["out_done"], 1)

                for n in range(2 * NCH + 1):
                    if n < 2 * NCH:
                        item(n, n % NCH, shared[:, n // NCH], None)
                    if n:
                        st, c = (n - 1) // NCH, (n - 1) % NCH
                        down(n - 1, c, c % 2, shared[:, st], st == 0)
                pe.wait_ge(S["pick_ready"], 1)
                with pe.Fori(0, PAIRS // 2) as i:
                    for b in range(2):
                        pe.wait_ge(w_loaded[b], 16 * i + 16)
                        base = i * (2 * NCH) + (2 + b) * NCH
                        for c in range(NCH):
                            item(base + c, c, w[b], i * 2 + b)
                            if c:
                                down(base + c - 1, c - 1, (c - 1) % 2, w[b], False)
                        down(base + NCH - 1, NCH - 1, (NCH - 1) % 2, w[b], False)
                        pe.wait_ge(S["out_done"], base + NCH + 2)
                        pe.sem_inc(S["w_used"], 1)

            @block.scalar
            def _(act):
                act.sem_inc(S["gate_ready"], 1)

                def gate_of(n, b):
                    act.wait_ge(S["x1_ready"], n + 1)
                    act.wait_ge(S["gated_ready"], n + 1)
                    nc.scalar.activation(gate[:, b, :], x1_ps[:], ACT.Silu).then_inc(S["gate_ready"], 1)
                for n in range(2 * NCH):
                    gate_of(n, n % 2)
                with act.Fori(0, PAIRS) as e:
                    for c in range(NCH):
                        gate_of(e * NCH + (2 * NCH + c), c % 2)

            @block.vector
            def _(dve):
                dve.sem_inc(S["gated_ready"], 1)
                dve.sem_inc(S["hidden_ready"], 1)

                def hide(n, b, cb):
                    dve.wait_ge(S["gate_ready"], n + 2)
                    dve.wait_ge(S["x3_ready"], n + 1)
                    dve.wait_ge(S["out_done"], n + 1)
                    if cb is None:
                        nc.vector.tensor_tensor(hidden[:, b, :], gate[:, b, :], x3_ps[:], ALU.mult).then_inc(S["gated_ready"], 1)
                        dve.wait_ge(S["gated_ready"], n + 2)
                        dve.sem_inc(S["hidden_ready"], 1)
                        return
                    nc.vector.tensor_tensor(gated[:, b, :], gate[:, b, :], x3_ps[:], ALU.mult).then_inc(S["gated_ready"], 1)
                    dve.wait_ge(S["gated_ready"], n + 2)
                    dve.wait_ge(S["cb_ready"], cb)
                    nc.vector.tensor_tensor(hidden[:, b, :], gated[:, b, :], cb_ps[:], ALU.mult).then_inc(S["hidden_ready"], 1)
                for n in range(2 * NCH):
                    hide(n, n % 2, None)
                with dve.Fori(0, PAIRS) as e:
                    for c in range(NCH):
                        hide(e * NCH + (2 * NCH + c), c % 2, e * NCH + (c + 1))
                for c in range(NCH):
                    dve.wait_ge(S["out_done"], (PAIRS + 2) * NCH + 2)
                    cols = slice(c * CH, (c + 1) * CH)
                    nc.vector.tensor_tensor(h[:, cols], h[:, cols], out_ps[:, c, :], ALU.add).then_inc(S["stored"], 1)


def lay_out_moe(inp):
    a = {k: np.asarray(v) for k, v in inp.items()}
    w1, w3, w2 = (a[f"L0_ffn_{n}"].reshape(PAIRS, D, D) for n in ("w1", "w3", "w2"))
    packed = np.stack([w1.transpose(0, 2, 1), w3.transpose(0, 2, 1), w2], axis=2).reshape(PAIRS * D, 3 * D)
    sg, su, sd = a["L0_ffn_w_sg"], a["L0_ffn_w_su"], a["L0_ffn_w_sd"]
    shared = np.stack([np.stack([sg[i * D:(i + 1) * D].T, su[i * D:(i + 1) * D].T, sd[:, i * D:(i + 1) * D].T], 1)
                       for i in range(2)], 1).reshape(D, 6 * D)
    masks = np.zeros((D, 2), np.float32)
    masks[64:, 0] = -1.0
    masks[64:, 1] = 1.0
    eye = np.eye(EXPERTS, dtype=np.float32)
    return {"rt_gate": np.ascontiguousarray(a["L0_ffn_w_gate"].T), "rt_masks": masks,
            "moe_w": np.ascontiguousarray(packed), "moe_shared": np.ascontiguousarray(shared),
            "moe_ident": np.concatenate([eye, eye])}


PK_HEADS = 8
N_KEYS = 64
TOPK = 16
GROUPS = 2 * PK_HEADS
ROWS = [TOPK // (i + 1) for i in range(TOPK)]
SINGLE = ROWS.index(1)
STARTS = [sum(ROWS[:i]) for i in range(TOPK)]
CAND = sum(ROWS)
NSIM = GROUPS * N_KEYS


def product_keys(nc, dram, xn, h):
    with Scope(nc, "pk") as s:
        wq = s.sb("wq", [N_KEYS, GROUPS, D])
        keys = s.sb("keys", [N_KEYS, GROUPS, N_KEYS])
        up = s.sb("up", [CAND, D])
        ident = s.sb("ident", [D, D])
        w = s.sb("w", [D, NSIM + CAND])
        delta = s.sb("delta", [D, TT + 1, D])
        buf = []
        for b in range(2):
            buf.append({n: s.sb(f"{n}{b}", shape) for n, shape in dict(
                xt=[D, D], left=[D, GROUPS, N_KEYS], top=[D, GROUPS, TOPK], cand=[D, PK_HEADS, CAND],
                left2=[D, PK_HEADS, CAND], left3=[D, PK_HEADS, CAND], top2=[D, PK_HEADS, TOPK],
                shifted=[D, PK_HEADS, CAND], chosen=[D, PK_HEADS, CAND], masked=[D, PK_HEADS, CAND],
                total=[D, PK_HEADS], inverse=[D, PK_HEADS], act=[D, CAND], weight=[D, CAND], gw=[D, CAND],
                gwt=[CAND, D]).items()})
            buf[b]["sim"] = s.ps(f"sim{b}", [D, GROUPS, N_KEYS])
        xd_ps = s.ps("xd", [D, 2, CH])
        turn_ps = s.ps("turn", [D, D])
        out_ps = s.ps("out", [D, D])
        S = {n: s.sem(n) for n in ("loaded w_ps_ready w_stored xt_ready sims_ready xd_ready top_a cut_a top1_done "
                                   "cand_ready gelu_ready top_b cut_b top_c cut_c shifted exp_ready chosen masked "
                                   "total inverse scaled weight gw_ready turned gwt_ready out_ready delta_stored "
                                   "zeroed added dve_passed pe_passed").split()}
        flat = lambda ap: ap.rearrange("p a b -> p (a b)")
        with nc.Block() as block:
            @block.sync
            def _(sp):
                for dst, src in ((flat(wq[:]), "pk_wq"), (flat(keys[:]), "pk_keys"), (up[:], "pk_up"),
                                 (ident[:], "ident"), (w[:, NSIM:], "pk_down")):
                    sp.dma_start(dst, dram[src]).then_inc(S["loaded"], 16)

            @block.gpsimd
            def _(pool):
                pool.sem_inc(S["cand_ready"], 2)
                nc.gpsimd.memset(xn[:, T:], 0.0).then_inc(S["zeroed"], 1)
                nc.gpsimd.memset(buf[1]["gwt"][:], 0.0).then_inc(S["zeroed"], 1)

                def candidates(n, b):
                    pool.wait_ge(S["top1_done"], n + 3)
                    pool.wait_ge(S["shifted"], n + 1)
                    pool.wait_ge(S["chosen"], n + 1)
                    top, cand = buf[b]["top"], buf[b]["cand"]
                    for i in range(SINGLE):
                        nc.gpsimd.tensor_tensor(
                            cand[:, :, STARTS[i]:STARTS[i] + ROWS[i]],
                            top[:, 0:PK_HEADS, i:i + 1].broadcast_to([D, PK_HEADS, ROWS[i]]),
                            top[:, PK_HEADS:, 0:ROWS[i]], ALU.add)
                    n1 = TOPK - SINGLE
                    nc.gpsimd.tensor_tensor(cand[:, :, STARTS[SINGLE]:], top[:, 0:PK_HEADS, SINGLE:],
                                            top[:, PK_HEADS:, 0:1].broadcast_to([D, PK_HEADS, n1]),
                                            ALU.add).then_inc(S["cand_ready"], 1)
                candidates(0, 0)
                with pool.Fori(0, TT // 2) as i:
                    for b in range(2):
                        candidates(i * 2 + (b + 1), 1 - b)

            @block.tensor
            def _(pe):
                pe.sem_inc(S["xd_ready"], 2)
                pe.wait_ge(S["loaded"], 80)
                for g in range(GROUPS):
                    mm = nc.tensor.matmul(buf[0]["sim"][:, g, :], wq[:, g, :], keys[:, g, :], start=(g % 8 == 0),
                                          stop=(g % 8 == 7), skip_group_check=True)
                mm.then_inc(S["w_ps_ready"], 1)
                pe.wait_ge(S["w_stored"], 1)
                pe.wait_ge(S["zeroed"], 2)
                nc.tensor.matmul(out_ps[:], up[:], buf[1]["gwt"][:], start=True, stop=True).then_inc(S["out_ready"], 1)

                def sims(n, b):
                    pe.wait_ge(S["xt_ready"], n + 1)
                    pe.wait_ge(S["top1_done"], n + 1)
                    sim = flat(buf[b]["sim"][:])
                    for j in range(2):
                        mm = nc.tensor.matmul(sim[:, j * CH:(j + 1) * CH], buf[b]["xt"][:],
                                              w[:, j * CH:(j + 1) * CH], start=True, stop=True)
                    mm.then_inc(S["sims_ready"], 1)
                    pe.wait_ge(S["gelu_ready"], n + 1)
                    nc.tensor.matmul(xd_ps[:, b, 0:CAND], buf[b]["xt"][:], w[:, NSIM:], start=True, stop=True,
                                     skip_group_check=True).then_inc(S["xd_ready"], 1)
                sims(0, 0)
                with pe.Fori(0, TT // 2) as i:
                    for b in range(2):
                        n = i * 2 + b
                        sims(n + 1, 1 - b)
                        pe.wait_ge(S["gw_ready"], n + 1)
                        pe.sem_inc(S["pe_passed"], 1)
                        nc.tensor.transpose(turn_ps[0:CAND, :], buf[b]["gw"][:], ident[:]).then_inc(S["turned"], 1)
                        pe.wait_ge(S["gwt_ready"], n + 1)
                        pe.wait_ge(S["delta_stored"], n + 1)
                        nc.tensor.matmul(out_ps[:], up[:], buf[b]["gwt"][:], start=True,
                                         stop=True).then_inc(S["out_ready"], 1)

            @block.scalar
            def _(act):
                act.sem_inc(S["gelu_ready"], 2)
                act.wait_ge(S["zeroed"], 2)

                def stage_tile(n, b):
                    act.wait_ge(S["xd_ready"], n + 1)
                    nc.scalar.activation(buf[b]["xt"][:], xn[:, bass.ds(n * D, D)], ACT.Copy).then_inc(S["xt_ready"], 1)
                stage_tile(0, 0)
                with act.Fori(0, TT // 2) as i:
                    for b in range(2):
                        n = i * 2 + b
                        stage_tile(n + 1, 1 - b)
                        act.wait_ge(S["xd_ready"], n + 3)
                        nc.scalar.activation(buf[b]["act"][:], xd_ps[:, b, 0:CAND], ACT.Gelu).then_inc(S["gelu_ready"], 1)
                        act.wait_ge(S["shifted"], n + 3)
                        nc.scalar.activation(buf[b]["shifted"][:], buf[b]["shifted"][:], ACT.Exp).then_inc(S["exp_ready"], 1)
                        act.wait_ge(S["turned"], n + 1)
                        nc.scalar.activation(buf[b]["gwt"][:], turn_ps[0:CAND, :], ACT.Copy).then_inc(S["gwt_ready"], 1)
                act.wait_ge(S["xd_ready"], TT + 3)

            @block.vector
            def _(dve):
                dve.sem_inc(S["top1_done"], 2)
                dve.sem_inc(S["shifted"], 2)
                dve.sem_inc(S["chosen"], 2)
                dve.wait_ge(S["w_ps_ready"], 1)
                nc.vector.tensor_copy(w[:, 0:NSIM], flat(buf[0]["sim"][:])).then_inc(S["w_stored"], 1)

                def rank_keys(n, b):
                    sim, left, top = buf[b]["sim"], buf[b]["left"], buf[b]["top"]
                    dve.wait_ge(S["sims_ready"], n + 1)
                    dve.wait_ge(S["cand_ready"], n + 1)
                    dve.sem_inc(S["dve_passed"], 1)
                    for g in range(GROUPS):
                        x = nc.vector.max(top[:, g, 0:8], sim[:, g, :])
                    x.then_inc(S["top_a"], 1)
                    dve.wait_ge(S["top_a"], n + 1)
                    dve.sem_inc(S["dve_passed"], 1)
                    for g in range(GROUPS):
                        x = nc.vector.match_replace(left[:, g, :], top[:, g, 0:8], sim[:, g, :], -BIG)
                    x.then_inc(S["cut_a"], 1)
                    dve.wait_ge(S["cut_a"], n + 1)
                    dve.sem_inc(S["dve_passed"], 1)
                    for g in range(GROUPS):
                        x = nc.vector.max(top[:, g, 8:16], left[:, g, :])
                    x.then_inc(S["top1_done"], 1)

                def rank_sums(n, b):
                    B = buf[b]
                    dve.wait_ge(S["cand_ready"], n + 3)
                    dve.sem_inc(S["dve_passed"], 1)
                    for g in range(PK_HEADS):
                        x = nc.vector.max(B["top2"][:, g, 0:8], B["cand"][:, g, :])
                    x.then_inc(S["top_b"], 1)
                    dve.wait_ge(S["top_b"], n + 1)
                    nc.vector.tensor_tensor(B["shifted"][:], B["cand"][:],
                                            B["top2"][:, :, 0:1].broadcast_to([D, PK_HEADS, CAND]),
                                            ALU.subtract).then_inc(S["shifted"], 1)
                    dve.sem_inc(S["dve_passed"], 1)
                    for g in range(PK_HEADS):
                        x = nc.vector.match_replace(B["left2"][:, g, :], B["top2"][:, g, 0:8], B["cand"][:, g, :], -BIG)
                    x.then_inc(S["cut_b"], 1)
                    dve.wait_ge(S["cut_b"], n + 1)
                    dve.sem_inc(S["dve_passed"], 1)
                    for g in range(PK_HEADS):
                        x = nc.vector.max(B["top2"][:, g, 8:16], B["left2"][:, g, :])
                    x.then_inc(S["top_c"], 1)
                    dve.wait_ge(S["top_c"], n + 1)
                    dve.sem_inc(S["dve_passed"], 1)
                    for g in range(PK_HEADS):
                        x = nc.vector.match_replace(B["left3"][:, g, :], B["top2"][:, g, 8:16], B["left2"][:, g, :], -BIG)
                    x.then_inc(S["cut_c"], 1)
                    dve.wait_ge(S["cut_c"], n + 1)
                    nc.vector.tensor_tensor(B["chosen"][:], B["left3"][:], B["cand"][:],
                                            ALU.not_equal).then_inc(S["chosen"], 1)

                def store_delta(n):
                    dve.wait_ge(S["out_ready"], n + 1)
                    nc.vector.tensor_copy(delta[:, bass.ds(n, 1), :].rearrange("p a b -> p (a b)"), out_ps[:]).then_inc(S["delta_stored"], 1)

                def weigh(n, b):
                    B = buf[b]
                    dve.wait_ge(S["chosen"], n + 3)
                    dve.wait_ge(S["exp_ready"], n + 1)
                    nc.vector.tensor_tensor(B["masked"][:], B["shifted"][:], B["chosen"][:], ALU.mult).then_inc(S["masked"], 1)
                    dve.wait_ge(S["masked"], n + 1)
                    nc.vector.reduce_sum(B["total"][:], B["masked"][:], AX_X).then_inc(S["total"], 1)
                    dve.wait_ge(S["total"], n + 1)
                    nc.vector.reciprocal(B["inverse"][:], B["total"][:]).then_inc(S["inverse"], 1)
                    dve.wait_ge(S["inverse"], n + 1)
                    nc.vector.tensor_tensor(B["chosen"][:], B["masked"][:],
                                            B["inverse"][:].unsqueeze(2).broadcast_to([D, PK_HEADS, CAND]),
                                            ALU.mult).then_inc(S["scaled"], 1)
                    dve.wait_ge(S["scaled"], n + 1)
                    nc.vector.reduce_sum(B["weight"][:], B["chosen"][:].rearrange("p h c -> p c h"), AX_X).then_inc(S["weight"], 1)
                    dve.wait_ge(S["weight"], n + 1)
                    dve.wait_ge(S["gelu_ready"], n + 3)
                    nc.vector.tensor_tensor(B["gw"][:], B["weight"][:], B["act"][:], ALU.mult).then_inc(S["gw_ready"], 1)

                rank_keys(0, 0)
                with dve.Fori(0, TT // 2) as i:
                    for b in range(2):
                        n = i * 2 + b
                        rank_sums(n, b)
                        store_delta(n)
                        rank_keys(n + 1, 1 - b)
                        weigh(n, b)
                store_delta(TT)
                dve.wait_ge(S["delta_stored"], TT + 1)
                nc.vector.tensor_tensor(h[:], h[:], flat(delta[:, 1:, :]), ALU.add).then_inc(S["added"], 1)


def lay_out_pk(inp):
    a = {k: np.asarray(v) for k, v in inp.items()}
    places = [i * TOPK + j for i in range(TOPK) for j in range(ROWS[i])]
    wq = a["L1_ffn_W_q"].T.reshape(GROUPS, N_KEYS, D).transpose(1, 0, 2).reshape(N_KEYS, GROUPS * D)
    keys = a["L1_ffn_keys"].transpose(3, 2, 0, 1).reshape(N_KEYS, GROUPS * N_KEYS)
    return {"pk_wq": np.ascontiguousarray(wq), "pk_keys": np.ascontiguousarray(keys),
            "pk_down": np.ascontiguousarray(a["L1_ffn_down_embed"][places].T),
            "pk_up": np.ascontiguousarray(a["L1_ffn_up_embed"][places])}


MB = 8
NMB = T // MB
RW = MB * HEADS
QUAD = 4
EXT = DH + 1
TTT_EPS = 1e-6


def fetch_rows(sp, turned, rows, written, rows_read):
    for x in written:
        sp.wait_ge(x, 16 * 2 * NCH // 2)
    for a in (1, 0):
        sp.dma_start(rows[:, a, 0:NMB], turned[a].rearrange("(n m) (h e) -> (m h) n e", m=MB, e=DH)).then_inc(rows_read, 16)


def ttt_project(nc, dram, xn, kT, qT, eta, turned, written):
    with Scope(nc, "tp") as s:
        wk, wkp, wq, wqp, wv = (s.sb(n, [D, D]) for n in ("wk", "wkp", "wq", "wqp", "wv"))
        cos, sin = s.sb("cos", [D, T]), s.sb("sin", [D, T])
        lr_w, lr_b = s.sb("lr_w", [D, MB, RW]), s.sb("lr_b", [RW, 1])
        ident = s.sb("ident", [D, D])
        kv, cc = s.sb("kv", [D, T]), s.sb("cc", [D, T])
        g, bn = s.sb("g", [D, 1]), s.sb("bn", [D, 1])
        centre = s.sb("centre", [D, D])
        ca, sa = s.sb("ca", [D, 2, CH]), s.sb("sa", [D, 2, CH])
        token = s.sb("token", [D, 2, CH])
        pr = [s.ps(f"pr{j}", [D, CH]) for j in range(5)]
        lr_ps = s.ps("lr", [RW, NMB])
        turn_ps = s.ps("turn", [D, 2, CH])
        S = {n: s.sem(n) for n in ("loaded projected cos_done sin_done rotated kv_done lr_ready lr_stored "
                                   "turned token_ready halved target_done cc_ready cc_stored").split()}
        cols = lambda c: slice(c * CH, (c + 1) * CH)
        weights = (wk, wkp, wq, wqp, wv)
        turns = [(a, c) for a in (1, 0) for c in range(NCH)]
        with nc.Block() as block:
            @block.sync
            def _(sp):
                for dst, src in zip(weights, ("ttt_wk", "ttt_wkp", "ttt_wq", "ttt_wqp", "ttt_wv")):
                    sp.dma_start(dst[:], dram[src]).then_inc(S["loaded"], 16)
                for dst, src in ((cos, "cos"), (sin, "sin"), (lr_b, "ttt_lrb"), (ident, "ident")):
                    sp.dma_start(dst[:], dram[src]).then_inc(S["loaded"], 16)
                sp.dma_start(lr_w[:].rearrange("p a b -> p (a b)"), dram["ttt_lrw"]).then_inc(S["loaded"], 16)
                for dst, src in ((g, "ttt_g_col"), (bn, "ttt_b_col"), (centre, "ttt_centre")):
                    sp.dma_start(dst[:], dram[src]).then_inc(S["loaded"], 16)
                for n in range(2 * NCH):
                    a, c = turns[n]
                    sp.wait_ge(S["token_ready"], n + 1)
                    sp.dma_start(turned[a, cols(c), :].rearrange("(q p) d -> p q d", p=D),
                                 token[:, n % 2, :].rearrange("p (q d) -> p q d", d=D)).then_inc(written[n % 2], 16)

            @block.tensor
            def _(pe):
                pe.wait_ge(S["loaded"], 208)
                for c in range(NCH):
                    for j in range(5):
                        if c:
                            pe.wait_ge(S["sin_done"], 2 * c)
                            pe.wait_ge(S["kv_done"], c)
                        nc.tensor.matmul(pr[j][:], weights[j][:], xn[:, cols(c)], start=True,
                                         stop=True).then_inc(S["projected"], 1)
                by_token = xn[:, 0:T].rearrange("p (n m) -> p m n", m=MB)
                for m in range(MB):
                    mm = nc.tensor.matmul(lr_ps[:], lr_w[:, m, :], by_token[:, m, :], start=(m == 0), stop=(m == MB - 1))
                mm.then_inc(S["lr_ready"], 1)
                pe.wait_ge(S["rotated"], 2 * NCH)
                pe.wait_ge(S["kv_done"], NCH)
                for c in range(NCH):
                    pe.wait_ge(S["target_done"], c + 1)
                    nc.tensor.matmul(pr[c][:], centre[:], kv[:, cols(c)], start=True, stop=True).then_inc(S["cc_ready"], 1)
                for n in range(2 * NCH):
                    a, c = turns[n]
                    src = (cc, kT)[a]
                    if a == 0:
                        pe.wait_ge(S["cc_stored"], c + 1)
                    if n >= 2:
                        pe.wait_ge(S["token_ready"], n - 1)
                    for q in range(4):
                        mm = nc.tensor.transpose(turn_ps[:, n % 2, q * D:(q + 1) * D],
                                                 src[:, c * CH + q * D:c * CH + (q + 1) * D], ident[:])
                    mm.then_inc(S["turned"], 1)

            @block.scalar
            def _(act):
                act.wait_ge(S["lr_ready"], 1)
                nc.scalar.activation(eta[:, 0:NMB], lr_ps[:], ACT.Sigmoid, bias=lr_b[:]).then_inc(S["lr_stored"], 1)
                for n in range(2 * NCH):
                    act.wait_ge(S["turned"], n + 1)
                    if n >= 2:
                        act.wait_ge(written[n % 2], 16 * (n // 2))
                    nc.scalar.activation(token[:, n % 2, :], turn_ps[:, n % 2, :], ACT.Copy).then_inc(S["token_ready"], 1)

            @block.vector
            def _(dve):
                dve.wait_ge(S["loaded"], 208)
                for c in range(NCH):
                    dve.wait_ge(S["projected"], 5 * c + 5)
                    for j, dst in enumerate((kT, qT)):
                        n = 2 * c + j
                        nc.vector.tensor_tensor(ca[:, j, :], pr[2 * j][:], cos[:, cols(c)], ALU.mult).then_inc(S["cos_done"], 1)
                        nc.vector.tensor_tensor(sa[:, j, :], pr[2 * j + 1][:], sin[:, cols(c)], ALU.mult).then_inc(S["sin_done"], 1)
                        dve.wait_ge(S["sin_done"], n + 1)
                        dve.wait_ge(S["cos_done"], n + 1)
                        nc.vector.tensor_tensor(dst[:, cols(c)], ca[:, j, :], sa[:, j, :], ALU.add).then_inc(S["rotated"], 1)
                    dve.wait_ge(S["rotated"], 2 * c + 2)
                    nc.vector.tensor_tensor(kv[:, cols(c)], kT[:, cols(c)], pr[4][:], ALU.subtract).then_inc(S["kv_done"], 1)
                    dve.wait_ge(S["kv_done"], c + 1)
                    nc.vector.tensor_scalar(kv[:, cols(c)], kv[:, cols(c)], bn[:], g[:], ALU.add,
                                            ALU.mult).then_inc(S["target_done"], 1)
                for c in range(NCH):
                    dve.wait_ge(S["cc_ready"], c + 1)
                    nc.vector.tensor_copy(cc[:, cols(c)], pr[c][:]).then_inc(S["cc_stored"], 1)
                dve.wait_ge(S["lr_stored"], 1)
                nc.vector.tensor_scalar(eta[:, 0:NMB], eta[:, 0:NMB], 1.0 / DH, None, ALU.mult).then_inc(S["halved"], 1)


def chain_constants(s):
    return {n: s.sb(n, shape) for n, shape in (
        ("head_cols", [D, HEADS]), ("head_rows", [RW, HEADS]), ("mask_ab", [RW, 2, MB, HEADS]), ("mask_b", [RW, RW]),
        ("tok", [RW, 2 * MB]), ("tok_delta", [RW, MB]), ("g", [RW, DH]), ("ident", [D, D]), ("w0", [D, EXT]),
        ("b0", [D, EXT]))}


CHAIN_LOADED = 16 * 10


def fetch_constants(sp, dram, k, loaded):
    for dst, src in ((k["head_cols"][:], "ttt_head_cols"), (k["head_rows"][:], "ttt_head_rows"),
                     (k["mask_ab"][:].rearrange("p a b c -> p (a b c)"), "ttt_mask_ab"), (k["mask_b"][:], "ttt_mask_b"),
                     (k["tok"][:, 0:MB], "ttt_inv"), (k["g"][:], "ttt_g"), (k["ident"][:], "ident"),
                     (k["w0"][:, 0:DH], "ttt_w0"), (k["b0"][RW:D, 0:DH], "ttt_b0")):
        sp.dma_start(dst, dram[src]).then_inc(loaded, 16)
    sp.dma_start(k["tok_delta"][:], dram["ttt_tid"].partition_broadcast(RW)).then_inc(loaded, 16)


def ttt_chain(nc, constants, loaded, kT, qT, rows, rows_read, eta, zbar):
    with Scope(nc, "tc") as s:
        cc = rows[0:RW, 0, 0:NMB]
        krow, krow_pad = rows[0:RW, 1, 0:NMB], rows[0:RW, 1]
        first = s.sb("first", [D, D])
        kq = [s.sb(f"kq{b}", [D, QUAD, 2, RW]) for b in range(2)]
        ab = [s.sb(f"ab{b}", [D, QUAD, D]) for b in range(2)]
        up = [s.sb(f"up{b}", [RW, QUAD, HEADS, DH]) for b in range(2)]
        bup = [s.sb(f"bup{b}", [RW, QUAD, RW]) for b in range(2)]
        em = [s.sb(f"em{b}", [RW, QUAD, D]) for b in range(2)]
        head_cols, head_rows, mask_ab, mask_b, tok, tok_delta, g, ident, w0, b0 = (constants[n] for n in (
            "head_cols", "head_rows", "mask_ab", "mask_b", "tok", "tok_delta", "g", "ident", "w0", "b0"))
        g2 = s.sb("g2", [RW, DH])
        wb_mean = s.sb("wb_mean", [D, 2])
        eta_k = s.sb("eta_k", [RW, NMB])
        w_sb = [s.sb(f"w_sb{b}", [D, EXT]) for b in range(2)]
        gb = [s.sb(f"gb{b}", [D, EXT]) for b in range(2)]
        zs = [s.sb(f"zs{b}", [RW, EXT]) for b in range(2)]
        gz, prod, square, prod2, w, cr = (s.sb(n, [RW, EXT]) for n in ("gz", "prod", "square", "prod2", "w", "cr"))
        sums = s.sb("sums", [RW, 4])
        tiny = s.sb("tiny", [RW, 5])
        p_ps = [s.ps(f"p{b}", [D, CH]) for b in range(2)]
        state_ps = s.ps("state", [D, CH])
        gram_ps = [s.ps(f"gram{x}", [RW, 2, D]) for x in range(2)]
        S = {n: s.sem(n) for n in (
            "consts idents krow_ready kq_ready em_ready up_ready bup_ready gram_ready ab_ready z_ready z_stored var_done "
            "gz_done prod_done prod2_done r2_done root_done scaled mean_done factor_done cr_done w_done "
            "grad_done state_ready zbar_ready w_stored b_stored zbar_stored prep chain_init ones_set").split()}

        CONSTS = 3 + 4
        with nc.Block() as block:
            @block.gpsimd
            def _(pool):
                for x in (first, gb[0], gb[1]):
                    nc.gpsimd.memset(x[:], 0.0).then_inc(S["consts"], 1)
                pool.wait_ge(loaded, CHAIN_LOADED)
                pool.wait_ge(S["consts"], 3)
                for x in (kT[:, T:], qT[:, T:], eta[:, NMB:], rows[:, 1, NMB:]):
                    nc.gpsimd.memset(x, 0.0).then_inc(S["consts"], 1)
                pool.wait_ge(S["consts"], CONSTS)
                pool.wait_ge(S["prep"], 1)
                nc.gpsimd.tensor_tensor(first[:, 0:RW].rearrange("p (m h) -> p m h", h=HEADS),
                                        kT[:, 0:MB].unsqueeze(2).broadcast_to([D, MB, HEADS]),
                                        head_cols[:].unsqueeze(1).broadcast_to([D, MB, HEADS]),
                                        ALU.mult).then_inc(S["ones_set"], 1)

                def prepare(q, b):
                    shape = [D, QUAD, MB, HEADS]
                    if not isinstance(q, int):
                        pool.wait_ge(S["state_ready"], q * QUAD - (QUAD - 1))
                    for half, (src, off) in enumerate(((kT, MB), (qT, 0))):
                        x = src[:, bass.ds(q * (QUAD * MB) + off, QUAD * MB)] if half == 0 else \
                            src[:, bass.ds(q * (QUAD * MB), QUAD * MB)]
                        x = x.rearrange("p (j m) -> p j m", m=MB)
                        for j in range(QUAD):
                            i_ = nc.gpsimd.tensor_tensor(
                                kq[b][:, j, half, :].rearrange("p (m h) -> p m h", h=HEADS),
                                x[:, j, :].unsqueeze(2).broadcast_to([D, MB, HEADS]),
                                head_cols[:].unsqueeze(1).broadcast_to([D, MB, HEADS]), ALU.mult)
                    i_.then_inc(S["kq_ready"], 1)
                    eq = eta[:, bass.ds(q * QUAD, QUAD)].unsqueeze(2).broadcast_to([RW, QUAD, D])
                    if not isinstance(q, int):
                        pool.wait_ge(S["ab_ready"], q * QUAD - (QUAD - 1))
                    nc.gpsimd.tensor_tensor(em[b][:], eq,
                                            mask_ab[:].rearrange("p a b c -> p (a b c)").unsqueeze(1).broadcast_to([RW, QUAD, D]),
                                            ALU.mult).then_inc(S["em_ready"], 1)
                    kr = krow_pad[:, bass.ds(q * QUAD, QUAD), :]
                    pool.wait_ge(S["krow_ready"], 1)
                    for j in range(QUAD):
                        i_ = nc.gpsimd.tensor_tensor(up[b][:, j], kr[:, j, :].unsqueeze(1).broadcast_to([RW, HEADS, DH]),
                                                     head_rows[:].unsqueeze(2).broadcast_to([RW, HEADS, DH]), ALU.mult)
                    i_.then_inc(S["up_ready"], 1)
                    nc.gpsimd.tensor_tensor(bup[b][:], eq[:, :, 0:RW], mask_b[:].unsqueeze(1).broadcast_to([RW, QUAD, RW]),
                                            ALU.mult).then_inc(S["bup_ready"], 1)

                prepare(0, 0)
                prepare(1, 1)
                with pool.Fori(0, NMB // (2 * QUAD)) as i:
                    for b in range(2):
                        prepare(i * 2 + (b + 2), b)

            @block.tensor
            def _(pe):
                pe.wait_ge(loaded, CHAIN_LOADED)
                pe.wait_ge(S["chain_init"], 1)
                pe.sem_inc(S["zbar_ready"], 1)
                pe.wait_ge(S["consts"], CONSTS)
                pe.wait_ge(S["idents"], 2)
                pe.wait_ge(S["ones_set"], 1)
                nc.tensor.matmul(state_ps[:, 0:EXT], ident[:], w0[:], start=True, stop=True, skip_group_check=True)
                nc.tensor.matmul(state_ps[:, 32:32 + EXT], ident[:], b0[:], start=False, stop=True,
                                 skip_group_check=True).then_inc(S["state_ready"], 1)
                nc.tensor.matmul(p_ps[0][:, 0:EXT], first[:], w0[:], start=True, stop=False, skip_group_check=True)
                pe.wait_ge(S["b_stored"], 1)
                pe.wait_ge(S["em_ready"], 1)
                nc.tensor.matmul(p_ps[0][:, 0:EXT], ab[0][RW:D, 0, :], gb[0][RW:D, :], start=False, stop=True,
                                 skip_group_check=True).then_inc(S["z_ready"], 1)

                def gram(q, b, j):
                    start = isinstance(q, int)
                    if j == 0:
                        pe.wait_ge(S["kq_ready"], q + 1)
                    if j % 2 == 0 and not start:
                        pe.wait_ge(S["ab_ready"], q * QUAD - (1 - j))
                    lhs = kq[b][:, j - 1, 0, :] if j else first[:, 0:RW] if start else kq[1 - b][:, QUAD - 1, 0, :]
                    nc.tensor.matmul(gram_ps[j // 2][:, j % 2, :], lhs, kq[b][:, j].rearrange("p a b -> p (a b)"),
                                     start=(j % 2 == 0), stop=(j % 2 == 1),
                                     skip_group_check=True).then_inc(S["gram_ready"], 1)
                for j in range(QUAD):
                    gram(0, 0, j)
                with pe.Fori(0, NMB // (2 * QUAD)) as i:
                    for b in range(2):
                        for j in range(QUAD):
                            n = i * (2 * QUAD) + (b * QUAD + j)
                            pb = (j + 1) % 2
                            pe.wait_ge(S["z_stored"], n + 1)
                            pe.wait_ge(S["zbar_stored"], n + 1)
                            pe.wait_ge(S["w_stored"], n + 2)
                            nc.tensor.matmul(p_ps[pb][:, 0:EXT], kq[b][:, j].rearrange("p a b -> p (a b)"), w_sb[j % 2][:],
                                             start=True, stop=False, skip_group_check=True)
                            if j == 0:
                                pe.wait_ge(S["up_ready"], 2 * i + (b + 1))
                                pe.wait_ge(S["bup_ready"], 2 * i + (b + 1))
                            pe.wait_ge(S["ab_ready"], n + 2)
                            pe.wait_ge(S["b_stored"], n + 2)
                            pe.wait_ge(S["grad_done"], n + 1)
                            nc.tensor.matmul(p_ps[pb][0:RW, 0:EXT], ab[b][:, j, 0:RW], gb[j % 2][:],
                                             start=False, stop=True, skip_group_check=True).then_inc(S["z_ready"], 1)
                            nc.tensor.matmul(state_ps[:, 0:EXT], up[b][:, j].rearrange("p a b -> p (a b)"), gb[j % 2][0:RW, :],
                                             start=False, stop=True, skip_group_check=True)
                            nc.tensor.matmul(state_ps[RW:D, 32:32 + EXT], bup[b][:, j, :], gb[j % 2][0:RW, :],
                                             start=False, stop=True, skip_group_check=True).then_inc(S["state_ready"], 1)
                            nc.tensor.matmul(p_ps[pb][RW:D, 0:EXT], ab[b][:, j, RW:D], gb[j % 2][:], start=False,
                                             stop=True, skip_group_check=True).then_inc(S["zbar_ready"], 1)
                            gram(i * 2 + (b + 1), 1 - b, j)

            @block.scalar
            def _(act):
                def store_state(n, j):
                    act.wait_ge(S["state_ready"], n + 1)
                    nc.scalar.activation(w_sb[j % 2][:], state_ps[:, 0:EXT], ACT.Copy).then_inc(S["w_stored"], 1)
                    nc.scalar.activation(gb[j % 2][RW:D, :], state_ps[RW:D, 32:32 + EXT], ACT.Copy).then_inc(S["b_stored"], 1)

                def keep_zbar(n, jj):
                    act.wait_ge(S["zbar_ready"], n + 1)
                    nc.scalar.activation(zbar[RW:D, bass.ds(n, 1), :].rearrange("p a e -> p (a e)"),
                                         p_ps[jj % 2][RW:D, 0:DH], ACT.Copy).then_inc(S["zbar_stored"], 1)
                act.sem_inc(S["zbar_stored"], 1)
                act.wait_ge(S["consts"], 3)
                store_state(0, 0)
                with act.Fori(0, NMB // (2 * QUAD)) as i:
                    for jj in range(2 * QUAD):
                        n = i * (2 * QUAD) + jj
                        act.wait_ge(S["r2_done"], n + 1)
                        nc.scalar.activation(tiny[:, 1:2], tiny[:, 0:1], ACT.Sqrt).then_inc(S["root_done"], 1)
                        store_state(n, jj)
                        keep_zbar(n, jj)
                keep_zbar(NMB, 0)

            @block.vector
            def _(dve):
                dve.wait_ge(loaded, CHAIN_LOADED)
                count = [0]

                def then(x):
                    count[0] += 1
                    x.then_inc(S["mean_done"], 1)
                    dve.wait_ge(S["mean_done"], count[0])
                V = nc.vector
                for x in range(2):
                    V.tensor_copy(ab[x][RW:D].rearrange("p j (a b) -> p (j a) b", a=2),
                                  ident[RW:D, RW:D].unsqueeze(1).broadcast_to([RW, 2 * QUAD, RW])).then_inc(S["idents"], 1)
                then(V.tensor_tensor(tok[:, MB:], tok[:, 0:MB], tok_delta[:], ALU.add))
                then(V.tensor_scalar(tok[:, 0:MB], tok[:, MB:], 0.0, None, ALU.max))
                then(V.tensor_tensor(mask_ab[:, 1], mask_ab[:, 1], tok[:, 0:MB].unsqueeze(2).broadcast_to([RW, MB, HEADS]), ALU.mult))
                then(V.tensor_scalar(mask_ab[:, 0], mask_ab[:, 0], tok[:, MB - 1:MB], None, ALU.mult))
                then(V.tensor_scalar(mask_b[:], mask_b[:], tok[:, MB - 1:MB], None, ALU.mult))
                then(V.tensor_scalar(eta_k[:], eta[:, 0:NMB], tok[:, MB - 1:MB], -1.0, ALU.mult, ALU.mult))
                then(V.scalar_tensor_tensor(out=g2[:], in0=g[:], scalar=1.0, in1=g[:], op0=ALU.mult, op1=ALU.mult))
                then(V.memset(b0[0:RW, :], 0.0))
                for x, p in ((w0, slice(0, D)), (b0, slice(RW, D))):
                    then(V.reduce_sum(wb_mean[p, 0:1], x[p, 0:DH], AX_X))
                    then(V.tensor_scalar(wb_mean[p, 1:2], wb_mean[p, 0:1], 1.0 / DH, None, ALU.mult))
                    then(V.tensor_scalar(x[p, 0:DH], x[p, 0:DH], wb_mean[p, 1:2], None, ALU.subtract))
                then(V.memset(w0[:, DH:], 0.0))
                then(V.memset(b0[RW:D, DH:], (DH * TTT_EPS) ** 0.5))
                dve.sem_inc(S["prep"], 1)
                dve.sem_inc(S["chain_init"], 1)
                dve.wait_ge(rows_read, 32)
                V.tensor_tensor(krow, krow, eta_k[:].unsqueeze(2).broadcast_to([RW, NMB, DH]), ALU.mult).then_inc(S["krow_ready"], 1)
                dve.sem_inc(S["z_stored"], 1)
                dve.sem_inc(S["ab_ready"], 1)
                dve.wait_ge(S["consts"], CONSTS)

                def make_ab(q, b, j):
                    if j == 0:
                        dve.wait_ge(S["em_ready"], q + 1)
                        if not isinstance(q, int):
                            dve.wait_ge(S["state_ready"], q * QUAD - (QUAD - 1))
                    dve.wait_ge(S["gram_ready"], q * QUAD + (2 + j // 2 * 2))
                    V.scalar_tensor_tensor(out=ab[b][0:RW, j, :], in0=gram_ps[j // 2][:, j % 2, :], scalar=1.0,
                                           in1=em[b][:, j, :], op0=ALU.add, op1=ALU.mult).then_inc(S["ab_ready"], 1)
                for j in range(2):
                    make_ab(0, 0, j)

                def store_z(n, jj):
                    dve.wait_ge(S["z_ready"], n + 1)
                    V.tensor_copy(zs[jj % 2][:], p_ps[jj % 2][0:RW, 0:EXT]).then_inc(S["z_stored"], 1)
                with dve.Fori(0, NMB // (2 * QUAD)) as i:
                    for jj in range(2 * QUAD):
                        b, j = jj // QUAD, jj % QUAD
                        n = i * (2 * QUAD) + jj
                        z = zs[jj % 2][0:RW, 0:DH]
                        c = cc[:, bass.ds(n, 1), :].rearrange("p a e -> p (a e)")
                        store_z(n, jj)
                        dve.wait_ge(S["z_stored"], n + 2)
                        V.scalar_tensor_tensor(out=square[:], in0=zs[jj % 2][0:RW, :], scalar=1.0 / DH, in1=zs[jj % 2][0:RW, :],
                                               op0=ALU.mult, op1=ALU.mult, accum_out=sums[:, 3:4]).then_inc(S["var_done"], 1)
                        V.scalar_tensor_tensor(out=gz[:, 0:DH], in0=z, scalar=1.0, in1=g2[:], op0=ALU.mult, op1=ALU.mult,
                                               accum_out=sums[:, 1:2]).then_inc(S["gz_done"], 1)
                        dve.wait_ge(S["var_done"], n + 1)
                        V.reciprocal(tiny[:, 0:1], sums[:, 3:4]).then_inc(S["r2_done"], 1)
                        dve.wait_ge(S["gz_done"], n + 1)
                        V.scalar_tensor_tensor(out=prod2[:, 0:DH], in0=z, scalar=1.0, in1=gz[:, 0:DH], op0=ALU.mult, op1=ALU.mult,
                                               accum_out=sums[:, 0:1]).then_inc(S["prod2_done"], 1)
                        V.scalar_tensor_tensor(out=prod[:, 0:DH], in0=z, scalar=-1.0 / DH, in1=c, op0=ALU.mult, op1=ALU.mult,
                                               accum_out=sums[:, 2:3]).then_inc(S["prod_done"], 1)
                        dve.wait_ge(S["prod2_done"], n + 1)
                        V.tensor_scalar(tiny[:, 2:4], sums[:, 0:2], tiny[:, 0:1], -1.0 / DH, ALU.mult,
                                        ALU.mult).then_inc(S["scaled"], 1)
                        dve.wait_ge(S["scaled"], n + 1)
                        dve.wait_ge(S["root_done"], n + 1)
                        V.tensor_scalar(tiny[:, 4:5], sums[:, 2:3], tiny[:, 1:2], tiny[:, 2:3], ALU.mult,
                                        ALU.add).then_inc(S["factor_done"], 1)
                        V.tensor_scalar(cr[:, 0:DH], c, tiny[:, 1:2], tiny[:, 3:4], ALU.mult, ALU.add).then_inc(S["cr_done"], 1)
                        dve.wait_ge(S["factor_done"], n + 1)
                        V.scalar_tensor_tensor(out=w[:, 0:DH], in0=z, scalar=tiny[:, 4:5], in1=gz[:, 0:DH], op0=ALU.mult,
                                               op1=ALU.add).then_inc(S["w_done"], 1)
                        dve.wait_ge(S["w_done"], n + 1)
                        V.scalar_tensor_tensor(out=gb[jj % 2][0:RW, 0:DH], in0=w[:, 0:DH], scalar=tiny[:, 0:1], in1=cr[:, 0:DH],
                                               op0=ALU.mult, op1=ALU.add).then_inc(S["grad_done"], 1)
                        if j < 2:
                            make_ab(i * 2 + b, b, j + 2)
                        else:
                            make_ab(i * 2 + (b + 1), 1 - b, j - 2)


def ttt_finish(nc, dram, qT, zbar, hidden):
    scratch = nc.dram_tensor("hidden_scratch", [T, D], F32, kind="Internal").ap()
    with Scope(nc, "tf") as s:
        H = slice(RW, D)
        g, bn = s.sb("g", [D, 1]), s.sb("bn", [D, 1])
        sq = s.sb("sq", [D, NMB, DH])
        y = s.sb("y", [D, NMB, DH])
        scaled = s.sb("scaled", [D, T])
        var = s.sb("var", [D, NMB])
        eps = s.sb("eps", [D, 1])
        tokens = s.sb("tokens", [D, TT, D])
        ident = s.sb("ident", [D, D])
        turn_ps = s.ps("turn", [D, NCH, CH])
        S = {n: s.sem(n) for n in ("loaded sq_done var_done root_done inv_done y_done written read_0 read_1 turned "
                                   "scaled_ready stored eps_set").split()}
        zb = zbar[H, 1:NMB + 1, :]
        N2, T2 = NMB // 2, TT // 2
        with nc.Block() as block:
            @block.sync
            def _(sp):
                sp.dma_start(g[:], dram["ttt_g_col"]).then_inc(S["loaded"], 16)
                sp.dma_start(bn[:], dram["ttt_b_col"]).then_inc(S["loaded"], 16)
                sp.dma_start(ident[:], dram["ident"]).then_inc(S["loaded"], 16)
                by_row = scratch.rearrange("(n m) (h e) -> (m h) n e", m=MB, e=DH)
                by_token = scratch.rearrange("(t p) d -> p t d", p=D)
                for k in range(2):
                    sp.wait_ge(S["y_done"], k + 1)
                    sp.dma_start(by_row[:, k * N2:(k + 1) * N2], y[H, k * N2:(k + 1) * N2, :]).then_inc(S["written"], 16)
                    sp.wait_ge(S["written"], 16 * (k + 1))
                    sp.dma_start(tokens[:, k * T2:(k + 1) * T2, :],
                                 by_token[:, k * T2:(k + 1) * T2]).then_inc(S[f"read_{k}"], 16)

            @block.gpsimd
            def _(pool):
                pool.memset(eps[:], TTT_EPS).then_inc(S["eps_set"], 1)

            @block.scalar
            def _(act):
                act.wait_ge(S["eps_set"], 1)
                nc.scalar.activation(sq[H], zb, ACT.Square).then_inc(S["sq_done"], 1)
                act.wait_ge(S["var_done"], 1)
                nc.scalar.activation(var[H], var[H], ACT.Sqrt, scale=1.0 / DH, bias=eps[H]).then_inc(S["root_done"], 1)

            @block.vector
            def _(dve):
                V = nc.vector
                dve.wait_ge(S["sq_done"], 1)
                V.reduce_sum(var[H], sq[H], AX_X).then_inc(S["var_done"], 1)
                dve.wait_ge(S["root_done"], 1)
                V.reciprocal(var[H], var[H]).then_inc(S["inv_done"], 1)
                dve.wait_ge(S["inv_done"], 1)
                for k in range(2):
                    part = slice(k * N2, (k + 1) * N2)
                    V.tensor_tensor(y[H, part], zbar[H, 1 + k * N2:1 + (k + 1) * N2, :],
                                    var[H, part].unsqueeze(2).broadcast_to([RW, N2, DH]), ALU.mult).then_inc(S["y_done"], 1)
                dve.wait_ge(S["loaded"], 48)
                for c in range(NCH):
                    cols = slice(c * CH, (c + 1) * CH)
                    dve.wait_ge(S["turned"], c + 1)
                    V.tensor_scalar(scaled[:, cols], turn_ps[:, c, :], g[:], bn[:], ALU.mult, ALU.add).then_inc(S["scaled_ready"], 1)
                    dve.wait_ge(S["scaled_ready"], c + 1)
                    V.tensor_tensor(hidden[:, cols], scaled[:, cols], qT[:, cols], ALU.add).then_inc(S["stored"], 1)

            @block.tensor
            def _(pe):
                pe.wait_ge(S["loaded"], 48)
                for c in range(NCH):
                    if c % 2 == 0:
                        pe.wait_ge(S[f"read_{c // 2}"], 16)
                    for q in range(4):
                        mm = nc.tensor.transpose(turn_ps[:, c, q * D:(q + 1) * D], tokens[:, 4 * c + q, :], ident[:])
                    mm.then_inc(S["turned"], 1)


def lay_out_ttt(inp):
    a = {k: np.asarray(v) for k, v in inp.items()}
    wk, wq, wv = (a[f"L1_attn_{n}"] for n in ("wk", "wq", "wv"))
    feat = np.arange(D)
    d = feat % DH
    perm = np.where(d < DH // 2, feat + DH // 2, feat - DH // 2)
    inv = (1.0 / np.float32(10000.0) ** (np.arange(0, DH, 2, dtype=np.float32) / np.float32(DH))).astype(np.float32)
    f = np.arange(T, dtype=np.float32)[None, :] * inv[d % (DH // 2)][:, None]
    sign = np.where(d < DH // 2, -1.0, 1.0).astype(np.float32)[:, None]
    lrw = a["L1_attn_lr_w"][:, 0, :]
    lr = np.zeros((D, MB, MB, HEADS), np.float32)
    for m in range(MB):
        lr[:, m, m, :] = lrw.T
    row_head = np.arange(RW) % HEADS
    row_tok = np.arange(RW) // HEADS
    same = row_head[:, None, None] == np.arange(HEADS)[None, None, :]
    mask = np.zeros((RW, 2, MB, HEADS), np.float32)
    mask[:, 0] = np.where(same, -1.0, 0.0)
    mask[:, 1] = np.where(same & (row_tok[:, None, None] <= np.arange(MB)[None, :, None]), -1.0, 0.0)
    mask_b = np.where(row_head[:, None] == row_head[None, :], -1.0, 0.0).astype(np.float32)
    tile_rows = lambda x: np.ascontiguousarray(np.tile(x, (MB, 1)))
    return {
        "ttt_wk": np.ascontiguousarray(wk.T), "ttt_wkp": np.ascontiguousarray(wk[perm].T),
        "ttt_wq": np.ascontiguousarray(wq.T), "ttt_wqp": np.ascontiguousarray(wq[perm].T),
        "ttt_wv": np.ascontiguousarray(wv.T),
        "cos": np.cos(f).astype(np.float32), "sin": (np.sin(f) * sign).astype(np.float32),
        "ttt_lrw": lr.reshape(D, MB * RW), "ttt_lrb": tile_rows(a["L1_attn_lr_b"].reshape(HEADS, 1)),
        "ttt_head_cols": (np.arange(D)[:, None] // DH == np.arange(HEADS)[None, :]).astype(np.float32),
        "ttt_head_rows": (row_head[:, None] == np.arange(HEADS)[None, :]).astype(np.float32),
        "ttt_g_col": a["L1_attn_ttt_norm_w"].reshape(D, 1), "ttt_b_col": a["L1_attn_ttt_norm_b"].reshape(D, 1),
        "ttt_centre": (np.eye(D) - np.kron(np.eye(HEADS), np.full((DH, DH), 1.0 / DH))).astype(np.float32),
        "ttt_mask_ab": mask.reshape(RW, D), "ttt_mask_b": mask_b,
        "ttt_inv": np.tile((np.float32(1) / np.arange(1, MB + 1, dtype=np.float32))[None], (RW, 1)),
        "ttt_tid": a["L1_attn_token_idx_delta"],
        "ttt_g": tile_rows(a["L1_attn_ttt_norm_w"]),
        "ttt_w0": a["L1_attn_W1"].reshape(D, DH), "ttt_b0": tile_rows(a["L1_attn_b1"][:, 0, :]),
        "ln1_w": a["L1_attn_ln_w"].reshape(D, 1), "ln1_b": a["L1_attn_ln_b"].reshape(D, 1),
        "post_w": a["L1_attn_post_norm_w"].reshape(D, 1), "post_b": a["L1_attn_post_norm_b"].reshape(D, 1),
    }


NT = 6
NS = 8
K3 = 3 * NS
XD = 96 + K3
WIN = 5


def longhorn_inputs(nc, dram, xn, xc, xd, xd_parts, picks):
    with Scope(nc, "li") as s:
        w_in = [s.sb(f"w_in{b}", [D, D]) for b in range(2)]
        w_x = s.sb("w_x", [D, NT, XD])
        conv_w, conv_b = s.sb("conv_w", [D, NT, 3]), s.sb("conv_b", [D, NT])
        xl = [s.sb(f"xl{b}", [D, 2 + T]) for b in range(2)]
        acc = [s.sb(f"acc{b}", [D, T]) for b in range(2)]
        acc2 = [s.sb(f"acc2{b}", [D, T]) for b in range(2)]
        sum_k = s.sb("sum_k", [XD, D // NCH])
        spread = s.sb("spread", [D, NCH, XD])
        k_rows = s.sb("k_rows", [96, T])
        sq = s.sb("sq", [XD, T])
        den, inv = s.sb("den", [D, CH]), s.sb("inv", [D, CH])
        part1, part2 = s.sb("part1", [XD, T], BF16), s.sb("part2", [XD, T], BF16)
        rest = s.sb("rest", [XD, T])
        masks = s.sb("masks", [XD, 2])
        picks_f = [s.sb(f"pick_{x}", [XD, NS, D]) for x in ("nk2", "k", "q")]
        xl_ps = s.ps("xl", [D, NCH, CH])
        xd_ps = s.ps("xd", [XD, NCH, CH])
        S = {n: s.sem(n) for n in ("loaded w_a w_b padded xl_ready xl_stored first_tap second_tap third_tap "
                                   "xc_ready w_used xd_ready xd_stored cleared sq_done ks_ready log_done den_ready "
                                   "spread_ready k_stored inv_ready k_ready nk2_ready part1_ready rest_ready part2_ready parts_ready "
                                   "picks_loaded picks_ready").split()}
        w_loaded = (S["w_a"], S["w_b"])
        flat = lambda ap: ap.rearrange("p a b -> p (a b)")
        with nc.Block() as block:
            @block.sync
            def _(sp):
                for i in range(NT):
                    if i >= 2:
                        sp.wait_ge(S["w_used"], i - 1)
                    sp.dma_start(w_in[i % 2][:], dram["lh_in"][i * D:(i + 1) * D, :]).then_inc(w_loaded[i % 2], 16)
                    if i == 0:
                        sp.dma_start(flat(w_x[:]), dram["lh_x"]).then_inc(S["loaded"], 16)
                        sp.dma_start(flat(conv_w[:]), dram["lh_conv_w"]).then_inc(S["loaded"], 16)
                        sp.dma_start(conv_b[:], dram["lh_conv_b"]).then_inc(S["loaded"], 16)
                        sp.dma_start(sum_k[:], dram["lh_sum_k"]).then_inc(S["loaded"], 16)
                        sp.dma_start(masks[:], dram["lh_masks"]).then_inc(S["loaded"], 16)
                        sp.dma_start(flat(spread[:]), dram["lh_spread"]).then_inc(S["loaded"], 16)
                for dst, src in zip(picks_f, ("lh_pick_nk2", "lh_pick_k", "lh_pick_q")):
                    sp.dma_start(flat(dst[:]), dram[src]).then_inc(S["picks_loaded"], 16)

            @block.gpsimd
            def _(pool):
                for b in range(2):
                    pool.memset(xl[b][:, 0:2], 0.0).then_inc(S["padded"], 1)
                pool.memset(xd[:], 0.0).then_inc(S["cleared"], 1)
                pool.memset(xd_parts[:, T:], 0.0).then_inc(S["cleared"], 1)
                pool.wait_ge(S["picks_loaded"], 48)
                for dst, src in zip(picks, picks_f):
                    nc.gpsimd.tensor_copy(dst[:], src[:]).then_inc(S["picks_ready"], 1)

            @block.tensor
            def _(pe):
                pe.wait_ge(S["loaded"], 96)
                for i in range(NT):
                    pe.wait_ge(w_loaded[i % 2], 16 * (i // 2 + 1))
                    for c in range(NCH):
                        if i:
                            pe.wait_ge(S["xl_stored"], (i - 1) * NCH + c + 1)
                        mm = nc.tensor.matmul(xl_ps[:, c, :], w_in[i % 2][:], xn[:, c * CH:(c + 1) * CH], start=True,
                                              stop=True)
                        mm.then_inc(S["xl_ready"], 1)
                        if c == NCH - 1:
                            pe.wait_ge(S["xl_ready"], (i + 1) * NCH)
                            pe.sem_inc(S["w_used"], 1)
                for i in range(NT):
                    pe.wait_ge(S["xc_ready"], i + 1)
                    for c in range(NCH):
                        mm = nc.tensor.matmul(xd_ps[:, c, :], w_x[:, i, :], xc[:, i, c * CH:(c + 1) * CH],
                                              start=(i == 0), stop=(i == NT - 1))
                        if i == NT - 1:
                            mm.then_inc(S["xd_ready"], 1)
                for c in range(NCH):
                    pe.wait_ge(S["sq_done"], c + 1)
                    nc.tensor.matmul(xl_ps[32 * c:32 * c + 32, 0, :], sum_k[:], sq[:, c * CH:(c + 1) * CH], start=True,
                                     stop=True, skip_group_check=True).then_inc(S["ks_ready"], 1)
                pe.wait_ge(S["inv_ready"], 1)
                for c in range(NCH):
                    nc.tensor.matmul(xl_ps[0:XD, c, :], spread[:, c, :], inv[:], start=True,
                                     stop=True).then_inc(S["spread_ready"], 1)

            @block.scalar
            def _(act):
                act.wait_ge(S["loaded"], 96)
                act.wait_ge(S["padded"], 2)
                for i in range(NT + 1):
                    b = i % 2
                    if i == NT:
                        act.wait_ge(S["third_tap"], i)
                        nc.scalar.activation(xc[:, i - 1, :], acc[1 - b][:], ACT.Silu).then_inc(S["xc_ready"], 1)
                        break
                    for c in range(NCH):
                        act.wait_ge(S["xl_ready"], i * NCH + c + 1)
                        if i >= 2 and c == 0:
                            act.wait_ge(S["third_tap"], i - 1)
                        nc.scalar.activation(xl[b][:, 2 + c * CH:2 + (c + 1) * CH], xl_ps[:, c, :],
                                             ACT.Copy).then_inc(S["xl_stored"], 1)
                    act.wait_ge(S["xl_stored"], (i + 1) * NCH)
                    if i >= 2:
                        act.wait_ge(S["xc_ready"], i - 1)
                    nc.scalar.activation(acc[b][:], xl[b][:, 0:T], ACT.Identity, scale=conv_w[:, i, 0:1],
                                         bias=conv_b[:, i:i + 1]).then_inc(S["first_tap"], 1)
                    if i:
                        act.wait_ge(S["third_tap"], i)
                        nc.scalar.activation(xc[:, i - 1, :], acc[1 - b][:], ACT.Silu).then_inc(S["xc_ready"], 1)
                for c in range(NCH):
                    act.wait_ge(S["xd_ready"], c + 1)
                    nc.scalar.activation(sq[:, c * CH:(c + 1) * CH], xd_ps[:, c, :], ACT.Square).then_inc(S["sq_done"], 1)
                nc.scalar.activation(k_rows[32:32 + K3, :], flat(xd_ps[32:32 + K3]), ACT.Copy).then_inc(S["k_stored"], 1)
                act.wait_ge(S["cleared"], 1)
                nc.scalar.activation(xd[64:64 + K3, 0:T], flat(xd_ps[64:64 + K3]), ACT.Copy).then_inc(S["xd_stored"], 1)
                act.wait_ge(S["xd_stored"], 1)
                for c in range(NCH):
                    cols = slice(c * CH, (c + 1) * CH)
                    act.wait_ge(S["nk2_ready"], c + 1)
                    nc.scalar.activation(part1[:, cols], xd[:, cols], ACT.Copy).then_inc(S["part1_ready"], 1)
                for c in range(NCH):
                    cols = slice(c * CH, (c + 1) * CH)
                    act.wait_ge(S["rest_ready"], c + 1)
                    nc.scalar.activation(part2[:, cols], rest[:, cols], ACT.Copy).then_inc(S["part2_ready"], 1)
                nc.scalar.activation(xd[0:2 * NS, 0:T], flat(xl_ps[0:2 * NS]), ACT.Ln).then_inc(S["log_done"], 1)
                act.wait_ge(S["log_done"], 1)
                nc.scalar.activation(xd[0:NS, 0:T], flat(xd_ps[0:NS]), ACT.Copy).then_inc(S["xd_stored"], 1)

            @block.vector
            def _(dve):
                for i in range(NT):
                    b = i % 2
                    dve.wait_ge(S["first_tap"], i + 1)
                    nc.vector.scalar_tensor_tensor(out=acc2[b][:], in0=xl[b][:, 1:1 + T], scalar=conv_w[:, i, 1:2],
                                                   in1=acc[b][:], op0=ALU.mult, op1=ALU.add).then_inc(S["second_tap"], 1)
                    dve.wait_ge(S["second_tap"], i + 1)
                    nc.vector.scalar_tensor_tensor(out=acc[b][:], in0=xl[b][:, 2:2 + T], scalar=conv_w[:, i, 2:3],
                                                   in1=acc2[b][:], op0=ALU.mult, op1=ALU.add).then_inc(S["third_tap"], 1)
                dve.wait_ge(S["cleared"], 1)
                K = slice(32, 32 + K3)

                def split(c):
                    cols = slice(c * CH, (c + 1) * CH)
                    dve.wait_ge(S["part1_ready"], c + 1)
                    nc.vector.scalar_tensor_tensor(out=rest[:, cols], in0=part1[:, cols], scalar=masks[:, 0:1],
                                                   in1=xd[:, cols], op0=ALU.mult, op1=ALU.add).then_inc(S["rest_ready"], 1)

                def split_again(c):
                    cols = slice(c * CH, (c + 1) * CH)
                    dve.wait_ge(S["part2_ready"], c + 1)
                    nc.vector.scalar_tensor_tensor(out=xd_parts[:, cols], in0=part2[:, cols], scalar=masks[:, 1:2],
                                                   in1=rest[:, cols], op0=ALU.mult, op1=ALU.add).then_inc(S["parts_ready"], 1)

                dve.wait_ge(S["ks_ready"], NCH)
                nc.vector.tensor_scalar(den[:], xl_ps[:, 0, :], 1.0, None, ALU.add).then_inc(S["den_ready"], 1)
                dve.wait_ge(S["den_ready"], 1)
                nc.vector.reciprocal(inv[:], den[:]).then_inc(S["inv_ready"], 1)
                dve.wait_ge(S["k_stored"], 1)
                for c in range(NCH):
                    cols = slice(c * CH, (c + 1) * CH)
                    dve.wait_ge(S["spread_ready"], c + 1)
                    nc.vector.tensor_tensor(xd[K, cols], k_rows[K, cols], xl_ps[K, c, :], ALU.mult).then_inc(S["k_ready"], 1)
                    dve.wait_ge(S["k_ready"], c + 1)
                    nc.vector.scalar_tensor_tensor(out=xd[96:96 + K3, cols], in0=k_rows[K, cols], scalar=-1.0,
                                                   in1=xd[K, cols], op0=ALU.mult, op1=ALU.mult).then_inc(S["nk2_ready"], 1)
                for c in range(NCH):
                    split(c)
                for c in range(NCH):
                    split_again(c)


def longhorn_scan(nc, dram, xn, xc, xd, xd_parts, picks, h_red):
    PAIRS_N = NS // 2
    PA = PAIRS_N - 1
    ITEMS = 6
    PER = NT * PAIRS_N
    ROWS = PAIRS_N * ITEMS
    with Scope(nc, "ls") as s:
        w_z = s.sb("w_z", [D, NT, D])
        w_dt = s.sb("w_dt", [XD, NT, D])
        w_red = s.sb("w_red", [D, NT, D])
        dt_b, d_par = s.sb("dt_b", [D, NT]), s.sb("d_par", [D, NT])
        ident = s.sb("ident", [D, D])
        d_diag = s.sb("d_diag", [D, NT, D])
        nk2, kk, qq = (s.sb(n, [D, NS, CH]) for n in ("nk2", "kk", "qq"))
        zg = [s.sb(f"zg{b}", [D, CH]) for b in range(2)]
        sig = [s.sb(f"sig{b}", [D, CH]) for b in range(2)]
        dx = [s.sb(f"dx{b}", [D, CH]) for b in range(2)]
        a_ = [s.sb(f"a{b}", [D, 2, CH]) for b in range(2)]
        b_ = [s.sb(f"b{b}", [D, 2, CH]) for b in range(2)]
        st = [s.sb(f"st{b}", [D, 2, CH]) for b in range(2)]
        qs = [s.sb(f"qs{b}", [D, 2, CH]) for b in range(2)]
        carry = s.sb("carry", [D, NT, NS])
        yg = s.sb("yg", [D, CH])
        bc_ps = s.ps("bc", [D, 2, CH])
        dt_ps, z_ps = s.ps("dt", [D, CH]), s.ps("z", [D, CH])
        y_ps = s.ps("y", [D, 2, CH])
        red_ps = s.ps("red", [D, CH])
        S = {n: s.sem(n) for n in (
            "loaded diag zero_carry bc_ready bc_stored z_ready zg_ready dt_ready sig_ready dx_ready a_ready "
            "last_a_ready a1_ready b_ready st_ready carry_ready qs_ready y_ready yg_ready red_ready red_stored").split()}
        flat = lambda ap: ap.rearrange("p a b -> p (a b)")
        LOADED = 16 * 6
        item = lambda m: ((nk2, kk, qq)[m // 2], picks[m // 2], m % 2)
        with nc.Block() as block:
            @block.sync
            def _(sp):
                for dst, src in ((flat(w_dt[:]), "lh_dt"), (dt_b[:], "lh_dt_b"),
                                 (flat(w_z[:]), "lh_z"), (ident[:], "ident"), (d_par[:], "lh_d"),
                                 (flat(w_red[:]), "lh_red")):
                    sp.dma_start(dst, dram[src]).then_inc(S["loaded"], 16)

            @block.gpsimd
            def _(pool):
                wide = lambda x: x[:].unsqueeze(1).broadcast_to([D, 2, CH])
                nc.gpsimd.memset(carry[:], 0.0).then_inc(S["zero_carry"], 1)
                with pool.Fori(0, NCH) as c:
                    for i in range(NT):
                        for p in range(PAIRS_N):
                            n = c * PER + (i * PAIRS_N + p)
                            pair = slice(2 * p, 2 * p + 2)
                            if p == 0:
                                pool.wait_ge(S["dx_ready"], c * NT + (i + 1))
                            if i == 0:
                                pool.wait_ge(S["bc_stored"], c * ROWS + (ITEMS * (p + 1) + 2))
                            pool.wait_ge(S["st_ready"], n + 1)
                            if p == PAIRS_N - 1:
                                nc.gpsimd.tensor_tensor(a_[p % 2][:], wide(sig[i % 2]), nk2[:, pair, :],
                                                        ALU.mult).then_inc(S["last_a_ready"], 1)
                            nc.gpsimd.tensor_tensor(b_[p % 2][:], wide(dx[i % 2]), kk[:, pair, :],
                                                    ALU.mult).then_inc(S["b_ready"], 1)

            @block.tensor
            def _(pe):
                pe.sem_inc(S["y_ready"], 2)
                pe.sem_inc(S["red_ready"], 1)
                pe.wait_ge(S["loaded"], LOADED)

                def refill(p, chunk, first):
                    for m in range(ITEMS):
                        array, pick, j = item(m)
                        pe.wait_ge(S["bc_stored"], first + (m + 1))
                        nc.tensor.matmul(bc_ps[:, m % 2, :], pick[:, 2 * p + j, :], xd_parts[:, bass.ds(chunk * CH, CH)],
                                         start=True, stop=True).then_inc(S["bc_ready"], 1)

                def project_dt(k, i, chunk):
                    nc.tensor.matmul(dt_ps[:], w_dt[:, i, :], xd[:, bass.ds(chunk * CH, CH)], start=True,
                                     stop=True).then_inc(S["dt_ready"], 1)

                project_dt(0, 0, 0)
                for p in range(PAIRS_N - 1):
                    refill(p, 0, ITEMS * p)
                pe.wait_ge(S["diag"], NT)
                with pe.Fori(0, NCH) as c:
                    cols = bass.ds(c * CH, CH)

                    def reduce_tile(i):
                        k = c * NT + i
                        pe.wait_ge(S["yg_ready"], k + 3)
                        if i == 0:
                            pe.wait_ge(S["red_stored"], c + 1)
                        nc.tensor.matmul(red_ps[:], w_red[:, i, :], yg[:], start=(i == 0),
                                         stop=(i == NT - 1)).then_inc(S["red_ready"], 1)

                    for i in range(NT):
                        k = c * NT + i
                        pe.wait_ge(S["zg_ready"], k + 1)
                        nc.tensor.matmul(z_ps[:], w_z[:, i, :], xn[:, cols], start=True, stop=True).then_inc(S["z_ready"], 1)
                        pe.wait_ge(S["sig_ready"], k + 1)
                        project_dt(k + 1, (i + 1) % NT, c + (i + 1) // NT)
                        pe.wait_ge(S["yg_ready"], k + 1)
                        nc.tensor.matmul(y_ps[:, i % 2, :], d_diag[:, i, :], xc[:, i, cols], start=True, stop=False)
                        for p in range(PAIRS_N):
                            pe.wait_ge(S["qs_ready"], c * PER + (i * PAIRS_N + p + 3))
                            for j in range(2):
                                mm = nc.tensor.matmul(y_ps[:, i % 2, :], ident[:], qs[p % 2][:, j, :], start=False,
                                                      stop=(p == PAIRS_N - 1 and j == 1))
                            mm.then_inc(S["y_ready"], 1)
                            if i and p == 1:
                                reduce_tile(i - 1)
                            if i == 0 and p == 0:
                                refill(PAIRS_N - 1, c, c * ROWS + (PAIRS_N - 1) * ITEMS)
                            if i == NT - 1 and p < PAIRS_N - 1:
                                refill(p, c + 1, c * ROWS + (PAIRS_N + p) * ITEMS)
                    reduce_tile(NT - 1)

            @block.scalar
            def _(act):
                act.sem_inc(S["bc_stored"], 2)
                act.sem_inc(S["zg_ready"], 1)
                act.sem_inc(S["red_stored"], 1)
                act.wait_ge(S["loaded"], LOADED)

                def refill(p, first):
                    for m in range(ITEMS):
                        array, pick, j = item(m)
                        act.wait_ge(S["bc_ready"], first + (m + 1))
                        nc.scalar.activation(array[:, 2 * p + j, :], bc_ps[:, m % 2, :], ACT.Copy).then_inc(S["bc_stored"], 1)

                def gate(k, i):
                    act.wait_ge(S["dt_ready"], k + 1)
                    nc.scalar.activation(sig[i % 2][:], dt_ps[:], ACT.Sigmoid,
                                         bias=dt_b[:, i:i + 1]).then_inc(S["sig_ready"], 1)

                gate(0, 0)
                for p in range(PAIRS_N - 1):
                    refill(p, ITEMS * p)
                with act.Fori(0, NCH) as c:
                    cols = bass.ds(c * CH, CH)
                    for i in range(NT):
                        k = c * NT + i
                        for p in range(PAIRS_N):
                            n = c * PER + (i * PAIRS_N + p)
                            if p < PA:
                                act.wait_ge(S["a_ready"], k * PA + (p + 1))
                            else:
                                act.wait_ge(S["last_a_ready"], k + 1)
                            nc.scalar.activation(a_[p % 2][:], a_[p % 2][:], ACT.Copy, bias=1.0).then_inc(S["a1_ready"], 1)
                            if i == NT - 1 and p >= 1:
                                act.wait_ge(S["b_ready"], n)
                                act.wait_ge(S["qs_ready"], n + 2)
                                refill(p - 1, c * ROWS + (PAIRS_N + p - 1) * ITEMS)
                            if p == 1:
                                gate(k + 1, (i + 1) % NT)
                                act.wait_ge(S["z_ready"], k + 1)
                                act.wait_ge(S["yg_ready"], k + 1)
                                nc.scalar.activation(zg[i % 2][:], z_ps[:], ACT.Silu).then_inc(S["zg_ready"], 1)
                            if i == 0 and p == 1:
                                act.wait_ge(S["b_ready"], n)
                                act.wait_ge(S["qs_ready"], c * PER + 2)
                                refill(PAIRS_N - 1, c * ROWS + (PAIRS_N - 1) * ITEMS)
                    act.wait_ge(S["red_ready"], c * NT + (NT + 1))
                    nc.scalar.activation(h_red[:, cols], red_ps[:], ACT.Copy).then_inc(S["red_stored"], 1)

            @block.vector
            def _(dve):
                V = nc.vector
                dve.sem_inc(S["st_ready"], 2)
                dve.sem_inc(S["qs_ready"], 2)
                dve.sem_inc(S["yg_ready"], 2)
                dve.wait_ge(S["loaded"], LOADED)
                for i in range(NT):
                    V.tensor_scalar(d_diag[:, i, :], ident[:], d_par[:, i:i + 1], None, ALU.mult).then_inc(S["diag"], 1)
                dve.wait_ge(S["zero_carry"], 1)

                xc_flat = flat(xc[:])

                def make_dx(k, i, chunk):
                    dve.wait_ge(S["sig_ready"], k + 1)
                    V.tensor_tensor(dx[i % 2][:], sig[i % 2][:], xc_flat[:, bass.ds(chunk * CH + i * T, CH)],
                                    ALU.mult).then_inc(S["dx_ready"], 1)

                def make_a(chunk, i, p):
                    if i == 0:
                        dve.wait_ge(S["bc_stored"], chunk * ROWS + (ITEMS * (p + 1) + 2))
                    V.tensor_tensor(a_[p % 2][:], sig[i % 2][:].unsqueeze(1).broadcast_to([D, 2, CH]),
                                    nk2[:, 2 * p:2 * p + 2, :], ALU.mult).then_inc(S["a_ready"], 1)

                make_dx(0, 0, 0)
                make_a(0, 0, 0)
                with dve.Fori(0, NCH) as c:
                    def gate_tile(i):
                        k = c * NT + i
                        dve.wait_ge(S["y_ready"], k * PAIRS_N + (PAIRS_N + 2))
                        dve.wait_ge(S["zg_ready"], k + 2)
                        dve.wait_ge(S["red_ready"], k + 1)
                        V.tensor_tensor(yg[:], y_ps[:, i % 2, :], zg[i % 2][:], ALU.mult).then_inc(S["yg_ready"], 1)

                    for i in range(NT):
                        k = c * NT + i
                        for p in range(PAIRS_N):
                            n = c * PER + (i * PAIRS_N + p)
                            if p + 1 < PA:
                                make_a(c, i, p + 1)
                            elif p + 1 == PA:
                                make_dx(k + 1, (i + 1) % NT, c + (i + 1) // NT)
                            else:
                                make_a(c + (i + 1) // NT, (i + 1) % NT, 0)
                            dve.wait_ge(S["a1_ready"], n + 1)
                            dve.wait_ge(S["b_ready"], n + 1)
                            for j in range(2):
                                x = V.tensor_tensor_scan(st[p % 2][:, j, :], a_[p % 2][:, j, :], b_[p % 2][:, j, :],
                                                         carry[:, i, 2 * p + j:2 * p + j + 1], ALU.mult, ALU.add)
                            x.then_inc(S["st_ready"], 1)
                            dve.wait_ge(S["st_ready"], n + 3)
                            V.tensor_copy(carry[:, i, 2 * p:2 * p + 2], st[p % 2][:, :, CH - 1]).then_inc(S["carry_ready"], 1)
                            dve.wait_ge(S["y_ready"], n + 1)
                            if i == 0 and p == PAIRS_N - 1:
                                dve.wait_ge(S["bc_stored"], c * ROWS + (ROWS + 2))
                            V.tensor_tensor(qs[p % 2][:], st[p % 2][:], qq[:, 2 * p:2 * p + 2, :],
                                            ALU.mult).then_inc(S["qs_ready"], 1)
                            if i and p == 0:
                                gate_tile(i - 1)
                    gate_tile(NT - 1)


def gains(nc, dram, xn, gain, beside):
    W = D + 2 * WIN
    with Scope(nc, "gn") as s:
        w_q, w_k = s.sb("w_q", [D, D]), s.sb("w_k", [D, D])
        ident = s.sb("ident", [D, D])
        ones = s.sb("ones", [D, D])
        band = s.sb("band", [D, W])
        qg, kg = s.sb("qg", [D, T]), s.sb("kg", [D, T + 2 * WIN])
        sc = s.sb("sc", [D, TT, W])
        mx, nmx, tot, inv, gcol = (s.sb(n, [D, TT]) for n in ("mx", "nmx", "tot", "inv", "gcol"))
        junk = s.sb("junk", [D, TT, W])
        diag = [s.sb(f"diag{b}", [D, D]) for b in range(2)]
        two = s.sb("two", [D, 1])
        pr_ps = s.ps("pr", [D, 2, CH])
        sc_ps = s.ps("sc", [D, 2, CH])
        g_ps = s.ps("g", [D, NCH, CH])
        S = {n: s.sem(n) for n in ("loaded set pr_ready pr_stored edges sc_ready sc_masked mx_ready nmx_ready ex_ready "
                                   "inv_ready g_ready diag_ready out_ready stored").split()}
        with nc.Block() as block:
            @block.sync
            def _(sp):
                for dst, src in ((w_q, "gn_q"), (w_k, "gn_k"), (ident, "ident"), (band, "gn_band")):
                    sp.dma_start(dst[:], dram[src]).then_inc(S["loaded"], 16)
                beside(sp)

            @block.gpsimd
            def _(pool):
                pool.memset(ones[:], 1.0).then_inc(S["set"], 1)
                pool.memset(two[:], -2.0).then_inc(S["set"], 1)

            @block.tensor
            def _(pe):
                pe.wait_ge(S["loaded"], 64)
                for n in range(2 * NCH):
                    c = n // 2
                    if n >= 2:
                        pe.wait_ge(S["pr_stored"], n - 1)
                    nc.tensor.matmul(pr_ps[:, n % 2, :], (w_q, w_k)[n % 2][:], xn[:, c * CH:(c + 1) * CH], start=True,
                                     stop=True).then_inc(S["pr_ready"], 1)
                pe.wait_ge(S["pr_stored"], 2 * NCH)
                pe.wait_ge(S["edges"], 1)
                for t in range(TT):
                    if t >= 2:
                        pe.wait_ge(S["sc_masked"], t - 1)
                    nc.tensor.matmul(sc_ps[:, t % 2, 0:W], qg[:, t * D:(t + 1) * D], kg[:, t * D:t * D + W], start=True,
                                     stop=True).then_inc(S["sc_ready"], 1)
                pe.wait_ge(S["set"], 2)
                for t in range(TT):
                    pe.wait_ge(S["diag_ready"], t + 1)
                    nc.tensor.matmul(g_ps[:, t // 4, (t % 4) * D:(t % 4 + 1) * D], ones[:], diag[t % 2][:],
                                     start=(t % 4 == 0), stop=(t % 4 == 3), skip_group_check=True).then_inc(S["out_ready"], 1)

            @block.scalar
            def _(act):
                for n in range(2 * NCH):
                    c = n // 2
                    act.wait_ge(S["pr_ready"], n + 1)
                    dst = kg[:, WIN + c * CH:WIN + (c + 1) * CH] if n % 2 else qg[:, c * CH:(c + 1) * CH]
                    nc.scalar.activation(dst, pr_ps[:, n % 2, :], ACT.Copy).then_inc(S["pr_stored"], 1)
                for t in range(TT):
                    act.wait_ge(S["nmx_ready"], 1)
                    x = nc.scalar.activation(junk[:, t, :], sc[:, t, :], ACT.Exp, scale=float(D) ** -0.5,
                                             bias=nmx[:, t:t + 1], accum_out=tot[:, t:t + 1])
                x.then_inc(S["ex_ready"], 1)
                act.wait_ge(S["inv_ready"], 1)
                act.wait_ge(S["set"], 2)
                nc.scalar.activation(gcol[:], inv[:], ACT.Sigmoid, scale=4.0, bias=two[:]).then_inc(S["g_ready"], 1)

            @block.vector
            def _(dve):
                V = nc.vector
                dve.wait_ge(S["pr_stored"], 2 * NCH)
                V.tensor_copy(kg[:, 0:WIN], kg[:, WIN:WIN + 1].broadcast_to([D, WIN]))
                V.tensor_copy(kg[:, WIN + T:], kg[:, WIN + T - 1:WIN + T].broadcast_to([D, WIN])).then_inc(S["edges"], 1)
                dve.wait_ge(S["loaded"], 64)
                for t in range(TT):
                    dve.wait_ge(S["sc_ready"], t + 1)
                    V.tensor_tensor(sc[:, t, :], sc_ps[:, t % 2, 0:W], band[:], ALU.add).then_inc(S["sc_masked"], 1)
                dve.wait_ge(S["sc_masked"], TT)
                V.reduce_max(mx[:], sc[:], AX_X).then_inc(S["mx_ready"], 1)
                dve.wait_ge(S["mx_ready"], 1)
                V.tensor_scalar(nmx[:], mx[:], -float(D) ** -0.5, None, ALU.mult).then_inc(S["nmx_ready"], 1)
                dve.wait_ge(S["ex_ready"], 1)
                V.reciprocal(inv[:], tot[:]).then_inc(S["inv_ready"], 1)
                dve.wait_ge(S["g_ready"], 1)
                for t in range(TT):
                    if t >= 2:
                        dve.wait_ge(S["out_ready"], t - 1)
                    V.tensor_scalar(diag[t % 2][:], ident[:], gcol[:, t:t + 1], None, ALU.mult).then_inc(S["diag_ready"], 1)
                for c in range(NCH):
                    dve.wait_ge(S["out_ready"], TT)
                    V.tensor_copy(gain[:, c * CH:(c + 1) * CH], g_ps[:, c, :]).then_inc(S["stored"], 1)


def mix(nc, dram, h_red, hidden, gain, h):
    with Scope(nc, "mx") as s:
        w = s.sb("w", [D, D])
        m = s.sb("m", [D, T])
        ps = s.ps("out", [D, NCH, CH])
        S = {n: s.sem(n) for n in "loaded diff scaled mixed out_ready added".split()}
        with nc.Block() as block:
            @block.sync
            def _(sp):
                sp.dma_start(w[:], dram["qnet"]).then_inc(S["loaded"], 16)

            @block.tensor
            def _(pe):
                pe.wait_ge(S["loaded"], 16)
                for c in range(NCH):
                    pe.wait_ge(S["mixed"], c + 1)
                    nc.tensor.matmul(ps[:, c, :], w[:], m[:, c * CH:(c + 1) * CH], start=True, stop=True).then_inc(S["out_ready"], 1)

            @block.vector
            def _(dve):
                V = nc.vector
                for c in range(NCH):
                    cols = slice(c * CH, (c + 1) * CH)
                    V.tensor_tensor(m[:, cols], hidden[:, cols], h_red[:, cols], ALU.subtract).then_inc(S["diff"], 1)
                    dve.wait_ge(S["diff"], c + 1)
                    V.tensor_tensor(m[:, cols], m[:, cols], gain[:, cols], ALU.mult).then_inc(S["scaled"], 1)
                    dve.wait_ge(S["scaled"], c + 1)
                    V.tensor_tensor(m[:, cols], m[:, cols], h_red[:, cols], ALU.add).then_inc(S["mixed"], 1)
                for c in range(NCH):
                    cols = slice(c * CH, (c + 1) * CH)
                    dve.wait_ge(S["out_ready"], c + 1)
                    V.tensor_tensor(h[:, cols], h[:, cols], ps[:, c, :], ALU.add).then_inc(S["added"], 1)


def lay_out_lh(inp):
    a = {k: np.asarray(v) for k, v in inp.items()}
    w_in = a["L1_attn_in_proj_w"]
    DI = NT * D
    by_tile = lambda w: np.ascontiguousarray(w.reshape(NT, D, -1).transpose(2, 0, 1).reshape(w.shape[1], NT * D))
    col = lambda v: np.ascontiguousarray(v.reshape(NT, D).T)
    xp = a["L1_attn_x_proj_w"]
    w_x = np.zeros((D, NT, XD), np.float32)
    for j in range(3):
        for copy in range(3 if j else 1):
            at = 32 * j + NS * copy
            w_x[:, :, at:at + NS] = xp[NS * j:NS * (j + 1)].reshape(NS, NT, D).transpose(2, 1, 0)
    w_dt = np.zeros((XD, NT * D), np.float32)
    w_dt[:NS] = by_tile(a["L1_attn_dt_head_w"])
    w_dt[NS] = -1.0
    pick = np.zeros((3, XD, NS, D), np.float32)
    for n in range(NS):
        for x in range(3):
            for part in range(3):
                pick[x, 32 * (x + 1) + NS * part + n, n] = 1.0
    masks = np.zeros((XD, 2), np.float32)
    for x in range(1, 4):
        masks[32 * x + NS:32 * x + K3, 0] = -1.0
        masks[32 * x + 2 * NS:32 * x + K3, 1] = -1.0
    spread = np.zeros((D, NCH, XD), np.float32)
    for c in range(NCH):
        spread[32 * c:32 * c + 32, c] = 1.0 / 32
    sum_k = np.zeros((XD, D // NCH), np.float32)
    sum_k[32:32 + NS] = 1.0
    W = D + 2 * WIN
    off = np.arange(W)[None, :] - np.arange(D)[:, None]
    band = np.where((off >= 0) & (off <= 2 * WIN), 0.0, -1e30).astype(np.float32)
    return {
        "lh_in": np.ascontiguousarray(w_in[:DI].reshape(NT, D, D).transpose(0, 2, 1).reshape(NT * D, D)),
        "lh_z": by_tile(w_in[DI:]), "lh_x": w_x.reshape(D, NT * XD),
        "lh_conv_w": np.ascontiguousarray(a["L1_attn_conv_w"].reshape(NT, D, 3).transpose(1, 0, 2).reshape(D, NT * 3)),
        "lh_conv_b": col(a["L1_attn_conv_b"]), "lh_dt": w_dt,
        "lh_dt_b": col(a["L1_attn_dt_head_b"]), "lh_d": col(a["L1_attn_D_param"]),
        "lh_red": np.ascontiguousarray(a["L1_attn_reduce_w"].reshape(D, NT, D).transpose(2, 1, 0).reshape(D, NT * D)),
        "lh_pick_k": pick[0].reshape(XD, NS * D), "lh_pick_q": pick[1].reshape(XD, NS * D),
        "lh_pick_nk2": pick[2].reshape(XD, NS * D), "lh_sum_k": sum_k, "lh_masks": masks,
        "lh_spread": spread.reshape(D, NCH * XD),
        "gn_q": np.ascontiguousarray(a["L1_attn_gain_q_w"].T), "gn_k": np.ascontiguousarray(a["L1_attn_gain_k_w"].T),
        "gn_band": band, "qnet": np.ascontiguousarray(a["L1_attn_qnet_w"].T),
    }


def tower(nc, dram, out):
    with Scope(nc, "top") as s:
        h = s.sb("h", [D, T])
        ones_over_d = s.sb("ones_over_d", [D, D])
        norms = s.sb("norms", [D, 6])
        loaded, stored = s.sem("loaded"), s.sem("stored")
        with nc.Block() as block:
            @block.sync
            def _(sp):
                sp.dma_start(ones_over_d[:], dram["ones_over_d"]).then_inc(loaded, 16)
                for n, name in enumerate(("att_gamma", "att_beta", "ln1_w", "ln1_b", "post_w", "post_b")):
                    sp.dma_start(norms[:, n:n + 1], dram[name]).then_inc(loaded, 16)
                sp.wait_ge(loaded, 16 * 7)
        embed(nc, dram["ids"], dram["table"], h)

        with Scope(nc, "l0a") as a:
            xn = a.sb("xn", [D, HT + SLOTS * HT])
            ao = a.sb("ao", [D, HT + T])
            layer_norm(nc, "ln_a", h, xn[:, HT:], ones_over_d, 1e-5)
            attention0(nc, dram, xn, ao)
            layer_norm(nc, "ln_b", ao[:, HT:], h, ones_over_d, 1e-5, gamma=norms[:, 0:1], beta=norms[:, 1:2], add_to=h)

        with Scope(nc, "l0f") as a:
            xn = a.sb("xn", [D, T])
            comb_a, comb_b = a.sb("comb_a", [D, T], BF16), a.sb("comb_b", [D, T], BF16)
            layer_norm(nc, "ln_c", h, xn, ones_over_d, 1e-5)
            router(nc, dram, xn, comb_a, comb_b)
            experts(nc, dram, xn, h, comb_a, comb_b)

        with Scope(nc, "l1a") as a:
            xn = a.sb("xn", [D, T])
            h_red = a.sb("h_red", [D, T])
            layer_norm(nc, "ln_d", h, h_red, ones_over_d, 1e-5)
            layer_norm(nc, "ln_e", h_red, xn, ones_over_d, 1e-6, gamma=norms[:, 2:3], beta=norms[:, 3:4])
            with Scope(nc, "l1s") as b:
                xc = b.sb("xc", [D, NT, T])
                xd = b.sb("xd", [XD, T + CH])
                xd_parts = b.sb("xd_parts", [XD, T + CH], BF16)
                picks = [b.sb(f"pick_{x}", [XD, NS, D], BF16) for x in ("nk2", "k", "q")]
                longhorn_inputs(nc, dram, xn, xc, xd, xd_parts, picks)
                longhorn_scan(nc, dram, xn, xc, xd, xd_parts, picks, h_red)
            gain = a.sb("gain", [D, T])
            hidden = a.sb("hidden", [D, T])
            with Scope(nc, "l1t") as b:
                kT, qT = b.sb("kT", [D, T + 9 * MB]), b.sb("qT", [D, T + 8 * MB])
                rows = b.sb("rows", [RW, 2, NMB + 2 * QUAD, DH])
                eta = b.sb("eta", [RW, NMB + 2 * QUAD])
                zbar = b.sb("zbar", [D, NMB + 1, DH])
                raw = b.sb("raw", [D, T])
                turned = nc.dram_tensor("turned_scratch", [2, T, D], F32, kind="Internal").ap()
                written, rows_read = (b.sem("even_written"), b.sem("odd_written")), b.sem("rows_read")
                constants, constants_loaded = chain_constants(b), b.sem("constants_loaded")

                def fetch_for_chain(sp):
                    fetch_rows(sp, turned, rows, written, rows_read)
                    fetch_constants(sp, dram, constants, constants_loaded)

                ttt_project(nc, dram, xn, kT, qT, eta, turned, written)
                gains(nc, dram, xn, gain, beside=fetch_for_chain)
                ttt_chain(nc, constants, constants_loaded, kT, qT, rows, rows_read, eta, zbar)
                ttt_finish(nc, dram, qT, zbar, raw)
                layer_norm(nc, "ln_f", raw, hidden, ones_over_d, TTT_EPS, gamma=norms[:, 4:5], beta=norms[:, 5:6])
            mix(nc, dram, h_red, hidden, gain, h)

        with Scope(nc, "l1f") as a:
            xn = a.sb("xn", [D, T + D])
            layer_norm(nc, "ln_g", h, xn, ones_over_d, 1e-5)
            product_keys(nc, dram, xn, h)

        turn_out(nc, dram["ident"], h, out)


def turn_out(nc, ident_dram, h, out):
    with Scope(nc, "out") as s:
        ident = s.sb("ident", [D, D])
        tokens = s.sb("tokens", [D, TT, D])
        ps = s.ps("turn", [D, NCH, CH])
        loaded, turned, copied, stored = (s.sem(n) for n in ("loaded", "turned", "copied", "stored"))
        with nc.Block() as block:
            @block.sync
            def _(sp):
                sp.dma_start(ident[:], ident_dram).then_inc(loaded, 16)
                for c in range(NCH):
                    sp.wait_ge(copied, c + 1)
                    sp.dma_start(out[c * CH:(c + 1) * CH, :].rearrange("(q p) d -> p q d", p=D),
                                 tokens[:, 4 * c:4 * c + 4, :]).then_inc(stored, 16)
                sp.wait_ge(stored, 16 * NCH)

            @block.tensor
            def _(pe):
                pe.wait_ge(loaded, 16)
                for c in range(NCH):
                    for q in range(4):
                        t = 4 * c + q
                        mm = nc.tensor.transpose(ps[:, c, q * D:(q + 1) * D], h[:, t * D:(t + 1) * D], ident[:])
                    mm.then_inc(turned, 1)

            @block.vector
            def _(dve):
                for c in range(NCH):
                    dve.wait_ge(turned, c + 1)
                    nc.vector.tensor_copy(tokens[:, 4 * c:4 * c + 4, :].rearrange("p a b -> p (a b)"),
                                          ps[:, c, :]).then_inc(copied, 1)


def kernel(**inputs):
    import concourse.bacc as _bacc
    from concourse.bass_utils import run_bass_kernel_spmd as _run

    laid_out = {}
    for lay_out in (lay_out_attention, lay_out_moe, lay_out_lh, lay_out_ttt, lay_out_pk):
        laid_out.update(lay_out(inputs))
    nc = _bacc.Bacc("TRN2", target_bir_lowering=False, num_devices=1)
    arrays, dram = {}, {}
    for name, a in laid_out.items():
        arrays[f"in_{name}"] = np.ascontiguousarray(a)
        dram[name] = nc.dram_tensor(f"in_{name}", a.shape, mybir.dt.from_np(a.dtype), kind="ExternalInput").ap()
    out = nc.dram_tensor("out_0", (T, D), F32, kind="ExternalOutput").ap()
    tower(nc, dram, out)
    r = _run(nc, [arrays], core_ids=[0])
    return r.results[0]["out_0"].reshape(1, T, D)
```
